# Optimizing a Trainium2 kernel written in Bass

```python
import numpy as np
import jax
import jax.numpy as jnp

def _softmax(x, axis=-1):
    return jax.nn.softmax(x, axis=axis)

def _gelu(x):
    return jax.nn.gelu(x, approximate=True)

def _silu(x):
    return jax.nn.silu(x)

def _sigmoid(x):
    return jax.nn.sigmoid(x)

def _layernorm(x, axis=-1, eps=1e-05):
    m = jnp.mean(x, axis=axis, keepdims=True)
    v = jnp.var(x, axis=axis, keepdims=True)
    return (x - m) / jnp.sqrt(v + eps)

def _scatter_add(tgt, idx, src, axis=0):
    return tgt.at[idx].add(src)

def _segment_sum(src, seg, n):
    return jax.ops.segment_sum(src, seg, n)
kernel_name = 'mk_adaln_d4_jaxref_r8_e17499'

def setup_inputs(seed: int=0):
    np.random.seed(seed)
    _w = jnp.asarray

    def _L0_attn_setup():
        import jax, jax.numpy as jnp
        import numpy as np
        N_HEADS = 16
        INPUT_DIM = 128
        EMBED_DIM = 128
        KEY_DIM = EMBED_DIM // N_HEADS
        BATCH = 4
        SEQ = 256

        def _uniform(key, shape, bound):
            return jax.random.uniform(key, shape, jnp.float32, -bound, bound)
        key = jax.random.key(seed)
        kq, k1, k2, k3, k4 = jax.random.split(key, 5)
        stdv_k = 1.0 / np.sqrt(KEY_DIM)
        stdv_e = 1.0 / np.sqrt(EMBED_DIM)
        return {'q': jax.random.normal(kq, (BATCH, SEQ, INPUT_DIM), jnp.float32), 'W_query': _uniform(k1, (N_HEADS, INPUT_DIM, KEY_DIM), stdv_k), 'W_key': _uniform(k2, (N_HEADS, INPUT_DIM, KEY_DIM), stdv_k), 'W_val': _uniform(k3, (N_HEADS, INPUT_DIM, KEY_DIM), stdv_k), 'W_out': _uniform(k4, (N_HEADS, KEY_DIM, EMBED_DIM), stdv_e)}
    _L0_attn_in = _L0_attn_setup()

    def _L0_ffn_setup():
        import jax, jax.numpy as jnp
        import numpy as np
        D_MODEL = 128
        NUM_SLOTS = 64
        TOP_K = 8
        B, T = (4, 512)

        def _forward(x, slot_init, slot_scale, w1, b1, w2, b2, gru_wih, gru_whh, gru_bih, gru_bhh, wv, bv, wo, bo, tau):
            Bn, Tn, D = x.shape
            Sn = slot_init.shape[0]
            S = jnp.broadcast_to((slot_init * slot_scale)[None], (Bn, Sn, D)).astype(x.dtype)
            slot_mean = S.mean(axis=1, keepdims=True)
            ctx = jnp.concatenate([x, jnp.broadcast_to(slot_mean, x.shape)], axis=-1)
            h = jax.nn.gelu(ctx @ w1.T + b1, approximate=False)
            route_logits = (h @ w2.T + b2) / (jnp.abs(tau) + 0.1)
            topk_vals, topk_idx = jax.lax.top_k(route_logits, TOP_K)
            topk_w = jax.nn.softmax(topk_vals, axis=-1)
            alpha = jnp.sum(topk_w[..., None] * jax.nn.one_hot(topk_idx, Sn, dtype=x.dtype), axis=-2)
            slot_input = jnp.einsum('bts,btd->bsd', alpha, x)
            slot_wsum = alpha.sum(axis=1) + 1e-08
            gi = (slot_input / slot_wsum[..., None]).reshape(Bn * Sn, D)
            hs = S.reshape(Bn * Sn, D)
            gx = gi @ gru_wih.T + gru_bih
            gh = hs @ gru_whh.T + gru_bhh
            xr, xz, xn = jnp.split(gx, 3, axis=-1)
            hr, hz, hn = jnp.split(gh, 3, axis=-1)
            r = jax.nn.sigmoid(xr + hr)
            z = jax.nn.sigmoid(xz + hz)
            n = jnp.tanh(xn + r * hn)
            h_new = (1.0 - z) * n + z * hs
            S_new = h_new.reshape(Bn, Sn, D)
            slot_values = S_new @ wv.T + bv
            out = jnp.einsum('bts,bsd->btd', alpha, slot_values)
            return out @ wo.T + bo
        key = jax.random.key(seed)
        ks = jax.random.split(key, 16)
        D, S = (D_MODEL, NUM_SLOTS)
        H = D // 2
        sc = lambda fan_in: 1.0 / np.sqrt(fan_in)
        inp = {'x': jax.random.normal(ks[0], (B, T, D), dtype=jnp.float32), 'slot_init': jax.random.normal(ks[1], (S, D), dtype=jnp.float32) * 0.1, 'slot_scale': jnp.ones((S, 1), dtype=jnp.float32), 'w1': jax.random.normal(ks[2], (H, 2 * D), dtype=jnp.float32) * sc(2 * D), 'b1': jnp.zeros((H,), dtype=jnp.float32), 'w2': jax.random.normal(ks[3], (S, H), dtype=jnp.float32) * sc(H), 'b2': jnp.zeros((S,), dtype=jnp.float32), 'gru_wih': jax.random.normal(ks[4], (3 * D, D), dtype=jnp.float32) * sc(D), 'gru_whh': jax.random.normal(ks[5], (3 * D, D), dtype=jnp.float32) * sc(D), 'gru_bih': jnp.zeros((3 * D,), dtype=jnp.float32), 'gru_bhh': jnp.zeros((3 * D,), dtype=jnp.float32), 'wv': jax.random.normal(ks[6], (D, D), dtype=jnp.float32) * sc(D), 'bv': jnp.zeros((D,), dtype=jnp.float32), 'wo': jax.random.normal(ks[7], (D, D), dtype=jnp.float32) * sc(D), 'bo': jnp.zeros((D,), dtype=jnp.float32), 'tau': jnp.ones((1,), dtype=jnp.float32)}
        return inp
    _L0_ffn_in = _L0_ffn_setup()
    _L0_c = _w((lambda *s: np.random.randn(*s).astype(np.float32) * 0.05)(1, 128))
    _L0_wmod = _w((lambda *s: np.random.randn(*s).astype(np.float32) * 0.05)(128, 6 * 128) * 128 ** (-0.5))

    def _L1_attn_setup():
        import jax, jax.numpy as jnp
        import numpy as np
        B, L, D = (8, 256, 128)
        LN_EPS = 1e-05
        L2_EPS = 1e-12

        def _delta_scan(q, k, v, beta):

            def step(S, inp):
                qt, kt, vt, bt = inp
                v_adj = bt * (vt - kt @ S)
                S = S + kt[:, None] * v_adj[None, :]
                return (S, qt @ S)
            S0 = jnp.zeros((D, D), dtype=q.dtype)
            _, o = jax.lax.scan(step, S0, (q, k, v, beta))
            return o
        key = jax.random.key(seed)
        ks = jax.random.split(key, 5)
        s = 1.0 / np.sqrt(D)
        x = jax.random.normal(ks[0], (B, L, D), dtype=jnp.float32)
        Wq = jax.random.normal(ks[1], (D, D), dtype=jnp.float32) * s
        Wk = jax.random.normal(ks[2], (D, D), dtype=jnp.float32) * s
        Wv = jax.random.normal(ks[3], (D, D), dtype=jnp.float32) * s
        Wb = jax.random.normal(ks[4], (D,), dtype=jnp.float32) * s
        ln_g = jnp.ones((D,), dtype=jnp.float32)
        ln_b = jnp.zeros((D,), dtype=jnp.float32)
        return {'x': x, 'Wq': Wq, 'Wk': Wk, 'Wv': Wv, 'Wb': Wb, 'ln_g': ln_g, 'ln_b': ln_b}
    _L1_attn_in = _L1_attn_setup()

    def _L1_ffn_setup():
        import jax, jax.numpy as jnp
        import numpy as np
        B, S, D, O, E = (8, 512, 128, 128, 64)
        key = jax.random.key(seed)
        kx, kgw, kgb, kew, keb = jax.random.split(key, 5)
        x = jax.random.normal(kx, (B, S, D), dtype=jnp.float32)
        gate_w = jax.random.normal(kgw, (E, D), dtype=jnp.float32) * 0.02
        gate_b = jnp.zeros((E,), dtype=jnp.float32)
        expert_w = jax.random.normal(kew, (E, D, O), dtype=jnp.float32) * 0.02
        expert_b = jnp.zeros((E, O), dtype=jnp.float32)
        return {'x': x, 'gate_w': gate_w, 'gate_b': gate_b, 'expert_w': expert_w, 'expert_b': expert_b}
    _L1_ffn_in = _L1_ffn_setup()
    _L1_c = _w((lambda *s: np.random.randn(*s).astype(np.float32) * 0.05)(1, 128))
    _L1_wmod = _w((lambda *s: np.random.randn(*s).astype(np.float32) * 0.05)(128, 6 * 128) * 128 ** (-0.5))

    def _L2_attn_setup():
        import jax, jax.numpy as jnp
        import numpy as np
        TAU_INV = 0.5
        V_TH = 1.0
        DECAY = 0.9
        ATAN_ALPHA = 2.0
        LN_EPS = 1e-05

        @jax.custom_vjp
        def spike(x):
            return (x >= 0.0).astype(x.dtype)

        def _spike_fwd(x):
            return (spike(x), x)

        def _spike_bwd(x, g):
            sg = ATAN_ALPHA * 0.5 / (1.0 + (jnp.pi * 0.5 * ATAN_ALPHA * x) ** 2)
            return (g * sg,)
        spike.defvjp(_spike_fwd, _spike_bwd)

        def lif_step(v, x_t):
            v = v + (x_t - v) * TAU_INV
            s = spike(v - V_TH)
            v = v * (1.0 - s)
            return (v, s)

        def lif_scan(x):
            xT = jnp.swapaxes(x, 0, 1)
            _, sT = jax.lax.scan(lif_step, jnp.zeros_like(xT[0]), xT)
            return jnp.swapaxes(sT, 0, 1)

        def layernorm(x, g, b):
            mu = jnp.mean(x, axis=-1, keepdims=True)
            var = jnp.mean((x - mu) ** 2, axis=-1, keepdims=True)
            return (x - mu) * jax.lax.rsqrt(var + LN_EPS) * g + b

        def srwkv_forward(x, Wr, Wk, Wv, Wo, W1, b1, W2, b2, ln1_g, ln1_b, ln2_g, ln2_b):
            residual = x
            R = jnp.einsum('btd,ed->bte', x, Wr)
            K = jnp.einsum('btd,ed->bte', x, Wk)
            V = jnp.einsum('btd,ed->bte', x, Wv)
            RT = jnp.swapaxes(R, 0, 1)
            KT = jnp.swapaxes(K, 0, 1)
            VT = jnp.swapaxes(V, 0, 1)
            B, _, D = x.shape
            z = jnp.zeros((B, D), dtype=x.dtype)

            def step(carry, inp):
                h, vr, vk, vv = carry
                r_in, k_in, v_in = inp
                vr, r = lif_step(vr, r_in)
                vk, k = lif_step(vk, k_in)
                vv, v = lif_step(vv, v_in)
                h = h * DECAY + k * v
                y = r * h
                return ((h, vr, vk, vv), y)
            _, yT = jax.lax.scan(step, (z, z, z, z), (RT, KT, VT))
            attn_out = jnp.einsum('tbd,ed->bte', yT, Wo)
            x1 = layernorm(residual + attn_out, ln1_g, ln1_b)
            h1 = jnp.einsum('btd,fd->btf', x1, W1) + b1
            s1 = lif_scan(h1)
            h2 = jnp.einsum('btf,df->btd', s1, W2) + b2
            ffn_out = lif_scan(h2)
            return layernorm(x1 + ffn_out, ln2_g, ln2_b)
        key = jax.random.key(seed)
        ks = jax.random.split(key, 8)
        B, T, D, F = (8, 128, 128, 512)
        s_d = 1.0 / np.sqrt(D)
        s_f = 1.0 / np.sqrt(F)
        return {'x': jax.random.normal(ks[0], (B, T, D), jnp.float32), 'Wr': jax.random.normal(ks[1], (D, D), jnp.float32) * s_d, 'Wk': jax.random.normal(ks[2], (D, D), jnp.float32) * s_d, 'Wv': jax.random.normal(ks[3], (D, D), jnp.float32) * s_d, 'Wo': jax.random.normal(ks[4], (D, D), jnp.float32) * s_d, 'W1': jax.random.normal(ks[5], (F, D), jnp.float32) * s_d, 'b1': jnp.zeros((F,), jnp.float32), 'W2': jax.random.normal(ks[6], (D, F), jnp.float32) * s_f, 'b2': jnp.zeros((D,), jnp.float32), 'ln1_g': jnp.ones((D,), jnp.float32), 'ln1_b': jnp.zeros((D,), jnp.float32), 'ln2_g': jnp.ones((D,), jnp.float32), 'ln2_b': jnp.zeros((D,), jnp.float32)}
    _L2_attn_in = _L2_attn_setup()

    def _L2_ffn_setup():
        import jax, jax.numpy as jnp
        import numpy as np
        B, S, K, N = (8, 1024, 128, 128)
        key = jax.random.key(seed)
        k1, k2, k3, k4 = jax.random.split(key, 4)
        x = jax.random.normal(k1, (B, S, K), dtype=jnp.float32)
        CB = jnp.clip(jnp.round(jax.random.normal(k2, (N, K), dtype=jnp.float32) * 42.0), -127.0, 127.0)
        SCB = jax.random.uniform(k3, (N,), dtype=jnp.float32, minval=0.5, maxval=2.0)
        bias = jax.random.normal(k4, (N,), dtype=jnp.float32) * 0.02
        return {'x': x, 'CB': CB, 'SCB': SCB, 'bias': bias}
    _L2_ffn_in = _L2_ffn_setup()
    _L2_c = _w((lambda *s: np.random.randn(*s).astype(np.float32) * 0.05)(1, 128))
    _L2_wmod = _w((lambda *s: np.random.randn(*s).astype(np.float32) * 0.05)(128, 6 * 128) * 128 ** (-0.5))

    def _L3_attn_setup():
        import jax, jax.numpy as jnp
        import numpy as np
        D_MODEL = 128
        N_HEADS = 16
        LATENT_HEADS = 8
        LATENT_DIM = 64
        N_LATENTS = 64
        WINDOW = 32
        HEAD_DIM = D_MODEL // N_HEADS
        LAT_HD = LATENT_DIM // LATENT_HEADS
        B, S = (2, 512)

        def _pool_to_latents(x):
            Bx, Sx, C = x.shape
            chunk = max(1, Sx // N_LATENTS)
            return x.reshape(Bx, N_LATENTS, chunk, C).mean(axis=2)

        def _local_window_attn(Q, K, V):
            Bx, H, Sx, D = Q.shape
            W = WINDOW
            nb = Sx // W
            Qb = Q.reshape(Bx, H, nb, W, D)
            Kp = jnp.pad(K, ((0, 0), (0, 0), (W, 0), (0, 0))).reshape(Bx, H, nb + 1, W, D)
            Vp = jnp.pad(V, ((0, 0), (0, 0), (W, 0), (0, 0))).reshape(Bx, H, nb + 1, W, D)
            Kw = jnp.concatenate([Kp[:, :, :-1], Kp[:, :, 1:]], axis=3)
            Vw = jnp.concatenate([Vp[:, :, :-1], Vp[:, :, 1:]], axis=3)
            i = jnp.arange(W)[:, None]
            j = jnp.arange(2 * W)[None, :]
            base = (j > i) & (j <= i + W)
            blk0 = (jnp.arange(nb) > 0)[:, None, None] | (j >= W)[None, :, :]
            mask = base[None, :, :] & blk0
            sc = jnp.einsum('bhnid,bhnjd->bhnij', Qb, Kw) / np.sqrt(D).astype(np.float32)
            sc = jnp.where(mask[None, None], sc, -jnp.inf)
            p = jax.nn.softmax(sc, axis=-1)
            out = jnp.einsum('bhnij,bhnjd->bhnid', p, Vw)
            return out.reshape(Bx, H, Sx, D)
        key = jax.random.key(seed)
        ks = jax.random.split(key, 11)
        std = 0.02
        w = lambda k, shp: jax.random.normal(k, shp, jnp.float32) * std
        return {'x': jax.random.normal(ks[0], (B, S, D_MODEL), jnp.float32), 'wq': w(ks[1], (D_MODEL, D_MODEL)), 'wk': w(ks[2], (D_MODEL, D_MODEL)), 'wv': w(ks[3], (D_MODEL, D_MODEL)), 'wgq': w(ks[4], (D_MODEL, LATENT_DIM)), 'wgk': w(ks[5], (D_MODEL, LATENT_DIM)), 'wgv': w(ks[6], (D_MODEL, LATENT_DIM)), 'r_out_w': w(ks[7], (LATENT_DIM, D_MODEL)), 'gate_local_w': w(ks[8], (N_HEADS, HEAD_DIM)), 'gate_remote_w': w(ks[9], (N_HEADS, HEAD_DIM)), 'w_out': w(ks[10], (D_MODEL, D_MODEL))}
    _L3_attn_in = _L3_attn_setup()

    def _L3_ffn_setup():
        import jax, jax.numpy as jnp
        import numpy as np
        LN_EPS = 1e-05

        def layer_norm(x, g, b):
            mu = jnp.mean(x, axis=-1, keepdims=True)
            var = jnp.var(x, axis=-1, keepdims=True)
            return (x - mu) / jnp.sqrt(var + LN_EPS) * g + b

        def balanced_assignment(scores):
            T, E = scores.shape
            C = T // E
            taken = jnp.zeros((T,), dtype=bool)
            parts = []
            for e in range(E):
                s = jnp.where(taken, -jnp.inf, scores[:, e])
                _, idx = jax.lax.top_k(s, C)
                parts.append(idx)
                taken = taken.at[idx].set(True)
            return jnp.concatenate(parts)
        key = jax.random.key(seed)
        ks = jax.random.split(key, 4)
        B, S, D, F, E = (4, 256, 128, 512, 8)
        return {'x': jax.random.normal(ks[0], (B, S, D), dtype=jnp.float32), 'centroids': jax.random.normal(ks[1], (E, D), dtype=jnp.float32) * 0.1, 'ln_g': jnp.ones((D,), dtype=jnp.float32), 'ln_b': jnp.zeros((D,), dtype=jnp.float32), 'w1': jax.random.normal(ks[2], (E, D, F), dtype=jnp.float32) * 0.02, 'b1': jnp.zeros((E, F), dtype=jnp.float32), 'w2': jax.random.normal(ks[3], (E, F, D), dtype=jnp.float32) * 0.02, 'b2': jnp.zeros((E, D), dtype=jnp.float32)}
    _L3_ffn_in = _L3_ffn_setup()
    _L3_c = _w((lambda *s: np.random.randn(*s).astype(np.float32) * 0.05)(1, 128))
    _L3_wmod = _w((lambda *s: np.random.randn(*s).astype(np.float32) * 0.05)(128, 6 * 128) * 128 ** (-0.5))
    _d = {'L0_attn_q': _L0_attn_in['q'], 'L0_attn_W_query': _L0_attn_in['W_query'], 'L0_attn_W_key': _L0_attn_in['W_key'], 'L0_attn_W_val': _L0_attn_in['W_val'], 'L0_attn_W_out': _L0_attn_in['W_out'], 'L0_ffn_slot_init': _L0_ffn_in['slot_init'], 'L0_ffn_slot_scale': _L0_ffn_in['slot_scale'], 'L0_ffn_w1': _L0_ffn_in['w1'], 'L0_ffn_b1': _L0_ffn_in['b1'], 'L0_ffn_w2': _L0_ffn_in['w2'], 'L0_ffn_b2': _L0_ffn_in['b2'], 'L0_ffn_gru_wih': _L0_ffn_in['gru_wih'], 'L0_ffn_gru_whh': _L0_ffn_in['gru_whh'], 'L0_ffn_gru_bih': _L0_ffn_in['gru_bih'], 'L0_ffn_gru_bhh': _L0_ffn_in['gru_bhh'], 'L0_ffn_wv': _L0_ffn_in['wv'], 'L0_ffn_bv': _L0_ffn_in['bv'], 'L0_ffn_wo': _L0_ffn_in['wo'], 'L0_ffn_bo': _L0_ffn_in['bo'], 'L0_ffn_tau': _L0_ffn_in['tau'], 'L0_c': _L0_c, 'L0_wmod': _L0_wmod, 'L1_attn_Wq': _L1_attn_in['Wq'], 'L1_attn_Wk': _L1_attn_in['Wk'], 'L1_attn_Wv': _L1_attn_in['Wv'], 'L1_attn_Wb': _L1_attn_in['Wb'], 'L1_attn_ln_g': _L1_attn_in['ln_g'], 'L1_attn_ln_b': _L1_attn_in['ln_b'], 'L1_ffn_gate_w': _L1_ffn_in['gate_w'], 'L1_ffn_gate_b': _L1_ffn_in['gate_b'], 'L1_ffn_expert_w': _L1_ffn_in['expert_w'], 'L1_ffn_expert_b': _L1_ffn_in['expert_b'], 'L1_c': _L1_c, 'L1_wmod': _L1_wmod, 'L2_attn_Wr': _L2_attn_in['Wr'], 'L2_attn_Wk': _L2_attn_in['Wk'], 'L2_attn_Wv': _L2_attn_in['Wv'], 'L2_attn_Wo': _L2_attn_in['Wo'], 'L2_attn_W1': _L2_attn_in['W1'], 'L2_attn_b1': _L2_attn_in['b1'], 'L2_attn_W2': _L2_attn_in['W2'], 'L2_attn_b2': _L2_attn_in['b2'], 'L2_attn_ln1_g': _L2_attn_in['ln1_g'], 'L2_attn_ln1_b': _L2_attn_in['ln1_b'], 'L2_attn_ln2_g': _L2_attn_in['ln2_g'], 'L2_attn_ln2_b': _L2_attn_in['ln2_b'], 'L2_ffn_CB': _L2_ffn_in['CB'], 'L2_ffn_SCB': _L2_ffn_in['SCB'], 'L2_ffn_bias': _L2_ffn_in['bias'], 'L2_c': _L2_c, 'L2_wmod': _L2_wmod, 'L3_attn_wq': _L3_attn_in['wq'], 'L3_attn_wk': _L3_attn_in['wk'], 'L3_attn_wv': _L3_attn_in['wv'], 'L3_attn_wgq': _L3_attn_in['wgq'], 'L3_attn_wgk': _L3_attn_in['wgk'], 'L3_attn_wgv': _L3_attn_in['wgv'], 'L3_attn_r_out_w': _L3_attn_in['r_out_w'], 'L3_attn_gate_local_w': _L3_attn_in['gate_local_w'], 'L3_attn_gate_remote_w': _L3_attn_in['gate_remote_w'], 'L3_attn_w_out': _L3_attn_in['w_out'], 'L3_ffn_centroids': _L3_ffn_in['centroids'], 'L3_ffn_ln_g': _L3_ffn_in['ln_g'], 'L3_ffn_ln_b': _L3_ffn_in['ln_b'], 'L3_ffn_w1': _L3_ffn_in['w1'], 'L3_ffn_b1': _L3_ffn_in['b1'], 'L3_ffn_w2': _L3_ffn_in['w2'], 'L3_ffn_b2': _L3_ffn_in['b2'], 'L3_c': _L3_c, 'L3_wmod': _L3_wmod}
    _x0 = _d['L0_attn_q']
    _d['L0_attn_q'] = jax.random.normal(jax.random.fold_in(jax.random.key(seed), 1), (1, 2048, 128), dtype=_x0.dtype)
    del _x0
    return _d

def reference(L0_attn_q, L0_attn_W_query, L0_attn_W_key, L0_attn_W_val, L0_attn_W_out, L0_ffn_slot_init, L0_ffn_slot_scale, L0_ffn_w1, L0_ffn_b1, L0_ffn_w2, L0_ffn_b2, L0_ffn_gru_wih, L0_ffn_gru_whh, L0_ffn_gru_bih, L0_ffn_gru_bhh, L0_ffn_wv, L0_ffn_bv, L0_ffn_wo, L0_ffn_bo, L0_ffn_tau, L0_c, L0_wmod, L1_attn_Wq, L1_attn_Wk, L1_attn_Wv, L1_attn_Wb, L1_attn_ln_g, L1_attn_ln_b, L1_ffn_gate_w, L1_ffn_gate_b, L1_ffn_expert_w, L1_ffn_expert_b, L1_c, L1_wmod, L2_attn_Wr, L2_attn_Wk, L2_attn_Wv, L2_attn_Wo, L2_attn_W1, L2_attn_b1, L2_attn_W2, L2_attn_b2, L2_attn_ln1_g, L2_attn_ln1_b, L2_attn_ln2_g, L2_attn_ln2_b, L2_ffn_CB, L2_ffn_SCB, L2_ffn_bias, L2_c, L2_wmod, L3_attn_wq, L3_attn_wk, L3_attn_wv, L3_attn_wgq, L3_attn_wgk, L3_attn_wgv, L3_attn_r_out_w, L3_attn_gate_local_w, L3_attn_gate_remote_w, L3_attn_w_out, L3_ffn_centroids, L3_ffn_ln_g, L3_ffn_ln_b, L3_ffn_w1, L3_ffn_b1, L3_ffn_w2, L3_ffn_b2, L3_c, L3_wmod):

    def _L0_attn_ref(q, W_query, W_key, W_val, W_out):
        import jax, jax.numpy as jnp
        import numpy as np
        N_HEADS = 16
        INPUT_DIM = 128
        EMBED_DIM = 128
        KEY_DIM = EMBED_DIM // N_HEADS
        BATCH = 4
        SEQ = 256

        def _uniform(key, shape, bound):
            return jax.random.uniform(key, shape, jnp.float32, -bound, bound)
        norm = 1.0 / np.sqrt(KEY_DIM)
        Q = jnp.einsum('bsd,hdk->hbsk', q, W_query)
        K = jnp.einsum('bsd,hdk->hbsk', q, W_key)
        V = jnp.einsum('bsd,hdv->hbsv', q, W_val)
        scores = norm * jnp.einsum('hbqk,hbnk->hbqn', Q, K)
        attn = jax.nn.softmax(scores, axis=-1)
        heads = jnp.einsum('hbqn,hbnv->hbqv', attn, V)
        out = jnp.einsum('hbqv,hve->bqe', heads, W_out)
        return out

    def _L0_ffn_ref(x, slot_init, slot_scale, w1, b1, w2, b2, gru_wih, gru_whh, gru_bih, gru_bhh, wv, bv, wo, bo, tau):
        import jax, jax.numpy as jnp
        import numpy as np
        D_MODEL = 128
        NUM_SLOTS = 64
        TOP_K = 8
        B, T = (4, 512)

        def _forward(x, slot_init, slot_scale, w1, b1, w2, b2, gru_wih, gru_whh, gru_bih, gru_bhh, wv, bv, wo, bo, tau):
            Bn, Tn, D = x.shape
            Sn = slot_init.shape[0]
            S = jnp.broadcast_to((slot_init * slot_scale)[None], (Bn, Sn, D)).astype(x.dtype)
            slot_mean = S.mean(axis=1, keepdims=True)
            ctx = jnp.concatenate([x, jnp.broadcast_to(slot_mean, x.shape)], axis=-1)
            h = jax.nn.gelu(ctx @ w1.T + b1, approximate=False)
            route_logits = (h @ w2.T + b2) / (jnp.abs(tau) + 0.1)
            topk_vals, topk_idx = jax.lax.top_k(route_logits, TOP_K)
            topk_w = jax.nn.softmax(topk_vals, axis=-1)
            alpha = jnp.sum(topk_w[..., None] * jax.nn.one_hot(topk_idx, Sn, dtype=x.dtype), axis=-2)
            slot_input = jnp.einsum('bts,btd->bsd', alpha, x)
            slot_wsum = alpha.sum(axis=1) + 1e-08
            gi = (slot_input / slot_wsum[..., None]).reshape(Bn * Sn, D)
            hs = S.reshape(Bn * Sn, D)
            gx = gi @ gru_wih.T + gru_bih
            gh = hs @ gru_whh.T + gru_bhh
            xr, xz, xn = jnp.split(gx, 3, axis=-1)
            hr, hz, hn = jnp.split(gh, 3, axis=-1)
            r = jax.nn.sigmoid(xr + hr)
            z = jax.nn.sigmoid(xz + hz)
            n = jnp.tanh(xn + r * hn)
            h_new = (1.0 - z) * n + z * hs
            S_new = h_new.reshape(Bn, Sn, D)
            slot_values = S_new @ wv.T + bv
            out = jnp.einsum('bts,bsd->btd', alpha, slot_values)
            return out @ wo.T + bo
        return _forward(x, slot_init, slot_scale, w1, b1, w2, b2, gru_wih, gru_whh, gru_bih, gru_bhh, wv, bv, wo, bo, tau)

    def _L1_attn_ref(x, Wq, Wk, Wv, Wb, ln_g, ln_b):
        import jax, jax.numpy as jnp
        import numpy as np
        B, L, D = (8, 256, 128)
        LN_EPS = 1e-05
        L2_EPS = 1e-12

        def _delta_scan(q, k, v, beta):

            def step(S, inp):
                qt, kt, vt, bt = inp
                v_adj = bt * (vt - kt @ S)
                S = S + kt[:, None] * v_adj[None, :]
                return (S, qt @ S)
            S0 = jnp.zeros((D, D), dtype=q.dtype)
            _, o = jax.lax.scan(step, S0, (q, k, v, beta))
            return o
        scale = D ** (-0.5)
        q = x @ Wq * scale
        k = x @ Wk
        k = k / jnp.maximum(jnp.linalg.norm(k, axis=-1, keepdims=True), L2_EPS)
        v = jax.nn.silu(x @ Wv)
        beta = jax.nn.sigmoid(x @ Wb)
        o = jax.vmap(_delta_scan)(q, k, v, beta)
        mu = jnp.mean(o, axis=-1, keepdims=True)
        var = jnp.mean(jnp.square(o - mu), axis=-1, keepdims=True)
        return (o - mu) * jax.lax.rsqrt(var + LN_EPS) * ln_g + ln_b

    def _L1_ffn_ref(x, gate_w, gate_b, expert_w, expert_b):
        import jax, jax.numpy as jnp
        import numpy as np
        B, S, D, O, E = (8, 512, 128, 128, 64)
        b, s, d = x.shape
        xt = x.reshape(-1, d)
        logits = xt @ gate_w.T + gate_b
        gates = jax.nn.softmax(logits, axis=-1)
        sel = jnp.argmax(gates, axis=-1)
        order = jnp.argsort(sel)
        xs = xt[order]
        counts = jnp.bincount(sel, length=E).astype(jnp.int32)
        ys = jax.lax.ragged_dot(xs, expert_w, counts)
        ys = ys + expert_b[sel[order]]
        out = jnp.zeros((xt.shape[0], expert_w.shape[-1]), dtype=ys.dtype)
        out = out.at[order].set(ys)
        return out.reshape(b, s, -1)

    def _L2_attn_ref(x, Wr, Wk, Wv, Wo, W1, b1, W2, b2, ln1_g, ln1_b, ln2_g, ln2_b):
        import jax, jax.numpy as jnp
        import numpy as np
        TAU_INV = 0.5
        V_TH = 1.0
        DECAY = 0.9
        ATAN_ALPHA = 2.0
        LN_EPS = 1e-05

        @jax.custom_vjp
        def spike(x):
            return (x >= 0.0).astype(x.dtype)

        def _spike_fwd(x):
            return (spike(x), x)

        def _spike_bwd(x, g):
            sg = ATAN_ALPHA * 0.5 / (1.0 + (jnp.pi * 0.5 * ATAN_ALPHA * x) ** 2)
            return (g * sg,)
        spike.defvjp(_spike_fwd, _spike_bwd)

        def lif_step(v, x_t):
            v = v + (x_t - v) * TAU_INV
            s = spike(v - V_TH)
            v = v * (1.0 - s)
            return (v, s)

        def lif_scan(x):
            xT = jnp.swapaxes(x, 0, 1)
            _, sT = jax.lax.scan(lif_step, jnp.zeros_like(xT[0]), xT)
            return jnp.swapaxes(sT, 0, 1)

        def layernorm(x, g, b):
            mu = jnp.mean(x, axis=-1, keepdims=True)
            var = jnp.mean((x - mu) ** 2, axis=-1, keepdims=True)
            return (x - mu) * jax.lax.rsqrt(var + LN_EPS) * g + b

        def srwkv_forward(x, Wr, Wk, Wv, Wo, W1, b1, W2, b2, ln1_g, ln1_b, ln2_g, ln2_b):
            residual = x
            R = jnp.einsum('btd,ed->bte', x, Wr)
            K = jnp.einsum('btd,ed->bte', x, Wk)
            V = jnp.einsum('btd,ed->bte', x, Wv)
            RT = jnp.swapaxes(R, 0, 1)
            KT = jnp.swapaxes(K, 0, 1)
            VT = jnp.swapaxes(V, 0, 1)
            B, _, D = x.shape
            z = jnp.zeros((B, D), dtype=x.dtype)

            def step(carry, inp):
                h, vr, vk, vv = carry
                r_in, k_in, v_in = inp
                vr, r = lif_step(vr, r_in)
                vk, k = lif_step(vk, k_in)
                vv, v = lif_step(vv, v_in)
                h = h * DECAY + k * v
                y = r * h
                return ((h, vr, vk, vv), y)
            _, yT = jax.lax.scan(step, (z, z, z, z), (RT, KT, VT))
            attn_out = jnp.einsum('tbd,ed->bte', yT, Wo)
            x1 = layernorm(residual + attn_out, ln1_g, ln1_b)
            h1 = jnp.einsum('btd,fd->btf', x1, W1) + b1
            s1 = lif_scan(h1)
            h2 = jnp.einsum('btf,df->btd', s1, W2) + b2
            ffn_out = lif_scan(h2)
            return layernorm(x1 + ffn_out, ln2_g, ln2_b)
        return srwkv_forward(x, Wr, Wk, Wv, Wo, W1, b1, W2, b2, ln1_g, ln1_b, ln2_g, ln2_b)

    def _L2_ffn_ref(x, CB, SCB, bias):
        import jax, jax.numpy as jnp
        import numpy as np
        B, S, K, N = (8, 1024, 128, 128)
        out = jnp.einsum('bsk,nk->bsn', x, CB)
        out = out * (SCB * (1.0 / 127.0)) + bias
        return out

    def _L3_attn_ref(x, wq, wk, wv, wgq, wgk, wgv, r_out_w, gate_local_w, gate_remote_w, w_out):
        import jax, jax.numpy as jnp
        import numpy as np
        D_MODEL = 128
        N_HEADS = 16
        LATENT_HEADS = 8
        LATENT_DIM = 64
        N_LATENTS = 64
        WINDOW = 32
        HEAD_DIM = D_MODEL // N_HEADS
        LAT_HD = LATENT_DIM // LATENT_HEADS
        B, S = (2, 512)

        def _pool_to_latents(x):
            Bx, Sx, C = x.shape
            chunk = max(1, Sx // N_LATENTS)
            return x.reshape(Bx, N_LATENTS, chunk, C).mean(axis=2)

        def _local_window_attn(Q, K, V):
            Bx, H, Sx, D = Q.shape
            W = WINDOW
            nb = Sx // W
            Qb = Q.reshape(Bx, H, nb, W, D)
            Kp = jnp.pad(K, ((0, 0), (0, 0), (W, 0), (0, 0))).reshape(Bx, H, nb + 1, W, D)
            Vp = jnp.pad(V, ((0, 0), (0, 0), (W, 0), (0, 0))).reshape(Bx, H, nb + 1, W, D)
            Kw = jnp.concatenate([Kp[:, :, :-1], Kp[:, :, 1:]], axis=3)
            Vw = jnp.concatenate([Vp[:, :, :-1], Vp[:, :, 1:]], axis=3)
            i = jnp.arange(W)[:, None]
            j = jnp.arange(2 * W)[None, :]
            base = (j > i) & (j <= i + W)
            blk0 = (jnp.arange(nb) > 0)[:, None, None] | (j >= W)[None, :, :]
            mask = base[None, :, :] & blk0
            sc = jnp.einsum('bhnid,bhnjd->bhnij', Qb, Kw) / np.sqrt(D).astype(np.float32)
            sc = jnp.where(mask[None, None], sc, -jnp.inf)
            p = jax.nn.softmax(sc, axis=-1)
            out = jnp.einsum('bhnij,bhnjd->bhnid', p, Vw)
            return out.reshape(Bx, H, Sx, D)
        Bx, Sx, _ = x.shape
        chunk = max(1, Sx // N_LATENTS)
        Q = (x @ wq).reshape(Bx, Sx, N_HEADS, HEAD_DIM).transpose(0, 2, 1, 3)
        K = (x @ wk).reshape(Bx, Sx, N_HEADS, HEAD_DIM).transpose(0, 2, 1, 3)
        V = (x @ wv).reshape(Bx, Sx, N_HEADS, HEAD_DIM).transpose(0, 2, 1, 3)
        local = _local_window_attn(Q, K, V)
        GQ = (x @ wgq).reshape(Bx, Sx, LATENT_HEADS, LAT_HD).transpose(0, 2, 1, 3)
        GK = _pool_to_latents(x @ wgk).reshape(Bx, N_LATENTS, LATENT_HEADS, LAT_HD).transpose(0, 2, 1, 3)
        GV = _pool_to_latents(x @ wgv).reshape(Bx, N_LATENTS, LATENT_HEADS, LAT_HD).transpose(0, 2, 1, 3)
        lsc = jnp.einsum('bhsd,bhnd->bhsn', GQ, GK) / np.sqrt(LAT_HD).astype(np.float32)
        lmask = jnp.arange(N_LATENTS)[None, :] <= (jnp.arange(Sx) // chunk)[:, None]
        lsc = jnp.where(lmask[None, None], lsc, -jnp.inf)
        lp = jax.nn.softmax(lsc, axis=-1)
        rem = jnp.einsum('bhsn,bhnd->bhsd', lp, GV)
        rem = rem.transpose(0, 2, 1, 3).reshape(Bx, Sx, LATENT_DIM) @ r_out_w
        rem = rem.reshape(Bx, Sx, N_HEADS, HEAD_DIM).transpose(0, 2, 1, 3)
        gl = jax.nn.sigmoid(jnp.einsum('bhsd,hd->bhs', Q, gate_local_w))[..., None]
        gr = jax.nn.sigmoid(jnp.einsum('bhsd,hd->bhs', Q, gate_remote_w))[..., None]
        out = gl * local + gr * rem
        out = out.transpose(0, 2, 1, 3).reshape(Bx, Sx, D_MODEL)
        return out @ w_out

    def _L3_ffn_ref(x, centroids, ln_g, ln_b, w1, b1, w2, b2):
        import jax, jax.numpy as jnp
        import numpy as np
        LN_EPS = 1e-05

        def layer_norm(x, g, b):
            mu = jnp.mean(x, axis=-1, keepdims=True)
            var = jnp.var(x, axis=-1, keepdims=True)
            return (x - mu) / jnp.sqrt(var + LN_EPS) * g + b

        def balanced_assignment(scores):
            T, E = scores.shape
            C = T // E
            taken = jnp.zeros((T,), dtype=bool)
            parts = []
            for e in range(E):
                s = jnp.where(taken, -jnp.inf, scores[:, e])
                _, idx = jax.lax.top_k(s, C)
                parts.append(idx)
                taken = taken.at[idx].set(True)
            return jnp.concatenate(parts)
        D = x.shape[-1]
        feat = x.reshape(-1, D)
        T = feat.shape[0]
        E = centroids.shape[0]
        C = T // E
        norm = layer_norm(feat, ln_g, ln_b)
        scores = jax.lax.stop_gradient(norm @ centroids.T)
        sort_by_expert = balanced_assignment(scores)
        routed = feat[sort_by_expert].reshape(E, C, D)
        h = layer_norm(routed, ln_g, ln_b)
        h = jax.nn.gelu(jnp.einsum('ecd,edf->ecf', h, w1) + b1[:, None, :])
        h = jnp.einsum('ecf,efd->ecd', h, w2) + b2[:, None, :]
        out = routed + h
        inv = jnp.zeros((T,), dtype=jnp.int32).at[sort_by_expert].set(jnp.arange(T, dtype=jnp.int32))
        return out.reshape(T, D)[inv].reshape(x.shape)
    x = L0_attn_q
    mod = (_silu(L0_c) @ L0_wmod).reshape(L0_c.shape[0], 6, 1, -1)
    sa, ca, ga, sb, cb, gb = (mod[:, 0], mod[:, 1], mod[:, 2], mod[:, 3], mod[:, 4], mod[:, 5])
    ga = (2 * (ga >= 0) - 1) * jnp.maximum(jnp.abs(ga), 0.25)
    gb = (2 * (gb >= 0) - 1) * jnp.maximum(jnp.abs(gb), 0.25)
    h = _layernorm(x, axis=-1) * (1 + ca) + sa
    x = x + ga * _L0_attn_ref(h, L0_attn_W_query, L0_attn_W_key, L0_attn_W_val, L0_attn_W_out)
    h = _layernorm(x, axis=-1) * (1 + cb) + sb
    x = x + gb * _L0_ffn_ref(h, L0_ffn_slot_init, L0_ffn_slot_scale, L0_ffn_w1, L0_ffn_b1, L0_ffn_w2, L0_ffn_b2, L0_ffn_gru_wih, L0_ffn_gru_whh, L0_ffn_gru_bih, L0_ffn_gru_bhh, L0_ffn_wv, L0_ffn_bv, L0_ffn_wo, L0_ffn_bo, L0_ffn_tau)
    mod = (_silu(L1_c) @ L1_wmod).reshape(L1_c.shape[0], 6, 1, -1)
    sa, ca, ga, sb, cb, gb = (mod[:, 0], mod[:, 1], mod[:, 2], mod[:, 3], mod[:, 4], mod[:, 5])
    ga = (2 * (ga >= 0) - 1) * jnp.maximum(jnp.abs(ga), 0.25)
    gb = (2 * (gb >= 0) - 1) * jnp.maximum(jnp.abs(gb), 0.25)
    h = _layernorm(x, axis=-1) * (1 + ca) + sa
    x = x + ga * _L1_attn_ref(h, L1_attn_Wq, L1_attn_Wk, L1_attn_Wv, L1_attn_Wb, L1_attn_ln_g, L1_attn_ln_b)
    h = _layernorm(x, axis=-1) * (1 + cb) + sb
    x = x + gb * _L1_ffn_ref(h, L1_ffn_gate_w, L1_ffn_gate_b, L1_ffn_expert_w, L1_ffn_expert_b)
    mod = (_silu(L2_c) @ L2_wmod).reshape(L2_c.shape[0], 6, 1, -1)
    sa, ca, ga, sb, cb, gb = (mod[:, 0], mod[:, 1], mod[:, 2], mod[:, 3], mod[:, 4], mod[:, 5])
    ga = (2 * (ga >= 0) - 1) * jnp.maximum(jnp.abs(ga), 0.25)
    gb = (2 * (gb >= 0) - 1) * jnp.maximum(jnp.abs(gb), 0.25)
    h = _layernorm(x, axis=-1) * (1 + ca) + sa
    x = x + ga * _L2_attn_ref(h, L2_attn_Wr, L2_attn_Wk, L2_attn_Wv, L2_attn_Wo, L2_attn_W1, L2_attn_b1, L2_attn_W2, L2_attn_b2, L2_attn_ln1_g, L2_attn_ln1_b, L2_attn_ln2_g, L2_attn_ln2_b)
    h = _layernorm(x, axis=-1) * (1 + cb) + sb
    x = x + gb * _L2_ffn_ref(h, L2_ffn_CB, L2_ffn_SCB, L2_ffn_bias)
    mod = (_silu(L3_c) @ L3_wmod).reshape(L3_c.shape[0], 6, 1, -1)
    sa, ca, ga, sb, cb, gb = (mod[:, 0], mod[:, 1], mod[:, 2], mod[:, 3], mod[:, 4], mod[:, 5])
    ga = (2 * (ga >= 0) - 1) * jnp.maximum(jnp.abs(ga), 0.25)
    gb = (2 * (gb >= 0) - 1) * jnp.maximum(jnp.abs(gb), 0.25)
    h = _layernorm(x, axis=-1) * (1 + ca) + sa
    x = x + ga * _L3_attn_ref(h, L3_attn_wq, L3_attn_wk, L3_attn_wv, L3_attn_wgq, L3_attn_wgk, L3_attn_wgv, L3_attn_r_out_w, L3_attn_gate_local_w, L3_attn_gate_remote_w, L3_attn_w_out)
    h = _layernorm(x, axis=-1) * (1 + cb) + sb
    x = x + gb * _L3_ffn_ref(h, L3_ffn_centroids, L3_ffn_ln_g, L3_ffn_ln_b, L3_ffn_w1, L3_ffn_b1, L3_ffn_w2, L3_ffn_b2)
    return x

_drawn_inputs = setup_inputs


def setup_inputs(seed=0):
    import zlib

    import numpy as np

    out = dict(_drawn_inputs(seed))
    spreads = {'L0_ffn_slot_scale': (1.0, 0.6),
     'L0_ffn_b1': (0.0, 0.8),
     'L0_ffn_b2': (0.0, 0.8),
     'L0_ffn_gru_bih': (0.0, 0.515),
     'L0_ffn_gru_bhh': (0.0, 0.792),
     'L0_ffn_bv': (0.0, 0.279),
     'L0_ffn_bo': (0.0, 0.1),
     'L1_attn_ln_g': (1.0, 0.2),
     'L1_attn_ln_b': (0.0, 0.303),
     'L1_ffn_gate_b': (0.0, 0.1),
     'L1_ffn_expert_b': (0.0, 0.33),
     'L2_attn_b1': (0.0, 0.1),
     'L2_attn_b2': (0.0, 0.1),
     'L2_attn_ln1_g': (1.0, 0.2),
     'L2_attn_ln1_b': (0.0, 0.284),
     'L2_attn_ln2_g': (1.0, 0.2),
     'L2_attn_ln2_b': (0.0, 0.353),
     'L3_ffn_ln_g': (1.0, 0.6),
     'L3_ffn_ln_b': (0.0, 0.8),
     'L3_ffn_b1': (0.0, 0.8),
     'L3_ffn_b2': (0.0, 0.555)}
    factors = {'L0_ffn_slot_init': 7.622,
     'L0_ffn_w1': 5.768,
     'L0_ffn_w2': 6.183,
     'L0_ffn_gru_wih': 5.701,
     'L0_ffn_gru_whh': 8.0,
     'L0_ffn_wv': 2.958,
     'L2_attn_Wr': 8.0,
     'L2_attn_Wk': 8.0,
     'L2_attn_Wv': 8.0,
     'L2_attn_Wo': 8.0,
     'L2_ffn_bias': 8.0,
     'L3_attn_wq': 8.0,
     'L3_attn_wk': 8.0,
     'L3_attn_wv': 8.0,
     'L3_attn_wgq': 8.0,
     'L3_attn_wgk': 8.0,
     'L3_attn_wgv': 8.0,
     'L3_attn_r_out_w': 8.0,
     'L3_attn_gate_local_w': 8.0,
     'L3_attn_gate_remote_w': 8.0,
     'L3_attn_w_out': 8.0,
     'L3_ffn_centroids': 3.528,
     'L3_ffn_w1': 6.959,
     'L3_ffn_w2': 6.339}
    for name, (base, spread) in spreads.items():
        noise = np.random.default_rng([zlib.crc32(name.encode()), seed]).standard_normal(out[name].shape)
        drawn = base * np.exp(spread * noise) if base else spread * noise
        out[name] = jnp.asarray(drawn.astype(out[name].dtype))
    for name, factor in factors.items():
        out[name] = (out[name] * factor).astype(out[name].dtype)
    return out
```

```python
from contextlib import ExitStack

import numpy as np

import concourse.bass as bass
from concourse import mybir

F32 = mybir.dt.float32
BF16 = mybir.dt.bfloat16
I32 = mybir.dt.int32
U32 = mybir.dt.uint32
ALU = mybir.AluOpType
ACT = mybir.ActivationFunctionType
AX_X = mybir.AxisListType.X

P = 128
S = 2048
NT = S // P
BANK = 512
NC4 = S // BANK
LN_EPS = 1e-5
SHIFT_A, SCALE_A, GATE_A, SHIFT_B, SCALE_B, GATE_B = range(6)


class Chain:

    def __init__(self, eng, sem):
        self.eng, self.sem, self.n = eng, sem, 0

    def mark(self, ins):
        self.n += 1
        return ins.then_inc(self.sem, 1)

    def wait(self):
        self.eng.wait_ge(self.sem, self.n)

    def __call__(self, ins):
        self.mark(ins)
        self.wait()


class Stage:

    def __init__(self, nc, name):
        self.nc, self.name, self.ctx = nc, name, ExitStack()

    def __enter__(self):
        self.ctx.__enter__()
        return self

    def __exit__(self, *e):
        return self.ctx.__exit__(*e)

    def sb(self, name, shape, dt=F32):
        return self.ctx.enter_context(self.nc.sbuf_tensor(f"{self.name}_{name}", shape, dt))

    def ps(self, name, shape, dt=F32):
        return self.ctx.enter_context(self.nc.psum_tensor(f"{self.name}_{name}", shape, dt))

    def sem(self, name):
        return self.nc.alloc_semaphore(f"{self.name}_{name}")

    def block(self):
        return self.nc.Block(no_gpsimd_drain=True)


def bcast(ap, *shape):
    return ap.broadcast_to(list(shape))


def c4(j):
    return slice(j * BANK, (j + 1) * BANK)


def c1(t):
    return slice(t * P, (t + 1) * P)



def stage_setup(nc, d, g):
    with Stage(nc, "setup") as st:
        wmod = st.sb("wmod", [P, 4, 6 * P])
        c_cols = st.sb("c_cols", [P, 4])
        sig = st.sb("sig", [P, 4])
        silu = st.sb("silu", [P, 4])
        silu_rep = st.sb("silu_rep", [P, 4, P])
        floor_r = st.sb("floor_r", [P, 4, 2, P])
        sign_r = st.sb("sign_r", [P, 4, 2, P])
        ones = st.sb("ones", [P, P])
        ps = st.ps("ps", [P, 8, BANK])
        loaded = st.sem("loaded")
        sig_done = st.sem("sig_done")
        rep_done = st.sem("rep_done")
        rows_done = st.sem("rows_done")
        rows_copied = st.sem("rows_copied")
        cols_done = st.sem("cols_done")
        chain = st.sem("chain")
        with st.block() as block:

            @block.sync
            def _(sp):
                sp.dma_start(c_cols[:], d["c_cols"]).then_inc(loaded, 16)
                sp.dma_start(wmod[:], d["wmod"]).then_inc(loaded, 16)
                sp.dma_start(g.ident[:], d["ident"]).then_inc(loaded, 16)
                sp.dma_start(g.x[:], d["x"].rearrange("(t p) f -> p t f", p=P)).then_inc(loaded, 16)

            @block.scalar
            def _(act):
                act.wait_ge(loaded, 64)
                act.activation(sig[:], c_cols[:], ACT.Sigmoid).then_inc(sig_done, 1)

            @block.tensor
            def _(pe):
                pe.wait_ge(rep_done, 1)
                for l in range(4):
                    for half in range(2):
                        mm = pe.matmul(ps[:, 2 * l + half, 0:384], silu_rep[:, l, :],
                                       wmod[:, l, 384 * half:384 * half + 384], start=True, stop=True)
                    mm.then_inc(rows_done, 1)
                pe.wait_ge(rows_copied, 8)
                for l in range(4):
                    for j in range(6):
                        mm = pe.matmul(ps[:, 0, 6 * l + j:6 * l + j + 1], wmod[:, l, c1(j)],
                                       silu[:, l:l + 1], start=True, stop=True)
                mm.then_inc(cols_done, 1)

            @block.vector
            def _(dve):
                link = Chain(dve, chain)
                link(dve.memset(ones[:], 1.0))
                dve.wait_ge(sig_done, 1)
                link(dve.tensor_tensor(silu[:], sig[:], c_cols[:], ALU.mult))
                for l in range(4):
                    ins = dve.tensor_scalar(silu_rep[:, l, :], ones[:], silu[:, l:l + 1], None, ALU.mult)
                ins.then_inc(rep_done, 1)
                for l in range(4):
                    dve.wait_ge(rows_done, l + 1)
                    for half in range(2):
                        rows = g.mod_rows[:, l, 3 * half:3 * half + 3, :]
                        dve.tensor_copy(rows, ps[:, 2 * l + half, 0:384].rearrange(
                            "p (j f) -> p j f", j=3)).then_inc(rows_copied, 1)
                dve.wait_ge(rows_copied, 8)
                dve.wait_ge(cols_done, 1)
                link(dve.tensor_copy(g.mod_cols[:], ps[:, 0, 0:24]))
                gates_r = g.mod_rows[:, :, GATE_A::3, :]
                link.mark(dve.tensor_scalar(floor_r[:], gates_r, -1.0, None, ALU.mult))
                link(dve.tensor_scalar(sign_r[:], gates_r, 0.0, 2.0, ALU.is_ge, ALU.mult))
                link.mark(dve.tensor_tensor(floor_r[:], floor_r[:], gates_r, ALU.max))
                link(dve.tensor_scalar(sign_r[:], sign_r[:], -1.0, None, ALU.add))
                link(dve.tensor_scalar(floor_r[:], floor_r[:], 0.25, None, ALU.max))
                link.mark(dve.tensor_tensor(gates_r, floor_r[:], sign_r[:], ALU.mult))
                cols = g.mod_cols[:].rearrange("p (l j) -> p l j", l=4)
                gates_c, floor_c, sign_c = cols[:, :, GATE_A::3], floor_r[:, 0, 0, 0:8], sign_r[:, 0, 0, 0:8]
                floor_c = floor_c.rearrange("p (l j) -> p l j", l=4)
                sign_c = sign_c.rearrange("p (l j) -> p l j", l=4)
                link.wait()
                link.mark(dve.tensor_scalar(floor_c, gates_c, -1.0, None, ALU.mult))
                link(dve.tensor_scalar(sign_c, gates_c, 0.0, 2.0, ALU.is_ge, ALU.mult))
                link.mark(dve.tensor_tensor(floor_c, floor_c, gates_c, ALU.max))
                link(dve.tensor_scalar(sign_c, sign_c, -1.0, None, ALU.add))
                link(dve.tensor_scalar(floor_c, floor_c, 0.25, None, ALU.max))
                link(dve.tensor_tensor(gates_c, floor_c, sign_c, ALU.mult))
                for scale in (SCALE_A, SCALE_B):
                    link.mark(dve.tensor_scalar(cols[:, :, scale], cols[:, :, scale], 1.0, None, ALU.add))
                    link.mark(dve.tensor_scalar(g.mod_rows[:, :, scale, :], g.mod_rows[:, :, scale, :], 1.0, None,
                                                ALU.add))
                link.wait()



def stage_norm(nc, g, name, src, normed, turned=None, scale_col=None, shift_col=None):
    with Stage(nc, name) as st:
        stats = st.sb("stats", [P, NT, 6])
        mv = st.sb("mv", [P, NT, 2])
        var = st.sb("var", [P, NT])
        std = st.sb("std", [P, NT])
        rstd = st.sb("rstd", [P, NT])
        corr = st.sb("corr", [P, NT])
        ps = st.ps("ps", [P, 4, BANK])
        var_ready = st.sem("var_ready")
        std_ready = st.sem("std_ready")
        tile_normed = st.sem("tile_normed")
        bank_full = st.sem("bank_full")
        chain = st.sem("chain")
        with st.block() as block:

            @block.vector
            def _(dve):
                link = Chain(dve, chain)
                for t in range(NT):
                    link.mark(dve.bn_stats(stats[:, t, :], src[:, t, :]))
                link.wait()
                for t in range(NT):
                    link.mark(dve.bn_aggr(mv[:, t, :], stats[:, t, :]))
                link.wait()
                dve.tensor_scalar(var[:], mv[:, :, 1], LN_EPS, None, ALU.add).then_inc(var_ready, 1)
                dve.wait_ge(std_ready, 1)
                link(dve.reciprocal(rstd[:], std[:]))
                link(dve.tensor_tensor(corr[:], rstd[:], rstd[:], ALU.mult))
                link(dve.tensor_tensor(corr[:], corr[:], var[:], ALU.mult))
                link(dve.tensor_scalar(corr[:], corr[:], -0.5, 1.5, ALU.mult, ALU.add))
                link(dve.tensor_tensor(rstd[:], rstd[:], corr[:], ALU.mult))
                for t in range(NT):
                    dve.tensor_scalar(normed[:, t, :], src[:, t, :], mv[:, t, 0:1], rstd[:, t:t + 1],
                                      ALU.subtract, ALU.mult).then_inc(tile_normed, 1)

            @block.tensor
            def _(pe):
                for t in range(NT if turned is not None else 0):
                    pe.wait_ge(tile_normed, t + 1)
                    mm = pe.transpose(ps[:, t // 4, c1(t % 4)], normed[:, t, :], g.ident[:])
                    if t % 4 == 3:
                        mm.then_inc(bank_full, 1)

            @block.scalar
            def _(act):
                act.wait_ge(var_ready, 1)
                act.activation(std[:], var[:], ACT.Sqrt).then_inc(std_ready, 1)
                for j in range(NC4 if turned is not None else 0):
                    act.wait_ge(bank_full, j + 1)
                    act.activation(turned[:, c4(j)], ps[:, j, :], ACT.Identity, bias=shift_col, scale=scale_col)


def mod_col(g, layer, which):
    return g.mod_cols[:, 6 * layer + which:6 * layer + which + 1]


def mod_row(g, layer, which):
    return g.mod_rows[:, layer, which, :]


def adaln(nc, g, layer, scale, shift):
    stage_norm(nc, g, f"ada{layer}{scale}", g.x, g.xn, g.hT, mod_col(g, layer, scale), mod_col(g, layer, shift))



L0_H, L0_K = 16, 8
GROUP = 4
SPLITS_Q = (0, 0, 1, 0, 1, 2)
SPLITS_K = (0, 1, 0, 2, 1, 0)
MAX_ROW = 64
MASK_BIG = -1e30


def splits_of(link, dve, parts, rest, full, done):
    link(dve.tensor_copy(parts[0], full))
    link(dve.tensor_tensor(rest, full, parts[0], ALU.subtract))
    link(dve.tensor_copy(parts[1], rest))
    dve.tensor_tensor(parts[2], rest, parts[1], ALU.subtract).then_inc(done, 1)


def stage_project_parts(nc, d, g, name, w_name, V_aug, q_parts, k_parts, q):
    with Stage(nc, name) as st:
        w = st.sb("w", [P, 3, P])
        k = st.sb("k", [P, S])
        rest = st.sb("rest", [P, S])
        qp = [st.sb(f"qp{i}", [P, S], BF16) for i in range(3)]
        kp = [st.sb(f"kp{i}", [P, S], BF16) for i in range(3)]
        ps = st.ps("ps", [P, 8, BANK])
        w_loaded = st.sem("w_loaded")
        chunk_done = st.sem("chunk_done")
        chunk_read = st.sem("chunk_read")
        q_done = st.sem("q_done")
        v_done = st.sem("v_done")
        v_zero = st.sem("v_zero")
        parts_done = st.sem("parts_done")
        stored = st.sem("stored")
        chain = st.sem("chain")
        with st.block() as block:

            @block.sync
            def _(sp):
                sp.dma_start(w[:], d[w_name]).then_inc(w_loaded, 16)
                for n, (parts, dram) in enumerate(((qp, q_parts), (kp, k_parts))):
                    sp.wait_ge(parts_done, n + 1)
                    for i in range(3):
                        sp.dma_start(dram[i], parts[i][:]).then_inc(stored, 16)
                sp.wait_ge(stored, 16 * 6)

            @block.tensor
            def _(pe):
                pe.wait_ge(w_loaded, 16)
                for m in range(2):
                    for j in range(NC4):
                        pe.matmul(ps[:, 4 * m + j, :], w[:, m, :], g.hT[:, c4(j)], start=True,
                                  stop=True).then_inc(chunk_done, 1)
                for t in range(NT):
                    if t % 4 == 0:
                        pe.wait_ge(chunk_read, t // 4 + 1)
                    mm = pe.matmul(ps[:, t // 4, c1(t % 4)], g.hT[:, c1(t)], w[:, 2, :], start=True, stop=True)
                    if t % 4 == 3:
                        mm.then_inc(v_done, 1)

            @block.scalar
            def _(act):
                for n in range(2 * NC4):
                    act.wait_ge(chunk_done, n + 1)
                    dst, scale = (q, L0_K ** -0.5) if n < NC4 else (k, 1.0)
                    act.activation(dst[:, c4(n % NC4)], ps[:, n, :], ACT.Identity,
                                   scale=scale).then_inc(chunk_read, 1)
                act.wait_ge(v_zero, 2)
                for j in range(NC4):
                    act.wait_ge(v_done, j + 1)
                    for t in range(4):
                        act.activation(V_aug[:, 4 * j + t, :, 0:L0_K],
                                       ps[:, j, c1(t)].rearrange("p (h k) -> p h k", h=L0_H), ACT.Identity)

            @block.vector
            def _(dve):
                link = Chain(dve, chain)
                for n, (parts, full) in enumerate(((qp, q), (kp, k))):
                    dve.wait_ge(chunk_read, NC4 * (n + 1))
                    splits_of(link, dve, [p[:] for p in parts], rest[:], full[:], parts_done)
                    dve.wait_ge(parts_done, n + 1)

            @block.gpsimd
            def _(pool):
                pool.memset(V_aug[:], 0.0).then_inc(v_zero, 1)
                pool.wait_ge(v_zero, 1)
                pool.memset(V_aug[:, :, :, L0_K:L0_K + 1], 1.0).then_inc(v_zero, 1)


def stage_l0_attend(nc, d, g, V_aug, q_parts, k_parts, O):
    steps = (L0_H // GROUP) * NC4
    with Stage(nc, "l0att") as st:
        Q = st.sb("Q", [P, 2, GROUP, S], BF16)
        K = st.sb("K", [P, 2, GROUP, S], BF16)
        probs = st.sb("probs", [P, 2, GROUP, BANK])
        half_max = st.sb("half_max", [P, NT, 2])
        negmax = st.sb("negmax", [P, NT])
        rest = st.sb("rest", [P, NT])
        nm = st.sb("nm", [P, 2, 3, NT], BF16)
        nm_rows = st.sb("nm_rows", [3 * NT, 2, P], BF16)
        pv_sb = st.sb("pv_sb", [P, 2, BANK])
        rden = st.sb("rden", [P, 4, GROUP])
        ident16 = st.sb("ident16", [P, P], BF16)
        ps_s = st.ps("ps_s", [P, 3, BANK])
        ps_m = st.ps("ps_m", [P, 2, 2 * BANK])
        ps_v = st.ps("ps_v", [P, BANK])
        zeroed = st.sem("zeroed")
        cleared = st.sem("cleared")
        loaded = [st.sem("loaded0"), st.sem("loaded1")]
        scored = st.sem("scored")
        expd = st.sem("expd")
        pv_done = st.sem("pv_done")
        pv_copied = st.sem("pv_copied")
        m_filled = st.sem("m_filled")
        m_read = st.sem("m_read")
        nm_ready = st.sem("nm_ready")
        nm_placed = [st.sem("nm_placed0"), st.sem("nm_placed1")]
        chain = st.sem("chain")
        NG = L0_H // GROUP

        turns = []
        place = {}

        def use(*what):
            place[what] = len(turns)
            turns.append(what)

        plan = []
        for s in range(-NC4, steps):
            grp, j = s // NC4 + 1, s % NC4
            slots = []
            for kt in range(NT):
                slot = []
                if kt == 3 and s >= 1:
                    slot.append(("pv", s - 1))
                if kt == 0 and j == 0 and s >= 0:
                    slot.append(("nm", grp - 1, GROUP - 1))
                if kt == 2 and j > 0 and grp < NG:
                    slot.append(("nm", grp, j - 1))
                if grp < NG:
                    slot += [("max", grp, j, kt, half) for half in range(2)]
                slots.append(slot)
            plan.append(slots)
        copies = {}
        for s, slots in zip(range(-NC4, steps), plan):
            if s >= 1:
                copies[len(turns)] = s - 1
            for slot in slots:
                for what in slot:
                    use(*what)
        copies[len(turns)] = steps - 1
        use("pv", steps - 1)

        with st.block() as block:

            @block.sync
            def _(sp):
                sp.dma_start(ident16[:], d["ident16"]).then_inc(loaded[0], 16)
                sp.wait_ge(zeroed, 4)
                for grp in range(NG):
                    par = grp % 2
                    if grp >= 2:
                        sp.wait_ge(scored, (grp - 1) * NC4 * NT * GROUP)
                    for r in range(6):
                        for buf, dram, part in ((Q, q_parts, SPLITS_Q[r]), (K, k_parts, SPLITS_K[r])):
                            src = dram[part, 32 * grp:32 * grp + 32, :].rearrange("(h k) t -> k h t", k=L0_K)
                            sp.dma_start(buf[8 * r:8 * r + 8, par, :, :], src).then_inc(loaded[par], 16)

            @block.gpsimd
            def _(pool):
                for par in range(2):
                    pool.memset(Q[:, par, :, :].bitcast(F32), 0.0).then_inc(zeroed, 1)
                    pool.memset(K[:, par, :, :].bitcast(F32), 0.0).then_inc(zeroed, 1)
                pool.wait_ge(zeroed, 4)
                for par in range(2):
                    pool.memset(K[MAX_ROW:MAX_ROW + 3, par, :, :], 1.0).then_inc(cleared, 1)
                for grp in range(NG):
                    if grp >= 2:
                        pool.wait_ge(scored, (grp - 1) * NC4 * NT * GROUP)
                        pool.memset(Q[MAX_ROW:MAX_ROW + 3, grp % 2, :, :], 0.0).then_inc(cleared, 1)
                    for j in range(GROUP):
                        n = GROUP * grp + j
                        pool.wait_ge(m_read, place[("nm", grp, j)] + 1)
                        pool.dma_start(Q[MAX_ROW:MAX_ROW + 3, grp % 2, j, :],
                                       nm_rows[:, n % 2, :]).then_inc(nm_placed[n % 2], 16)

            @block.tensor
            def _(pe):
                def claim(*what):
                    n = place[what]
                    if n >= 2:
                        pe.wait_ge(m_read, n - 1)
                    return ps_m[:, n % 2, :]

                def run(what):
                    dst = claim(*what)
                    if what[0] == "max":
                        _, grp, j, t, half = what
                        if t == 0 and half == 0 and j == 0:
                            pe.wait_ge(loaded[grp % 2], 16 * 12 * (grp // 2 + 1) + (16 if grp % 2 == 0 else 0))
                            pe.wait_ge(cleared, 2 if grp < 2 else grp + 1)
                        for i in range(2):
                            c = 2 * half + i
                            mm = pe.matmul(dst[:, i * BANK:(i + 1) * BANK], Q[:, grp % 2, j, c1(t)],
                                           K[:, grp % 2, j, c4(c)], start=True, stop=True)
                    elif what[0] == "nm":
                        _, grp, j = what
                        n = GROUP * grp + j
                        pe.wait_ge(nm_ready, n + 1)
                        mm = pe.transpose(dst[0:3 * NT, 0:P // 2].bitcast(BF16), nm[:, n % 2, :, :].rearrange(
                            "p s t -> p (s t)"), ident16[:])
                    else:
                        s = what[1]
                        pe.wait_ge(pv_copied, s + 1)
                        for i in range(4):
                            mm = pe.transpose(dst[:, c1(i)], pv_sb[:, s % 2, c1(i)], g.ident[:])
                    mm.then_inc(m_filled, 1)

                def values(s, kt):
                    grp = s // NC4
                    if kt == 0 and s >= 1:
                        pe.wait_ge(pv_copied, s)
                    for h in range(GROUP):
                        n = (s * NT + kt) * GROUP + h
                        pe.wait_ge(expd, n + 1)
                        mm = pe.matmul(ps_v[32 * h:32 * h + 32, :], V_aug[:, kt, GROUP * grp + h, :],
                                       probs[:, kt % 2, h, :], start=(kt == 0), stop=(kt == NT - 1))
                    mm.then_inc(pv_done, 1)

                for s, slots in zip(range(-NC4, steps), plan):
                    for kt in range(NT):
                        if s < 0:
                            for what in slots[kt]:
                                run(what)
                            continue
                        grp, qc = s // NC4, s % NC4
                        todo = list(slots[kt])
                        if todo and todo[0][0] == "nm" and kt == 0:
                            run(todo.pop(0))
                        for h in range(GROUP):
                            n = (s * NT + kt) * GROUP + h
                            if n >= 3:
                                pe.wait_ge(expd, n - 2)
                            if kt == 0 and qc == 0:
                                pe.wait_ge(nm_placed[h % 2], 16 * ((GROUP * grp + h) // 2 + 1))
                            pe.matmul(ps_s[:, n % 3, :], K[:, grp % 2, h, c1(kt)], Q[:, grp % 2, h, c4(qc)],
                                      start=True, stop=True).then_inc(scored, 1)
                            if todo:
                                run(todo.pop(0))
                        for what in todo:
                            run(what)
                        if kt >= 1:
                            values(s, kt - 1)
                    if s >= 0:
                        values(s, NT - 1)
                run(("pv", steps - 1))

            @block.scalar
            def _(act):
                for n in range(steps * NT * GROUP):
                    kt, h = n // GROUP % NT, n % GROUP
                    act.wait_ge(scored, n + 1)
                    if n // GROUP >= 2:
                        act.wait_ge(pv_done, n // GROUP - 1)
                    act.activation(probs[:, kt % 2, h, :], ps_s[:, n % 3, :], ACT.Exp).then_inc(expd, 1)

            @block.vector
            def _(dve):
                link = Chain(dve, chain)

                def negate(grp, j, i):
                    n = GROUP * grp + j
                    dve.wait_ge(m_read, i)
                    link(dve.tensor_tensor(negmax[:], half_max[:, :, 0], half_max[:, :, 1], ALU.max))
                    link(dve.tensor_scalar(negmax[:], negmax[:], -1.0, None, ALU.mult))
                    if n >= 2:
                        dve.wait_ge(m_filled, place[("nm", (n - 2) // GROUP, (n - 2) % GROUP)] + 1)
                    splits_of(link, dve, [nm[:, n % 2, i, :] for i in range(3)], rest[:], negmax[:],
                              nm_ready)

                def copy_values(s):
                    dve.wait_ge(pv_done, NT * (s + 1))
                    if s >= 2:
                        dve.wait_ge(m_filled, place[("pv", s - 2)] + 1)
                    dve.tensor_copy(pv_sb[:, s % 2, :], ps_v[:]).then_inc(pv_copied, 1)

                for i, what in enumerate(turns):
                    if what[0] == "nm":
                        negate(what[1], what[2], i)
                    if i in copies:
                        copy_values(copies[i])
                    dve.wait_ge(m_filled, i + 1)
                    src = ps_m[:, i % 2, :]
                    if what[0] == "max":
                        _, grp, j, t, half = what
                        dve.tensor_reduce(half_max[:, t, half:half + 1], src, AX_X, ALU.max).then_inc(m_read, 1)
                    elif what[0] == "nm":
                        n = GROUP * what[1] + what[2]
                        if n >= 2:
                            dve.wait_ge(nm_placed[n % 2], 16 * (n // 2))
                        dve.tensor_copy(nm_rows[:, n % 2, :], src[0:3 * NT, 0:P // 2].bitcast(BF16))\
                           .then_inc(m_read, 1)
                    else:
                        s = what[1]
                        grp, qc = s // NC4, s % NC4
                        v = src[:, 0:BANK].rearrange("p (t h k) -> p t h k", t=4, h=GROUP)
                        link(dve.reciprocal(rden[:], v[:, :, :, L0_K]))
                        o = O[:, 4 * qc:4 * qc + 4, :].rearrange("p t (h k) -> p t h k", k=L0_K)
                        for t in range(4):
                            ins = dve.tensor_tensor(o[:, t, GROUP * grp:GROUP * grp + GROUP, :], v[:, t, :, 0:L0_K],
                                                    bcast(rden[:, t, :].unsqueeze(2), P, GROUP, L0_K), ALU.mult)
                        ins.then_inc(m_read, 1)


def stage_project_out(nc, d, g, name, O, w_name, gate_row):
    with Stage(nc, name) as st:
        w = st.sb("w", [P, P])
        OT = st.sb("OT", [P, S])
        ps_t = st.ps("ps_t", [P, 4, BANK])
        ps_o = st.ps("ps_o", [P, 4, BANK])
        w_loaded = st.sem("w_loaded")
        w_gated = st.sem("w_gated")
        turned = st.sem("turned")
        copied = st.sem("copied")
        summed = st.sem("summed")
        with st.block() as block:

            @block.sync
            def _(sp):
                sp.dma_start(w[:], d[w_name]).then_inc(w_loaded, 16)

            @block.tensor
            def _(pe):
                for t in range(NT):
                    mm = pe.transpose(ps_t[:, t // 4, c1(t % 4)], O[:, t, :], g.ident[:])
                    if t % 4 == 3:
                        mm.then_inc(turned, 1)
                pe.wait_ge(w_gated, 1)
                for t in range(NT):
                    if t % 4 == 0:
                        pe.wait_ge(copied, t // 4 + 1)
                    mm = pe.matmul(ps_o[:, t // 4, c1(t % 4)], OT[:, c1(t)], w[:], start=True, stop=True)
                    if t % 4 == 3:
                        mm.then_inc(summed, 1)

            @block.scalar
            def _(act):
                for j in range(NC4):
                    act.wait_ge(turned, j + 1)
                    act.activation(OT[:, c4(j)], ps_t[:, j, :], ACT.Identity).then_inc(copied, 1)

            @block.vector
            def _(dve):
                dve.wait_ge(w_loaded, 16)
                dve.tensor_tensor(w[:], w[:], gate_row, ALU.mult).then_inc(w_gated, 1)
                for j in range(NC4):
                    dve.wait_ge(summed, j + 1)
                    xs = g.x[:, 4 * j:4 * j + 4, :]
                    dve.tensor_tensor(xs, ps_o[:, j, :].rearrange("p (t f) -> p t f", t=4), xs, ALU.add)


def layer0_attention(nc, d, g):
    adaln(nc, g, 0, SCALE_A, SHIFT_A)
    q_parts = nc.dram_tensor("q_parts", [3, P, S], BF16, kind="Internal").ap()
    k_parts = nc.dram_tensor("k_parts", [3, P, S], BF16, kind="Internal").ap()
    with Stage(nc, "l0") as st:
        V_aug = st.sb("V_aug", [P, NT, L0_H, 32])
        with Stage(nc, "l0q") as st_q:
            stage_project_parts(nc, d, g, "l0proj", "l0_wqkv", V_aug, q_parts, k_parts, st_q.sb("q", [P, S]))
        O = st.sb("O", [P, NT, P])
        stage_l0_attend(nc, d, g, V_aug, q_parts, k_parts, O)
        stage_project_out(nc, d, g, "l0out", O, "l0_wout", mod_row(g, 0, GATE_A))



SLOTS, TOPK, HID = 64, 8, 64


def stage_l0_route(nc, d, g, alpha, alphaT, w):
    with Stage(nc, "l0route") as st:
        hidT = st.sb("hidT", [HID + 1, S])
        b1 = st.sb("b1", [HID, 1])
        bias1 = st.sb("bias1", [HID, 1])
        w1T = st.sb("w1T", [P, 2, HID])
        w2T = st.sb("w2T", [HID + 1, SLOTS])
        tau = st.sb("tau", [P, 1])
        itau = st.sb("itau", [P, 1])
        mean_w = st.sb("mean_w", [SLOTS, 1])
        mean_slot = st.sb("mean_slot", [P, 1])
        logits = st.sb("logits", [P, NT, SLOTS])
        left = st.sb("left", [P, NT, SLOTS])
        top = st.sb("top", [P, NT, TOPK])
        negtop = st.sb("negtop", [P, NT])
        total = st.sb("total", [P, NT])
        ps_h = st.ps("ps_h", [HID, 4, BANK])
        ps_l = st.ps("ps_l", [P, 2, BANK])
        ps_m = st.ps("ps_m", [P, BANK])
        loaded = st.sem("loaded")
        slots_ready = st.sem("slots_ready")
        mean_done = st.sem("mean_done")
        mean_copied = st.sem("mean_copied")
        bias_done = st.sem("bias_done")
        bias_ready = st.sem("bias_ready")
        hid_done = st.sem("hid_done")
        hid_ready = st.sem("hid_ready")
        logits_done = st.sem("logits_done")
        left_ready = st.sem("left_ready")
        exp_done = st.sem("exp_done")
        alpha_ready = st.sem("alpha_ready")
        ones_row = st.sem("ones_row")
        turned = st.sem("turned")
        chain = st.sem("chain")
        with st.block() as block:

            @block.sync
            def _(sp):
                for dst, name in ((b1, "l0_b1"), (w1T, "l0_w1T"), (w2T, "l0_w2T"), (tau, "l0_tau"),
                                  (w.slots, "l0_slots"), (w.slot_scale, "l0_slot_scale")):
                    sp.dma_start(dst[:], d[name]).then_inc(loaded, 16)

            @block.tensor
            def _(pe):
                pe.wait_ge(slots_ready, 1)
                pe.matmul(ps_m[:, 0:1], w.slots[:], mean_w[:], start=True, stop=True).then_inc(mean_done, 1)
                for j in range(NC4):
                    pe.matmul(ps_h[:, j, :], w1T[:, 0, :], g.hT[:, c4(j)], start=True, stop=True).then_inc(hid_done, 1)
                pe.wait_ge(mean_copied, 1)
                pe.matmul(ps_m[0:HID, 1:2], w1T[:, 1, :], mean_slot[:], start=True, stop=True).then_inc(bias_done, 1)
                for t in range(NT):
                    if t % 4 == 0:
                        pe.wait_ge(hid_ready, t // 4 + 1)
                    mm = pe.matmul(ps_l[:, t // 8, (t % 8) * SLOTS:(t % 8 + 1) * SLOTS], hidT[:, c1(t)], w2T[:],
                                   start=True, stop=True)
                    if t % 8 == 7:
                        mm.then_inc(logits_done, 1)
                pe.wait_ge(alpha_ready, 1)
                for t in range(NT):
                    mm = pe.transpose(ps_h[:, t // 4, c1(t % 4)], alpha[:, t, :], g.ident[:])
                    if t % 4 == 3:
                        mm.then_inc(turned, 1)

            @block.scalar
            def _(act):
                act.wait_ge(bias_ready, 1)
                for j in range(NC4):
                    act.wait_ge(hid_done, j + 1)
                    act.activation(hidT[0:HID, c4(j)], ps_h[:, j, :], ACT.Gelu, bias=bias1[:]).then_inc(hid_ready, 1)
                for t in range(NT):
                    if t == 0:
                        act.wait_ge(left_ready, 1)
                    act.activation(alpha[:, t, :], logits[:, t, :], ACT.Exp, bias=negtop[:, t:t + 1])\
                       .then_inc(exp_done, 1)
                for j in range(NC4):
                    act.wait_ge(turned, j + 1)
                    act.activation(alphaT[0:SLOTS, c4(j)], ps_h[:, j, :], ACT.Identity)

            @block.gpsimd
            def _(pool):
                pool.memset(alphaT[SLOTS:SLOTS + 1, :], 1.0).then_inc(ones_row, 1)
                pool.wait_ge(ones_row, 1)

            @block.vector
            def _(dve):
                link = Chain(dve, chain)
                link.mark(dve.memset(mean_w[:], 1.0 / SLOTS))
                link(dve.memset(hidT[HID:HID + 1, :], 1.0))
                dve.wait_ge(loaded, 16 * 6)
                dve.tensor_scalar(w.slots[:], w.slots[:], w.slot_scale[:], None, ALU.mult).then_inc(slots_ready, 1)
                link(dve.tensor_scalar(itau[:], tau[:], -1.0, None, ALU.mult))
                link(dve.tensor_tensor(itau[:], itau[:], tau[:], ALU.max))
                link(dve.tensor_scalar(itau[:], itau[:], 0.1, None, ALU.add))
                link(dve.reciprocal(itau[:], itau[:]))
                dve.wait_ge(mean_done, 1)
                dve.tensor_copy(mean_slot[:], ps_m[:, 0:1]).then_inc(mean_copied, 1)
                dve.wait_ge(bias_done, 1)
                dve.tensor_tensor(bias1[:], ps_m[0:HID, 1:2], b1[:], ALU.add).then_inc(bias_ready, 1)
                for b in range(2):
                    dve.wait_ge(logits_done, b + 1)
                    link.mark(dve.tensor_scalar(logits[:, 8 * b:8 * b + 8, :].rearrange("p t s -> p (t s)"),
                                                ps_l[:, b, :], itau[:], None, ALU.mult))
                link.wait()
                for t in range(NT):
                    link.mark(dve.max(top[:, t, :], logits[:, t, :]))
                link.wait()
                for t in range(NT):
                    link.mark(dve.match_replace(left[:, t, :], top[:, t, :], logits[:, t, :], -3e38))
                dve.tensor_scalar(negtop[:], top[:, :, 0], -1.0, None, ALU.mult).then_inc(left_ready, 1)
                link.wait()
                link(dve.tensor_tensor(left[:], left[:], logits[:], ALU.is_lt))
                dve.wait_ge(exp_done, NT)
                link(dve.tensor_tensor(alpha[:], alpha[:], left[:], ALU.mult))
                link(dve.tensor_reduce(total[:], alpha[:], AX_X, ALU.add))
                link(dve.reciprocal(total[:], total[:]))
                dve.tensor_tensor(alpha[:], alpha[:], bcast(total[:].unsqueeze(2), P, NT, SLOTS), ALU.mult)\
                   .then_inc(alpha_ready, 1)


def stage_l0_slots(nc, d, g, alpha, alphaT, w):
    with Stage(nc, "l0slots") as st:
        wih = st.sb("wih", [P, 3, P])
        whh = st.sb("whh", [P, 3, P])
        b_ih = st.sb("b_ih", [1, 3 * P])
        b_hh = st.sb("b_hh", [1, 3 * P])
        wv = st.sb("wv", [P, P])
        bv = st.sb("bv", [P, 1])
        wo = st.sb("wo", [P, P])
        out_w = st.sb("out_w", [SLOTS + 1, P])
        ones = st.sb("ones", [P, SLOTS])
        raw = st.sb("raw", [SLOTS, P + 1])
        gi = st.sb("gi", [SLOTS, P])
        shift = st.sb("shift", [SLOTS, P])
        wsum = st.sb("wsum", [SLOTS, 1])
        giT = st.sb("giT", [P, SLOTS])
        slotsT = st.sb("slotsT", [P, SLOTS])
        rz = st.sb("rz", [SLOTS, 2 * P])
        hn = st.sb("hn", [SLOTS, P])
        n = st.sb("n", [SLOTS, P])
        newT = st.sb("newT", [P, SLOTS])
        svT = st.sb("svT", [P, SLOTS])
        ps_i = st.ps("ps_i", [SLOTS, BANK])
        ps_g = st.ps("ps_g", [SLOTS, BANK])
        ps_t = st.ps("ps_t", [P, BANK])
        ps_o = st.ps("ps_o", [P, 4, BANK])
        loaded = st.sem("loaded")
        ones_ready = st.sem("ones_ready")
        raw_done = st.sem("raw_done")
        gi_ready = st.sem("gi_ready")
        turned = st.sem("turned")
        turns_copied = st.sem("turns_copied")
        gates_done = st.sem("gates_done")
        rz_ready = st.sem("rz_ready")
        n_in = st.sem("n_in")
        n_ready = st.sem("n_ready")
        new_ready = st.sem("new_ready")
        sv_done = st.sem("sv_done")
        sv_ready = st.sem("sv_ready")
        ow_done = st.sem("ow_done")
        ow_ready = st.sem("ow_ready")
        out_done = st.sem("out_done")
        chain = st.sem("chain")
        with st.block() as block:

            @block.sync
            def _(sp):
                for dst, name in ((wih[:], "l0_wihT"), (whh[:], "l0_whhT"), (b_ih[:], "l0_bih"), (b_hh[:], "l0_bhh"),
                                  (wv[:], "l0_wvT"), (bv[:], "l0_bv"), (wo[:], "l0_woT"),
                                  (out_w[SLOTS:SLOTS + 1, :], "l0_bo")):
                    sp.dma_start(dst, d[name]).then_inc(loaded, 16)

            @block.tensor
            def _(pe):
                pe.wait_ge(ones_ready, 1)
                for t in range(NT):
                    pe.matmul(ps_i[:, 0:P], alpha[:, t, :], g.xn[:, t, :], start=(t == 0), stop=(t == NT - 1))
                for t in range(NT):
                    mm = pe.matmul(ps_i[:, P:P + 1], alpha[:, t, :], ones[:, 0:1], start=(t == 0), stop=(t == NT - 1),
                                   skip_group_check=True)
                mm.then_inc(raw_done, 1)
                pe.transpose(ps_t[:, 0:SLOTS], w.slots[:], g.ident[0:SLOTS, 0:SLOTS])
                pe.wait_ge(gi_ready, 1)
                pe.transpose(ps_t[:, SLOTS:2 * SLOTS], gi[:], g.ident[0:SLOTS, 0:SLOTS]).then_inc(turned, 1)
                pe.wait_ge(turns_copied, 1)
                pe.wait_ge(loaded, 16 * 8)
                one = ones[0:1, :]
                pe.matmul(ps_g[:, 0:256], giT[:], wih[:, 0:2, :].rearrange("p a b -> p (a b)"), start=True, stop=False)
                pe.matmul(ps_g[:, 0:256], one, b_ih[:, 0:256], start=False, stop=False)
                pe.matmul(ps_g[:, 0:256], slotsT[:], whh[:, 0:2, :].rearrange("p a b -> p (a b)"), start=False,
                          stop=False)
                pe.matmul(ps_g[:, 0:256], one, b_hh[:, 0:256], start=False, stop=True)
                pe.matmul(ps_g[:, 256:384], giT[:], wih[:, 2, :], start=True, stop=False, skip_group_check=True)
                pe.matmul(ps_g[:, 256:384], one, b_ih[:, 256:384], start=False, stop=True, skip_group_check=True)
                pe.matmul(ps_g[:, 384:512], slotsT[:], whh[:, 2, :], start=True, stop=False, skip_group_check=True)
                pe.matmul(ps_g[:, 384:512], one, b_hh[:, 256:384], start=False, stop=True,
                          skip_group_check=True).then_inc(gates_done, 1)
                pe.wait_ge(new_ready, 1)
                pe.transpose(ps_t[:, 0:SLOTS], n[:], g.ident[0:SLOTS, 0:SLOTS]).then_inc(turned, 1)
                pe.wait_ge(turns_copied, 2)
                pe.matmul(ps_t[:, SLOTS:2 * SLOTS], wv[:], newT[:], start=True, stop=True).then_inc(sv_done, 1)
                pe.wait_ge(sv_ready, 1)
                pe.matmul(ps_i[:, 0:P], svT[:], wo[:], start=True, stop=True).then_inc(ow_done, 1)
                pe.wait_ge(ow_ready, 2)
                for t in range(NT):
                    mm = pe.matmul(ps_o[:, t // 4, c1(t % 4)], alphaT[:, c1(t)], out_w[:], start=True, stop=True)
                    if t % 4 == 3:
                        mm.then_inc(out_done, 1)

            @block.scalar
            def _(act):
                act.wait_ge(gates_done, 1)
                act.activation(rz[:], ps_g[:, 0:256], ACT.Sigmoid).then_inc(rz_ready, 1)
                act.wait_ge(n_in, 1)
                act.activation(n[:], hn[:], ACT.Tanh).then_inc(n_ready, 1)

            @block.vector
            def _(dve):
                link = Chain(dve, chain)
                dve.memset(ones[:], 1.0).then_inc(ones_ready, 1)
                dve.wait_ge(raw_done, 1)
                link(dve.tensor_copy(raw[:], ps_i[:, 0:P + 1]))
                link.mark(dve.tensor_scalar(wsum[:], raw[:, P:P + 1], 1e-8, None, ALU.add))
                link.mark(dve.tensor_tensor(gi[:], raw[:, 0:P], mod_row(g, 0, SCALE_B)[0:SLOTS], ALU.mult))
                link(dve.tensor_scalar(shift[:], mod_row(g, 0, SHIFT_B)[0:SLOTS], raw[:, P:P + 1], None, ALU.mult))
                link.mark(dve.reciprocal(wsum[:], wsum[:]))
                link(dve.tensor_tensor(gi[:], gi[:], shift[:], ALU.add))
                dve.tensor_scalar(gi[:], gi[:], wsum[:], None, ALU.mult).then_inc(gi_ready, 1)
                dve.wait_ge(turned, 1)
                link(dve.tensor_copy(slotsT[:], ps_t[:, 0:SLOTS]))
                dve.tensor_copy(giT[:], ps_t[:, SLOTS:2 * SLOTS]).then_inc(turns_copied, 1)
                dve.wait_ge(rz_ready, 1)
                link(dve.tensor_tensor(hn[:], rz[:, 0:P], ps_g[:, 384:512], ALU.mult))
                dve.tensor_tensor(hn[:], hn[:], ps_g[:, 256:384], ALU.add).then_inc(n_in, 1)
                dve.wait_ge(n_ready, 1)
                link(dve.tensor_tensor(hn[:], w.slots[:], n[:], ALU.subtract))
                link(dve.tensor_tensor(hn[:], hn[:], rz[:, P:2 * P], ALU.mult))
                dve.tensor_tensor(n[:], n[:], hn[:], ALU.add).then_inc(new_ready, 1)
                dve.wait_ge(turned, 2)
                dve.tensor_copy(newT[:], ps_t[:, 0:SLOTS]).then_inc(turns_copied, 1)
                dve.wait_ge(sv_done, 1)
                dve.tensor_scalar(svT[:], ps_t[:, SLOTS:2 * SLOTS], bv[:], None, ALU.add).then_inc(sv_ready, 1)
                dve.wait_ge(ow_done, 1)
                dve.tensor_tensor(out_w[0:SLOTS, :], ps_i[:, 0:P], mod_row(g, 0, GATE_B)[0:SLOTS], ALU.mult)\
                   .then_inc(ow_ready, 1)
                dve.tensor_tensor(out_w[SLOTS:SLOTS + 1, :], out_w[SLOTS:SLOTS + 1, :],
                                  mod_row(g, 0, GATE_B)[SLOTS:SLOTS + 1], ALU.mult).then_inc(ow_ready, 1)
                for j in range(NC4):
                    dve.wait_ge(out_done, j + 1)
                    xs = g.x[:, 4 * j:4 * j + 4, :]
                    dve.tensor_tensor(xs, ps_o[:, j, :].rearrange("p (t f) -> p t f", t=4), xs, ALU.add)


def layer0_slots(nc, d, g):
    adaln(nc, g, 0, SCALE_B, SHIFT_B)
    with Stage(nc, "l0ffn") as st:
        w = Persistent()
        w.slots = st.sb("slots", [SLOTS, P])
        w.slot_scale = st.sb("slot_scale", [SLOTS, 1])
        alpha = st.sb("alpha", [P, NT, SLOTS])
        alphaT = st.sb("alphaT", [SLOTS + 1, S])
        stage_l0_route(nc, d, g, alpha, alphaT, w)
        stage_l0_slots(nc, d, g, alpha, alphaT, w)



LEVELS = (2, 4, 8, 16, 32, 64)


def stage_l1_project(nc, d, g, w):
    with Stage(nc, "l1proj") as st:
        wq = st.sb("wq", [P, P])
        wkvb = st.sb("wkvb", [P, 2 * P + 1])
        raw = st.sb("raw", [P, NT, 2 * P + 1])
        sq = st.sb("sq", [P, NT, P])
        ss = st.sb("ss", [P, NT])
        norm = st.sb("norm", [P, NT])
        quot = st.sb("quot", [P, NT])
        ps_q = st.ps("ps_q", [P, 4, BANK])
        ps_k = st.ps("ps_k", [P, 4, BANK])
        loaded = st.sem("loaded")
        q_done = st.sem("q_done")
        kvb_done = st.sem("kvb_done")
        kvb_copied = st.sem("kvb_copied")
        sums_ready = st.sem("sums_ready")
        roots_done = st.sem("roots_done")
        sig_done = st.sem("sig_done")
        q_copied = st.sem("q_copied")
        k_ready = st.sem("k_ready")
        turned = st.sem("turned")
        chain = st.sem("chain")
        with st.block() as block:

            @block.sync
            def _(sp):
                sp.dma_start(wq[:], d["l1_wq"]).then_inc(loaded, 16)
                sp.dma_start(wkvb[:], d["l1_wkvb"]).then_inc(loaded, 16)

            @block.tensor
            def _(pe):
                pe.wait_ge(loaded, 32)
                for t in range(NT):
                    if t >= 4:
                        pe.wait_ge(kvb_copied, t - 3)
                    pe.matmul(ps_k[:, t % 4, 0:2 * P + 1], g.hT[:, c1(t)], wkvb[:], start=True, stop=True)\
                      .then_inc(kvb_done, 1)
                for j in range(NC4):
                    pe.matmul(ps_q[:, j, :], wq[:], g.hT[:, c4(j)], start=True, stop=True).then_inc(q_done, 1)
                pe.wait_ge(k_ready, 1)
                for t in range(NT):
                    if t % 4 == 0:
                        pe.wait_ge(q_copied, t // 4 + 1)
                    mm = pe.transpose(ps_q[:, t // 4, c1(t % 4)], w.k[:, t, :], g.ident[:])
                    if t % 4 == 3:
                        mm.then_inc(turned, 1)

            @block.scalar
            def _(act):
                for j in range(NC4):
                    act.wait_ge(q_done, j + 1)
                    act.activation(w.qT[:, c4(j)], ps_q[:, j, :], ACT.Identity, scale=P ** -0.5).then_inc(q_copied, 1)
                act.wait_ge(kvb_copied, NT)
                act.activation(w.bv[:], raw[:, :, P:2 * P], ACT.Sigmoid)
                act.activation(w.beta[:], raw[:, :, 2 * P], ACT.Sigmoid).then_inc(sig_done, 1)
                act.wait_ge(sums_ready, 1)
                act.activation(norm[:], ss[:], ACT.Sqrt).then_inc(roots_done, 1)
                for j in range(NC4):
                    act.wait_ge(turned, j + 1)
                    act.activation(w.kT[:, c4(j)], ps_q[:, j, :], ACT.Identity)

            @block.vector
            def _(dve):
                link = Chain(dve, chain)
                for t in range(NT):
                    dve.wait_ge(kvb_done, t + 1)
                    dve.tensor_copy(raw[:, t, :], ps_k[:, t % 4, 0:2 * P + 1]).then_inc(kvb_copied, 1)
                dve.wait_ge(kvb_copied, NT)
                k_raw, v_raw = raw[:, :, 0:P], raw[:, :, P:2 * P]
                link(dve.tensor_tensor(sq[:], k_raw, k_raw, ALU.mult))
                link(dve.tensor_reduce(ss[:], sq[:], AX_X, ALU.add))
                dve.tensor_scalar(ss[:], ss[:], 1e-30, None, ALU.max).then_inc(sums_ready, 1)
                dve.wait_ge(sig_done, 1)
                link(dve.tensor_tensor(w.bv[:], w.bv[:], v_raw, ALU.mult))
                link(dve.tensor_tensor(w.bv[:], w.bv[:], bcast(w.beta[:].unsqueeze(2), P, NT, P), ALU.mult))
                dve.wait_ge(roots_done, 1)
                link(dve.reciprocal(quot[:], norm[:]))
                link(dve.tensor_tensor(quot[:], quot[:], ss[:], ALU.mult))
                link(dve.tensor_tensor(norm[:], norm[:], quot[:], ALU.add))
                link(dve.tensor_scalar(norm[:], norm[:], 0.5, 1e-12, ALU.mult, ALU.max))
                link(dve.reciprocal(norm[:], norm[:]))
                dve.tensor_tensor(w.k[:], k_raw, bcast(norm[:].unsqueeze(2), P, NT, P), ALU.mult).then_inc(k_ready, 1)
                dve.wait_ge(k_ready, 1)
                dve.tensor_tensor(w.bk[:], w.k[:], bcast(w.beta[:].unsqueeze(2), P, NT, P), ALU.mult)


def stage_l1_chunks(nc, d, g, w):
    with Stage(nc, "l1chunk") as st:
        masks = st.sb("masks", [P, len(LEVELS) + 2, P])
        A = st.sb("A", [P, NT, P])
        C = st.sb("C", [P, 2, NT, P])
        T = st.sb("T", [P, NT, P])
        X = st.sb("X", [P, NT, P])
        Y = st.sb("Y", [P, 2, BANK])
        ps_y = st.ps("ps_y", [P, 2, BANK])
        ps_t = st.ps("ps_t", [P, 2, BANK])
        ps_x = st.ps("ps_x", [P, 2, BANK])
        loaded = st.sem("loaded")
        g_done = st.sem("g_done")
        a_ready = st.sem("a_ready")
        c_ready = st.sem("c_ready")
        t_init = st.sem("t_init")
        x_turned = st.sem("x_turned")
        x_copied = st.sem("x_copied")
        y_done = st.sem("y_done")
        y_copied = st.sem("y_copied")
        tx_done = st.sem("tx_done")
        tx_ready = st.sem("tx_ready")
        m_done = st.sem("m_done")
        m_copied = st.sem("m_copied")
        u_copied = st.sem("u_copied")
        wt_copied = st.sem("wt_copied")
        wt_done = st.sem("wt_done")
        chain = st.sem("chain")
        tiles = lambda buf, j: buf[:, 4 * j:4 * j + 4, :].rearrange("p t f -> p (t f)")

        def mask(i, n):
            return bcast(masks[:, i:i + 1, :], P, n, P)

        with st.block() as block:

            @block.sync
            def _(sp):
                sp.dma_start(masks[:], d["masks"]).then_inc(loaded, 16)

            @block.tensor
            def _(pe):
                for j in range(NC4):
                    for t in range(4):
                        c = c1(4 * j + t)
                        mm = pe.matmul((ps_y if j < 2 else ps_t)[:, j % 2, c1(t)], w.kT[:, c], w.kT[:, c], start=True,
                                       stop=True)
                    mm.then_inc(g_done, 1)
                for j in range(NC4):
                    if j >= 2:
                        pe.wait_ge(m_copied, j - 1)
                    for t in range(4):
                        c = c1(4 * j + t)
                        mm = pe.matmul(ps_x[:, j % 2, c1(t)], w.kT[:, c], w.qT[:, c], start=True, stop=True)
                    mm.then_inc(m_done, 1)
                for j in range(NC4):
                    pe.wait_ge(t_init, j + 1)
                    pe.wait_ge(a_ready, min(j + 3, NC4))
                    if j >= 2:
                        pe.wait_ge(x_copied, j - 1)
                    for t in range(4):
                        mm = pe.transpose(ps_y[:, j % 2, c1(t)], T[:, 4 * j + t, :], g.ident[:])
                    mm.then_inc(x_turned, 1)
                for l in range(len(LEVELS)):
                    last = l == len(LEVELS) - 1

                    def join(j):
                        n = NC4 * l + j
                        pe.wait_ge(y_copied, n + 1)
                        if n >= 2:
                            pe.wait_ge(tx_ready, n - 1)
                        for t in range(4):
                            y = Y[:, n % 2, c1(t)]
                            if not last:
                                pe.matmul(ps_t[:, n % 2, c1(t)], y, T[:, 4 * j + t, :], start=True, stop=True)
                            mm = pe.matmul(ps_x[:, n % 2, c1(t)], T[:, 4 * j + t, :], y, start=True, stop=True)
                        mm.then_inc(tx_done, 1)

                    for j in range(NC4):
                        n = NC4 * l + j
                        if j == 0:
                            pe.wait_ge(c_ready, l + 2)
                        if l == 0:
                            pe.wait_ge(x_copied, NC4 if j == 0 else j + 1)
                            pe.wait_ge(m_copied, NC4)
                        else:
                            pe.wait_ge(tx_ready, n - NC4 + 1)
                        if n >= 2:
                            pe.wait_ge(y_copied, n - 1)
                        for t in range(4):
                            mm = pe.matmul(ps_y[:, n % 2, c1(t)], C[:, (l + 1) % 2, 4 * j + t, :], X[:, 4 * j + t, :],
                                           start=True, stop=True)
                        mm.then_inc(y_done, 1)
                        if j >= 1:
                            join(j - 1)
                    join(NC4 - 1)
                total = NC4 * len(LEVELS)
                for j in range(NC4):
                    pe.wait_ge(tx_ready, total - NC4 + j + 1)
                    if j == 0:
                        pe.wait_ge(y_copied, total)
                        pe.wait_ge(tx_ready, total)
                    if j >= 2:
                        pe.wait_ge(u_copied, j - 1)
                        pe.wait_ge(wt_copied, j - 1)
                    for t in range(4):
                        i = 4 * j + t
                        pe.matmul(ps_t[:, j % 2, c1(t)], X[:, i, :], w.bv[:, i, :], start=True, stop=True)
                        mm = pe.matmul(ps_x[:, j % 2, c1(t)], w.bk[:, i, :], X[:, i, :], start=True, stop=True)
                    mm.then_inc(wt_done, 1)

            @block.gpsimd
            def _(pool):
                pool.wait_ge(loaded, 16)
                for l in range(len(LEVELS) + 1):
                    if l == 0:
                        pool.wait_ge(a_ready, NC4)
                    if l == 2:
                        pool.wait_ge(t_init, NC4)
                    if l >= 3:
                        pool.wait_ge(y_done, NC4 * (l - 2))
                    pool.tensor_tensor(C[:, l % 2, :, :], A[:], mask(l, NT), ALU.mult).then_inc(c_ready, 1)

            @block.scalar
            def _(act):
                for j in range(NC4):
                    act.wait_ge(x_turned, j + 1)
                    act.activation(tiles(X, j), ps_y[:, j % 2, :], ACT.Identity).then_inc(x_copied, 1)
                for n in range(NC4 * len(LEVELS)):
                    act.wait_ge(y_done, n + 1)
                    if n >= 2:
                        act.wait_ge(tx_done, n - 1)
                    act.activation(Y[:, n % 2, :], ps_y[:, n % 2, :], ACT.Identity).then_inc(y_copied, 1)
                for j in range(NC4):
                    act.wait_ge(wt_done, j + 1)
                    act.activation(w.WT[:, c4(j)], ps_x[:, j % 2, :], ACT.Identity).then_inc(wt_copied, 1)

            @block.vector
            def _(dve):
                link = Chain(dve, chain)
                for j in range(NC4):
                    dve.wait_ge(g_done, j + 1)
                    src = (ps_y if j < 2 else ps_t)[:, j % 2, :].rearrange("p (t f) -> p t f", t=4)
                    dve.tensor_tensor(A[:, 4 * j:4 * j + 4, :], src, bcast(
                        w.beta[:, 4 * j:4 * j + 4].unsqueeze(2), P, 4, P), ALU.mult).then_inc(a_ready, 1)
                dve.wait_ge(loaded, 16)
                for j in range(NC4):
                    dve.wait_ge(m_done, j + 1)
                    dve.tensor_tensor(w.MT[:, 4 * j:4 * j + 4, :], ps_x[:, j % 2, :].rearrange(
                        "p (t f) -> p t f", t=4), mask(len(LEVELS) + 1, 4), ALU.mult).then_inc(m_copied, 1)
                dve.wait_ge(c_ready, 1)
                for j in range(NC4):
                    dve.tensor_tensor(T[:, 4 * j:4 * j + 4, :], bcast(g.ident[:].unsqueeze(1), P, 4, P),
                                      C[:, 0, 4 * j:4 * j + 4, :], ALU.subtract).then_inc(t_init, 1)
                for n in range(NC4 * len(LEVELS)):
                    j, last = n % NC4, n >= NC4 * (len(LEVELS) - 1)
                    dve.wait_ge(tx_done, n + 1)
                    if not last:
                        dve.tensor_tensor(tiles(T, j), tiles(T, j), ps_t[:, n % 2, :], ALU.subtract)
                    dve.tensor_tensor(tiles(X, j), tiles(X, j), ps_x[:, n % 2, :], ALU.subtract)\
                       .then_inc(tx_ready, 1)
                for j in range(NC4):
                    dve.wait_ge(wt_done, j + 1)
                    dve.tensor_copy(tiles(w.U, j), ps_t[:, j % 2, :]).then_inc(u_copied, 1)


def stage_l1_states(nc, d, g, w, O):
    with Stage(nc, "l1state") as st:
        state = st.sb("state", [P, 2, P])
        V = st.sb("V", [P, 2, P])
        ps_v = st.ps("ps_v", [P, 2, BANK])
        ps_s = st.ps("ps_s", [P, BANK])
        ps_o = st.ps("ps_o", [P, 2, BANK])
        ws_done = st.sem("ws_done")
        v_ready = st.sem("v_ready")
        s_done = st.sem("s_done")
        s_ready = st.sem("s_ready")
        o_done = st.sem("o_done")
        o_copied = st.sem("o_copied")
        with st.block() as block:

            @block.tensor
            def _(pe):
                for c in range(NT):
                    if c >= 1:
                        pe.wait_ge(s_ready, c)
                        pe.matmul(ps_v[:, c % 2, 0:P], w.WT[:, c1(c)], state[:, c % 2, :], start=True,
                                  stop=True).then_inc(ws_done, 1)
                    if c >= 2:
                        pe.wait_ge(o_copied, c - 1)
                    if c >= 1:
                        pe.matmul(ps_o[:, c % 2, 0:P], w.qT[:, c1(c)], state[:, c % 2, :], start=True, stop=False)
                    pe.wait_ge(v_ready, c + 1)
                    if c < NT - 1:
                        pe.matmul(ps_s[:, 0:P], w.k[:, c, :], V[:, c % 2, :], start=(c == 0), stop=True,
                                  skip_group_check=True).then_inc(s_done, 1)
                    pe.matmul(ps_o[:, c % 2, 0:P], w.MT[:, c, :], V[:, c % 2, :], start=(c == 0),
                              stop=True).then_inc(o_done, 1)

            @block.scalar
            def _(act):
                for c in range(NT):
                    act.wait_ge(o_done, c + 1)
                    act.activation(O[:, c, :], ps_o[:, c % 2, 0:P], ACT.Identity).then_inc(o_copied, 1)

            @block.vector
            def _(dve):
                for c in range(NT):
                    if c >= 2:
                        dve.wait_ge(o_done, c - 1)
                    if c == 0:
                        dve.tensor_copy(V[:, 0, :], w.U[:, 0, :]).then_inc(v_ready, 1)
                    else:
                        dve.wait_ge(ws_done, c)
                        dve.tensor_tensor(V[:, c % 2, :], w.U[:, c, :], ps_v[:, c % 2, 0:P],
                                          ALU.subtract).then_inc(v_ready, 1)
                    if c < NT - 1:
                        dve.wait_ge(s_done, c + 1)
                        dve.tensor_copy(state[:, (c + 1) % 2, :], ps_s[:, 0:P]).then_inc(s_ready, 1)


def stage_add_affine(nc, d, g, name, normed, g_name, b_name, gate_row):
    with Stage(nc, name) as st:
        gain = st.sb("gain", [P, P])
        shift = st.sb("shift", [P, P])
        tmp = st.sb("tmp", [P, NT, P])
        loaded = st.sem("loaded")
        rows_ready = st.sem("rows_ready")
        shifted = st.sem("shifted")
        chain = st.sem("chain")
        with st.block() as block:

            @block.sync
            def _(sp):
                sp.dma_start(gain[:], d[g_name]).then_inc(loaded, 16)
                sp.dma_start(shift[:], d[b_name]).then_inc(loaded, 16)

            @block.gpsimd
            def _(pool):
                pool.wait_ge(rows_ready, 1)
                pool.tensor_tensor(g.x[:], g.x[:], bcast(shift[:].unsqueeze(1), P, NT, P), ALU.add)\
                    .then_inc(shifted, 1)
                pool.wait_ge(shifted, 1)

            @block.vector
            def _(dve):
                link = Chain(dve, chain)
                dve.wait_ge(loaded, 32)
                link.mark(dve.tensor_tensor(gain[:], gain[:], gate_row, ALU.mult))
                dve.tensor_tensor(shift[:], shift[:], gate_row, ALU.mult).then_inc(rows_ready, 1)
                link.wait()
                link(dve.tensor_tensor(tmp[:], normed[:], bcast(gain[:].unsqueeze(1), P, NT, P), ALU.mult))
                dve.wait_ge(shifted, 1)
                dve.tensor_tensor(g.x[:], g.x[:], tmp[:], ALU.add)


def layer1_delta(nc, d, g):
    adaln(nc, g, 1, SCALE_A, SHIFT_A)
    with Stage(nc, "l1") as st:
        w = Persistent()
        O = st.sb("O", [P, NT, P])
        w.qT = st.sb("qT", [P, S])
        w.kT = st.sb("kT", [P, S])
        w.k, w.bk, w.bv, w.MT, w.U = (st.sb(n, [P, NT, P]) for n in ("k", "bk", "bv", "MT", "U"))
        w.WT = st.sb("WT", [P, S])
        w.beta = st.sb("beta", [P, NT])
        stage_l1_project(nc, d, g, w)
        stage_l1_chunks(nc, d, g, w)
        stage_l1_states(nc, d, g, w, O)
        stage_norm(nc, g, "l1norm", O, g.xn)
        stage_add_affine(nc, d, g, "l1add", g.xn, "l1_lng", "l1_lnb", mod_row(g, 1, GATE_A))



EXPERTS = 64


def stage_l1_route(nc, d, g, eT, onehotT):
    with Stage(nc, "l1route") as st:
        gw = st.sb("gw", [P, EXPERTS])
        gb = st.sb("gb", [1, EXPERTS])
        ones = st.sb("ones", [P, P])
        iota = st.sb("iota", [P, 1])
        logits = st.sb("logits", [P, NT, EXPERTS])
        top = st.sb("top", [P, NT, 8])
        idx = st.sb("idx", [P, NT, 8], U32)
        e = st.sb("e", [P, NT])
        diag = st.sb("diag", [P, NT, P])
        ps_l = st.ps("ps_l", [P, 2, BANK])
        ps_e = st.ps("ps_e", [P, 4, BANK])
        loaded = st.sem("loaded")
        ones_ready = st.sem("ones_ready")
        logits_done = st.sem("logits_done")
        diag_ready = st.sem("diag_ready")
        e_done = st.sem("e_done")
        e_copied = st.sem("e_copied")
        chain = st.sem("chain")
        with st.block() as block:

            @block.sync
            def _(sp):
                sp.dma_start(gw[:], d["l1_gateT"]).then_inc(loaded, 16)
                sp.dma_start(gb[:], d["l1_gate_b"]).then_inc(loaded, 16)
                sp.dma_start(iota[:], d["iota"]).then_inc(loaded, 16)

            @block.tensor
            def _(pe):
                pe.wait_ge(ones_ready, 1)
                pe.wait_ge(loaded, 48)
                for t in range(NT):
                    dst = ps_l[:, t // 8, (t % 8) * EXPERTS:(t % 8 + 1) * EXPERTS]
                    pe.matmul(dst, g.hT[:, c1(t)], gw[:], start=True, stop=False, skip_group_check=True)
                    mm = pe.matmul(dst, ones[0:1, :], gb[:], start=False, stop=True, skip_group_check=True)
                    if t % 8 == 7:
                        mm.then_inc(logits_done, 1)
                pe.wait_ge(diag_ready, 1)
                for t in range(NT):
                    mm = pe.matmul(ps_e[:, t // 4, c1(t % 4)], ones[:], diag[:, t, :], start=True, stop=True)
                    if t % 4 == 3:
                        mm.then_inc(e_done, 1)

            @block.scalar
            def _(act):
                for j in range(NC4):
                    act.wait_ge(e_done, j + 1)
                    act.activation(eT[:, c4(j)], ps_e[:, j, :], ACT.Identity).then_inc(e_copied, 1)

            @block.vector
            def _(dve):
                link = Chain(dve, chain)
                dve.memset(ones[:], 1.0).then_inc(ones_ready, 1)
                for b in range(2):
                    dve.wait_ge(logits_done, b + 1)
                    link.mark(dve.tensor_copy(logits[:, 8 * b:8 * b + 8, :].rearrange("p t s -> p (t s)"),
                                              ps_l[:, b, :]))
                link.wait()
                for t in range(NT):
                    link.mark(dve.max(top[:, t, :], logits[:, t, :]))
                link.wait()
                for t in range(NT):
                    link.mark(dve.max_index(idx[:, t, :], top[:, t, :], logits[:, t, :]))
                link.wait()
                link(dve.tensor_copy(e[:], idx[:, :, 0]))
                dve.tensor_tensor(diag[:], bcast(g.ident[:].unsqueeze(1), P, NT, P),
                                  bcast(e[:].unsqueeze(2), P, NT, P), ALU.mult).then_inc(diag_ready, 1)
                dve.wait_ge(loaded, 48)
                dve.wait_ge(e_copied, NC4)
                dve.tensor_scalar(onehotT[:], eT[0:EXPERTS, :], iota[0:EXPERTS, :], None, ALU.is_equal)


def stage_l1_experts(nc, d, g, eT, onehotT):
    with Stage(nc, "l1exp") as st:
        W = st.sb("W", [P, 4, 4, P])
        bias = st.sb("bias", [EXPERTS, P])
        masked = st.sb("masked", [P, 2, S])
        y = st.sb("y", [P, S])
        ps_y = st.ps("ps_y", [P, 4, BANK])
        ps_t = st.ps("ps_t", [P, 4, BANK])
        bias_loaded = st.sem("bias_loaded")
        W_loaded = [st.sem(f"W_loaded{i}") for i in range(4)]
        masked_ready = st.sem("masked_ready")
        expert_done = st.sem("expert_done")
        y_copied = st.sem("y_copied")
        turned = st.sem("turned")
        with st.block() as block:

            @block.sync
            def _(sp):
                sp.dma_start(bias[:], d["l1_expert_b"]).then_inc(bias_loaded, 16)
                for n in range(EXPERTS // 4):
                    if n >= 4:
                        sp.wait_ge(expert_done, 4 * (n - 3))
                    sp.dma_start(W[:, n % 4, :, :], d["l1_expert_w"][4 * n:4 * n + 4].rearrange("e d o -> d e o"))\
                      .then_inc(W_loaded[n % 4], 16)

            @block.tensor
            def _(pe):
                for e in range(EXPERTS):
                    if e % 4 == 0:
                        pe.wait_ge(W_loaded[e // 4 % 4], 16 * (e // 16 + 1))
                    pe.wait_ge(masked_ready, e + 1)
                    for j in range(NC4):
                        mm = pe.matmul(ps_y[:, j, :], W[:, e // 4 % 4, e % 4, :], masked[:, e % 2, c4(j)],
                                       start=(e == 0), stop=False)
                    mm.then_inc(expert_done, 1)
                pe.wait_ge(bias_loaded, 16)
                for j in range(NC4):
                    mm = pe.matmul(ps_y[:, j, :], bias[:], onehotT[:, c4(j)], start=False, stop=True)
                mm.then_inc(expert_done, 1)
                for t in range(NT):
                    if t % 4 == 0:
                        pe.wait_ge(y_copied, t // 4 + 1)
                    mm = pe.transpose(ps_t[:, t // 4, c1(t % 4)], y[:, c1(t)], g.ident[:])
                    if t % 4 == 3:
                        mm.then_inc(turned, 1)

            @block.scalar
            def _(act):
                act.wait_ge(expert_done, EXPERTS + 1)
                for j in range(NC4):
                    act.activation(y[:, c4(j)], ps_y[:, j, :], ACT.Identity, scale=mod_col(g, 1, GATE_B))\
                       .then_inc(y_copied, 1)

            @block.vector
            def _(dve):
                for e in range(EXPERTS):
                    if e >= 2:
                        dve.wait_ge(expert_done, e - 1)
                    dve.scalar_tensor_tensor(masked[:, e % 2, :], eT[:], float(e), g.hT[:], ALU.is_equal,
                                             ALU.mult).then_inc(masked_ready, 1)
                for j in range(NC4):
                    dve.wait_ge(turned, j + 1)
                    xs = g.x[:, 4 * j:4 * j + 4, :]
                    dve.tensor_tensor(xs, ps_t[:, j, :].rearrange("p (t f) -> p t f", t=4), xs, ALU.add)


def layer1_experts(nc, d, g):
    adaln(nc, g, 1, SCALE_B, SHIFT_B)
    with Stage(nc, "l1ffn") as st:
        eT = st.sb("eT", [P, S])
        onehotT = st.sb("onehotT", [EXPERTS, S])
        stage_l1_route(nc, d, g, eT, onehotT)
        stage_l1_experts(nc, d, g, eT, onehotT)



LIF_LEN = 64
LIF_CHUNKS = S // LIF_LEN


class LifMemory:

    def __init__(self, st, groups):
        self.v = st.sb("lif_v", [P, groups, LIF_CHUNKS])
        self.ends = st.sb("lif_ends", [P, groups, LIF_CHUNKS])
        self.differ = st.sb("lif_differ", [P, groups, LIF_CHUNKS])
        self.count = st.sb("lif_count", [P, 32])
        self.count_turned = st.sb("lif_count_turned", [P, 32])
        self.count_int = st.sb("lif_count_int", [P, 1], I32)
        self.step = st.sem("lif_step")


def lif(dve, name, X, U, groups, m):
    flat = lambda ap: ap.rearrange("p g c -> p (g c)")
    u_of = U.rearrange("p g (c l) -> p (g c) l", l=LIF_LEN)
    x_of = X.rearrange("p g (c l) -> p (g c) l", l=LIF_LEN)
    v_of, ends = m.v[:, 0:groups, :], m.ends[:, 0:groups, :]
    v, differ = flat(v_of), flat(m.differ[:, 0:groups, :])
    unsettled = dve.alloc_register(f"{name}_unsettled")
    parts = [dve.alloc_register(f"{name}_unsettled_in_quadrant{i}") for i in range(4)]
    dve.sem_clear(m.step)
    link = Chain(dve, m.step)
    link.mark(dve.memset(m.ends[:], 0.0))
    link.mark(dve.memset(m.v[:], 0.0))
    link(dve.memset(m.count[:], 0.0))
    dve.reg_mov(unsettled, 1)
    with dve.While(lambda: dve.snap(unsettled)):
        dve.sem_clear(m.step)
        link = Chain(dve, m.step)
        link(dve.tensor_copy(v_of[:, :, 1:LIF_CHUNKS], ends[:, :, 0:LIF_CHUNKS - 1]))
        link(dve.memset(v_of[:, :, 0:1], 0.0))
        for t in range(LIF_LEN):
            link(dve.scalar_tensor_tensor(u_of[:, :, t], v, 0.5, x_of[:, :, t], ALU.mult, ALU.add))
            link(dve.scalar_tensor_tensor(v, u_of[:, :, t], 1.0, u_of[:, :, t], ALU.is_lt, ALU.mult))
        link(dve.tensor_tensor(differ, v, flat(ends), ALU.not_equal))
        link.mark(dve.tensor_copy(ends, v_of))
        link(dve.tensor_reduce(m.count[:, 0:1], differ, AX_X, ALU.add))
        link(dve.transpose(m.count_turned[:], m.count[:]))
        link(dve.tensor_reduce(m.differ[:, 0, 0:1], m.count_turned[:], AX_X, ALU.add))
        link(dve.tensor_copy(m.count_int[:], m.differ[:, 0, 0:1]))
        for i, part in enumerate(parts):
            dve.reg_load(part, m.count_int[32 * i:32 * i + 1, 0:1])
        dve.reg_add(unsettled, parts[0], parts[1])
        dve.reg_add(unsettled, unsettled, parts[2])
        dve.reg_add(unsettled, unsettled, parts[3])
    for r in parts + [unsettled]:
        dve.free_register(r)


def stage_l2_mix(nc, d, g, h_tm, r):
    with Stage(nc, "l2mix") as st:
        w = st.sb("w", [P, 4, P])
        X = st.sb("X", [P, 3, S])
        U = st.sb("U", [P, 3, S])
        decay = st.sb("decay", [P, S])
        m = LifMemory(st, 3)
        ps = st.ps("ps", [P, 8, BANK])
        loaded = st.sem("loaded")
        in_done = st.sem("in_done")
        in_copied = st.sem("in_copied")
        h_scaled = st.sem("h_scaled")
        y_ready = st.sem("y_ready")
        out_done = st.sem("out_done")
        chain = st.sem("chain")
        with st.block() as block:

            @block.sync
            def _(sp):
                sp.dma_start(w[:], d["l2_wrkvo"]).then_inc(loaded, 16)

            @block.tensor
            def _(pe):
                pe.wait_ge(loaded, 16)
                for n in range(3 * NC4):
                    if n >= 8:
                        pe.wait_ge(in_copied, n - 7)
                    pe.matmul(ps[:, n % 8, :], w[:, n // NC4, :], g.hT[:, c4(n % NC4)], start=True,
                              stop=True).then_inc(in_done, 1)
                pe.wait_ge(y_ready, 1)
                for t in range(NT):
                    mm = pe.matmul(ps[:, t // 4, c1(t % 4)], X[:, 0, c1(t)], w[:, 3, :], start=True, stop=True)
                    if t % 4 == 3:
                        mm.then_inc(out_done, 1)

            @block.scalar
            def _(act):
                for n in range(3 * NC4):
                    act.wait_ge(in_done, n + 1)
                    act.activation(X[:, n // NC4, c4(n % NC4)], ps[:, n % 8, :], ACT.Identity,
                                   scale=0.5).then_inc(in_copied, 1)

            @block.gpsimd
            def _(pool):
                pool.tensor_tensor(h_tm[:], g.xn[:], bcast(mod_row(g, 2, SCALE_A).unsqueeze(1), P, NT, P),
                                   ALU.mult).then_inc(h_scaled, 1)
                pool.wait_ge(h_scaled, 1)
                pool.tensor_tensor(h_tm[:], h_tm[:], bcast(mod_row(g, 2, SHIFT_A).unsqueeze(1), P, NT, P),
                                   ALU.add).then_inc(h_scaled, 1)
                pool.wait_ge(h_scaled, 2)

            @block.vector
            def _(dve):
                link = Chain(dve, chain)
                link.mark(dve.memset(decay[:], 0.9))
                dve.wait_ge(in_copied, 3 * NC4)
                lif(dve, "rkv", X[:], U[:], 3, m)
                r_u, k_u, v_u = (U[:, i, :] for i in range(3))
                y, kv, acc = (X[:, i, :] for i in range(3))
                link(dve.tensor_scalar(v_u, v_u, 1.0, None, ALU.is_ge))
                link(dve.scalar_tensor_tensor(kv, k_u, 1.0, v_u, ALU.is_ge, ALU.mult))
                link(dve.tensor_tensor_scan(acc, decay[:], kv, 0.0, ALU.mult, ALU.add))
                dve.scalar_tensor_tensor(y, r_u, 1.0, acc, ALU.is_ge, ALU.mult).then_inc(y_ready, 1)
                dve.wait_ge(h_scaled, 2)
                for j in range(NC4):
                    dve.wait_ge(out_done, j + 1)
                    ts = slice(4 * j, 4 * j + 4)
                    dve.tensor_tensor(r[:, ts, :], ps[:, j, :].rearrange("p (t f) -> p t f", t=4), h_tm[:, ts, :],
                                      ALU.add)


def stage_l2_hidden(nc, d, g, x1n, x1T, x1_tm, X):
    with Stage(nc, "l2hid") as st:
        w1 = st.sb("w1", [P, 4, P])
        b1 = st.sb("b1", [P, 4])
        half_b = st.sb("half_b", [P, 4])
        gain = st.sb("gain", [P, P])
        shift = st.sb("shift", [P, P])
        ps = st.ps("ps", [P, 8, BANK])
        loaded = st.sem("loaded")
        bias_ready = st.sem("bias_ready")
        in_done = st.sem("in_done")
        in_copied = st.sem("in_copied")
        x1_scaled = st.sem("x1_scaled")
        with st.block() as block:

            @block.sync
            def _(sp):
                for dst, name in ((w1, "l2_w1T"), (b1, "l2_b1"), (gain, "l2_ln1g"), (shift, "l2_ln1b")):
                    sp.dma_start(dst[:], d[name]).then_inc(loaded, 16)

            @block.tensor
            def _(pe):
                pe.wait_ge(loaded, 64)
                for n in range(4 * NC4):
                    if n >= 8:
                        pe.wait_ge(in_copied, n - 7)
                    pe.matmul(ps[:, n % 8, :], w1[:, n // NC4, :], x1T[:, c4(n % NC4)], start=True,
                              stop=True).then_inc(in_done, 1)

            @block.scalar
            def _(act):
                act.wait_ge(bias_ready, 1)
                for n in range(4 * NC4):
                    act.wait_ge(in_done, n + 1)
                    f = n // NC4
                    act.activation(X[:, f, c4(n % NC4)], ps[:, n % 8, :], ACT.Identity, scale=0.5,
                                   bias=half_b[:, f:f + 1]).then_inc(in_copied, 1)

            @block.vector
            def _(dve):
                dve.wait_ge(loaded, 64)
                dve.tensor_scalar(half_b[:], b1[:], 0.5, None, ALU.mult).then_inc(bias_ready, 1)

            @block.gpsimd
            def _(pool):
                pool.wait_ge(loaded, 64)
                pool.tensor_tensor(x1_tm[:], x1n[:], bcast(gain[:].unsqueeze(1), P, NT, P), ALU.mult)\
                    .then_inc(x1_scaled, 1)
                pool.wait_ge(x1_scaled, 1)
                pool.tensor_tensor(x1_tm[:], x1_tm[:], bcast(shift[:].unsqueeze(1), P, NT, P), ALU.add)\
                    .then_inc(x1_scaled, 1)
                pool.wait_ge(x1_scaled, 2)


def stage_l2_spikes(nc, d, g, X, x1_tm):
    with Stage(nc, "l2spk") as st:
        w2 = st.sb("w2", [P, 4, P])
        b2 = st.sb("b2", [P, 1])
        half_b = st.sb("half_b", [P, 1])
        U = st.sb("U", [P, 4, S])
        m = LifMemory(st, 4)
        ps = st.ps("ps", [P, 4, BANK])
        ps_t = st.ps("ps_t", [P, 4, BANK])
        loaded = st.sem("loaded")
        bias_ready = st.sem("bias_ready")
        s_ready = st.sem("s_ready")
        h2_done = st.sem("h2_done")
        h2_copied = st.sem("h2_copied")
        out_ready = st.sem("out_ready")
        turned = st.sem("turned")
        with st.block() as block:

            @block.sync
            def _(sp):
                sp.dma_start(w2[:], d["l2_w2T"]).then_inc(loaded, 16)
                sp.dma_start(b2[:], d["l2_b2"]).then_inc(loaded, 16)

            @block.tensor
            def _(pe):
                pe.wait_ge(loaded, 32)
                for f in range(4):
                    pe.wait_ge(s_ready, f + 1)
                    for j in range(NC4):
                        mm = pe.matmul(ps[:, j, :], w2[:, f, :], U[:, f, c4(j)], start=(f == 0), stop=(f == 3))
                mm.then_inc(h2_done, 1)
                pe.wait_ge(out_ready, 1)
                for t in range(NT):
                    mm = pe.transpose(ps_t[:, t // 4, c1(t % 4)], U[:, 0, c1(t)], g.ident[:])
                    if t % 4 == 3:
                        mm.then_inc(turned, 1)

            @block.scalar
            def _(act):
                act.wait_ge(bias_ready, 1)
                act.wait_ge(h2_done, 1)
                for j in range(NC4):
                    act.activation(X[:, 0, c4(j)], ps[:, j, :], ACT.Identity, scale=0.5, bias=half_b[:])\
                       .then_inc(h2_copied, 1)

            @block.vector
            def _(dve):
                dve.wait_ge(loaded, 32)
                dve.tensor_scalar(half_b[:], b2[:], 0.5, None, ALU.mult).then_inc(bias_ready, 1)
                lif(dve, "hidden", X[:], U[:], 4, m)
                for f in range(4):
                    dve.tensor_scalar(U[:, f, :], U[:, f, :], 1.0, None, ALU.is_ge).then_inc(s_ready, 1)
                dve.wait_ge(h2_copied, NC4)
                lif(dve, "out", X[:, 0:1, :], U[:, 0:1, :], 1, m)
                dve.tensor_scalar(U[:, 0, :], U[:, 0, :], 1.0, None, ALU.is_ge).then_inc(out_ready, 1)
                for j in range(NC4):
                    dve.wait_ge(turned, j + 1)
                    ts = slice(4 * j, 4 * j + 4)
                    dve.tensor_tensor(x1_tm[:, ts, :], ps_t[:, j, :].rearrange("p (t f) -> p t f", t=4),
                                      x1_tm[:, ts, :], ALU.add)


def layer2_spiking(nc, d, g):
    adaln(nc, g, 2, SCALE_A, SHIFT_A)
    with Stage(nc, "l2") as st:
        h_tm = st.sb("h_tm", [P, NT, P])
        x1_tm = st.sb("x1_tm", [P, NT, P])
        ln_cols = st.sb("ln_cols", [P, 2])
        cols_loaded = st.sem("cols_loaded")
        nc.sync.dma_start(ln_cols[:], d["l2_ln1cols"]).then_inc(cols_loaded, 16)
        nc.scalar.wait_ge(cols_loaded, 16)
        stage_l2_mix(nc, d, g, h_tm, x1_tm)
        stage_norm(nc, g, "l2norm1", x1_tm, h_tm, g.hT, ln_cols[:, 0:1], ln_cols[:, 1:2])
        X = st.sb("X", [P, 4, S])
        stage_l2_hidden(nc, d, g, h_tm, g.hT, x1_tm, X)
        stage_l2_spikes(nc, d, g, X, x1_tm)
        stage_norm(nc, g, "l2norm2", x1_tm, g.xn)
        stage_add_affine(nc, d, g, "l2add", g.xn, "l2_ln2g", "l2_ln2b", mod_row(g, 2, GATE_A))



def layer2_product(nc, d, g):
    adaln(nc, g, 2, SCALE_B, SHIFT_B)
    with Stage(nc, "l2ffn") as st:
        w = st.sb("w", [P, P])
        scale = st.sb("scale", [P, P])
        bias = st.sb("bias", [P, P])
        tmp = st.sb("tmp", [P, 2, 4, P])
        ps = st.ps("ps", [P, 4, BANK])
        loaded = st.sem("loaded")
        rows_ready = st.sem("rows_ready")
        done = st.sem("done")
        shifted = st.sem("shifted")
        chain = st.sem("chain")
        with st.block() as block:

            @block.sync
            def _(sp):
                for dst, name in ((w, "l2_CBT"), (scale, "l2_SCB"), (bias, "l2_bias")):
                    sp.dma_start(dst[:], d[name]).then_inc(loaded, 16)

            @block.tensor
            def _(pe):
                pe.wait_ge(loaded, 48)
                for t in range(NT):
                    mm = pe.matmul(ps[:, t // 4, c1(t % 4)], g.hT[:, c1(t)], w[:], start=True, stop=True)
                    if t % 4 == 3:
                        mm.then_inc(done, 1)

            @block.gpsimd
            def _(pool):
                pool.wait_ge(rows_ready, 1)
                pool.tensor_tensor(g.x[:], g.x[:], bcast(bias[:].unsqueeze(1), P, NT, P), ALU.add).then_inc(shifted, 1)
                pool.wait_ge(shifted, 1)

            @block.vector
            def _(dve):
                link = Chain(dve, chain)
                gate = mod_row(g, 2, GATE_B)
                dve.wait_ge(loaded, 48)
                link(dve.tensor_scalar(scale[:], scale[:], 1.0 / 127.0, None, ALU.mult))
                link.mark(dve.tensor_tensor(scale[:], scale[:], gate, ALU.mult))
                dve.tensor_tensor(bias[:], bias[:], gate, ALU.mult).then_inc(rows_ready, 1)
                link.wait()
                for j in range(NC4):
                    dve.wait_ge(done, j + 1)
                    link(dve.tensor_tensor(tmp[:, j % 2], ps[:, j, :].rearrange("p (t f) -> p t f", t=4),
                                           bcast(scale[:].unsqueeze(1), P, 4, P), ALU.mult))
                    if j == 0:
                        dve.wait_ge(shifted, 1)
                    xs = g.x[:, 4 * j:4 * j + 4, :]
                    dve.tensor_tensor(xs, xs, tmp[:, j % 2], ALU.add)



WINDOW = 32
SPAN = P + WINDOW
L3_H, L3_K = 16, 8
LAT_H, LAT_K, LATENTS = 8, 8, 64


def stage_l3_latent(nc, d, g, q, rem, gates):
    with Stage(nc, "l3lat") as st:
        wg = st.sb("wg", [P, 3, LATENTS])
        r_out = st.sb("r_out", [LATENTS, P])
        head_rows = st.sb("head_rows", [P, L3_H])
        gate_w = st.sb("gate_w", [P, 2])
        gate_m = st.sb("gate_m", [P, 2, L3_H])
        causal = st.sb("causal", [P, NT, LATENTS], BF16)
        ident16 = st.sb("ident16", [P, P], BF16)
        gqT = st.sb("gqT", [LATENTS, S])
        pooled = st.sb("pooled", [P, LATENTS])
        gk = st.sb("gk", [LATENTS, LAT_H, LATENTS])
        gv = st.sb("gv", [LATENTS, LAT_H, LATENTS])
        R = st.sb("R", [P, 4, P])
        sc = st.sb("sc", [P, 2, LAT_H, LATENTS])
        probs = st.sb("probs", [P, 2, LAT_H, LATENTS])
        top = st.sb("top", [P, 2, LAT_H])
        den = st.sb("den", [P, 2, LAT_H])
        PT = st.sb("PT", [P, 2, BANK])
        ps_a = st.ps("ps_a", [P, 4, BANK])
        ps_t = st.ps("ps_t", [P, 2, BANK])
        ps_r = st.ps("ps_r", [P, 2, BANK])
        loaded = st.sem("loaded")
        gq_done = st.sem("gq_done")
        gq_copied = st.sem("gq_copied")
        pool_ready = st.sem("pool_ready")
        gkv_done = st.sem("gkv_done")
        gkv_ready = st.sem("gkv_ready")
        r_done = st.sem("r_done")
        r_copied = st.sem("r_copied")
        gm_ready = st.sem("gm_ready")
        gates_done = st.sem("gates_done")
        gates_read = st.sem("gates_read")
        scored = st.sem("scored")
        sub_ready = st.sem("sub_ready")
        expd = st.sem("expd")
        p_ready = st.sem("p_ready")
        turned = st.sem("turned")
        pt_copied = st.sem("pt_copied")
        rem_done = st.sem("rem_done")
        rem_copied = st.sem("rem_copied")
        chain = st.sem("chain")
        with st.block() as block:

            @block.sync
            def _(sp):
                for dst, name in ((wg, "l3_wg"), (r_out, "l3_r_out"), (head_rows, "head_rows"), (gate_w, "l3_gates"),
                                  (causal, "lat_causal"), (ident16, "ident16")):
                    sp.dma_start(dst[:], d[name]).then_inc(loaded, 16)

            @block.tensor
            def _(pe):
                pe.wait_ge(loaded, 96)
                for j in range(NC4):
                    pe.matmul(ps_a[0:LATENTS, j, :], wg[:, 0, :], g.hT[:, c4(j)], start=True, stop=True)\
                      .then_inc(gq_done, 1)
                pe.wait_ge(pool_ready, 1)
                for i in range(2):
                    mm = pe.matmul(ps_t[0:LATENTS, i, 0:LATENTS], wg[:, 1 + i, :], pooled[:], start=True, stop=True)
                mm.then_inc(gkv_done, 1)
                pe.wait_ge(gm_ready, 1)
                for t in range(NT):
                    mm = pe.matmul(ps_r[:, 0, 2 * L3_H * t:2 * L3_H * (t + 1)], q[:, c1(t)],
                                   gate_m[:].rearrange("p a h -> p (a h)"), start=True, stop=True)
                mm.then_inc(gates_done, 1)
                pe.wait_ge(gkv_ready, 2)
                for c in range(4):
                    mm = pe.matmul(ps_r[:, 1, c1(c)], gv[:, 2 * c:2 * c + 2, :].rearrange("p h n -> p (h n)"),
                                   r_out[:], start=True, stop=True)
                mm.then_inc(r_done, 1)

                def score(t):
                    if t < 4:
                        pe.wait_ge(gq_copied, NC4)
                    else:
                        pe.wait_ge(sub_ready, t - 3)
                    pe.matmul(ps_a[:, t % 4, :], ident16[:], bcast(causal[:, t:t + 1, :], P, LAT_H, LATENTS),
                              start=True, stop=False)
                    pe.matmul(ps_a[:, t % 4, :], gqT[:, c1(t)], gk[:].rearrange("p h n -> p (h n)"), start=False,
                              stop=True).then_inc(scored, 1)

                def turn(t):
                    pe.wait_ge(p_ready, t + 1)
                    if t == 0:
                        pe.wait_ge(gkv_ready, 2)
                    if t >= 2:
                        pe.wait_ge(pt_copied, t - 1)
                    p = probs[:, t % 2, :, :].rearrange("p h n -> p (h n)")
                    for c in range(4):
                        mm = pe.transpose(ps_t[:, t % 2, c1(c)], p[:, c1(c)], g.ident[:])
                    mm.then_inc(turned, 1)

                def values(t):
                    pe.wait_ge(pt_copied, t + 1)
                    if t < 2:
                        pe.wait_ge(r_copied, 1)
                        pe.wait_ge(gates_read, 1)
                    else:
                        pe.wait_ge(rem_copied, t - 1)
                    for c in range(4):
                        mm = pe.matmul(ps_r[:, t % 2, 0:P], PT[:, t % 2, c1(c)], R[:, c, :], start=(c == 0),
                                       stop=(c == 3))
                    mm.then_inc(rem_done, 1)

                for t in range(NT + 2):
                    if t < NT:
                        score(t)
                    if 1 <= t <= NT:
                        turn(t - 1)
                    if t >= 2:
                        values(t - 2)

            @block.scalar
            def _(act):
                for j in range(NC4):
                    act.wait_ge(gq_done, j + 1)
                    act.activation(gqT[:, c4(j)], ps_a[0:LATENTS, j, :], ACT.Identity, scale=LAT_K ** -0.5)\
                       .then_inc(gq_copied, 1)
                act.wait_ge(gates_done, 1)
                act.activation(gates[:].rearrange("p a t h -> p t a h"),
                               ps_r[:, 0, :].rearrange("p (t a h) -> p t a h", t=NT, a=2), ACT.Sigmoid,
                               scale=L3_K ** 0.5).then_inc(gates_read, 1)
                act.wait_ge(r_done, 1)
                act.activation(R[:].rearrange("p c f -> p (c f)"), ps_r[:, 1, :], ACT.Identity).then_inc(r_copied, 1)
                for t in range(NT + 1):
                    if t < NT:
                        act.wait_ge(sub_ready, t + 1)
                        if t >= 2:
                            act.wait_ge(turned, t - 1)
                        act.activation(probs[:, t % 2], sc[:, t % 2], ACT.Exp).then_inc(expd, 1)
                    if t >= 1:
                        act.wait_ge(turned, t)
                        if t >= 3:
                            act.wait_ge(rem_done, t - 2)
                        act.activation(PT[:, (t - 1) % 2, :], ps_t[:, (t - 1) % 2, :], ACT.Identity)\
                           .then_inc(pt_copied, 1)

            @block.vector
            def _(dve):
                link = Chain(dve, chain)
                dve.wait_ge(loaded, 96)
                link.mark(dve.tensor_scalar(gate_m[:, 0, :], head_rows[:], gate_w[:, 0:1], None, ALU.mult))
                dve.tensor_scalar(gate_m[:, 1, :], head_rows[:], gate_w[:, 1:2], None, ALU.mult).then_inc(gm_ready, 1)
                link(dve.tensor_reduce(pooled[:], g.hT[:].rearrange("p (n c) -> p n c", c=S // LATENTS), AX_X,
                                       ALU.add))
                dve.tensor_scalar(pooled[:], pooled[:], LATENTS / S, None, ALU.mult).then_inc(pool_ready, 1)
                dve.wait_ge(gkv_done, 1)
                for i, blocks in enumerate((gk, gv)):
                    dve.tensor_tensor(blocks[:], bcast(ps_t[0:LATENTS, i:i + 1, 0:LATENTS], LATENTS, LAT_H, LATENTS),
                                      bcast(head_rows[0:LATENTS, 0:LAT_H].unsqueeze(2), LATENTS, LAT_H, LATENTS),
                                      ALU.mult).then_inc(gkv_ready, 1)
                for t in range(NT + 2):
                    if t < NT:
                        b = t % 2
                        dve.wait_ge(scored, t + 1)
                        s3 = ps_a[:, t % 4, :].rearrange("p (h n) -> p h n", h=LAT_H)
                        link(dve.tensor_reduce(top[:, b, :], s3, AX_X, ALU.max))
                        if t >= 2:
                            dve.wait_ge(expd, t - 1)
                        dve.tensor_tensor(sc[:, b], s3, bcast(top[:, b, :].unsqueeze(2), P, LAT_H, LATENTS),
                                          ALU.subtract).then_inc(sub_ready, 1)
                    if 1 <= t <= NT:
                        b = (t - 1) % 2
                        dve.wait_ge(expd, t)
                        link(dve.tensor_reduce(den[:, b, :], probs[:, b], AX_X, ALU.add))
                        link(dve.reciprocal(den[:, b, :], den[:, b, :]))
                        dve.tensor_tensor(probs[:, b], probs[:, b],
                                          bcast(den[:, b, :].unsqueeze(2), P, LAT_H, LATENTS), ALU.mult)\
                           .then_inc(p_ready, 1)
                    if t >= 2:
                        dve.wait_ge(rem_done, t - 1)
                        dve.tensor_copy(rem[:, t - 2, :], ps_r[:, t % 2, 0:P]).then_inc(rem_copied, 1)


def stage_l3_local(nc, d, g, V_aug, q_parts, k_parts, O):
    NG = L3_H // GROUP
    with Stage(nc, "l3loc") as st:
        Q = st.sb("Q", [P, 2, GROUP, S + WINDOW], BF16)
        K = st.sb("K", [P, 2, GROUP, WINDOW + S], BF16)
        mask_q = st.sb("mask_q", [P, 2, 1, SPAN], BF16)
        mask_k = st.sb("mask_k", [P, 1, SPAN], BF16)
        ident16 = st.sb("ident16", [P, P], BF16)
        maxima = st.sb("maxima", [P, NT, GROUP])
        negmax = st.sb("negmax", [P, GROUP, NT])
        rest = st.sb("rest", [P, GROUP, NT])
        nm = st.sb("nm", [P, GROUP, 3, NT], BF16)
        nm_rows = st.sb("nm_rows", [3 * NT, GROUP, P], BF16)
        probs = st.sb("probs", [P, 3, GROUP, SPAN])
        pv_sb = st.sb("pv_sb", [P, 2, BANK])
        rden = st.sb("rden", [P, 4, GROUP])
        ps_m = st.ps("ps_m", [P, 2, BANK])
        ps_s = st.ps("ps_s", [P, 4, BANK])
        ps_v = st.ps("ps_v", [P, BANK])
        ps_t = st.ps("ps_t", [P, BANK])
        zeroed = st.sem("zeroed")
        cleared = st.sem("cleared")
        consts_loaded = st.sem("consts_loaded")
        loaded = [st.sem("loaded0"), st.sem("loaded1")]
        m_done = st.sem("m_done")
        m_read = st.sem("m_read")
        nm_ready = st.sem("nm_ready")
        nm_turned = st.sem("nm_turned")
        nm_rows_ready = st.sem("nm_rows_ready")
        nm_placed = st.sem("nm_placed")
        scored = st.sem("scored")
        expd = st.sem("expd")
        pv_done = st.sem("pv_done")
        pv_copied = st.sem("pv_copied")
        pv_turned = st.sem("pv_turned")
        o_ready = st.sem("o_ready")
        chain = st.sem("chain")
        heads2 = lambda ap: ap.rearrange("p (h c) -> p h c", h=2)

        with st.block() as block:

            @block.sync
            def _(sp):
                for dst, name in ((mask_q, "mask_q"), (mask_k, "mask_k"), (ident16, "ident16")):
                    sp.dma_start(dst[:], d[name]).then_inc(consts_loaded, 16)
                sp.wait_ge(zeroed, 4)
                for grp in range(NG):
                    par = grp % 2
                    if grp >= 2:
                        sp.wait_ge(scored, (grp - 1) * NT)
                    for r in range(6):
                        for buf, dram, part, at in ((Q, q_parts, SPLITS_Q[r], 0), (K, k_parts, SPLITS_K[r], WINDOW)):
                            src = dram[part, 32 * grp:32 * grp + 32, :].rearrange("(h k) t -> k h t", k=L3_K)
                            sp.dma_start(buf[8 * r:8 * r + 8, par, :, at:at + S], src).then_inc(loaded[par], 16)

            @block.gpsimd
            def _(pool):
                for par in range(2):
                    pool.memset(Q[:, par, :, :].bitcast(F32), 0.0).then_inc(zeroed, 1)
                    pool.memset(K[:, par, :, :].bitcast(F32), 0.0).then_inc(zeroed, 1)
                pool.wait_ge(zeroed, 4)
                for par in range(2):
                    pool.memset(K[MAX_ROW:MAX_ROW + 3, par, :, :], 1.0).then_inc(cleared, 1)
                for grp in range(NG):
                    if grp >= 2:
                        pool.wait_ge(scored, (grp - 1) * NT)
                        pool.memset(Q[MAX_ROW:MAX_ROW + 3, grp % 2, :, :], 0.0).then_inc(cleared, 1)
                    pool.wait_ge(nm_rows_ready, grp + 1)
                    for h in range(GROUP):
                        pool.dma_start(Q[MAX_ROW:MAX_ROW + 3, grp % 2, h, 0:S],
                                       nm_rows[:, h, :]).then_inc(nm_placed, 16)

            @block.tensor
            def _(pe):
                pe.wait_ge(consts_loaded, 48)

                def maxima_of(grp):
                    par = grp % 2
                    pe.wait_ge(loaded[par], 16 * 12 * (grp // 2 + 1))
                    pe.wait_ge(cleared, 2 if grp < 2 else grp + 1)
                    for t in range(NT):
                        for half in range(2):
                            n = 2 * (NT * grp + t) + half
                            if n >= 2:
                                pe.wait_ge(m_read, n - 1)
                            dst = ps_m[:, n % 2, 0:2 * SPAN]
                            pe.matmul(dst, ident16[:], bcast(mask_q[:, min(t, 1), :, :], P, 2, SPAN), start=True,
                                      stop=False)
                            for i in range(2):
                                h = 2 * half + i
                                mm = pe.matmul(dst[:, i * SPAN:(i + 1) * SPAN], Q[:, par, h, c1(t)],
                                               K[:, par, h, t * P:t * P + SPAN], start=False, stop=(i == 1))
                            mm.then_inc(m_done, 1)

                def turn_maxima(grp):
                    pe.wait_ge(nm_ready, grp + 1)
                    if grp == 1:
                        pe.wait_ge(nm_rows_ready, 1)
                    elif grp >= 2:
                        pe.wait_ge(o_ready, NC4 * (grp - 1))
                    for h in range(GROUP):
                        mm = pe.transpose(ps_t[0:3 * NT, h * 64:h * 64 + 64].bitcast(BF16),
                                          nm[:, h, :, :].rearrange("p s t -> p (s t)"), ident16[:])
                    mm.then_inc(nm_turned, 1)

                def values(grp, t):
                    n = NT * grp + t
                    pe.wait_ge(expd, n + 1)
                    if t % 4 == 0 and n >= 4:
                        pe.wait_ge(pv_copied, n // 4)
                    for h in range(GROUP):
                        out = ps_v[32 * h:32 * h + 32, c1(t % 4)]
                        mm = pe.matmul(out, V_aug[:, t, GROUP * grp + h, :], probs[:, n % 3, h, 0:P], start=True,
                                       stop=(t == 0), skip_group_check=True)
                    if t >= 1:
                        for h in range(GROUP):
                            out = ps_v[32 * h:32 * h + 32, c1(t % 4)]
                            mm = pe.matmul(out[:, 0:WINDOW], V_aug[:, t - 1, GROUP * grp + h, :],
                                           probs[:, (n - 1) % 3, h, P:SPAN], start=False, stop=True,
                                           skip_group_check=True)
                    mm.then_inc(pv_done, 1)

                def turn_values(n):
                    pe.wait_ge(pv_copied, n + 1)
                    if n >= 1:
                        pe.wait_ge(o_ready, n)
                    if n % NC4 == 0:
                        pe.wait_ge(nm_rows_ready, min(n // NC4 + 2, NG))
                    for i in range(4):
                        mm = pe.transpose(ps_t[:, c1(i)], pv_sb[:, n % 2, c1(i)], g.ident[:])
                    mm.then_inc(pv_turned, 1)

                maxima_of(0)
                turn_maxima(0)
                for grp in range(NG):
                    if grp + 1 < NG:
                        maxima_of(grp + 1)
                        turn_maxima(grp + 1)
                    pe.wait_ge(nm_placed, 16 * GROUP * (grp + 1))
                    par = grp % 2
                    for t in range(NT + 1):
                        if t < NT:
                            n = NT * grp + t
                            if n >= 2:
                                pe.wait_ge(expd, n - 1)
                            for half in range(2):
                                dst = ps_s[:, 2 * (n % 2) + half, 0:2 * SPAN]
                                pe.matmul(dst, ident16[:], bcast(mask_k[:], P, 2, SPAN), start=True, stop=False)
                                for i in range(2):
                                    h = 2 * half + i
                                    mm = pe.matmul(dst[:, i * SPAN:(i + 1) * SPAN],
                                                   K[:, par, h, WINDOW + t * P:WINDOW + (t + 1) * P],
                                                   Q[:, par, h, t * P:t * P + SPAN], start=False, stop=(i == 1))
                            mm.then_inc(scored, 1)
                        if t >= 1:
                            values(grp, t - 1)
                        if t >= 6 and (t - 6) % 4 == 0:
                            turn_values(NC4 * grp + (t - 6) // 4)
                    turn_values(NC4 * grp + NC4 - 1)

            @block.scalar
            def _(act):
                for n in range(NG * NT):
                    act.wait_ge(scored, n + 1)
                    if n >= 3:
                        act.wait_ge(pv_done, n - 1)
                    b = 2 * (n % 2)
                    act.activation(probs[:, n % 3, :, :].rearrange("p (b h) c -> p b (h c)", b=2),
                                   ps_s[:, b:b + 2, 0:2 * SPAN], ACT.Exp).then_inc(expd, 1)

            @block.vector
            def _(dve):
                link = Chain(dve, chain)

                def maxima_of(grp):
                    for t in range(NT):
                        for half in range(2):
                            n = 2 * (NT * grp + t) + half
                            dve.wait_ge(m_done, n + 1)
                            dve.tensor_reduce(maxima[:, t, 2 * half:2 * half + 2], heads2(ps_m[:, n % 2, 0:2 * SPAN]),
                                              AX_X, ALU.max).then_inc(m_read, 1)
                    dve.wait_ge(m_read, 2 * NT * (grp + 1))
                    link(dve.tensor_scalar(negmax[:], maxima[:].rearrange("p t h -> p h t"), -1.0, None, ALU.mult))
                    if grp >= 1:
                        dve.wait_ge(nm_turned, grp)
                    splits_of(link, dve, [nm[:, :, i, :] for i in range(3)], rest[:], negmax[:], nm_ready)
                    dve.wait_ge(nm_turned, grp + 1)
                    if grp >= 1:
                        dve.wait_ge(nm_placed, 16 * GROUP * grp)
                    dve.tensor_copy(nm_rows[:], ps_t[0:3 * NT, 0:4 * 64].bitcast(BF16).rearrange(
                        "p (h q) -> p h q", h=GROUP)).then_inc(nm_rows_ready, 1)

                def values_of(n):
                    grp, c = n // NC4, n % NC4
                    dve.wait_ge(pv_done, 4 * (n + 1))
                    if n >= 2:
                        dve.wait_ge(pv_turned, n - 1)
                    dve.tensor_copy(pv_sb[:, n % 2, :], ps_v[:]).then_inc(pv_copied, 1)
                    dve.wait_ge(pv_turned, n + 1)
                    v = ps_t[:, 0:BANK].rearrange("p (t h k) -> p t h k", t=4, h=GROUP)
                    link(dve.reciprocal(rden[:], v[:, :, :, L3_K]))
                    o = O[:, 4 * c:4 * c + 4, :].rearrange("p t (h k) -> p t h k", k=L3_K)
                    for t in range(4):
                        ins = dve.tensor_tensor(o[:, t, GROUP * grp:GROUP * grp + GROUP, :], v[:, t, :, 0:L3_K],
                                                bcast(rden[:, t, :].unsqueeze(2), P, GROUP, L3_K), ALU.mult)
                    ins.then_inc(o_ready, 1)

                maxima_of(0)
                for grp in range(NG):
                    if grp + 1 < NG:
                        maxima_of(grp + 1)
                    for c in range(NC4):
                        values_of(NC4 * grp + c)


def stage_l3_mix(nc, d, g, O, rem, gates):
    with Stage(nc, "l3mix") as st:
        gated = st.sb("gated", [P, NT, P])
        remote_scaled = st.sem("remote_scaled")
        local_scaled = st.sem("local_scaled")
        heads = lambda ap: ap.rearrange("p t (h k) -> p (t h) k", k=L3_K)
        gate = lambda i: bcast(gates[:, i, :, :].rearrange("p t h -> p (t h)").unsqueeze(2), P, NT * L3_H, L3_K)
        with st.block() as block:

            @block.gpsimd
            def _(pool):
                pool.tensor_tensor(heads(gated[:]), heads(rem[:]), gate(1), ALU.mult)\
                    .then_inc(remote_scaled, 1)
                pool.wait_ge(remote_scaled, 1)

            @block.vector
            def _(dve):
                dve.tensor_tensor(heads(O[:]), heads(O[:]), gate(0), ALU.mult).then_inc(local_scaled, 1)
                dve.wait_ge(local_scaled, 1)
                dve.wait_ge(remote_scaled, 1)
                dve.tensor_tensor(O[:], O[:], gated[:], ALU.add)


def layer3_attention(nc, d, g):
    adaln(nc, g, 3, SCALE_A, SHIFT_A)
    q_parts = nc.dram_tensor("l3_q_parts", [3, P, S], BF16, kind="Internal").ap()
    k_parts = nc.dram_tensor("l3_k_parts", [3, P, S], BF16, kind="Internal").ap()
    with Stage(nc, "l3") as st:
        V_aug = st.sb("V_aug", [P, NT, L3_H, 32])
        rem = st.sb("rem", [P, NT, P])
        gates = st.sb("gates", [P, 2, NT, L3_H])
        with Stage(nc, "l3q") as st_q:
            q = st_q.sb("q", [P, S])
            stage_project_parts(nc, d, g, "l3proj", "l3_wqkv", V_aug, q_parts, k_parts, q)
            stage_l3_latent(nc, d, g, q, rem, gates)
        O = st.sb("O", [P, NT, P])
        stage_l3_local(nc, d, g, V_aug, q_parts, k_parts, O)
        stage_l3_mix(nc, d, g, O, rem, gates)
        stage_project_out(nc, d, g, "l3out", O, "l3_wout", mod_row(g, 3, GATE_A))



E3, F3 = 8, 512
CAP = S // E3
DIGITS, DIGIT = 8, 4
CAND = 2 ** DIGIT - 1
TAKEN = -3.0e38


def stage_l3_select(nc, d, g, nT, slot):
    with Stage(nc, "l3sel") as st:
        cent = st.sb("cent", [P, E3])
        digit_bits = st.sb("digit_bits", [P, DIGITS, CAND], I32)
        before = st.sb("before", [P, P], BF16)
        ones = st.sb("ones", [P, P], BF16)
        scores = st.sb("scores", [P, E3, NT])
        left = st.sb("left", [P, NT])
        s = st.sb("s", [P, NT])
        u = st.sb("u", [P, 1], I32)
        cand = st.sb("cand", [P, CAND], I32)
        flip = st.sb("flip", [P, CAND], I32)
        thr = st.sb("thr", [P, CAND], I32)
        reach = st.sb("reach", [P, CAND, NT])
        part = st.sb("part", [P, CAND], BF16)
        enough = st.sb("enough", [P, CAND])
        digit = st.sb("digit", [P, 1])
        digit_int = st.sb("digit_int", [P, 1], I32)
        masks = st.sb("masks", [P, 2, NT], BF16)
        eq = st.sb("eq", [P, NT])
        gt = st.sb("gt", [P, NT])
        upto = st.sb("upto", [P, NT])
        zero16 = st.sb("zero16", [P, NT])
        need = st.sb("need", [P, 1])
        member = st.sb("member", [P, E3, NT])
        member16 = st.sb("member16", [P, E3, NT], BF16)
        rank = st.sb("rank", [P, E3, NT])
        base = st.sb("base", [P, E3, NT])
        slot_f = st.sb("slot_f", [P, NT])
        ps_s = st.ps("ps_s", [P, BANK])
        ps_c = st.ps("ps_c", [P, 2, BANK])
        loaded = st.sem("loaded")
        consts = st.sem("consts")
        scored = st.sem("scored")
        part_ready = st.sem("part_ready")
        counted = st.sem("counted")
        masks_ready = st.sem("masks_ready")
        masks_counted = st.sem("masks_counted")
        members_ready = st.sem("members_ready")
        ranked = st.sem("ranked")
        chain = st.sem("chain")
        with st.block() as block:

            @block.sync
            def _(sp):
                for dst, name in ((cent, "l3_centT"), (digit_bits, "digit_bits"), (before, "before"), (base, "bases")):
                    sp.dma_start(dst[:], d[name]).then_inc(loaded, 16)

            @block.tensor
            def _(pe):
                pe.wait_ge(loaded, 64)
                for t in range(NT):
                    mm = pe.matmul(ps_s[:, E3 * t:E3 * t + E3], nT[:, c1(t)], cent[:], start=True, stop=True)
                mm.then_inc(scored, 1)
                for e in range(E3):
                    for i in range(DIGITS):
                        n = DIGITS * e + i
                        pe.wait_ge(part_ready, n + 1)
                        pe.matmul(ps_c[:, 0, 0:CAND], ones[:], part[:], start=True, stop=True).then_inc(counted, 1)
                    pe.wait_ge(masks_ready, e + 1)
                    m = masks[:].rearrange("p a t -> p (a t)")
                    pe.matmul(ps_c[:, 1, 0:2 * NT], before[:], m, start=True, stop=True)
                    pe.matmul(ps_c[:, 1, 2 * NT:4 * NT], ones[:], m, start=True, stop=True).then_inc(masks_counted, 1)
                pe.wait_ge(members_ready, 1)
                m = member16[:].rearrange("p e t -> p (e t)")
                pe.matmul(ps_s[:, 0:E3 * NT], before[:], m, start=True, stop=True)
                pe.matmul(ps_s[:, E3 * NT:2 * E3 * NT], ones[:], m, start=True, stop=True).then_inc(ranked, 1)

            @block.vector
            def _(dve):
                link = Chain(dve, chain)
                link.mark(dve.memset(ones[:], 1.0))
                link.mark(dve.memset(zero16[:], 1.0))
                link.mark(dve.memset(left[:], 0.0))
                dve.wait_ge(scored, 1)
                link(dve.tensor_copy(scores[:], ps_s[:, 0:E3 * NT].rearrange("p (t e) -> p e t", e=E3)))
                dve.wait_ge(loaded, 64)
                for e in range(E3):
                    link.mark(dve.memset(u[:], 0))
                    link(dve.tensor_tensor(s[:], scores[:, e, :], left[:], ALU.add))
                    for i in range(DIGITS):
                        n = DIGITS * e + i
                        link(dve.tensor_tensor(cand[:], bcast(u[:], P, CAND), digit_bits[:, i, :], ALU.bitwise_or))
                        link(dve.tensor_scalar(flip[:], cand[:], 31, -1, ALU.arith_shift_right, ALU.bitwise_xor))
                        link(dve.tensor_scalar(flip[:], flip[:], -2 ** 31, None, ALU.bitwise_or))
                        link(dve.tensor_tensor(thr[:], flip[:], cand[:], ALU.bitwise_xor))
                        link(dve.tensor_tensor(reach[:], bcast(s[:].unsqueeze(1), P, CAND, NT),
                                               bcast(thr[:].bitcast(F32).unsqueeze(2), P, CAND, NT), ALU.is_ge))
                        with nc.allow_low_precision(reason="counts up to 16 are exact in bfloat16"):
                            dve.tensor_reduce(part[:], reach[:], AX_X, ALU.add).then_inc(part_ready, 1)
                        dve.wait_ge(counted, n + 1)
                        link(dve.tensor_scalar(enough[:], ps_c[:, 0, 0:CAND], float(CAP), None, ALU.is_ge))
                        link(dve.tensor_reduce(digit[:], enough[:], AX_X, ALU.add))
                        link(dve.tensor_copy(digit_int[:], digit[:]))
                        shift = 32 - DIGIT * (i + 1)
                        link(dve.tensor_scalar(digit_int[:], digit_int[:], shift, None, ALU.logical_shift_left))
                        link(dve.tensor_tensor(u[:], u[:], digit_int[:], ALU.bitwise_or))
                    link(dve.tensor_scalar(flip[:, 0:1], u[:], 31, -1, ALU.arith_shift_right, ALU.bitwise_xor))
                    link(dve.tensor_scalar(flip[:, 0:1], flip[:, 0:1], -2 ** 31, None, ALU.bitwise_or))
                    link(dve.tensor_tensor(thr[:, 0:1], flip[:, 0:1], u[:], ALU.bitwise_xor))
                    v = thr[:, 0:1].bitcast(F32)
                    link.mark(dve.tensor_scalar(gt[:], s[:], v, None, ALU.is_gt))
                    link(dve.tensor_scalar(eq[:], s[:], v, None, ALU.is_equal))
                    link.mark(dve.tensor_copy(masks[:, 0, :], eq[:]))
                    dve.tensor_copy(masks[:, 1, :], gt[:]).then_inc(masks_ready, 1)
                    dve.wait_ge(masks_counted, e + 1)
                    within, tot_eq, tot_gt = ps_c[:, 1, 0:NT], ps_c[:, 1, 2 * NT:3 * NT], ps_c[:, 1, 3 * NT:4 * NT]
                    link.mark(dve.tensor_reduce(need[:], tot_gt, AX_X, ALU.add))
                    link(dve.tensor_tensor_scan(upto[:], zero16[:], tot_eq, 0.0, ALU.mult, ALU.add))
                    link.mark(dve.tensor_scalar(need[:], need[:], -1.0, float(CAP), ALU.mult, ALU.add))
                    link(dve.tensor_tensor(upto[:], upto[:], tot_eq, ALU.subtract))
                    link(dve.tensor_tensor(upto[:], upto[:], within, ALU.add))
                    link(dve.scalar_tensor_tensor(eq[:], upto[:], need[:], eq[:], ALU.is_lt, ALU.mult))
                    link(dve.tensor_tensor(member[:, e, :], gt[:], eq[:], ALU.add))
                    link(dve.scalar_tensor_tensor(left[:], member[:, e, :], TAKEN, left[:], ALU.mult, ALU.add))
                dve.tensor_copy(member16[:], member[:]).then_inc(members_ready, 1)
                dve.wait_ge(ranked, 1)
                within = ps_s[:, 0:E3 * NT].rearrange("p (e t) -> p e t", e=E3)
                totals = ps_s[:, E3 * NT:2 * E3 * NT].rearrange("p (e t) -> p e t", e=E3)
                for e in range(E3):
                    link.mark(dve.tensor_tensor_scan(rank[:, e, :], zero16[:], totals[:, e, :], 0.0, ALU.mult, ALU.add))
                link.wait()
                link(dve.tensor_tensor(rank[:], rank[:], totals, ALU.subtract))
                link(dve.tensor_tensor(rank[:], rank[:], within, ALU.add))
                link(dve.tensor_tensor(rank[:], rank[:], base[:], ALU.add))
                link(dve.tensor_tensor(rank[:], rank[:], member[:], ALU.mult))
                link(dve.tensor_reduce(slot_f[:], rank[:].rearrange("p e t -> p t e"), AX_X, ALU.add))
                link(dve.tensor_copy(slot[:], slot_f[:]))


def stage_l3_mlp(nc, d, g, n_tm, h_tm, slot, sorted_in, sorted_out):
    with Stage(nc, "l3mlp") as st:
        w1 = st.sb("w1", [P, E3, F3])
        w2 = st.sb("w2", [P, E3, 4, P])
        b1 = st.sb("b1", [P, E3, 4])
        b2 = st.sb("b2", [1, E3, P])
        ones = st.sb("ones", [1, P])
        rows = st.sb("rows", [P, NT, P])
        rowsT = st.sb("rowsT", [P, S])
        hid = st.sb("hid", [P, 2, 4, CAP])
        y = st.sb("y", [P, NT, P])
        back = st.sb("back", [P, NT, P])
        ps_t = st.ps("ps_t", [P, 2, BANK])
        ps_h = st.ps("ps_h", [P, 4, BANK])
        ps_y = st.ps("ps_y", [P, 2, BANK])
        loaded = st.sem("loaded")
        ones_ready = st.sem("ones_ready")
        scattered = st.sem("scattered")
        rows_loaded = st.sem("rows_loaded")
        turned = st.sem("turned")
        rows_ready = st.sem("rows_ready")
        hid_done = st.sem("hid_done")
        hid_ready = st.sem("hid_ready")
        y_done = st.sem("y_done")
        y_copied = st.sem("y_copied")
        y_stored = st.sem("y_stored")
        gathered = st.sem("gathered")
        chain = st.sem("chain")
        with st.block() as block:

            @block.sync
            def _(sp):
                for dst, name in ((w1, "l3_w1"), (w2, "l3_w2"), (b1, "l3_b1"), (b2, "l3_b2")):
                    sp.dma_start(dst[:], d[name]).then_inc(loaded, 16)
                sp.wait_ge(scattered, 16 * NT)
                sp.dma_start(rows[:], sorted_in.rearrange("(t p) f -> p t f", p=P)).then_inc(rows_loaded, 16)
                sp.wait_ge(y_copied, E3)
                sp.dma_start(sorted_out.rearrange("(t p) f -> p t f", p=P), y[:]).then_inc(y_stored, 16)
                sp.wait_ge(y_stored, 16)

            @block.gpsimd
            def _(pool):
                for t in range(NT):
                    pool.indirect_dma_start(out=sorted_in, out_offset=bass.IndirectOffsetOnAxis(
                        ap=slot[:, t:t + 1], axis=0), in_=n_tm[:, t, :], in_offset=None).then_inc(scattered, 16)
                pool.wait_ge(y_stored, 16)
                for t in range(NT):
                    pool.indirect_dma_start(out=back[:, t, :], out_offset=None, in_=sorted_out,
                                            in_offset=bass.IndirectOffsetOnAxis(ap=slot[:, t:t + 1], axis=0))\
                        .then_inc(gathered, 16)
                pool.wait_ge(gathered, 16 * NT)

            @block.tensor
            def _(pe):
                pe.wait_ge(rows_loaded, 16)
                for j in range(NC4):
                    if j >= 2:
                        pe.wait_ge(rows_ready, j - 1)
                    for i in range(4):
                        mm = pe.transpose(ps_t[:, j % 2, c1(i)], rows[:, 4 * j + i, :], g.ident[:])
                    mm.then_inc(turned, 1)
                pe.wait_ge(loaded, 64)
                pe.wait_ge(ones_ready, 1)

                def down(e):
                    pe.wait_ge(hid_ready, 4 * (e + 1))
                    if e >= 2:
                        pe.wait_ge(y_copied, e - 1)
                    for i in range(2):
                        dst = ps_y[:, e % 2, c1(i)]
                        for f in range(4):
                            pe.matmul(dst, hid[:, e % 2, f, c1(i)], w2[:, e, f, :], start=(f == 0), stop=False,
                                      skip_group_check=True)
                        mm = pe.matmul(dst, ones[:], b2[:, e, :], start=False, stop=True, skip_group_check=True)
                    mm.then_inc(y_done, 1)

                for e in range(E3):
                    pe.wait_ge(rows_ready, e // 2 + 1)
                    if e >= 2:
                        pe.wait_ge(hid_ready, 4 * (e - 1))
                    for f in range(4):
                        pe.matmul(ps_h[:, 2 * (e % 2) + f // 2, CAP * (f % 2):CAP * (f % 2) + CAP], w1[:, e, c1(f)],
                                  rowsT[:, CAP * e:CAP * (e + 1)], start=True, stop=True).then_inc(hid_done, 1)
                    if e >= 1:
                        down(e - 1)
                down(E3 - 1)

            @block.scalar
            def _(act):
                for j in range(NC4):
                    act.wait_ge(turned, j + 1)
                    act.activation(rowsT[:, c4(j)], ps_t[:, j % 2, :], ACT.Identity).then_inc(rows_ready, 1)
                act.wait_ge(loaded, 64)
                for e in range(E3):
                    if e >= 2:
                        act.wait_ge(y_done, e - 1)
                    for f in range(4):
                        act.wait_ge(hid_done, 4 * e + 2 * (f // 2) + 2)
                        act.activation(hid[:, e % 2, f, :],
                                       ps_h[:, 2 * (e % 2) + f // 2, CAP * (f % 2):CAP * (f % 2) + CAP],
                                       ACT.Gelu_apprx_tanh, bias=b1[:, e, f:f + 1]).then_inc(hid_ready, 1)

            @block.vector
            def _(dve):
                link = Chain(dve, chain)
                dve.memset(ones[:], 1.0).then_inc(ones_ready, 1)
                gate = bcast(mod_row(g, 3, GATE_B).unsqueeze(1), P, NT, P)
                for e in range(E3):
                    dve.wait_ge(y_done, e + 1)
                    dve.tensor_copy(y[:, 2 * e:2 * e + 2, :].rearrange("p t f -> p (t f)"), ps_y[:, e % 2, 0:2 * P])\
                       .then_inc(y_copied, 1)
                dve.wait_ge(gathered, 16 * NT)
                link(dve.tensor_tensor(back[:], back[:], h_tm[:], ALU.add))
                link(dve.tensor_tensor(back[:], back[:], gate, ALU.mult))
                dve.tensor_tensor(g.x[:], g.x[:], back[:], ALU.add)


def stage_affine(nc, g, name, jobs):
    with Stage(nc, name) as st:
        done = st.sem("done")
        with st.block() as block:

            @block.gpsimd
            def _(pool):
                n = 0
                for out, in_, scale_row, shift_row in jobs:
                    pool.tensor_tensor(out[:], in_[:], bcast(scale_row.unsqueeze(1), P, NT, P), ALU.mult)\
                        .then_inc(done, 1)
                    n += 1
                    pool.wait_ge(done, n)
                    pool.tensor_tensor(out[:], out[:], bcast(shift_row.unsqueeze(1), P, NT, P), ALU.add)\
                        .then_inc(done, 1)
                    n += 1
                pool.wait_ge(done, n)


def layer3_experts(nc, d, g):
    adaln(nc, g, 3, SCALE_B, SHIFT_B)
    sorted_in = nc.dram_tensor("sorted_in", [S, P], F32, kind="Internal").ap()
    sorted_out = nc.dram_tensor("sorted_out", [S, P], F32, kind="Internal").ap()
    with Stage(nc, "l3f") as st:
        h_tm = st.sb("h_tm", [P, NT, P])
        n_tm = st.sb("n_tm", [P, NT, P])
        slot = st.sb("slot", [P, NT], I32)
        ln_cols = st.sb("ln_cols", [P, 2])
        ln_rows = st.sb("ln_rows", [P, 2, P])
        ln_loaded = st.sem("ln_loaded")
        nc.sync.dma_start(ln_cols[:], d["l3_lncols"]).then_inc(ln_loaded, 16)
        nc.sync.dma_start(ln_rows[:], d["l3_lnrows"]).then_inc(ln_loaded, 16)
        nc.scalar.wait_ge(ln_loaded, 32)
        nc.gpsimd.wait_ge(ln_loaded, 32)
        stage_affine(nc, g, "l3h", [(h_tm, g.xn, mod_row(g, 3, SCALE_B), mod_row(g, 3, SHIFT_B))])
        stage_norm(nc, g, "l3norm", h_tm, n_tm, g.hT, ln_cols[:, 0:1], ln_cols[:, 1:2])
        stage_l3_select(nc, d, g, g.hT, slot)
        stage_affine(nc, g, "l3n", [(n_tm, n_tm, ln_rows[:, 0, :], ln_rows[:, 1, :])])
        stage_l3_mlp(nc, d, g, n_tm, h_tm, slot, sorted_in, sorted_out)



class Persistent:
    pass


def program(nc, d, out, stages=None):
    with ExitStack() as ctx:
        g = Persistent()

        def sb(name, shape, dt=F32):
            return ctx.enter_context(nc.sbuf_tensor(name, shape, dt))

        d = {name: ap.bitcast(BF16) if name in BF16_CONSTANTS else ap for name, ap in d.items()}
        g.x = sb("x_res", [P, NT, P])
        g.xn = sb("xn", [P, NT, P])
        g.hT = sb("hT", [P, S])
        g.mod_rows = sb("mod_rows", [P, 4, 6, P])
        g.mod_cols = sb("mod_cols", [P, 24])
        g.ident = sb("ident_sb", [P, P])
        stage_setup(nc, d, g)
        for layer_part in (stages or ALL_STAGES):
            with nc.cleanup_on_exit():
                layer_part(nc, d, g)
        stage_store(nc, g, out)


def stage_store(nc, g, out):
    with Stage(nc, "store") as st:
        stored = st.sem("stored")
        with st.block() as block:

            @block.sync
            def _(sp):
                sp.dma_start(out.rearrange("a (t p) f -> p (a t) f", p=P), g.x[:]).then_inc(stored, 16)
                sp.wait_ge(stored, 16)


ALL_STAGES = [layer0_attention, layer0_slots, layer1_delta, layer1_experts,
              layer2_spiking, layer2_product, layer3_attention, layer3_experts]


BF16_CONSTANTS = ("ident16", "lat_causal", "mask_q", "mask_k", "before")


def lay_out(inp):

    def bits16(constant):
        return (constant.astype(np.float32).view(np.uint32) >> 16).astype(np.uint16)

    a = {k: np.asarray(v) for k, v in inp.items()}
    heads = lambda w: w.transpose(1, 0, 2).reshape(P, P)
    d = {
        "x": a["L0_attn_q"][0],
        "c_cols": np.concatenate([a[f"L{l}_c"] for l in range(4)], 0).T,
        "wmod": np.stack([a[f"L{l}_wmod"] for l in range(4)], 1),
        "ident": np.eye(P, dtype=np.float32),
        "ident16": bits16(np.eye(P)),
        "l0_wqkv": np.stack([heads(a[f"L0_attn_W_{n}"]) for n in ("query", "key", "val")], 1),
        "l0_wout": a["L0_attn_W_out"].reshape(P, P),
    }
    w1T = a["L0_ffn_w1"].T
    d.update({
        "l0_b1": a["L0_ffn_b1"][:, None], "l0_w1T": np.stack([w1T[:P], w1T[P:]], 1),
        "l0_w2T": np.concatenate([a["L0_ffn_w2"].T, a["L0_ffn_b2"][None]], 0),
        "l0_tau": np.repeat(a["L0_ffn_tau"][None], P, 0),
        "l0_slots": a["L0_ffn_slot_init"], "l0_slot_scale": a["L0_ffn_slot_scale"],
        "l0_wihT": a["L0_ffn_gru_wih"].T.reshape(P, 3, P), "l0_whhT": a["L0_ffn_gru_whh"].T.reshape(P, 3, P),
        "l0_bih": a["L0_ffn_gru_bih"][None], "l0_bhh": a["L0_ffn_gru_bhh"][None],
        "l0_wvT": a["L0_ffn_wv"].T, "l0_bv": a["L0_ffn_bv"][:, None], "l0_woT": a["L0_ffn_wo"].T,
        "l0_bo": a["L0_ffn_bo"][None],
    })
    i, j = np.arange(P)[:, None], np.arange(P)[None, :]
    level = lambda s: (i // (2 * s) == j // (2 * s)) & (i // s % 2 == 1) & (j // s % 2 == 0)
    rows = lambda v: np.repeat(v[None], P, 0)
    d.update({
        "masks": np.stack([level(s) for s in (1,) + LEVELS] + [j >= i], 1).astype(np.float32),
        "iota": i.astype(np.float32),
        "l1_wq": a["L1_attn_Wq"],
        "l1_wkvb": np.concatenate([a["L1_attn_Wk"], a["L1_attn_Wv"], a["L1_attn_Wb"][:, None]], 1),
        "l1_lng": rows(a["L1_attn_ln_g"]), "l1_lnb": rows(a["L1_attn_ln_b"]),
        "l1_gateT": a["L1_ffn_gate_w"].T, "l1_gate_b": a["L1_ffn_gate_b"][None],
        "l1_expert_w": a["L1_ffn_expert_w"], "l1_expert_b": a["L1_ffn_expert_b"],
    })
    d.update({
        "l2_wrkvo": np.stack([a[f"L2_attn_W{n}"].T for n in "rkvo"], 1),
        "l2_w1T": a["L2_attn_W1"].T.reshape(P, 4, P), "l2_b1": a["L2_attn_b1"].reshape(4, P).T,
        "l2_w2T": a["L2_attn_W2"].T.reshape(4, P, P).transpose(1, 0, 2), "l2_b2": a["L2_attn_b2"][:, None],
        "l2_ln1g": rows(a["L2_attn_ln1_g"]), "l2_ln1b": rows(a["L2_attn_ln1_b"]),
        "l2_ln1cols": np.stack([a["L2_attn_ln1_g"], a["L2_attn_ln1_b"]], 1),
        "l2_ln2g": rows(a["L2_attn_ln2_g"]), "l2_ln2b": rows(a["L2_attn_ln2_b"]),
        "l2_CBT": a["L2_ffn_CB"].T, "l2_SCB": rows(a["L2_ffn_SCB"]), "l2_bias": rows(a["L2_ffn_bias"]),
    })
    neg = lambda seen: bits16(np.where(seen, 0.0, MASK_BIG))
    c = np.arange(SPAN)[None, :]
    seen_q = (c > i) & (c <= i + WINDOW)
    seen_k = (c >= i) & (c < i + WINDOW)
    tokens = i + P * np.arange(NT)[None, :]
    d.update({
        "l3_wqkv": np.stack([a[f"L3_attn_w{n}"] for n in "qkv"], 1),
        "l3_wg": np.stack([a[f"L3_attn_wg{n}"] for n in "qkv"], 1),
        "l3_r_out": a["L3_attn_r_out_w"], "l3_wout": a["L3_attn_w_out"],
        "l3_gates": np.stack([a["L3_attn_gate_local_w"].reshape(P), a["L3_attn_gate_remote_w"].reshape(P)], 1),
        "head_rows": (i // L3_K == np.arange(L3_H)[None, :]).astype(np.float32),
        "lat_causal": neg(np.arange(LATENTS)[None, None, :] <= tokens[:, :, None] // (S // LATENTS)),
        "mask_q": neg(np.stack([seen_q & (c >= WINDOW), seen_q], 1)[:, :, None, :]),
        "mask_k": neg(seen_k[:, None, :]),
        "l3_centT": a["L3_ffn_centroids"].T,
        "l3_lncols": np.stack([a["L3_ffn_ln_g"], a["L3_ffn_ln_b"]], 1),
        "l3_lnrows": np.stack([rows(a["L3_ffn_ln_g"]), rows(a["L3_ffn_ln_b"])], 1),
        "l3_w1": a["L3_ffn_w1"].transpose(1, 0, 2),
        "l3_w2": a["L3_ffn_w2"].reshape(E3, 4, P, P).transpose(2, 0, 1, 3),
        "l3_b1": a["L3_ffn_b1"].reshape(E3, 4, P).transpose(2, 0, 1), "l3_b2": a["L3_ffn_b2"][None],
        "before": bits16(i < j),
        "bases": np.broadcast_to((CAP * np.arange(E3, dtype=np.float32))[None, :, None], (P, E3, NT)),
        "digit_bits": np.broadcast_to(
            (np.arange(1, CAND + 1, dtype=np.int64)[None, :] << (32 - DIGIT * np.arange(1, DIGITS + 1)[:, None]))
            .astype(np.uint32).view(np.int32)[None], (P, DIGITS, CAND)),
    })
    return {k: np.ascontiguousarray(v) for k, v in d.items()}


OUT_SHAPE = (1, S, P)


def kernel(**inputs):
    import concourse.bacc as _bacc
    from concourse.bass_utils import run_bass_kernel_spmd as _run

    nc = _bacc.Bacc("TRN2", target_bir_lowering=False, num_devices=1)
    arrays, d = {}, {}
    for name, a in lay_out(inputs).items():
        arrays[f"in_{name}_dram"] = a
        d[name] = nc.dram_tensor(f"in_{name}_dram", a.shape, mybir.dt.from_np(a.dtype), kind="ExternalInput").ap()
    out = nc.dram_tensor("out_0_dram", OUT_SHAPE, F32, kind="ExternalOutput").ap()
    program(nc, d, out)
    r = _run(nc, [arrays], core_ids=[0])
    return r.results[0]["out_0_dram"]
```

```python
from contextlib import ExitStack

import numpy as np

import concourse.bass as bass
from concourse import mybir

F32 = mybir.dt.float32
BF16 = mybir.dt.bfloat16
I32 = mybir.dt.int32
U32 = mybir.dt.uint32
ALU = mybir.AluOpType
ACT = mybir.ActivationFunctionType
AX_X = mybir.AxisListType.X

P = 128
S = 2048
NT = S // P
BANK = 512
NC4 = S // BANK
LN_EPS = 1e-5
SHIFT_A, SCALE_A, GATE_A, SHIFT_B, SCALE_B, GATE_B = range(6)


class Chain:

    def __init__(self, eng, sem):
        self.eng, self.sem, self.n = eng, sem, 0

    def mark(self, ins):
        self.n += 1
        return ins.then_inc(self.sem, 1)

    def wait(self):
        self.eng.wait_ge(self.sem, self.n)

    def __call__(self, ins):
        self.mark(ins)
        self.wait()


class Stage:

    def __init__(self, nc, name):
        self.nc, self.name, self.ctx = nc, name, ExitStack()

    def __enter__(self):
        self.ctx.__enter__()
        return self

    def __exit__(self, *e):
        return self.ctx.__exit__(*e)

    def sb(self, name, shape, dt=F32):
        return self.ctx.enter_context(self.nc.sbuf_tensor(f"{self.name}_{name}", shape, dt))

    def ps(self, name, shape, dt=F32):
        return self.ctx.enter_context(self.nc.psum_tensor(f"{self.name}_{name}", shape, dt))

    def sem(self, name):
        return self.nc.alloc_semaphore(f"{self.name}_{name}")

    def block(self):
        return self.nc.Block(no_gpsimd_drain=True)


def bcast(ap, *shape):
    return ap.broadcast_to(list(shape))


def c4(j):
    return slice(j * BANK, (j + 1) * BANK)


def c1(t):
    return slice(t * P, (t + 1) * P)



def stage_setup(nc, d, g):
    with Stage(nc, "setup") as st:
        wmod = st.sb("wmod", [P, 4, 6 * P])
        c_cols = st.sb("c_cols", [P, 4])
        sig = st.sb("sig", [P, 4])
        silu = st.sb("silu", [P, 4])
        silu_rep = st.sb("silu_rep", [P, 4, P])
        floor_r = st.sb("floor_r", [P, 4, 2, P])
        sign_r = st.sb("sign_r", [P, 4, 2, P])
        ones = st.sb("ones", [P, P])
        ps = st.ps("ps", [P, 8, BANK])
        loaded = st.sem("loaded")
        sig_done = st.sem("sig_done")
        rep_done = st.sem("rep_done")
        rows_done = st.sem("rows_done")
        rows_copied = st.sem("rows_copied")
        cols_done = st.sem("cols_done")
        chain = st.sem("chain")
        with st.block() as block:

            @block.sync
            def _(sp):
                sp.dma_start(c_cols[:], d["c_cols"]).then_inc(loaded, 16)
                sp.dma_start(wmod[:], d["wmod"]).then_inc(loaded, 16)
                sp.dma_start(g.ident[:], d["ident"]).then_inc(loaded, 16)
                sp.dma_start(g.x[:], d["x"].rearrange("(t p) f -> p t f", p=P)).then_inc(loaded, 16)

            @block.scalar
            def _(act):
                act.wait_ge(loaded, 64)
                act.activation(sig[:], c_cols[:], ACT.Sigmoid).then_inc(sig_done, 1)

            @block.tensor
            def _(pe):
                pe.wait_ge(rep_done, 1)
                for l in range(4):
                    for half in range(2):
                        mm = pe.matmul(ps[:, 2 * l + half, 0:384], silu_rep[:, l, :],
                                       wmod[:, l, 384 * half:384 * half + 384], start=True, stop=True)
                    mm.then_inc(rows_done, 1)
                pe.wait_ge(rows_copied, 8)
                for l in range(4):
                    for j in range(6):
                        mm = pe.matmul(ps[:, 0, 6 * l + j:6 * l + j + 1], wmod[:, l, c1(j)],
                                       silu[:, l:l + 1], start=True, stop=True)
                mm.then_inc(cols_done, 1)

            @block.vector
            def _(dve):
                link = Chain(dve, chain)
                link(dve.memset(ones[:], 1.0))
                dve.wait_ge(sig_done, 1)
                link(dve.tensor_tensor(silu[:], sig[:], c_cols[:], ALU.mult))
                for l in range(4):
                    ins = dve.tensor_scalar(silu_rep[:, l, :], ones[:], silu[:, l:l + 1], None, ALU.mult)
                ins.then_inc(rep_done, 1)
                for l in range(4):
                    dve.wait_ge(rows_done, l + 1)
                    for half in range(2):
                        rows = g.mod_rows[:, l, 3 * half:3 * half + 3, :]
                        dve.tensor_copy(rows, ps[:, 2 * l + half, 0:384].rearrange(
                            "p (j f) -> p j f", j=3)).then_inc(rows_copied, 1)
                dve.wait_ge(rows_copied, 8)
                dve.wait_ge(cols_done, 1)
                link(dve.tensor_copy(g.mod_cols[:], ps[:, 0, 0:24]))
                gates_r = g.mod_rows[:, :, GATE_A::3, :]
                link.mark(dve.tensor_scalar(floor_r[:], gates_r, -1.0, None, ALU.mult))
                link(dve.tensor_scalar(sign_r[:], gates_r, 0.0, 2.0, ALU.is_ge, ALU.mult))
                link.mark(dve.tensor_tensor(floor_r[:], floor_r[:], gates_r, ALU.max))
                link(dve.tensor_scalar(sign_r[:], sign_r[:], -1.0, None, ALU.add))
                link(dve.tensor_scalar(floor_r[:], floor_r[:], 0.25, None, ALU.max))
                link.mark(dve.tensor_tensor(gates_r, floor_r[:], sign_r[:], ALU.mult))
                cols = g.mod_cols[:].rearrange("p (l j) -> p l j", l=4)
                gates_c, floor_c, sign_c = cols[:, :, GATE_A::3], floor_r[:, 0, 0, 0:8], sign_r[:, 0, 0, 0:8]
                floor_c = floor_c.rearrange("p (l j) -> p l j", l=4)
                sign_c = sign_c.rearrange("p (l j) -> p l j", l=4)
                link.wait()
                link.mark(dve.tensor_scalar(floor_c, gates_c, -1.0, None, ALU.mult))
                link(dve.tensor_scalar(sign_c, gates_c, 0.0, 2.0, ALU.is_ge, ALU.mult))
                link.mark(dve.tensor_tensor(floor_c, floor_c, gates_c, ALU.max))
                link(dve.tensor_scalar(sign_c, sign_c, -1.0, None, ALU.add))
                link(dve.tensor_scalar(floor_c, floor_c, 0.25, None, ALU.max))
                link(dve.tensor_tensor(gates_c, floor_c, sign_c, ALU.mult))
                for scale in (SCALE_A, SCALE_B):
                    link.mark(dve.tensor_scalar(cols[:, :, scale], cols[:, :, scale], 1.0, None, ALU.add))
                    link.mark(dve.tensor_scalar(g.mod_rows[:, :, scale, :], g.mod_rows[:, :, scale, :], 1.0, None,
                                                ALU.add))
                link.wait()



def stage_norm(nc, g, name, src, normed, turned=None, scale_col=None, shift_col=None):
    with Stage(nc, name) as st:
        stats = st.sb("stats", [P, NT, 6])
        mv = st.sb("mv", [P, NT, 2])
        var = st.sb("var", [P, NT])
        std = st.sb("std", [P, NT])
        rstd = st.sb("rstd", [P, NT])
        corr = st.sb("corr", [P, NT])
        ps = st.ps("ps", [P, 4, BANK])
        var_ready = st.sem("var_ready")
        std_ready = st.sem("std_ready")
        tile_normed = st.sem("tile_normed")
        bank_full = st.sem("bank_full")
        chain = st.sem("chain")
        with st.block() as block:

            @block.vector
            def _(dve):
                link = Chain(dve, chain)
                for t in range(NT):
                    link.mark(dve.bn_stats(stats[:, t, :], src[:, t, :]))
                link.wait()
                for t in range(NT):
                    link.mark(dve.bn_aggr(mv[:, t, :], stats[:, t, :]))
                link.wait()
                dve.tensor_scalar(var[:], mv[:, :, 1], LN_EPS, None, ALU.add).then_inc(var_ready, 1)
                dve.wait_ge(std_ready, 1)
                link(dve.reciprocal(rstd[:], std[:]))
                link(dve.tensor_tensor(corr[:], rstd[:], rstd[:], ALU.mult))
                link(dve.tensor_tensor(corr[:], corr[:], var[:], ALU.mult))
                link(dve.tensor_scalar(corr[:], corr[:], -0.5, 1.5, ALU.mult, ALU.add))
                link(dve.tensor_tensor(rstd[:], rstd[:], corr[:], ALU.mult))
                for t in range(NT):
                    dve.tensor_scalar(normed[:, t, :], src[:, t, :], mv[:, t, 0:1], rstd[:, t:t + 1],
                                      ALU.subtract, ALU.mult).then_inc(tile_normed, 1)

            @block.tensor
            def _(pe):
                for t in range(NT if turned is not None else 0):
                    pe.wait_ge(tile_normed, t + 1)
                    mm = pe.transpose(ps[:, t // 4, c1(t % 4)], normed[:, t, :], g.ident[:])
                    if t % 4 == 3:
                        mm.then_inc(bank_full, 1)

            @block.scalar
            def _(act):
                act.wait_ge(var_ready, 1)
                act.activation(std[:], var[:], ACT.Sqrt).then_inc(std_ready, 1)
                for j in range(NC4 if turned is not None else 0):
                    act.wait_ge(bank_full, j + 1)
                    act.activation(turned[:, c4(j)], ps[:, j, :], ACT.Identity, bias=shift_col, scale=scale_col)


def mod_col(g, layer, which):
    return g.mod_cols[:, 6 * layer + which:6 * layer + which + 1]


def mod_row(g, layer, which):
    return g.mod_rows[:, layer, which, :]


def adaln(nc, g, layer, scale, shift):
    stage_norm(nc, g, f"ada{layer}{scale}", g.x, g.xn, g.hT, mod_col(g, layer, scale), mod_col(g, layer, shift))



L0_H, L0_K = 16, 8
GROUP = 4
SPLITS_Q = (0, 0, 1, 0, 1, 2)
SPLITS_K = (0, 1, 0, 2, 1, 0)
HEAD_BUFS = 3
MAX_ROW = 64
MASK_BIG = -1e30


def splits_of(link, dve, parts, rest, full, done):
    link(dve.tensor_copy(parts[0], full))
    link(dve.tensor_tensor(rest, full, parts[0], ALU.subtract))
    link(dve.tensor_copy(parts[1], rest))
    dve.tensor_tensor(parts[2], rest, parts[1], ALU.subtract).then_inc(done, 1)


def clear_operands(pool, Q, K, cleared):
    for operand in (Q, K):
        pool.memset(operand[:].bitcast(F32), 0.0).then_inc(cleared, 1)
    pool.wait_ge(cleared, 2)
    pool.memset(K[MAX_ROW:MAX_ROW + 3], 1.0).then_inc(cleared, 1)
    pool.wait_ge(cleared, 3)


def stage_project_parts(nc, d, g, name, w_name, V_aug, q, qp, kp, Q, K, drams=()):
    with Stage(nc, name) as st:
        w = st.sb("w", [P, 3, P])
        k = st.sb("k", [P, S])
        rest = st.sb("rest", [P, S])
        ps = st.ps("ps", [P, 8, BANK])
        w_loaded = st.sem("w_loaded")
        chunk_done = st.sem("chunk_done")
        chunk_read = st.sem("chunk_read")
        q_done = st.sem("q_done")
        v_done = st.sem("v_done")
        v_zero = st.sem("v_zero")
        parts_done = st.sem("parts_done")
        stored = st.sem("stored")
        cleared = st.sem("cleared")
        chain = st.sem("chain")
        with st.block() as block:

            @block.sync
            def _(sp):
                sp.dma_start(w[:], d[w_name]).then_inc(w_loaded, 16)
                for n, (parts, dram) in enumerate(zip((qp, kp), drams)):
                    sp.wait_ge(parts_done, n + 1)
                    for i in range(3):
                        sp.dma_start(dram[i], parts[i][:]).then_inc(stored, 16)
                if drams:
                    sp.wait_ge(stored, 16 * 6)

            @block.tensor
            def _(pe):
                pe.wait_ge(w_loaded, 16)
                for m in range(2):
                    for j in range(NC4):
                        pe.matmul(ps[:, 4 * m + j, :], w[:, m, :], g.hT[:, c4(j)], start=True,
                                  stop=True).then_inc(chunk_done, 1)
                for t in range(NT):
                    if t % 4 == 0:
                        pe.wait_ge(chunk_read, t // 4 + 1)
                    mm = pe.matmul(ps[:, t // 4, c1(t % 4)], g.hT[:, c1(t)], w[:, 2, :], start=True, stop=True)
                    if t % 4 == 3:
                        mm.then_inc(v_done, 1)

            @block.scalar
            def _(act):
                for n in range(2 * NC4):
                    act.wait_ge(chunk_done, n + 1)
                    dst, scale = (q, L0_K ** -0.5) if n < NC4 else (k, 1.0)
                    act.activation(dst[:, c4(n % NC4)], ps[:, n, :], ACT.Identity,
                                   scale=scale).then_inc(chunk_read, 1)
                act.wait_ge(v_zero, 2)
                for j in range(NC4):
                    act.wait_ge(v_done, j + 1)
                    for t in range(4):
                        act.activation(V_aug[:, 4 * j + t, :, 0:L0_K],
                                       ps[:, j, c1(t)].rearrange("p (h k) -> p h k", h=L0_H), ACT.Identity)

            @block.vector
            def _(dve):
                link = Chain(dve, chain)
                for n, (parts, full) in enumerate(((qp, q), (kp, k))):
                    dve.wait_ge(chunk_read, NC4 * (n + 1))
                    splits_of(link, dve, [p[:] for p in parts], rest[:], full[:], parts_done)
                    dve.wait_ge(parts_done, n + 1)

            @block.gpsimd
            def _(pool):
                pool.memset(V_aug[:], 0.0).then_inc(v_zero, 1)
                pool.wait_ge(v_zero, 1)
                pool.memset(V_aug[:, :, :, L0_K:L0_K + 1], 1.0).then_inc(v_zero, 1)
                clear_operands(pool, Q, K, cleared)


def stage_l0_attend(nc, d, g, V_aug, qp, kp, Q, K, O):
    LEAD = 4
    with Stage(nc, "l0att") as st:
        probs = st.sb("probs", [P, 2, NC4, BANK])
        half_max = st.sb("half_max", [P, 2, NT, 2])
        negmax = st.sb("negmax", [P, NT])
        rest = st.sb("rest", [P, NT])
        nm = st.sb("nm", [P, 2, 3, NT], BF16)
        nm_rows = st.sb("nm_rows", [3 * NT, 2, P], BF16)
        pv_sb = st.sb("pv_sb", [P, 2, BANK])
        rden = st.sb("rden", [P, 4, NC4])
        ident16 = st.sb("ident16", [P, P], BF16)
        ps_s = st.ps("ps_s", [P, 3, BANK])
        ps_m = st.ps("ps_m", [P, 2, 2 * BANK])
        ps_v = st.ps("ps_v", [P, BANK])
        ident_loaded = st.sem("ident_loaded")
        cleared = st.sem("cleared")
        loaded = [st.sem(f"loaded{b}") for b in range(HEAD_BUFS)]
        scored = st.sem("scored")
        expd = st.sem("expd")
        pv_done = st.sem("pv_done")
        pv_copied = st.sem("pv_copied")
        m_filled = st.sem("m_filled")
        m_read = st.sem("m_read")
        nm_ready = st.sem("nm_ready")
        nm_placed = [st.sem("nm_placed0"), st.sem("nm_placed1")]
        chain = st.sem("chain")

        turns, place = [], {}
        negate_before = {}
        copy_before = {}
        plan = {}
        for s in range(-1, L0_H + 1):
            slots = range(NT + LEAD if s < 0 else NT if s < L0_H else 1)
            if s >= 1:
                copy_before[len(turns)] = s - 1
            for kt in slots:
                tile = kt if s < 0 else NT * (s + 1) + LEAD + kt
                uses = []
                if kt == 3 and 1 <= s < L0_H or s == L0_H:
                    uses.append(("pv", s - 1))
                head, t = tile // NT, tile % NT
                if t == 0 and 1 <= head <= L0_H:
                    negate_before[len(turns) + len(uses)] = head - 1
                if t == (0 if head == 1 else 1) and 1 <= head <= L0_H:
                    uses.append(("nm", head - 1))
                if head < L0_H:
                    uses += [("max", head, t, half) for half in range(2)]
                for what in uses:
                    place[what] = len(turns)
                    turns.append(what)
                plan[s, kt] = uses

        with st.block() as block:

            @block.sync
            def _(sp):
                sp.dma_start(ident16[:], d["ident16"]).then_inc(ident_loaded, 16)
                for h in range(L0_H):
                    if h >= HEAD_BUFS:
                        sp.wait_ge(scored, (h - HEAD_BUFS + 1) * NT * NC4)
                    for r in range(6):
                        for operand, parts, part in ((Q, qp, SPLITS_Q[r]), (K, kp, SPLITS_K[r])):
                            sp.dma_start(operand[L0_K * r:L0_K * (r + 1), h % HEAD_BUFS, :],
                                         parts[part][L0_K * h:L0_K * (h + 1), :]).then_inc(loaded[h % HEAD_BUFS], 16)

            @block.gpsimd
            def _(pool):
                for h in range(L0_H):
                    pool.wait_ge(m_read, place["nm", h] + 1)
                    pool.dma_start(Q[MAX_ROW:MAX_ROW + 3, h % HEAD_BUFS, :],
                                   nm_rows[:, h % 2, :]).then_inc(nm_placed[h % 2], 16)
                    if h >= 1 and h + HEAD_BUFS - 1 < L0_H:
                        pool.wait_ge(scored, h * NT * NC4)
                        pool.memset(Q[MAX_ROW:MAX_ROW + 3, (h - 1) % HEAD_BUFS, :], 0.0).then_inc(cleared, 1)

            @block.tensor
            def _(pe):
                def run(what):
                    n = place[what]
                    if n >= 2:
                        pe.wait_ge(m_read, n - 1)
                    dst = ps_m[:, n % 2, :]
                    if what[0] == "max":
                        _, h, t, half = what
                        if t == 0 and half == 0:
                            pe.wait_ge(loaded[h % HEAD_BUFS], 16 * 12 * (h // HEAD_BUFS + 1))
                            if h >= HEAD_BUFS:
                                pe.wait_ge(cleared, h - HEAD_BUFS + 1)
                        for c in (2 * half, 2 * half + 1):
                            mm = pe.matmul(dst[:, (c % 2) * BANK:(c % 2 + 1) * BANK], Q[:, h % HEAD_BUFS, c1(t)],
                                           K[:, h % HEAD_BUFS, c4(c)], start=True, stop=True)
                    elif what[0] == "nm":
                        h = what[1]
                        pe.wait_ge(nm_ready, h + 1)
                        if h == 0:
                            pe.wait_ge(ident_loaded, 16)
                        mm = pe.transpose(dst[0:3 * NT, 0:P // 2].bitcast(BF16), nm[:, h % 2, :, :].rearrange(
                            "p s t -> p (s t)"), ident16[:])
                    else:
                        h = what[1]
                        pe.wait_ge(pv_copied, h + 1)
                        for i in range(4):
                            mm = pe.transpose(dst[:, c1(i)], pv_sb[:, h % 2, c1(i)], g.ident[:])
                    mm.then_inc(m_filled, 1)

                def values(h, kt):
                    if kt == 0 and h >= 1:
                        pe.wait_ge(pv_copied, h)
                    for c in range(NC4):
                        pe.wait_ge(expd, (h * NT + kt) * NC4 + c + 1)
                        mm = pe.matmul(ps_v[32 * c:32 * c + 32, :], V_aug[:, kt, h, :], probs[:, kt % 2, c, :],
                                       start=(kt == 0), stop=(kt == NT - 1))
                    mm.then_inc(pv_done, 1)

                for kt in range(NT + LEAD):
                    for what in plan[-1, kt]:
                        run(what)
                for h in range(L0_H):
                    pe.wait_ge(nm_placed[h % 2], 16 * (h // 2 + 1))
                    for kt in range(NT):
                        todo = list(plan[h, kt])
                        for c in range(NC4):
                            n = (h * NT + kt) * NC4 + c
                            if n >= 3:
                                pe.wait_ge(expd, n - 2)
                            pe.matmul(ps_s[:, n % 3, :], K[:, h % HEAD_BUFS, c1(kt)], Q[:, h % HEAD_BUFS, c4(c)],
                                      start=True, stop=True).then_inc(scored, 1)
                            if todo:
                                run(todo.pop(0))
                        if kt >= 1:
                            values(h, kt - 1)
                    values(h, NT - 1)
                run(("pv", L0_H - 1))

            @block.scalar
            def _(act):
                for n in range(L0_H * NT * NC4):
                    kt, c = n // NC4 % NT, n % NC4
                    act.wait_ge(scored, n + 1)
                    if n // NC4 >= 2:
                        act.wait_ge(pv_done, n // NC4 - 1)
                    act.activation(probs[:, kt % 2, c, :], ps_s[:, n % 3, :], ACT.Exp).then_inc(expd, 1)

            @block.vector
            def _(dve):
                link = Chain(dve, chain)

                def negate(h):
                    dve.wait_ge(m_read, place["max", h, NT - 1, 1] + 1)
                    link(dve.tensor_tensor(negmax[:], half_max[:, h % 2, :, 0], half_max[:, h % 2, :, 1], ALU.max))
                    link(dve.tensor_scalar(negmax[:], negmax[:], -1.0, None, ALU.mult))
                    if h >= 2:
                        dve.wait_ge(m_filled, place["nm", h - 2] + 1)
                    splits_of(link, dve, [nm[:, h % 2, i, :] for i in range(3)], rest[:], negmax[:], nm_ready)

                def copy_values(h):
                    dve.wait_ge(pv_done, NT * (h + 1))
                    if h >= 2:
                        dve.wait_ge(m_filled, place["pv", h - 2] + 1)
                    dve.tensor_copy(pv_sb[:, h % 2, :], ps_v[:]).then_inc(pv_copied, 1)

                for i, what in enumerate(turns):
                    if i in copy_before:
                        copy_values(copy_before[i])
                    if i in negate_before:
                        negate(negate_before[i])
                    dve.wait_ge(m_filled, i + 1)
                    src = ps_m[:, i % 2, :]
                    h = what[1]
                    if what[0] == "max":
                        t, half = what[2:]
                        dve.tensor_reduce(half_max[:, h % 2, t, half:half + 1], src, AX_X, ALU.max)\
                           .then_inc(m_read, 1)
                    elif what[0] == "nm":
                        if h >= 2:
                            dve.wait_ge(nm_placed[h % 2], 16 * (h // 2))
                        dve.tensor_copy(nm_rows[:, h % 2, :], src[0:3 * NT, 0:P // 2].bitcast(BF16))\
                           .then_inc(m_read, 1)
                    else:
                        v = src[:, 0:BANK].rearrange("p (i c k) -> p i c k", i=4, c=NC4)
                        link(dve.reciprocal(rden[:], v[:, :, :, L0_K]))
                        o = O[:, :, L0_K * h:L0_K * (h + 1)].rearrange("p (c i) k -> p i c k", c=NC4)
                        dve.tensor_tensor(o, v[:, :, :, 0:L0_K], bcast(rden[:].unsqueeze(3), P, 4, NC4, L0_K),
                                          ALU.mult).then_inc(m_read, 1)


def stage_project_out(nc, d, g, name, O, w_name, gate_row):
    with Stage(nc, name) as st:
        w = st.sb("w", [P, P])
        OT = st.sb("OT", [P, S])
        ps_t = st.ps("ps_t", [P, 4, BANK])
        ps_o = st.ps("ps_o", [P, 4, BANK])
        w_loaded = st.sem("w_loaded")
        w_gated = st.sem("w_gated")
        turned = st.sem("turned")
        copied = st.sem("copied")
        summed = st.sem("summed")
        with st.block() as block:

            @block.sync
            def _(sp):
                sp.dma_start(w[:], d[w_name]).then_inc(w_loaded, 16)

            @block.tensor
            def _(pe):
                for t in range(NT):
                    mm = pe.transpose(ps_t[:, t // 4, c1(t % 4)], O[:, t, :], g.ident[:])
                    if t % 4 == 3:
                        mm.then_inc(turned, 1)
                pe.wait_ge(w_gated, 1)
                for t in range(NT):
                    if t % 4 == 0:
                        pe.wait_ge(copied, t // 4 + 1)
                    mm = pe.matmul(ps_o[:, t // 4, c1(t % 4)], OT[:, c1(t)], w[:], start=True, stop=True)
                    if t % 4 == 3:
                        mm.then_inc(summed, 1)

            @block.scalar
            def _(act):
                for j in range(NC4):
                    act.wait_ge(turned, j + 1)
                    act.activation(OT[:, c4(j)], ps_t[:, j, :], ACT.Identity).then_inc(copied, 1)

            @block.vector
            def _(dve):
                dve.wait_ge(w_loaded, 16)
                dve.tensor_tensor(w[:], w[:], gate_row, ALU.mult).then_inc(w_gated, 1)
                for j in range(NC4):
                    dve.wait_ge(summed, j + 1)
                    xs = g.x[:, 4 * j:4 * j + 4, :]
                    dve.tensor_tensor(xs, ps_o[:, j, :].rearrange("p (t f) -> p t f", t=4), xs, ALU.add)


def layer0_attention(nc, d, g):
    adaln(nc, g, 0, SCALE_A, SHIFT_A)
    with Stage(nc, "l0") as st:
        O = st.sb("O", [P, NT, P])
        V_aug = st.sb("V_aug", [P, NT, L0_H, 32])
        Q = st.sb("Q", [P, HEAD_BUFS, S], BF16)
        K = st.sb("K", [P, HEAD_BUFS, S], BF16)
        qp = [st.sb(f"qp{i}", [P, S], BF16) for i in range(3)]
        kp = [st.sb(f"kp{i}", [P, S], BF16) for i in range(3)]
        with Stage(nc, "l0q") as st_q:
            q = st_q.sb("q", [P, S])
            stage_project_parts(nc, d, g, "l0proj", "l0_wqkv", V_aug, q, qp, kp, Q, K)
        stage_l0_attend(nc, d, g, V_aug, qp, kp, Q, K, O)
        stage_project_out(nc, d, g, "l0out", O, "l0_wout", mod_row(g, 0, GATE_A))



SLOTS, TOPK, HID = 64, 8, 64


def stage_l0_route(nc, d, g, alpha, alphaT, w):
    with Stage(nc, "l0route") as st:
        hidT = st.sb("hidT", [HID + 1, S])
        b1 = st.sb("b1", [HID, 1])
        bias1 = st.sb("bias1", [HID, 1])
        w1T = st.sb("w1T", [P, 2, HID])
        w2T = st.sb("w2T", [HID + 1, SLOTS])
        tau = st.sb("tau", [P, 1])
        itau = st.sb("itau", [P, 1])
        mean_w = st.sb("mean_w", [SLOTS, 1])
        mean_slot = st.sb("mean_slot", [P, 1])
        logits = st.sb("logits", [P, NT, SLOTS])
        left = st.sb("left", [P, NT, SLOTS])
        top = st.sb("top", [P, NT, TOPK])
        negtop = st.sb("negtop", [P, NT])
        total = st.sb("total", [P, NT])
        ps_h = st.ps("ps_h", [HID, 4, BANK])
        ps_l = st.ps("ps_l", [P, 2, BANK])
        ps_m = st.ps("ps_m", [P, BANK])
        loaded = st.sem("loaded")
        slots_ready = st.sem("slots_ready")
        mean_done = st.sem("mean_done")
        mean_copied = st.sem("mean_copied")
        bias_done = st.sem("bias_done")
        bias_ready = st.sem("bias_ready")
        hid_done = st.sem("hid_done")
        hid_ready = st.sem("hid_ready")
        logits_done = st.sem("logits_done")
        left_ready = st.sem("left_ready")
        exp_done = st.sem("exp_done")
        alpha_ready = st.sem("alpha_ready")
        ones_row = st.sem("ones_row")
        turned = st.sem("turned")
        chain = st.sem("chain")
        with st.block() as block:

            @block.sync
            def _(sp):
                for dst, name in ((b1, "l0_b1"), (w1T, "l0_w1T"), (w2T, "l0_w2T"), (tau, "l0_tau"),
                                  (w.slots, "l0_slots"), (w.slot_scale, "l0_slot_scale")):
                    sp.dma_start(dst[:], d[name]).then_inc(loaded, 16)

            @block.tensor
            def _(pe):
                pe.wait_ge(slots_ready, 1)
                pe.matmul(ps_m[:, 0:1], w.slots[:], mean_w[:], start=True, stop=True).then_inc(mean_done, 1)
                for j in range(NC4):
                    pe.matmul(ps_h[:, j, :], w1T[:, 0, :], g.hT[:, c4(j)], start=True, stop=True).then_inc(hid_done, 1)
                pe.wait_ge(mean_copied, 1)
                pe.matmul(ps_m[0:HID, 1:2], w1T[:, 1, :], mean_slot[:], start=True, stop=True).then_inc(bias_done, 1)
                for t in range(NT):
                    if t % 4 == 0:
                        pe.wait_ge(hid_ready, t // 4 + 1)
                    mm = pe.matmul(ps_l[:, t // 8, (t % 8) * SLOTS:(t % 8 + 1) * SLOTS], hidT[:, c1(t)], w2T[:],
                                   start=True, stop=True)
                    if t % 8 == 7:
                        mm.then_inc(logits_done, 1)
                pe.wait_ge(alpha_ready, 1)
                for t in range(NT):
                    mm = pe.transpose(ps_h[:, t // 4, c1(t % 4)], alpha[:, t, :], g.ident[:])
                    if t % 4 == 3:
                        mm.then_inc(turned, 1)

            @block.scalar
            def _(act):
                act.wait_ge(bias_ready, 1)
                for j in range(NC4):
                    act.wait_ge(hid_done, j + 1)
                    act.activation(hidT[0:HID, c4(j)], ps_h[:, j, :], ACT.Gelu, bias=bias1[:]).then_inc(hid_ready, 1)
                for t in range(NT):
                    if t == 0:
                        act.wait_ge(left_ready, 1)
                    act.activation(alpha[:, t, :], logits[:, t, :], ACT.Exp, bias=negtop[:, t:t + 1])\
                       .then_inc(exp_done, 1)
                for j in range(NC4):
                    act.wait_ge(turned, j + 1)
                    act.activation(alphaT[0:SLOTS, c4(j)], ps_h[:, j, :], ACT.Identity)

            @block.gpsimd
            def _(pool):
                pool.memset(alphaT[SLOTS:SLOTS + 1, :], 1.0).then_inc(ones_row, 1)
                pool.wait_ge(ones_row, 1)

            @block.vector
            def _(dve):
                link = Chain(dve, chain)
                link.mark(dve.memset(mean_w[:], 1.0 / SLOTS))
                link(dve.memset(hidT[HID:HID + 1, :], 1.0))
                dve.wait_ge(loaded, 16 * 6)
                dve.tensor_scalar(w.slots[:], w.slots[:], w.slot_scale[:], None, ALU.mult).then_inc(slots_ready, 1)
                link(dve.tensor_scalar(itau[:], tau[:], -1.0, None, ALU.mult))
                link(dve.tensor_tensor(itau[:], itau[:], tau[:], ALU.max))
                link(dve.tensor_scalar(itau[:], itau[:], 0.1, None, ALU.add))
                link(dve.reciprocal(itau[:], itau[:]))
                dve.wait_ge(mean_done, 1)
                dve.tensor_copy(mean_slot[:], ps_m[:, 0:1]).then_inc(mean_copied, 1)
                dve.wait_ge(bias_done, 1)
                dve.tensor_tensor(bias1[:], ps_m[0:HID, 1:2], b1[:], ALU.add).then_inc(bias_ready, 1)
                for b in range(2):
                    dve.wait_ge(logits_done, b + 1)
                    link.mark(dve.tensor_scalar(logits[:, 8 * b:8 * b + 8, :].rearrange("p t s -> p (t s)"),
                                                ps_l[:, b, :], itau[:], None, ALU.mult))
                link.wait()
                for t in range(NT):
                    link.mark(dve.max(top[:, t, :], logits[:, t, :]))
                link.wait()
                for t in range(NT):
                    link.mark(dve.match_replace(left[:, t, :], top[:, t, :], logits[:, t, :], -3e38))
                dve.tensor_scalar(negtop[:], top[:, :, 0], -1.0, None, ALU.mult).then_inc(left_ready, 1)
                link.wait()
                link(dve.tensor_tensor(left[:], left[:], logits[:], ALU.is_lt))
                dve.wait_ge(exp_done, NT)
                link(dve.tensor_tensor(alpha[:], alpha[:], left[:], ALU.mult))
                link(dve.tensor_reduce(total[:], alpha[:], AX_X, ALU.add))
                link(dve.reciprocal(total[:], total[:]))
                dve.tensor_tensor(alpha[:], alpha[:], bcast(total[:].unsqueeze(2), P, NT, SLOTS), ALU.mult)\
                   .then_inc(alpha_ready, 1)


def stage_l0_slots(nc, d, g, alpha, alphaT, w):
    with Stage(nc, "l0slots") as st:
        wih = st.sb("wih", [P, 3, P])
        whh = st.sb("whh", [P, 3, P])
        b_ih = st.sb("b_ih", [1, 3 * P])
        b_hh = st.sb("b_hh", [1, 3 * P])
        wv = st.sb("wv", [P, P])
        bv = st.sb("bv", [P, 1])
        wo = st.sb("wo", [P, P])
        out_w = st.sb("out_w", [SLOTS + 1, P])
        ones = st.sb("ones", [P, SLOTS])
        raw = st.sb("raw", [SLOTS, P + 1])
        gi = st.sb("gi", [SLOTS, P])
        shift = st.sb("shift", [SLOTS, P])
        wsum = st.sb("wsum", [SLOTS, 1])
        giT = st.sb("giT", [P, SLOTS])
        slotsT = st.sb("slotsT", [P, SLOTS])
        rz = st.sb("rz", [SLOTS, 2 * P])
        hn = st.sb("hn", [SLOTS, P])
        n = st.sb("n", [SLOTS, P])
        newT = st.sb("newT", [P, SLOTS])
        svT = st.sb("svT", [P, SLOTS])
        ps_i = st.ps("ps_i", [SLOTS, BANK])
        ps_g = st.ps("ps_g", [SLOTS, BANK])
        ps_t = st.ps("ps_t", [P, BANK])
        ps_o = st.ps("ps_o", [P, 4, BANK])
        loaded = st.sem("loaded")
        ones_ready = st.sem("ones_ready")
        raw_done = st.sem("raw_done")
        gi_ready = st.sem("gi_ready")
        turned = st.sem("turned")
        turns_copied = st.sem("turns_copied")
        gates_done = st.sem("gates_done")
        rz_ready = st.sem("rz_ready")
        n_in = st.sem("n_in")
        n_ready = st.sem("n_ready")
        new_ready = st.sem("new_ready")
        sv_done = st.sem("sv_done")
        sv_ready = st.sem("sv_ready")
        ow_done = st.sem("ow_done")
        ow_ready = st.sem("ow_ready")
        out_done = st.sem("out_done")
        chain = st.sem("chain")
        with st.block() as block:

            @block.sync
            def _(sp):
                for dst, name in ((wih[:], "l0_wihT"), (whh[:], "l0_whhT"), (b_ih[:], "l0_bih"), (b_hh[:], "l0_bhh"),
                                  (wv[:], "l0_wvT"), (bv[:], "l0_bv"), (wo[:], "l0_woT"),
                                  (out_w[SLOTS:SLOTS + 1, :], "l0_bo")):
                    sp.dma_start(dst, d[name]).then_inc(loaded, 16)

            @block.tensor
            def _(pe):
                pe.wait_ge(ones_ready, 1)
                for t in range(NT):
                    pe.matmul(ps_i[:, 0:P], alpha[:, t, :], g.xn[:, t, :], start=(t == 0), stop=(t == NT - 1))
                for t in range(NT):
                    mm = pe.matmul(ps_i[:, P:P + 1], alpha[:, t, :], ones[:, 0:1], start=(t == 0), stop=(t == NT - 1),
                                   skip_group_check=True)
                mm.then_inc(raw_done, 1)
                pe.transpose(ps_t[:, 0:SLOTS], w.slots[:], g.ident[0:SLOTS, 0:SLOTS])
                pe.wait_ge(gi_ready, 1)
                pe.transpose(ps_t[:, SLOTS:2 * SLOTS], gi[:], g.ident[0:SLOTS, 0:SLOTS]).then_inc(turned, 1)
                pe.wait_ge(turns_copied, 1)
                pe.wait_ge(loaded, 16 * 8)
                one = ones[0:1, :]
                pe.matmul(ps_g[:, 0:256], giT[:], wih[:, 0:2, :].rearrange("p a b -> p (a b)"), start=True, stop=False)
                pe.matmul(ps_g[:, 0:256], one, b_ih[:, 0:256], start=False, stop=False)
                pe.matmul(ps_g[:, 0:256], slotsT[:], whh[:, 0:2, :].rearrange("p a b -> p (a b)"), start=False,
                          stop=False)
                pe.matmul(ps_g[:, 0:256], one, b_hh[:, 0:256], start=False, stop=True)
                pe.matmul(ps_g[:, 256:384], giT[:], wih[:, 2, :], start=True, stop=False, skip_group_check=True)
                pe.matmul(ps_g[:, 256:384], one, b_ih[:, 256:384], start=False, stop=True, skip_group_check=True)
                pe.matmul(ps_g[:, 384:512], slotsT[:], whh[:, 2, :], start=True, stop=False, skip_group_check=True)
                pe.matmul(ps_g[:, 384:512], one, b_hh[:, 256:384], start=False, stop=True,
                          skip_group_check=True).then_inc(gates_done, 1)
                pe.wait_ge(new_ready, 1)
                pe.transpose(ps_t[:, 0:SLOTS], n[:], g.ident[0:SLOTS, 0:SLOTS]).then_inc(turned, 1)
                pe.wait_ge(turns_copied, 2)
                pe.matmul(ps_t[:, SLOTS:2 * SLOTS], wv[:], newT[:], start=True, stop=True).then_inc(sv_done, 1)
                pe.wait_ge(sv_ready, 1)
                pe.matmul(ps_i[:, 0:P], svT[:], wo[:], start=True, stop=True).then_inc(ow_done, 1)
                pe.wait_ge(ow_ready, 2)
                for t in range(NT):
                    mm = pe.matmul(ps_o[:, t // 4, c1(t % 4)], alphaT[:, c1(t)], out_w[:], start=True, stop=True)
                    if t % 4 == 3:
                        mm.then_inc(out_done, 1)

            @block.scalar
            def _(act):
                act.wait_ge(gates_done, 1)
                act.activation(rz[:], ps_g[:, 0:256], ACT.Sigmoid).then_inc(rz_ready, 1)
                act.wait_ge(n_in, 1)
                act.activation(n[:], hn[:], ACT.Tanh).then_inc(n_ready, 1)

            @block.vector
            def _(dve):
                link = Chain(dve, chain)
                dve.memset(ones[:], 1.0).then_inc(ones_ready, 1)
                dve.wait_ge(raw_done, 1)
                link(dve.tensor_copy(raw[:], ps_i[:, 0:P + 1]))
                link.mark(dve.tensor_scalar(wsum[:], raw[:, P:P + 1], 1e-8, None, ALU.add))
                link.mark(dve.tensor_tensor(gi[:], raw[:, 0:P], mod_row(g, 0, SCALE_B)[0:SLOTS], ALU.mult))
                link(dve.tensor_scalar(shift[:], mod_row(g, 0, SHIFT_B)[0:SLOTS], raw[:, P:P + 1], None, ALU.mult))
                link.mark(dve.reciprocal(wsum[:], wsum[:]))
                link(dve.tensor_tensor(gi[:], gi[:], shift[:], ALU.add))
                dve.tensor_scalar(gi[:], gi[:], wsum[:], None, ALU.mult).then_inc(gi_ready, 1)
                dve.wait_ge(turned, 1)
                link(dve.tensor_copy(slotsT[:], ps_t[:, 0:SLOTS]))
                dve.tensor_copy(giT[:], ps_t[:, SLOTS:2 * SLOTS]).then_inc(turns_copied, 1)
                dve.wait_ge(rz_ready, 1)
                link(dve.tensor_tensor(hn[:], rz[:, 0:P], ps_g[:, 384:512], ALU.mult))
                dve.tensor_tensor(hn[:], hn[:], ps_g[:, 256:384], ALU.add).then_inc(n_in, 1)
                dve.wait_ge(n_ready, 1)
                link(dve.tensor_tensor(hn[:], w.slots[:], n[:], ALU.subtract))
                link(dve.tensor_tensor(hn[:], hn[:], rz[:, P:2 * P], ALU.mult))
                dve.tensor_tensor(n[:], n[:], hn[:], ALU.add).then_inc(new_ready, 1)
                dve.wait_ge(turned, 2)
                dve.tensor_copy(newT[:], ps_t[:, 0:SLOTS]).then_inc(turns_copied, 1)
                dve.wait_ge(sv_done, 1)
                dve.tensor_scalar(svT[:], ps_t[:, SLOTS:2 * SLOTS], bv[:], None, ALU.add).then_inc(sv_ready, 1)
                dve.wait_ge(ow_done, 1)
                dve.tensor_tensor(out_w[0:SLOTS, :], ps_i[:, 0:P], mod_row(g, 0, GATE_B)[0:SLOTS], ALU.mult)\
                   .then_inc(ow_ready, 1)
                dve.tensor_tensor(out_w[SLOTS:SLOTS + 1, :], out_w[SLOTS:SLOTS + 1, :],
                                  mod_row(g, 0, GATE_B)[SLOTS:SLOTS + 1], ALU.mult).then_inc(ow_ready, 1)
                for j in range(NC4):
                    dve.wait_ge(out_done, j + 1)
                    xs = g.x[:, 4 * j:4 * j + 4, :]
                    dve.tensor_tensor(xs, ps_o[:, j, :].rearrange("p (t f) -> p t f", t=4), xs, ALU.add)


def layer0_slots(nc, d, g):
    adaln(nc, g, 0, SCALE_B, SHIFT_B)
    with Stage(nc, "l0ffn") as st:
        w = Persistent()
        w.slots = st.sb("slots", [SLOTS, P])
        w.slot_scale = st.sb("slot_scale", [SLOTS, 1])
        alpha = st.sb("alpha", [P, NT, SLOTS])
        alphaT = st.sb("alphaT", [SLOTS + 1, S])
        stage_l0_route(nc, d, g, alpha, alphaT, w)
        stage_l0_slots(nc, d, g, alpha, alphaT, w)



LEVELS = (2, 4, 8, 16, 32, 64)


def stage_l1_project(nc, d, g, w):
    with Stage(nc, "l1proj") as st:
        wq = st.sb("wq", [P, P])
        wkvb = st.sb("wkvb", [P, 2 * P + 1])
        raw = st.sb("raw", [P, NT, 2 * P + 1])
        sq = st.sb("sq", [P, NT, P])
        ss = st.sb("ss", [P, NT])
        norm = st.sb("norm", [P, NT])
        quot = st.sb("quot", [P, NT])
        ps_q = st.ps("ps_q", [P, 4, BANK])
        ps_k = st.ps("ps_k", [P, 4, BANK])
        loaded = st.sem("loaded")
        q_done = st.sem("q_done")
        kvb_done = st.sem("kvb_done")
        kvb_copied = st.sem("kvb_copied")
        sums_ready = st.sem("sums_ready")
        roots_done = st.sem("roots_done")
        sig_done = st.sem("sig_done")
        q_copied = st.sem("q_copied")
        k_ready = st.sem("k_ready")
        turned = st.sem("turned")
        chain = st.sem("chain")
        with st.block() as block:

            @block.sync
            def _(sp):
                sp.dma_start(wq[:], d["l1_wq"]).then_inc(loaded, 16)
                sp.dma_start(wkvb[:], d["l1_wkvb"]).then_inc(loaded, 16)

            @block.tensor
            def _(pe):
                pe.wait_ge(loaded, 32)
                for t in range(NT):
                    if t >= 4:
                        pe.wait_ge(kvb_copied, t - 3)
                    pe.matmul(ps_k[:, t % 4, 0:2 * P + 1], g.hT[:, c1(t)], wkvb[:], start=True, stop=True)\
                      .then_inc(kvb_done, 1)
                for j in range(NC4):
                    pe.matmul(ps_q[:, j, :], wq[:], g.hT[:, c4(j)], start=True, stop=True).then_inc(q_done, 1)
                pe.wait_ge(k_ready, 1)
                for t in range(NT):
                    if t % 4 == 0:
                        pe.wait_ge(q_copied, t // 4 + 1)
                    mm = pe.transpose(ps_q[:, t // 4, c1(t % 4)], w.k[:, t, :], g.ident[:])
                    if t % 4 == 3:
                        mm.then_inc(turned, 1)

            @block.scalar
            def _(act):
                for j in range(NC4):
                    act.wait_ge(q_done, j + 1)
                    act.activation(w.qT[:, c4(j)], ps_q[:, j, :], ACT.Identity, scale=P ** -0.5).then_inc(q_copied, 1)
                act.wait_ge(kvb_copied, NT)
                act.activation(w.bv[:], raw[:, :, P:2 * P], ACT.Sigmoid)
                act.activation(w.beta[:], raw[:, :, 2 * P], ACT.Sigmoid).then_inc(sig_done, 1)
                act.wait_ge(sums_ready, 1)
                act.activation(norm[:], ss[:], ACT.Sqrt).then_inc(roots_done, 1)
                for j in range(NC4):
                    act.wait_ge(turned, j + 1)
                    act.activation(w.kT[:, c4(j)], ps_q[:, j, :], ACT.Identity)

            @block.vector
            def _(dve):
                link = Chain(dve, chain)
                for t in range(NT):
                    dve.wait_ge(kvb_done, t + 1)
                    dve.tensor_copy(raw[:, t, :], ps_k[:, t % 4, 0:2 * P + 1]).then_inc(kvb_copied, 1)
                dve.wait_ge(kvb_copied, NT)
                k_raw, v_raw = raw[:, :, 0:P], raw[:, :, P:2 * P]
                link(dve.tensor_tensor(sq[:], k_raw, k_raw, ALU.mult))
                link(dve.tensor_reduce(ss[:], sq[:], AX_X, ALU.add))
                dve.tensor_scalar(ss[:], ss[:], 1e-30, None, ALU.max).then_inc(sums_ready, 1)
                dve.wait_ge(sig_done, 1)
                link(dve.tensor_tensor(w.bv[:], w.bv[:], v_raw, ALU.mult))
                link(dve.tensor_tensor(w.bv[:], w.bv[:], bcast(w.beta[:].unsqueeze(2), P, NT, P), ALU.mult))
                dve.wait_ge(roots_done, 1)
                link(dve.reciprocal(quot[:], norm[:]))
                link(dve.tensor_tensor(quot[:], quot[:], ss[:], ALU.mult))
                link(dve.tensor_tensor(norm[:], norm[:], quot[:], ALU.add))
                link(dve.tensor_scalar(norm[:], norm[:], 0.5, 1e-12, ALU.mult, ALU.max))
                link(dve.reciprocal(norm[:], norm[:]))
                dve.tensor_tensor(w.k[:], k_raw, bcast(norm[:].unsqueeze(2), P, NT, P), ALU.mult).then_inc(k_ready, 1)
                dve.wait_ge(k_ready, 1)
                dve.tensor_tensor(w.bk[:], w.k[:], bcast(w.beta[:].unsqueeze(2), P, NT, P), ALU.mult)


def stage_l1_chunks(nc, d, g, w):
    with Stage(nc, "l1chunk") as st:
        masks = st.sb("masks", [P, len(LEVELS) + 2, P])
        A = st.sb("A", [P, NT, P])
        C = st.sb("C", [P, 2, NT, P])
        T = st.sb("T", [P, NT, P])
        X = st.sb("X", [P, NT, P])
        Y = st.sb("Y", [P, 2, BANK])
        ps_y = st.ps("ps_y", [P, 2, BANK])
        ps_t = st.ps("ps_t", [P, 2, BANK])
        ps_x = st.ps("ps_x", [P, 2, BANK])
        loaded = st.sem("loaded")
        g_done = st.sem("g_done")
        a_ready = st.sem("a_ready")
        c_ready = st.sem("c_ready")
        t_init = st.sem("t_init")
        x_turned = st.sem("x_turned")
        x_copied = st.sem("x_copied")
        y_done = st.sem("y_done")
        y_copied = st.sem("y_copied")
        tx_done = st.sem("tx_done")
        tx_ready = st.sem("tx_ready")
        m_done = st.sem("m_done")
        m_copied = st.sem("m_copied")
        u_copied = st.sem("u_copied")
        wt_copied = st.sem("wt_copied")
        wt_done = st.sem("wt_done")
        chain = st.sem("chain")
        tiles = lambda buf, j: buf[:, 4 * j:4 * j + 4, :].rearrange("p t f -> p (t f)")

        def mask(i, n):
            return bcast(masks[:, i:i + 1, :], P, n, P)

        with st.block() as block:

            @block.sync
            def _(sp):
                sp.dma_start(masks[:], d["masks"]).then_inc(loaded, 16)

            @block.tensor
            def _(pe):
                for j in range(NC4):
                    for t in range(4):
                        c = c1(4 * j + t)
                        mm = pe.matmul((ps_y if j < 2 else ps_t)[:, j % 2, c1(t)], w.kT[:, c], w.kT[:, c], start=True,
                                       stop=True)
                    mm.then_inc(g_done, 1)
                for j in range(NC4):
                    if j >= 2:
                        pe.wait_ge(m_copied, j - 1)
                    for t in range(4):
                        c = c1(4 * j + t)
                        mm = pe.matmul(ps_x[:, j % 2, c1(t)], w.kT[:, c], w.qT[:, c], start=True, stop=True)
                    mm.then_inc(m_done, 1)
                for j in range(NC4):
                    pe.wait_ge(t_init, j + 1)
                    pe.wait_ge(a_ready, min(j + 3, NC4))
                    if j >= 2:
                        pe.wait_ge(x_copied, j - 1)
                    for t in range(4):
                        mm = pe.transpose(ps_y[:, j % 2, c1(t)], T[:, 4 * j + t, :], g.ident[:])
                    mm.then_inc(x_turned, 1)
                for l in range(len(LEVELS)):
                    last = l == len(LEVELS) - 1

                    def join(j):
                        n = NC4 * l + j
                        pe.wait_ge(y_copied, n + 1)
                        if n >= 2:
                            pe.wait_ge(tx_ready, n - 1)
                        for t in range(4):
                            y = Y[:, n % 2, c1(t)]
                            if not last:
                                pe.matmul(ps_t[:, n % 2, c1(t)], y, T[:, 4 * j + t, :], start=True, stop=True)
                            mm = pe.matmul(ps_x[:, n % 2, c1(t)], T[:, 4 * j + t, :], y, start=True, stop=True)
                        mm.then_inc(tx_done, 1)

                    for j in range(NC4):
                        n = NC4 * l + j
                        if j == 0:
                            pe.wait_ge(c_ready, l + 2)
                        if l == 0:
                            pe.wait_ge(x_copied, NC4 if j == 0 else j + 1)
                            pe.wait_ge(m_copied, NC4)
                        else:
                            pe.wait_ge(tx_ready, n - NC4 + 1)
                        if n >= 2:
                            pe.wait_ge(y_copied, n - 1)
                        for t in range(4):
                            mm = pe.matmul(ps_y[:, n % 2, c1(t)], C[:, (l + 1) % 2, 4 * j + t, :], X[:, 4 * j + t, :],
                                           start=True, stop=True)
                        mm.then_inc(y_done, 1)
                        if j >= 1:
                            join(j - 1)
                    join(NC4 - 1)
                total = NC4 * len(LEVELS)
                for j in range(NC4):
                    pe.wait_ge(tx_ready, total - NC4 + j + 1)
                    if j == 0:
                        pe.wait_ge(y_copied, total)
                        pe.wait_ge(tx_ready, total)
                    if j >= 2:
                        pe.wait_ge(u_copied, j - 1)
                        pe.wait_ge(wt_copied, j - 1)
                    for t in range(4):
                        i = 4 * j + t
                        pe.matmul(ps_t[:, j % 2, c1(t)], X[:, i, :], w.bv[:, i, :], start=True, stop=True)
                        mm = pe.matmul(ps_x[:, j % 2, c1(t)], w.bk[:, i, :], X[:, i, :], start=True, stop=True)
                    mm.then_inc(wt_done, 1)

            @block.gpsimd
            def _(pool):
                pool.wait_ge(loaded, 16)
                for l in range(len(LEVELS) + 1):
                    if l == 0:
                        pool.wait_ge(a_ready, NC4)
                    if l == 2:
                        pool.wait_ge(t_init, NC4)
                    if l >= 3:
                        pool.wait_ge(y_done, NC4 * (l - 2))
                    pool.tensor_tensor(C[:, l % 2, :, :], A[:], mask(l, NT), ALU.mult).then_inc(c_ready, 1)

            @block.scalar
            def _(act):
                for j in range(NC4):
                    act.wait_ge(x_turned, j + 1)
                    act.activation(tiles(X, j), ps_y[:, j % 2, :], ACT.Identity).then_inc(x_copied, 1)
                for n in range(NC4 * len(LEVELS)):
                    act.wait_ge(y_done, n + 1)
                    if n >= 2:
                        act.wait_ge(tx_done, n - 1)
                    act.activation(Y[:, n % 2, :], ps_y[:, n % 2, :], ACT.Identity).then_inc(y_copied, 1)
                for j in range(NC4):
                    act.wait_ge(wt_done, j + 1)
                    act.activation(w.WT[:, c4(j)], ps_x[:, j % 2, :], ACT.Identity).then_inc(wt_copied, 1)

            @block.vector
            def _(dve):
                link = Chain(dve, chain)
                for j in range(NC4):
                    dve.wait_ge(g_done, j + 1)
                    src = (ps_y if j < 2 else ps_t)[:, j % 2, :].rearrange("p (t f) -> p t f", t=4)
                    dve.tensor_tensor(A[:, 4 * j:4 * j + 4, :], src, bcast(
                        w.beta[:, 4 * j:4 * j + 4].unsqueeze(2), P, 4, P), ALU.mult).then_inc(a_ready, 1)
                dve.wait_ge(loaded, 16)
                for j in range(NC4):
                    dve.wait_ge(m_done, j + 1)
                    dve.tensor_tensor(w.MT[:, 4 * j:4 * j + 4, :], ps_x[:, j % 2, :].rearrange(
                        "p (t f) -> p t f", t=4), mask(len(LEVELS) + 1, 4), ALU.mult).then_inc(m_copied, 1)
                dve.wait_ge(c_ready, 1)
                for j in range(NC4):
                    dve.tensor_tensor(T[:, 4 * j:4 * j + 4, :], bcast(g.ident[:].unsqueeze(1), P, 4, P),
                                      C[:, 0, 4 * j:4 * j + 4, :], ALU.subtract).then_inc(t_init, 1)
                for n in range(NC4 * len(LEVELS)):
                    j, last = n % NC4, n >= NC4 * (len(LEVELS) - 1)
                    dve.wait_ge(tx_done, n + 1)
                    if not last:
                        dve.tensor_tensor(tiles(T, j), tiles(T, j), ps_t[:, n % 2, :], ALU.subtract)
                    dve.tensor_tensor(tiles(X, j), tiles(X, j), ps_x[:, n % 2, :], ALU.subtract)\
                       .then_inc(tx_ready, 1)
                for j in range(NC4):
                    dve.wait_ge(wt_done, j + 1)
                    dve.tensor_copy(tiles(w.U, j), ps_t[:, j % 2, :]).then_inc(u_copied, 1)


def stage_l1_states(nc, d, g, w, O):
    with Stage(nc, "l1state") as st:
        state = st.sb("state", [P, 2, P])
        V = st.sb("V", [P, 2, P])
        ps_v = st.ps("ps_v", [P, 2, BANK])
        ps_s = st.ps("ps_s", [P, BANK])
        ps_o = st.ps("ps_o", [P, 2, BANK])
        ws_done = st.sem("ws_done")
        v_ready = st.sem("v_ready")
        s_done = st.sem("s_done")
        s_ready = st.sem("s_ready")
        o_done = st.sem("o_done")
        o_copied = st.sem("o_copied")
        with st.block() as block:

            @block.tensor
            def _(pe):
                for c in range(NT):
                    if c >= 1:
                        pe.wait_ge(s_ready, c)
                        pe.matmul(ps_v[:, c % 2, 0:P], w.WT[:, c1(c)], state[:, c % 2, :], start=True,
                                  stop=True).then_inc(ws_done, 1)
                    if c >= 2:
                        pe.wait_ge(o_copied, c - 1)
                    if c >= 1:
                        pe.matmul(ps_o[:, c % 2, 0:P], w.qT[:, c1(c)], state[:, c % 2, :], start=True, stop=False)
                    pe.wait_ge(v_ready, c + 1)
                    if c < NT - 1:
                        pe.matmul(ps_s[:, 0:P], w.k[:, c, :], V[:, c % 2, :], start=(c == 0), stop=True,
                                  skip_group_check=True).then_inc(s_done, 1)
                    pe.matmul(ps_o[:, c % 2, 0:P], w.MT[:, c, :], V[:, c % 2, :], start=(c == 0),
                              stop=True).then_inc(o_done, 1)

            @block.scalar
            def _(act):
                for c in range(NT):
                    act.wait_ge(o_done, c + 1)
                    act.activation(O[:, c, :], ps_o[:, c % 2, 0:P], ACT.Identity).then_inc(o_copied, 1)

            @block.vector
            def _(dve):
                for c in range(NT):
                    if c >= 2:
                        dve.wait_ge(o_done, c - 1)
                    if c == 0:
                        dve.tensor_copy(V[:, 0, :], w.U[:, 0, :]).then_inc(v_ready, 1)
                    else:
                        dve.wait_ge(ws_done, c)
                        dve.tensor_tensor(V[:, c % 2, :], w.U[:, c, :], ps_v[:, c % 2, 0:P],
                                          ALU.subtract).then_inc(v_ready, 1)
                    if c < NT - 1:
                        dve.wait_ge(s_done, c + 1)
                        dve.tensor_copy(state[:, (c + 1) % 2, :], ps_s[:, 0:P]).then_inc(s_ready, 1)


def stage_add_affine(nc, d, g, name, normed, g_name, b_name, gate_row):
    with Stage(nc, name) as st:
        gain = st.sb("gain", [P, P])
        shift = st.sb("shift", [P, P])
        tmp = st.sb("tmp", [P, NT, P])
        loaded = st.sem("loaded")
        rows_ready = st.sem("rows_ready")
        shifted = st.sem("shifted")
        chain = st.sem("chain")
        with st.block() as block:

            @block.sync
            def _(sp):
                sp.dma_start(gain[:], d[g_name]).then_inc(loaded, 16)
                sp.dma_start(shift[:], d[b_name]).then_inc(loaded, 16)

            @block.gpsimd
            def _(pool):
                pool.wait_ge(rows_ready, 1)
                pool.tensor_tensor(g.x[:], g.x[:], bcast(shift[:].unsqueeze(1), P, NT, P), ALU.add)\
                    .then_inc(shifted, 1)
                pool.wait_ge(shifted, 1)

            @block.vector
            def _(dve):
                link = Chain(dve, chain)
                dve.wait_ge(loaded, 32)
                link.mark(dve.tensor_tensor(gain[:], gain[:], gate_row, ALU.mult))
                dve.tensor_tensor(shift[:], shift[:], gate_row, ALU.mult).then_inc(rows_ready, 1)
                link.wait()
                link(dve.tensor_tensor(tmp[:], normed[:], bcast(gain[:].unsqueeze(1), P, NT, P), ALU.mult))
                dve.wait_ge(shifted, 1)
                dve.tensor_tensor(g.x[:], g.x[:], tmp[:], ALU.add)


def layer1_delta(nc, d, g):
    adaln(nc, g, 1, SCALE_A, SHIFT_A)
    with Stage(nc, "l1") as st:
        w = Persistent()
        O = st.sb("O", [P, NT, P])
        w.qT = st.sb("qT", [P, S])
        w.kT = st.sb("kT", [P, S])
        w.k, w.bk, w.bv, w.MT, w.U = (st.sb(n, [P, NT, P]) for n in ("k", "bk", "bv", "MT", "U"))
        w.WT = st.sb("WT", [P, S])
        w.beta = st.sb("beta", [P, NT])
        stage_l1_project(nc, d, g, w)
        stage_l1_chunks(nc, d, g, w)
        stage_l1_states(nc, d, g, w, O)
        stage_norm(nc, g, "l1norm", O, g.xn)
        stage_add_affine(nc, d, g, "l1add", g.xn, "l1_lng", "l1_lnb", mod_row(g, 1, GATE_A))



EXPERTS = 64
GANG = 64
GANGS = S // GANG + EXPERTS
GANG_LOAD = 8


def stage_l1_route(nc, d, g, W, zeros, sorted_in, zeroed, weights_loaded, slot, expert_int, gang_expert):
    with Stage(nc, "l1route") as st:
        gw = st.sb("gw", [P, EXPERTS])
        gb = st.sb("gb", [1, EXPERTS])
        ones1 = st.sb("ones1", [1, P])
        ones = st.sb("ones", [P, P], BF16)
        ones_row = st.sb("ones_row", [P, EXPERTS])
        not_yet = st.sb("not_yet", [P, P], BF16)
        iota_row = st.sb("iota_row", [P, EXPERTS])
        iota = st.sb("iota", [P, 1])
        carry = st.sb("carry", [P, EXPERTS, NT])
        logits = st.sb("logits", [P, NT, EXPERTS])
        top = st.sb("top", [P, NT, 8])
        idx = st.sb("idx", [P, NT, 8], U32)
        expert = st.sb("expert", [P, NT])
        member = st.sb("member", [P, EXPERTS, NT], BF16)
        place = st.sb("place", [P, EXPERTS, NT])
        gangs = st.sb("gangs", [P, EXPERTS])
        gangs_int = st.sb("gangs_int", [P, EXPERTS], I32)
        gangs_upto = st.sb("gangs_upto", [P, EXPERTS])
        first = st.sb("first", [P, EXPERTS])
        ended = st.sb("ended", [P, EXPERTS])
        gang_col = st.sb("gang_col", [P, 1])
        slot_f = st.sb("slot_f", [P, NT])
        ps_l = st.ps("ps_l", [P, 2, BANK])
        ps_n = st.ps("ps_n", [P, 4, BANK])
        ps_g = st.ps("ps_g", [P, BANK])
        loaded = st.sem("loaded")
        ones_ready = st.sem("ones_ready")
        logits_done = st.sem("logits_done")
        member_ready = st.sem("member_ready")
        counted = st.sem("counted")
        gang_ready = st.sem("gang_ready")
        gang_turned = st.sem("gang_turned")
        chain = st.sem("chain")
        with st.block() as block:

            @block.sync
            def _(sp):
                for dst, name in ((gw, "l1_gateT"), (gb, "l1_gate_b"), (iota, "iota"), (iota_row, "iota_row"),
                                  (not_yet, "not_yet"), (carry, "carry")):
                    sp.dma_start(dst[:], d[name]).then_inc(loaded, 16)
                sp.wait_ge(zeroed, 1)
                sp.dma_start(sorted_in.rearrange("(p i) f -> p i f", p=P),
                             bcast(zeros[:].unsqueeze(1), P, GANGS * GANG // P, P)).then_inc(zeroed, 16)
                sp.dma_start(W[:], d["l1_expert_w"].rearrange("e d o -> d e o")).then_inc(weights_loaded, 16)

            @block.gpsimd
            def _(pool):
                pool.memset(zeros[:], 0.0).then_inc(zeroed, 1)

            @block.tensor
            def _(pe):
                pe.wait_ge(ones_ready, 1)
                pe.wait_ge(loaded, 16 * 6)
                for t in range(NT):
                    dst = ps_l[:, t // 8, (t % 8) * EXPERTS:(t % 8 + 1) * EXPERTS]
                    pe.matmul(dst, g.hT[:, c1(t)], gw[:], start=True, stop=False, skip_group_check=True)
                    mm = pe.matmul(dst, ones1[:], gb[:], start=False, stop=True, skip_group_check=True)
                    if t % 8 == 7:
                        mm.then_inc(logits_done, 1)
                pe.wait_ge(member_ready, 1)
                m = member[:].rearrange("p e t -> p (e t)")
                for i in range(2):
                    pe.matmul(ps_n[:, i, :], ones[:], m[:, c4(i)], start=True, stop=True)
                    mm = pe.matmul(ps_n[:, 2 + i, :], not_yet[:], m[:, c4(i)], start=True, stop=True)
                mm.then_inc(counted, 1)
                pe.wait_ge(gang_ready, 1)
                pe.transpose(ps_g[0:1, 0:P], gang_col[:], g.ident[:]).then_inc(gang_turned, 1)

            @block.vector
            def _(dve):
                link = Chain(dve, chain)
                link.mark(dve.memset(ones1[:], 1.0))
                link.mark(dve.memset(ones_row[:], 1.0))
                link(dve.memset(ones[:], 1.0))
                dve.memset(gang_col[:], 0.0).then_inc(ones_ready, 1)
                for b in range(2):
                    dve.wait_ge(logits_done, b + 1)
                    link.mark(dve.tensor_copy(logits[:, 8 * b:8 * b + 8, :].rearrange("p t s -> p (t s)"),
                                              ps_l[:, b, :]))
                link.wait()
                for t in range(NT):
                    link.mark(dve.max(top[:, t, :], logits[:, t, :]))
                link.wait()
                for t in range(NT):
                    link.mark(dve.max_index(idx[:, t, :], top[:, t, :], logits[:, t, :]))
                link.wait()
                link(dve.tensor_copy(expert[:], idx[:, :, 0]))
                link.mark(dve.tensor_copy(expert_int[:], expert[:]))
                dve.wait_ge(loaded, 16 * 6)
                dve.tensor_tensor(member[:], bcast(iota_row[:].unsqueeze(2), P, EXPERTS, NT),
                                  bcast(expert[:].unsqueeze(1), P, EXPERTS, NT), ALU.is_equal)\
                   .then_inc(member_ready, 1)
                dve.wait_ge(counted, 1)
                flat = place[:].rearrange("p e t -> p (e t)")
                link(dve.tensor_tensor_scan(flat, carry[:].rearrange("p e t -> p (e t)"),
                                            ps_n[:, 0:2, :].rearrange("p b n -> p (b n)"), 0.0, ALU.mult, ALU.add))
                link(dve.tensor_scalar(gangs_int[:], place[:, :, NT - 1], float(GANG - 1), None, ALU.add))
                link(dve.tensor_scalar(gangs_int[:], gangs_int[:], GANG.bit_length() - 1, None,
                                       ALU.logical_shift_right))
                link(dve.tensor_copy(gangs[:], gangs_int[:]))
                link(dve.tensor_tensor_scan(gangs_upto[:], ones_row[:], gangs[:], 0.0, ALU.mult, ALU.add))
                link.mark(dve.tensor_tensor(first[:], gangs_upto[:], gangs[:], ALU.subtract))
                link(dve.tensor_scalar(ended[:], gangs_upto[:], iota[:], None, ALU.is_le))
                link(dve.tensor_reduce(gang_col[:], ended[:], AX_X, ALU.add))
                dve.tensor_scalar(gang_col[:], gang_col[:], float(EXPERTS - 1), None, ALU.min)\
                   .then_inc(gang_ready, 1)
                link(dve.tensor_tensor(flat, flat, ps_n[:, 2:4, :].rearrange("p b n -> p (b n)"), ALU.add))
                link(dve.scalar_tensor_tensor(place[:], bcast(first[:].unsqueeze(2), P, EXPERTS, NT), float(GANG),
                                              place[:], ALU.mult, ALU.add))
                link(dve.tensor_tensor(place[:], place[:], member[:], ALU.mult))
                link(dve.tensor_reduce(slot_f[:], place[:].rearrange("p e t -> p t e"), AX_X, ALU.add))
                link.mark(dve.tensor_copy(slot[:], slot_f[:]))
                dve.wait_ge(gang_turned, 1)
                dve.tensor_copy(gang_expert[:], ps_g[0:1, 0:GANGS])


def stage_l1_experts(nc, d, g, W, sorted_in, sorted_out, zeroed, weights_loaded, slot, expert_int, gang_expert):
    LOADS = 4
    pairs = GANGS // 2
    with Stage(nc, "l1exp") as st:
        rows = st.sb("rows", [P, pairs, P])
        rowsT = st.sb("rowsT", [P, 2, BANK])
        y = st.sb("y", [GANG, GANGS, P])
        back = st.sb("back", [P, NT, P])
        bias = st.sb("bias", [P, NT, P])
        ps_t = st.ps("ps_t", [P, 2, BANK])
        ps_y = st.ps("ps_y", [P, 4, BANK])
        scattered = st.sem("scattered")
        rows_loaded = [st.sem(f"rows_loaded{i}") for i in range(LOADS)]
        turned = st.sem("turned")
        rows_ready = st.sem("rows_ready")
        y_done = st.sem("y_done")
        y_copied = [st.sem("y_copied0"), st.sem("y_copied1")]
        y_stored = st.sem("y_stored")
        bias_gathered = st.sem("bias_gathered")
        gathered = st.sem("gathered")
        chain = st.sem("chain")
        QUADS = GANGS // 4
        with st.block() as block:

            @block.sync
            def _(sp):
                sp.wait_ge(scattered, 16 * NT)
                n = pairs // LOADS
                for i in range(LOADS):
                    src = sorted_in[i * n * P:(i + 1) * n * P, :]
                    sp.dma_start(rows[:, i * n:(i + 1) * n, :], src.rearrange("(k p) f -> p k f", p=P))\
                      .then_inc(rows_loaded[i], 16)
                for i in range(LOADS):
                    for copied in y_copied:
                        sp.wait_ge(copied, QUADS // LOADS * (i + 1) // 2)
                    m = GANGS // LOADS
                    dst = sorted_out[i * m * GANG:(i + 1) * m * GANG, :]
                    sp.dma_start(dst.rearrange("(k p) f -> p k f", p=GANG), y[:, i * m:(i + 1) * m, :])\
                      .then_inc(y_stored, 16)

            @block.gpsimd
            def _(pool):
                pool.wait_ge(zeroed, 17)
                for t in range(NT):
                    pool.indirect_dma_start(out=sorted_in, out_offset=bass.IndirectOffsetOnAxis(
                        ap=slot[:, t:t + 1], axis=0), in_=g.xn[:, t, :], in_offset=None).then_inc(scattered, 16)
                for t in range(NT):
                    pool.indirect_dma_start(out=bias[:, t, :], out_offset=None, in_=d["l1_expert_b"],
                                            in_offset=bass.IndirectOffsetOnAxis(ap=expert_int[:, t:t + 1], axis=0))\
                        .then_inc(bias_gathered, 16)
                pool.wait_ge(y_stored, 16 * LOADS)
                for t in range(NT):
                    pool.indirect_dma_start(out=back[:, t, :], out_offset=None, in_=sorted_out,
                                            in_offset=bass.IndirectOffsetOnAxis(ap=slot[:, t:t + 1], axis=0))\
                        .then_inc(gathered, 16)
                pool.wait_ge(gathered, 16 * NT)

            @block.tensor
            def _(pe):
                expert_regs = [pe.alloc_register(f"gang_expert{i}") for i in range(GANG_LOAD)]

                def turn(n):
                    if n % (QUADS // LOADS) == 0:
                        pe.wait_ge(rows_loaded[n // (QUADS // LOADS)], 16)
                    if n >= 2:
                        pe.wait_ge(rows_ready, n - 1)
                    for i in range(2):
                        mm = pe.transpose(ps_t[:, n % 2, c1(i)], rows[:, 2 * n + i, :], g.ident[:])
                    mm.then_inc(turned, 1)

                turn(0)
                pe.wait_ge(weights_loaded, 16)
                for n in range(QUADS):
                    if n + 1 < QUADS:
                        turn(n + 1)
                    if 4 * n % GANG_LOAD == 0:
                        for i, reg in enumerate(expert_regs):
                            pe.reg_load(reg, gang_expert[0:1, 4 * n + i:4 * n + i + 1])
                    pe.wait_ge(rows_ready, n + 1)
                    if n >= 4:
                        pe.wait_ge(y_copied[n % 2], (n - 4) // 2 + 1)
                    for i in range(4):
                        e = pe.snap(expert_regs[(4 * n + i) % GANG_LOAD], min_val=0, max_val=EXPERTS - 1)
                        mm = pe.matmul(ps_y[0:GANG, n % 4, c1(i)], rowsT[:, n % 2, GANG * i:GANG * (i + 1)],
                                       W[:, bass.ds(e, 1), :].rearrange("p a f -> p (a f)"), start=True, stop=True)
                    mm.then_inc(y_done, 1)
                for reg in expert_regs:
                    pe.free_register(reg)

            @block.scalar
            def _(act):
                for n in range(QUADS):
                    act.wait_ge(turned, n + 1)
                    if n >= 2:
                        act.wait_ge(y_done, n - 1)
                    act.activation(rowsT[:, n % 2, 0:2 * P], ps_t[:, n % 2, 0:2 * P], ACT.Identity,
                                   bias=mod_col(g, 1, SHIFT_B), scale=mod_col(g, 1, SCALE_B)).then_inc(rows_ready, 1)
                    if n % 2 == 1:
                        act.wait_ge(y_done, n)
                        act.activation(y[:, 4 * n - 4:4 * n, :].rearrange("p k f -> p (k f)"),
                                       ps_y[0:GANG, (n - 1) % 4, :], ACT.Identity).then_inc(y_copied[0], 1)

            @block.vector
            def _(dve):
                link = Chain(dve, chain)
                for n in range(1, QUADS, 2):
                    dve.wait_ge(y_done, n + 1)
                    dve.tensor_copy(y[:, 4 * n:4 * n + 4, :].rearrange("p k f -> p (k f)"), ps_y[0:GANG, n % 4, :])\
                       .then_inc(y_copied[1], 1)
                gate = bcast(mod_row(g, 1, GATE_B).unsqueeze(1), P, NT, P)
                dve.wait_ge(bias_gathered, 16 * NT)
                link(dve.tensor_tensor(bias[:], bias[:], gate, ALU.mult))
                link(dve.tensor_tensor(g.x[:], g.x[:], bias[:], ALU.add))
                dve.wait_ge(gathered, 16 * NT)
                link(dve.tensor_tensor(back[:], back[:], gate, ALU.mult))
                dve.tensor_tensor(g.x[:], g.x[:], back[:], ALU.add)


def layer1_experts(nc, d, g):
    sorted_in = nc.dram_tensor("l1_sorted_in", [GANGS * GANG, P], F32, kind="Internal").ap()
    sorted_out = nc.dram_tensor("l1_sorted_out", [GANGS * GANG, P], F32, kind="Internal").ap()
    adaln(nc, g, 1, SCALE_B, SHIFT_B)
    with Stage(nc, "l1ffn") as st:
        W = st.sb("W", [P, EXPERTS, P])
        zeros = st.sb("zeros", [P, P])
        slot = st.sb("slot", [P, NT], I32)
        expert_int = st.sb("expert_int", [P, NT], I32)
        gang_expert = st.sb("gang_expert", [1, GANGS], I32)
        zeroed = st.sem("zeroed")
        weights_loaded = st.sem("weights_loaded")
        stage_l1_route(nc, d, g, W, zeros, sorted_in, zeroed, weights_loaded, slot, expert_int, gang_expert)
        stage_l1_experts(nc, d, g, W, sorted_in, sorted_out, zeroed, weights_loaded, slot, expert_int, gang_expert)



LIF_CELLS = 256


class LifMemory:

    def __init__(self, st):
        self.v = st.sb("lif_v", [P, LIF_CELLS])
        self.mid = st.sb("lif_mid", [P, LIF_CELLS])
        self.differ = st.sb("lif_differ", [P, LIF_CELLS])
        self.shifted = st.sb("lif_shifted", [P, LIF_CELLS])
        self.count = st.sb("lif_count", [P, 32])
        self.count_turned = st.sb("lif_count_turned", [P, 32])
        self.count_int = st.sb("lif_count_int", [P, 1], I32)
        self.step = st.sem("lif_step")


def lif(dve, name, X, U, groups, length, check, m):
    chunks = S // length
    cells = groups * chunks
    assert cells <= LIF_CELLS and 0 < check <= length
    u_of = U.rearrange("p g (c l) -> p (g c) l", l=length)
    x_of = X.rearrange("p g (c l) -> p (g c) l", l=length)
    v, mid, differ, shifted = (buf[:, 0:cells] for buf in (m.v, m.mid, m.differ, m.shifted))
    by_group = lambda ap: ap.rearrange("p (g c) -> p g c", g=groups)
    unsettled = dve.alloc_register(f"{name}_unsettled")
    parts = [dve.alloc_register(f"{name}_unsettled_in_quadrant{i}") for i in range(4)]

    halves = (slice(0, cells // 2), slice(cells // 2, cells))

    def steps(link, first, last):
        for t in range(first, last):
            before = v if t > 0 else shifted
            for half in halves:
                link.mark(dve.scalar_tensor_tensor(u_of[:, half, t], before[:, half], 0.5, x_of[:, half, t],
                                                   ALU.mult, ALU.add))
                dve.wait_ge(m.step, link.n - 1)
            for half in halves:
                link.mark(dve.scalar_tensor_tensor(v[:, half], u_of[:, half, t], 1.0, u_of[:, half, t],
                                                   ALU.is_lt, ALU.mult))
                dve.wait_ge(m.step, link.n - 1)
        link.wait()

    dve.sem_clear(m.step)
    link = Chain(dve, m.step)
    link.mark(dve.memset(m.shifted[:], 0.0))
    link(dve.memset(m.count[:], 0.0))
    steps(link, 0, check)
    link(dve.tensor_copy(mid, v))
    dve.reg_mov(unsettled, 1)
    with dve.While(lambda: dve.snap(unsettled)):
        dve.sem_clear(m.step)
        link = Chain(dve, m.step)
        steps(link, check, length)
        link(dve.tensor_copy(by_group(shifted)[:, :, 1:chunks], by_group(v)[:, :, 0:chunks - 1]))
        steps(link, 0, check)
        link(dve.tensor_tensor(differ, v, mid, ALU.not_equal))
        link.mark(dve.tensor_copy(mid, v))
        link(dve.tensor_reduce(m.count[:, 0:1], differ, AX_X, ALU.add))
        link(dve.transpose(m.count_turned[:], m.count[:]))
        link(dve.tensor_reduce(m.differ[:, 0:1], m.count_turned[:], AX_X, ALU.add))
        link(dve.tensor_copy(m.count_int[:], m.differ[:, 0:1]))
        for i, part in enumerate(parts):
            dve.reg_load(part, m.count_int[32 * i:32 * i + 1, 0:1])
        dve.reg_add(unsettled, parts[0], parts[1])
        dve.reg_add(unsettled, unsettled, parts[2])
        dve.reg_add(unsettled, unsettled, parts[3])
    for r in parts + [unsettled]:
        dve.free_register(r)


def stage_l2_mix(nc, d, g, h_tm, r):
    with Stage(nc, "l2mix") as st:
        w = st.sb("w", [P, 4, P])
        X = st.sb("X", [P, 3, S])
        U = st.sb("U", [P, 3, S])
        decay = st.sb("decay", [P, S])
        m = LifMemory(st)
        ps = st.ps("ps", [P, 8, BANK])
        loaded = st.sem("loaded")
        in_done = st.sem("in_done")
        in_copied = st.sem("in_copied")
        h_scaled = st.sem("h_scaled")
        y_ready = st.sem("y_ready")
        out_done = st.sem("out_done")
        chain = st.sem("chain")
        with st.block() as block:

            @block.sync
            def _(sp):
                sp.dma_start(w[:], d["l2_wrkvo"]).then_inc(loaded, 16)

            @block.tensor
            def _(pe):
                pe.wait_ge(loaded, 16)
                for n in range(3 * NC4):
                    if n >= 8:
                        pe.wait_ge(in_copied, n - 7)
                    pe.matmul(ps[:, n % 8, :], w[:, n // NC4, :], g.hT[:, c4(n % NC4)], start=True,
                              stop=True).then_inc(in_done, 1)
                pe.wait_ge(y_ready, 1)
                for t in range(NT):
                    mm = pe.matmul(ps[:, t // 4, c1(t % 4)], X[:, 0, c1(t)], w[:, 3, :], start=True, stop=True)
                    if t % 4 == 3:
                        mm.then_inc(out_done, 1)

            @block.scalar
            def _(act):
                for n in range(3 * NC4):
                    act.wait_ge(in_done, n + 1)
                    act.activation(X[:, n // NC4, c4(n % NC4)], ps[:, n % 8, :], ACT.Identity,
                                   scale=0.5).then_inc(in_copied, 1)

            @block.gpsimd
            def _(pool):
                pool.tensor_tensor(h_tm[:], g.xn[:], bcast(mod_row(g, 2, SCALE_A).unsqueeze(1), P, NT, P),
                                   ALU.mult).then_inc(h_scaled, 1)
                pool.wait_ge(h_scaled, 1)
                pool.tensor_tensor(h_tm[:], h_tm[:], bcast(mod_row(g, 2, SHIFT_A).unsqueeze(1), P, NT, P),
                                   ALU.add).then_inc(h_scaled, 1)
                pool.wait_ge(h_scaled, 2)

            @block.vector
            def _(dve):
                link = Chain(dve, chain)
                link.mark(dve.memset(decay[:], 0.9))
                dve.wait_ge(in_copied, 3 * NC4)
                lif(dve, "rkv", X[:], U[:], 3, 32, 32, m)
                r_u, k_u, v_u = (U[:, i, :] for i in range(3))
                y, kv, acc = (X[:, i, :] for i in range(3))
                link(dve.tensor_scalar(v_u, v_u, 1.0, None, ALU.is_ge))
                link(dve.scalar_tensor_tensor(kv, k_u, 1.0, v_u, ALU.is_ge, ALU.mult))
                link(dve.tensor_tensor_scan(acc, decay[:], kv, 0.0, ALU.mult, ALU.add))
                dve.scalar_tensor_tensor(y, r_u, 1.0, acc, ALU.is_ge, ALU.mult).then_inc(y_ready, 1)
                dve.wait_ge(h_scaled, 2)
                for j in range(NC4):
                    dve.wait_ge(out_done, j + 1)
                    ts = slice(4 * j, 4 * j + 4)
                    dve.tensor_tensor(r[:, ts, :], ps[:, j, :].rearrange("p (t f) -> p t f", t=4), h_tm[:, ts, :],
                                      ALU.add)


def stage_l2_hidden(nc, d, g, x1n, x1T, x1_tm, X):
    with Stage(nc, "l2hid") as st:
        w1 = st.sb("w1", [P, 4, P])
        b1 = st.sb("b1", [P, 4])
        half_b = st.sb("half_b", [P, 4])
        gain = st.sb("gain", [P, P])
        shift = st.sb("shift", [P, P])
        ps = st.ps("ps", [P, 8, BANK])
        loaded = st.sem("loaded")
        bias_ready = st.sem("bias_ready")
        in_done = st.sem("in_done")
        in_copied = st.sem("in_copied")
        x1_scaled = st.sem("x1_scaled")
        with st.block() as block:

            @block.sync
            def _(sp):
                for dst, name in ((w1, "l2_w1T"), (b1, "l2_b1"), (gain, "l2_ln1g"), (shift, "l2_ln1b")):
                    sp.dma_start(dst[:], d[name]).then_inc(loaded, 16)

            @block.tensor
            def _(pe):
                pe.wait_ge(loaded, 64)
                for n in range(4 * NC4):
                    if n >= 8:
                        pe.wait_ge(in_copied, n - 7)
                    pe.matmul(ps[:, n % 8, :], w1[:, n // NC4, :], x1T[:, c4(n % NC4)], start=True,
                              stop=True).then_inc(in_done, 1)

            @block.scalar
            def _(act):
                act.wait_ge(bias_ready, 1)
                for n in range(4 * NC4):
                    act.wait_ge(in_done, n + 1)
                    f = n // NC4
                    act.activation(X[:, f, c4(n % NC4)], ps[:, n % 8, :], ACT.Identity, scale=0.5,
                                   bias=half_b[:, f:f + 1]).then_inc(in_copied, 1)

            @block.vector
            def _(dve):
                dve.wait_ge(loaded, 64)
                dve.tensor_scalar(half_b[:], b1[:], 0.5, None, ALU.mult).then_inc(bias_ready, 1)

            @block.gpsimd
            def _(pool):
                pool.wait_ge(loaded, 64)
                pool.tensor_tensor(x1_tm[:], x1n[:], bcast(gain[:].unsqueeze(1), P, NT, P), ALU.mult)\
                    .then_inc(x1_scaled, 1)
                pool.wait_ge(x1_scaled, 1)
                pool.tensor_tensor(x1_tm[:], x1_tm[:], bcast(shift[:].unsqueeze(1), P, NT, P), ALU.add)\
                    .then_inc(x1_scaled, 1)
                pool.wait_ge(x1_scaled, 2)


def stage_l2_spikes(nc, d, g, X, x1_tm):
    with Stage(nc, "l2spk") as st:
        w2 = st.sb("w2", [P, 4, P])
        b2 = st.sb("b2", [P, 1])
        half_b = st.sb("half_b", [P, 1])
        U = st.sb("U", [P, 4, S])
        m = LifMemory(st)
        ps = st.ps("ps", [P, 4, BANK])
        ps_t = st.ps("ps_t", [P, 4, BANK])
        loaded = st.sem("loaded")
        bias_ready = st.sem("bias_ready")
        s_ready = st.sem("s_ready")
        h2_done = st.sem("h2_done")
        h2_copied = st.sem("h2_copied")
        out_ready = st.sem("out_ready")
        turned = st.sem("turned")
        with st.block() as block:

            @block.sync
            def _(sp):
                sp.dma_start(w2[:], d["l2_w2T"]).then_inc(loaded, 16)
                sp.dma_start(b2[:], d["l2_b2"]).then_inc(loaded, 16)

            @block.tensor
            def _(pe):
                pe.wait_ge(loaded, 32)
                for f in range(4):
                    pe.wait_ge(s_ready, f + 1)
                    for j in range(NC4):
                        mm = pe.matmul(ps[:, j, :], w2[:, f, :], U[:, f, c4(j)], start=(f == 0), stop=(f == 3))
                mm.then_inc(h2_done, 1)
                pe.wait_ge(out_ready, 1)
                for t in range(NT):
                    mm = pe.transpose(ps_t[:, t // 4, c1(t % 4)], U[:, 0, c1(t)], g.ident[:])
                    if t % 4 == 3:
                        mm.then_inc(turned, 1)

            @block.scalar
            def _(act):
                act.wait_ge(bias_ready, 1)
                act.wait_ge(h2_done, 1)
                for j in range(NC4):
                    act.activation(X[:, 0, c4(j)], ps[:, j, :], ACT.Identity, scale=0.5, bias=half_b[:])\
                       .then_inc(h2_copied, 1)

            @block.vector
            def _(dve):
                dve.wait_ge(loaded, 32)
                dve.tensor_scalar(half_b[:], b2[:], 0.5, None, ALU.mult).then_inc(bias_ready, 1)
                lif(dve, "hidden", X[:], U[:], 4, 64, 44, m)
                for f in range(4):
                    dve.tensor_scalar(U[:, f, :], U[:, f, :], 1.0, None, ALU.is_ge).then_inc(s_ready, 1)
                dve.wait_ge(h2_copied, NC4)
                lif(dve, "out", X[:, 0:1, :], U[:, 0:1, :], 1, 16, 16, m)
                dve.tensor_scalar(U[:, 0, :], U[:, 0, :], 1.0, None, ALU.is_ge).then_inc(out_ready, 1)
                for j in range(NC4):
                    dve.wait_ge(turned, j + 1)
                    ts = slice(4 * j, 4 * j + 4)
                    dve.tensor_tensor(x1_tm[:, ts, :], ps_t[:, j, :].rearrange("p (t f) -> p t f", t=4),
                                      x1_tm[:, ts, :], ALU.add)


def layer2_spiking(nc, d, g):
    adaln(nc, g, 2, SCALE_A, SHIFT_A)
    with Stage(nc, "l2") as st:
        h_tm = st.sb("h_tm", [P, NT, P])
        x1_tm = st.sb("x1_tm", [P, NT, P])
        ln_cols = st.sb("ln_cols", [P, 2])
        cols_loaded = st.sem("cols_loaded")
        nc.sync.dma_start(ln_cols[:], d["l2_ln1cols"]).then_inc(cols_loaded, 16)
        nc.scalar.wait_ge(cols_loaded, 16)
        stage_l2_mix(nc, d, g, h_tm, x1_tm)
        stage_norm(nc, g, "l2norm1", x1_tm, h_tm, g.hT, ln_cols[:, 0:1], ln_cols[:, 1:2])
        X = st.sb("X", [P, 4, S])
        stage_l2_hidden(nc, d, g, h_tm, g.hT, x1_tm, X)
        stage_l2_spikes(nc, d, g, X, x1_tm)
        stage_norm(nc, g, "l2norm2", x1_tm, g.xn)
        stage_add_affine(nc, d, g, "l2add", g.xn, "l2_ln2g", "l2_ln2b", mod_row(g, 2, GATE_A))



def layer2_product(nc, d, g):
    adaln(nc, g, 2, SCALE_B, SHIFT_B)
    with Stage(nc, "l2ffn") as st:
        w = st.sb("w", [P, P])
        scale = st.sb("scale", [P, P])
        bias = st.sb("bias", [P, P])
        tmp = st.sb("tmp", [P, 2, 4, P])
        ps = st.ps("ps", [P, 4, BANK])
        loaded = st.sem("loaded")
        rows_ready = st.sem("rows_ready")
        done = st.sem("done")
        shifted = st.sem("shifted")
        chain = st.sem("chain")
        with st.block() as block:

            @block.sync
            def _(sp):
                for dst, name in ((w, "l2_CBT"), (scale, "l2_SCB"), (bias, "l2_bias")):
                    sp.dma_start(dst[:], d[name]).then_inc(loaded, 16)

            @block.tensor
            def _(pe):
                pe.wait_ge(loaded, 48)
                for t in range(NT):
                    mm = pe.matmul(ps[:, t // 4, c1(t % 4)], g.hT[:, c1(t)], w[:], start=True, stop=True)
                    if t % 4 == 3:
                        mm.then_inc(done, 1)

            @block.gpsimd
            def _(pool):
                pool.wait_ge(rows_ready, 1)
                pool.tensor_tensor(g.x[:], g.x[:], bcast(bias[:].unsqueeze(1), P, NT, P), ALU.add).then_inc(shifted, 1)
                pool.wait_ge(shifted, 1)

            @block.vector
            def _(dve):
                link = Chain(dve, chain)
                gate = mod_row(g, 2, GATE_B)
                dve.wait_ge(loaded, 48)
                link(dve.tensor_scalar(scale[:], scale[:], 1.0 / 127.0, None, ALU.mult))
                link.mark(dve.tensor_tensor(scale[:], scale[:], gate, ALU.mult))
                dve.tensor_tensor(bias[:], bias[:], gate, ALU.mult).then_inc(rows_ready, 1)
                link.wait()
                for j in range(NC4):
                    dve.wait_ge(done, j + 1)
                    link(dve.tensor_tensor(tmp[:, j % 2], ps[:, j, :].rearrange("p (t f) -> p t f", t=4),
                                           bcast(scale[:].unsqueeze(1), P, 4, P), ALU.mult))
                    if j == 0:
                        dve.wait_ge(shifted, 1)
                    xs = g.x[:, 4 * j:4 * j + 4, :]
                    dve.tensor_tensor(xs, xs, tmp[:, j % 2], ALU.add)



WINDOW = 32
SPAN = P + WINDOW
L3_H, L3_K = 16, 8
LAT_H, LAT_K, LATENTS = 8, 8, 64


def load_group(sp, Q, K, q_parts, k_parts, grp, loaded):
    for r in range(6):
        for operand, dram, part, at in ((Q, q_parts, SPLITS_Q[r], 0), (K, k_parts, SPLITS_K[r], WINDOW)):
            src = dram[part, GROUP * L3_K * grp:GROUP * L3_K * (grp + 1), :].rearrange("(h k) t -> k h t", k=L3_K)
            sp.dma_start(operand[L3_K * r:L3_K * (r + 1), grp % 2, :, at:at + S], src).then_inc(loaded[grp % 2], 16)


def stage_l3_latent(nc, d, g, q, rem, gates, Q, K, q_parts, k_parts, group_loaded):
    PROBS = 3
    with Stage(nc, "l3lat") as st:
        wg = st.sb("wg", [P, 3, LATENTS])
        r_out = st.sb("r_out", [LATENTS, P])
        head_rows = st.sb("head_rows", [P, L3_H])
        gate_w = st.sb("gate_w", [P, 2])
        gate_m = st.sb("gate_m", [P, 2, L3_H])
        causal = st.sb("causal", [P, NT, LATENTS], BF16)
        ident16 = st.sb("ident16", [P, P], BF16)
        gqT = st.sb("gqT", [LATENTS, S])
        pooled = st.sb("pooled", [P, LATENTS])
        gk = st.sb("gk", [LATENTS, LAT_H, LATENTS])
        gv = st.sb("gv", [LATENTS, LAT_H, LATENTS])
        R = st.sb("R", [P, 4, P])
        sc = st.sb("sc", [P, 2, LAT_H, LATENTS])
        probs = st.sb("probs", [P, PROBS, LAT_H, LATENTS])
        top = st.sb("top", [P, 2, LAT_H])
        den = st.sb("den", [P, 2, LAT_H])
        PT = st.sb("PT", [P, 2, BANK])
        ps_a = st.ps("ps_a", [P, 4, BANK])
        ps_t = st.ps("ps_t", [P, 2, BANK])
        ps_r = st.ps("ps_r", [P, 2, BANK])
        loaded = st.sem("loaded")
        gq_done = st.sem("gq_done")
        gq_copied = st.sem("gq_copied")
        pool_ready = st.sem("pool_ready")
        gkv_done = st.sem("gkv_done")
        gkv_ready = st.sem("gkv_ready")
        r_done = st.sem("r_done")
        r_copied = st.sem("r_copied")
        gm_ready = st.sem("gm_ready")
        gates_done = st.sem("gates_done")
        gates_read = st.sem("gates_read")
        scored = st.sem("scored")
        sub_ready = st.sem("sub_ready")
        expd = st.sem("expd")
        p_ready = st.sem("p_ready")
        turned = st.sem("turned")
        pt_copied = st.sem("pt_copied")
        rem_done = st.sem("rem_done")
        rem_copied = st.sem("rem_copied")
        chain = st.sem("chain")
        with st.block() as block:

            @block.sync
            def _(sp):
                for dst, name in ((wg, "l3_wg"), (r_out, "l3_r_out"), (head_rows, "head_rows"), (gate_w, "l3_gates"),
                                  (causal, "lat_causal"), (ident16, "ident16")):
                    sp.dma_start(dst[:], d[name]).then_inc(loaded, 16)
                sp.wait_ge(loaded, 96)
                for grp in range(2):
                    load_group(sp, Q, K, q_parts, k_parts, grp, group_loaded)

            @block.tensor
            def _(pe):
                pe.wait_ge(loaded, 96)
                for j in range(NC4):
                    pe.matmul(ps_a[0:LATENTS, j, :], wg[:, 0, :], g.hT[:, c4(j)], start=True, stop=True)\
                      .then_inc(gq_done, 1)
                pe.wait_ge(pool_ready, 1)
                for i in range(2):
                    mm = pe.matmul(ps_t[0:LATENTS, i, 0:LATENTS], wg[:, 1 + i, :], pooled[:], start=True, stop=True)
                mm.then_inc(gkv_done, 1)
                pe.wait_ge(gm_ready, 1)
                for t in range(NT):
                    mm = pe.matmul(ps_r[:, 0, 2 * L3_H * t:2 * L3_H * (t + 1)], q[:, c1(t)],
                                   gate_m[:].rearrange("p a h -> p (a h)"), start=True, stop=True)
                mm.then_inc(gates_done, 1)
                pe.wait_ge(gkv_ready, 2)
                for c in range(4):
                    mm = pe.matmul(ps_r[:, 1, c1(c)], gv[:, 2 * c:2 * c + 2, :].rearrange("p h n -> p (h n)"),
                                   r_out[:], start=True, stop=True)
                mm.then_inc(r_done, 1)

                def score(t):
                    if t < 4:
                        pe.wait_ge(gq_copied, NC4)
                    else:
                        pe.wait_ge(sub_ready, t - 3)
                    pe.matmul(ps_a[:, t % 4, :], ident16[:], bcast(causal[:, t:t + 1, :], P, LAT_H, LATENTS),
                              start=True, stop=False)
                    pe.matmul(ps_a[:, t % 4, :], gqT[:, c1(t)], gk[:].rearrange("p h n -> p (h n)"), start=False,
                              stop=True).then_inc(scored, 1)

                def turn(t):
                    pe.wait_ge(p_ready, t + 1)
                    if t == 0:
                        pe.wait_ge(gkv_ready, 2)
                    if t >= 2:
                        pe.wait_ge(pt_copied, t - 1)
                    p = probs[:, t % PROBS, :, :].rearrange("p h n -> p (h n)")
                    for c in range(4):
                        mm = pe.transpose(ps_t[:, t % 2, c1(c)], p[:, c1(c)], g.ident[:])
                    mm.then_inc(turned, 1)

                def values(t):
                    pe.wait_ge(pt_copied, t + 1)
                    if t < 2:
                        pe.wait_ge(r_copied, 1)
                        pe.wait_ge(gates_read, 1)
                    else:
                        pe.wait_ge(rem_copied, t - 1)
                    for c in range(4):
                        mm = pe.matmul(ps_r[:, t % 2, 0:P], PT[:, t % 2, c1(c)], R[:, c, :], start=(c == 0),
                                       stop=(c == 3))
                    mm.then_inc(rem_done, 1)

                score(0)
                score(1)
                for t in range(NT + 1):
                    if t + 2 < NT:
                        score(t + 2)
                    if t < NT:
                        turn(t)
                    if t >= 1:
                        values(t - 1)

            @block.scalar
            def _(act):
                for j in range(NC4):
                    act.wait_ge(gq_done, j + 1)
                    act.activation(gqT[:, c4(j)], ps_a[0:LATENTS, j, :], ACT.Identity, scale=LAT_K ** -0.5)\
                       .then_inc(gq_copied, 1)
                act.wait_ge(gates_done, 1)
                act.activation(gates[:].rearrange("p a t h -> p t a h"),
                               ps_r[:, 0, :].rearrange("p (t a h) -> p t a h", t=NT, a=2), ACT.Sigmoid,
                               scale=L3_K ** 0.5).then_inc(gates_read, 1)
                act.wait_ge(r_done, 1)
                act.activation(R[:].rearrange("p c f -> p (c f)"), ps_r[:, 1, :], ACT.Identity).then_inc(r_copied, 1)
                for t in range(NT + 1):
                    if t < NT:
                        act.wait_ge(sub_ready, t + 1)
                        if t >= PROBS:
                            act.wait_ge(turned, t - PROBS + 1)
                        act.activation(probs[:, t % PROBS], sc[:, t % 2], ACT.Exp).then_inc(expd, 1)
                    if t >= 1:
                        act.wait_ge(turned, t)
                        if t >= 3:
                            act.wait_ge(rem_done, t - 2)
                        act.activation(PT[:, (t - 1) % 2, :], ps_t[:, (t - 1) % 2, :], ACT.Identity)\
                           .then_inc(pt_copied, 1)

            @block.vector
            def _(dve):
                link = Chain(dve, chain)
                dve.wait_ge(loaded, 96)
                link.mark(dve.tensor_scalar(gate_m[:, 0, :], head_rows[:], gate_w[:, 0:1], None, ALU.mult))
                dve.tensor_scalar(gate_m[:, 1, :], head_rows[:], gate_w[:, 1:2], None, ALU.mult).then_inc(gm_ready, 1)
                link(dve.tensor_reduce(pooled[:], g.hT[:].rearrange("p (n c) -> p n c", c=S // LATENTS), AX_X,
                                       ALU.add))
                dve.tensor_scalar(pooled[:], pooled[:], LATENTS / S, None, ALU.mult).then_inc(pool_ready, 1)
                dve.wait_ge(gkv_done, 1)
                for i, blocks in enumerate((gk, gv)):
                    dve.tensor_tensor(blocks[:], bcast(ps_t[0:LATENTS, i:i + 1, 0:LATENTS], LATENTS, LAT_H, LATENTS),
                                      bcast(head_rows[0:LATENTS, 0:LAT_H].unsqueeze(2), LATENTS, LAT_H, LATENTS),
                                      ALU.mult).then_inc(gkv_ready, 1)
                for t in range(NT + 3):
                    if t < NT:
                        b = t % 2
                        dve.wait_ge(scored, t + 1)
                        s3 = ps_a[:, t % 4, :].rearrange("p (h n) -> p h n", h=LAT_H)
                        link(dve.tensor_reduce(top[:, b, :], s3, AX_X, ALU.max))
                        if t >= 2:
                            dve.wait_ge(expd, t - 1)
                        dve.tensor_tensor(sc[:, b], s3, bcast(top[:, b, :].unsqueeze(2), P, LAT_H, LATENTS),
                                          ALU.subtract).then_inc(sub_ready, 1)
                    if 1 <= t <= NT:
                        b, pb = (t - 1) % 2, (t - 1) % PROBS
                        dve.wait_ge(expd, t)
                        link(dve.tensor_reduce(den[:, b, :], probs[:, pb], AX_X, ALU.add))
                        link(dve.reciprocal(den[:, b, :], den[:, b, :]))
                        dve.tensor_tensor(probs[:, pb], probs[:, pb],
                                          bcast(den[:, b, :].unsqueeze(2), P, LAT_H, LATENTS), ALU.mult)\
                           .then_inc(p_ready, 1)
                    if t >= 3:
                        dve.wait_ge(rem_done, t - 2)
                        dve.tensor_copy(rem[:, t - 3, :], ps_r[:, (t - 3) % 2, 0:P]).then_inc(rem_copied, 1)


def stage_l3_local(nc, d, g, V_aug, Q, K, q_parts, k_parts, loaded, O):
    NG = L3_H // GROUP
    FIRST, PACE = 6, 2
    ahead = lambda t: range(PACE * (t - FIRST), PACE * (t - FIRST + 1)) if FIRST <= t < FIRST + NT // PACE else ()
    NEGATE = FIRST + NT // PACE
    with Stage(nc, "l3loc") as st:
        mask_q = st.sb("mask_q", [P, 2, 1, SPAN], BF16)
        mask_k = st.sb("mask_k", [P, 1, SPAN], BF16)
        ident16 = st.sb("ident16", [P, P], BF16)
        maxima = st.sb("maxima", [P, NT, GROUP])
        negmax = st.sb("negmax", [P, GROUP, NT])
        rest = st.sb("rest", [P, GROUP, NT])
        nm = st.sb("nm", [P, GROUP, 3, NT], BF16)
        nm_rows = st.sb("nm_rows", [3 * NT, GROUP, P], BF16)
        probs = st.sb("probs", [P, 3, GROUP, SPAN])
        pv_sb = st.sb("pv_sb", [P, 2, BANK])
        rden = st.sb("rden", [P, 4, GROUP])
        ps_m = st.ps("ps_m", [P, 2, BANK])
        ps_s = st.ps("ps_s", [P, 4, BANK])
        ps_v = st.ps("ps_v", [P, BANK])
        ps_t = st.ps("ps_t", [P, BANK])
        cleared = st.sem("cleared")
        consts_loaded = st.sem("consts_loaded")
        m_done = st.sem("m_done")
        m_read = st.sem("m_read")
        nm_ready = st.sem("nm_ready")
        nm_turned = st.sem("nm_turned")
        nm_rows_ready = st.sem("nm_rows_ready")
        nm_placed = st.sem("nm_placed")
        scored = st.sem("scored")
        expd = st.sem("expd")
        pv_done = st.sem("pv_done")
        pv_copied = st.sem("pv_copied")
        pv_turned = st.sem("pv_turned")
        o_ready = st.sem("o_ready")
        chain = st.sem("chain")
        heads2 = lambda ap: ap.rearrange("p (h c) -> p h c", h=2)

        with st.block() as block:

            @block.sync
            def _(sp):
                for dst, name in ((mask_q, "mask_q"), (mask_k, "mask_k"), (ident16, "ident16")):
                    sp.dma_start(dst[:], d[name]).then_inc(consts_loaded, 16)
                for grp in range(NG):
                    if grp >= 2:
                        sp.wait_ge(scored, (grp - 1) * NT)
                        load_group(sp, Q, K, q_parts, k_parts, grp, loaded)
                        sp.wait_ge(cleared, grp - 1)
                    sp.wait_ge(nm_rows_ready, grp + 1)
                    for h in range(GROUP):
                        sp.dma_start(Q[MAX_ROW:MAX_ROW + 3, grp % 2, h, 0:S], nm_rows[:, h, :]).then_inc(nm_placed, 16)

            @block.gpsimd
            def _(pool):
                for grp in range(2, NG):
                    pool.wait_ge(scored, (grp - 1) * NT)
                    pool.memset(Q[MAX_ROW:MAX_ROW + 3, grp % 2, :, :], 0.0).then_inc(cleared, 1)

            @block.tensor
            def _(pe):
                pe.wait_ge(consts_loaded, 48)

                def maxima_of(grp, t):
                    par = grp % 2
                    if t == 0:
                        pe.wait_ge(loaded[par], 16 * 12 * (grp // 2 + 1))
                        if grp >= 2:
                            pe.wait_ge(cleared, grp - 1)
                    for half in range(2):
                        n = 2 * (NT * grp + t) + half
                        if n >= 2:
                            pe.wait_ge(m_read, n - 1)
                        dst = ps_m[:, n % 2, 0:2 * SPAN]
                        pe.matmul(dst, ident16[:], bcast(mask_q[:, min(t, 1), :, :], P, 2, SPAN), start=True,
                                  stop=False)
                        for i in range(2):
                            h = 2 * half + i
                            mm = pe.matmul(dst[:, i * SPAN:(i + 1) * SPAN], Q[:, par, h, c1(t)],
                                           K[:, par, h, t * P:t * P + SPAN], start=False, stop=(i == 1))
                        mm.then_inc(m_done, 1)

                def turn_maxima(grp):
                    pe.wait_ge(nm_ready, grp + 1)
                    if grp >= 1:
                        pe.wait_ge(o_ready, NC4 * (grp - 1) + 3)
                    for h in range(GROUP):
                        mm = pe.transpose(ps_t[0:3 * NT, h * 64:h * 64 + 64].bitcast(BF16),
                                          nm[:, h, :, :].rearrange("p s t -> p (s t)"), ident16[:])
                    mm.then_inc(nm_turned, 1)

                def values(grp, t):
                    n = NT * grp + t
                    pe.wait_ge(expd, n + 1)
                    if t % 4 == 0 and n >= 4:
                        pe.wait_ge(pv_copied, n // 4)
                    for h in range(GROUP):
                        out = ps_v[32 * h:32 * h + 32, c1(t % 4)]
                        mm = pe.matmul(out, V_aug[:, t, GROUP * grp + h, :], probs[:, n % 3, h, 0:P], start=True,
                                       stop=(t == 0), skip_group_check=True)
                    if t >= 1:
                        for h in range(GROUP):
                            out = ps_v[32 * h:32 * h + 32, c1(t % 4)]
                            mm = pe.matmul(out[:, 0:WINDOW], V_aug[:, t - 1, GROUP * grp + h, :],
                                           probs[:, (n - 1) % 3, h, P:SPAN], start=False, stop=True,
                                           skip_group_check=True)
                    mm.then_inc(pv_done, 1)

                def turn_values(n):
                    pe.wait_ge(pv_copied, n + 1)
                    if n >= 1:
                        pe.wait_ge(o_ready, n)
                    if n % NC4 == NC4 - 1 and n // NC4 + 1 < NG:
                        pe.wait_ge(nm_rows_ready, n // NC4 + 2)
                    elif n == 0:
                        pe.wait_ge(nm_rows_ready, 1)
                    for i in range(4):
                        mm = pe.transpose(ps_t[:, c1(i)], pv_sb[:, n % 2, c1(i)], g.ident[:])
                    mm.then_inc(pv_turned, 1)

                for t in range(NT):
                    maxima_of(0, t)
                turn_maxima(0)
                for grp in range(NG):
                    pe.wait_ge(nm_placed, 16 * GROUP * (grp + 1))
                    par = grp % 2
                    for t in range(NT + 1):
                        if grp + 1 < NG:
                            for m in ahead(t)[:1]:
                                maxima_of(grp + 1, m)
                            if t == NT - 1:
                                turn_maxima(grp + 1)
                        if t < NT:
                            n = NT * grp + t
                            if n >= 2:
                                pe.wait_ge(expd, n - 1)
                            for half in range(2):
                                dst = ps_s[:, 2 * (n % 2) + half, 0:2 * SPAN]
                                pe.matmul(dst, ident16[:], bcast(mask_k[:], P, 2, SPAN), start=True, stop=False)
                                for i in range(2):
                                    h = 2 * half + i
                                    mm = pe.matmul(dst[:, i * SPAN:(i + 1) * SPAN],
                                                   K[:, par, h, WINDOW + t * P:WINDOW + (t + 1) * P],
                                                   Q[:, par, h, t * P:t * P + SPAN], start=False, stop=(i == 1))
                            mm.then_inc(scored, 1)
                        if grp + 1 < NG:
                            for m in ahead(t)[1:]:
                                maxima_of(grp + 1, m)
                        if t >= 1:
                            values(grp, t - 1)
                        if t >= 6 and (t - 6) % 4 == 0:
                            turn_values(NC4 * grp + (t - 6) // 4)
                    turn_values(NC4 * grp + NC4 - 1)

            @block.scalar
            def _(act):
                for n in range(NG * NT):
                    act.wait_ge(scored, n + 1)
                    if n >= 3:
                        act.wait_ge(pv_done, n - 1)
                    b = 2 * (n % 2)
                    act.activation(probs[:, n % 3, :, :].rearrange("p (b h) c -> p b (h c)", b=2),
                                   ps_s[:, b:b + 2, 0:2 * SPAN], ACT.Exp).then_inc(expd, 1)

            @block.vector
            def _(dve):
                link = Chain(dve, chain)

                def maxima_of(grp, t):
                    for half in range(2):
                        n = 2 * (NT * grp + t) + half
                        dve.wait_ge(m_done, n + 1)
                        dve.tensor_reduce(maxima[:, t, 2 * half:2 * half + 2], heads2(ps_m[:, n % 2, 0:2 * SPAN]),
                                          AX_X, ALU.max).then_inc(m_read, 1)

                def negate(grp):
                    dve.wait_ge(m_read, 2 * NT * (grp + 1))
                    link(dve.tensor_scalar(negmax[:], maxima[:].rearrange("p t h -> p h t"), -1.0, None, ALU.mult))
                    if grp >= 1:
                        dve.wait_ge(nm_turned, grp)
                    splits_of(link, dve, [nm[:, :, i, :] for i in range(3)], rest[:], negmax[:], nm_ready)

                def copy_maxima(grp):
                    dve.wait_ge(nm_turned, grp + 1)
                    if grp >= 1:
                        dve.wait_ge(nm_placed, 16 * GROUP * grp)
                    dve.tensor_copy(nm_rows[:], ps_t[0:3 * NT, 0:4 * 64].bitcast(BF16).rearrange(
                        "p (h q) -> p h q", h=GROUP)).then_inc(nm_rows_ready, 1)

                def copy_values(n):
                    dve.wait_ge(pv_done, 4 * (n + 1))
                    if n >= 2:
                        dve.wait_ge(pv_turned, n - 1)
                    dve.tensor_copy(pv_sb[:, n % 2, :], ps_v[:]).then_inc(pv_copied, 1)

                def values_of(n):
                    grp, c = n // NC4, n % NC4
                    dve.wait_ge(pv_turned, n + 1)
                    v = ps_t[:, 0:BANK].rearrange("p (t h k) -> p t h k", t=4, h=GROUP)
                    link(dve.reciprocal(rden[:], v[:, :, :, L3_K]))
                    o = O[:, 4 * c:4 * c + 4, L3_K * GROUP * grp:L3_K * GROUP * (grp + 1)].rearrange(
                        "p t (h k) -> p t h k", k=L3_K)
                    dve.tensor_tensor(o, v[:, :, :, 0:L3_K], bcast(rden[:].unsqueeze(3), P, 4, GROUP, L3_K),
                                      ALU.mult).then_inc(o_ready, 1)

                for t in range(NT):
                    maxima_of(0, t)
                negate(0)
                copy_maxima(0)
                for grp in range(NG):
                    for t in range(NT):
                        if grp + 1 < NG:
                            for m in ahead(t):
                                maxima_of(grp + 1, m)
                            if t == NEGATE:
                                negate(grp + 1)
                        if t >= 4 and t % 4 == 0:
                            copy_values(NC4 * grp + t // 4 - 1)
                        if t >= 6 and t % 4 == 2:
                            values_of(NC4 * grp + t // 4 - 1)
                    if grp + 1 < NG:
                        copy_maxima(grp + 1)
                    copy_values(NC4 * grp + NC4 - 1)
                    values_of(NC4 * grp + NC4 - 1)


def stage_l3_mix(nc, d, g, O, rem, gates):
    with Stage(nc, "l3mix") as st:
        gated = st.sb("gated", [P, NT, P])
        remote_scaled = st.sem("remote_scaled")
        local_scaled = st.sem("local_scaled")
        heads = lambda ap: ap.rearrange("p t (h k) -> p (t h) k", k=L3_K)
        gate = lambda i: bcast(gates[:, i, :, :].rearrange("p t h -> p (t h)").unsqueeze(2), P, NT * L3_H, L3_K)
        with st.block() as block:

            @block.gpsimd
            def _(pool):
                pool.tensor_tensor(heads(gated[:]), heads(rem[:]), gate(1), ALU.mult)\
                    .then_inc(remote_scaled, 1)
                pool.wait_ge(remote_scaled, 1)

            @block.vector
            def _(dve):
                dve.tensor_tensor(heads(O[:]), heads(O[:]), gate(0), ALU.mult).then_inc(local_scaled, 1)
                dve.wait_ge(local_scaled, 1)
                dve.wait_ge(remote_scaled, 1)
                dve.tensor_tensor(O[:], O[:], gated[:], ALU.add)


def layer3_attention(nc, d, g):
    adaln(nc, g, 3, SCALE_A, SHIFT_A)
    q_parts = nc.dram_tensor("l3_q_parts", [3, P, S], BF16, kind="Internal").ap()
    k_parts = nc.dram_tensor("l3_k_parts", [3, P, S], BF16, kind="Internal").ap()
    with Stage(nc, "l3") as st:
        V_aug = st.sb("V_aug", [P, NT, L3_H, 32])
        rem = st.sb("rem", [P, NT, P])
        gates = st.sb("gates", [P, 2, NT, L3_H])
        Q = st.sb("Q", [P, 2, GROUP, S + WINDOW], BF16)
        K = st.sb("K", [P, 2, GROUP, WINDOW + S], BF16)
        loaded = [st.sem("loaded0"), st.sem("loaded1")]
        with Stage(nc, "l3q") as st_q:
            q = st_q.sb("q", [P, S])
            with Stage(nc, "l3parts") as st_p:
                qp = [st_p.sb(f"qp{i}", [P, S], BF16) for i in range(3)]
                kp = [st_p.sb(f"kp{i}", [P, S], BF16) for i in range(3)]
                stage_project_parts(nc, d, g, "l3proj", "l3_wqkv", V_aug, q, qp, kp, Q, K, (q_parts, k_parts))
            stage_l3_latent(nc, d, g, q, rem, gates, Q, K, q_parts, k_parts, loaded)
        O = st.sb("O", [P, NT, P])
        stage_l3_local(nc, d, g, V_aug, Q, K, q_parts, k_parts, loaded, O)
        stage_l3_mix(nc, d, g, O, rem, gates)
        stage_project_out(nc, d, g, "l3out", O, "l3_wout", mod_row(g, 3, GATE_A))



E3, F3 = 8, 512
CAP = S // E3
DIGIT, DIGITS = 4, 4
CAND = 2 ** DIGIT - 1
TAKEN = -4.0 * 2 ** 16


def stage_l3_select(nc, d, g, nT, slot):
    with Stage(nc, "l3sel") as st:
        cent = st.sb("cent", [P, E3])
        multiples = st.sb("multiples", [P, 1, CAND])
        before = st.sb("before", [P, P], BF16)
        not_yet = st.sb("not_yet", [P, P], BF16)
        ones = st.sb("ones", [P, P], BF16)
        scores = st.sb("scores", [P, E3, NT])
        flip = st.sb("flip", [P, E3, NT], I32)
        half_int = st.sb("half_int", [P, 2, E3, NT], I32)
        high = st.sb("high", [P, E3, NT])
        low1 = st.sb("low1", [P, E3, NT])
        left = st.sb("left", [P, NT])
        h = st.sb("h", [P, NT])
        key = st.sb("key", [P, NT])
        above = st.sb("above", [P, NT])
        cands = st.sb("cands", [P, 1, CAND])
        threshold = st.sb("threshold", [P, 2])
        reach = st.sb("reach", [P, CAND, NT])
        part = st.sb("part", [P, CAND], BF16)
        enough = st.sb("enough", [P, CAND])
        digit = st.sb("digit", [P, 1])
        masks = st.sb("masks", [P, 2, NT], BF16)
        eq = st.sb("eq", [P, NT])
        upto = st.sb("upto", [P, NT])
        ones_row = st.sb("ones_row", [P, NT])
        greater = st.sb("greater", [P, 1])
        member = st.sb("member", [P, E3, NT])
        member16 = st.sb("member16", [P, E3, NT], BF16)
        rank = st.sb("rank", [P, E3, NT])
        base = st.sb("base", [P, E3, NT])
        slot_f = st.sb("slot_f", [P, NT])
        ps_s = st.ps("ps_s", [P, BANK])
        ps_c = st.ps("ps_c", [P, 2, BANK])
        loaded = st.sem("loaded")
        ones_ready = st.sem("ones_ready")
        scored = st.sem("scored")
        part_ready = st.sem("part_ready")
        counted = st.sem("counted")
        masks_ready = st.sem("masks_ready")
        masks_counted = st.sem("masks_counted")
        members_ready = st.sem("members_ready")
        ranked = st.sem("ranked")
        chain = st.sem("chain")
        with st.block() as block:

            @block.sync
            def _(sp):
                for dst, name in ((cent, "l3_centT"), (multiples, "multiples"), (before, "before"),
                                  (not_yet, "not_yet"), (base, "bases")):
                    sp.dma_start(dst[:], d[name]).then_inc(loaded, 16)

            @block.tensor
            def _(pe):
                pe.wait_ge(loaded, 16 * 5)
                for t in range(NT):
                    mm = pe.matmul(ps_s[:, E3 * t:E3 * t + E3], nT[:, c1(t)], cent[:], start=True, stop=True)
                mm.then_inc(scored, 1)
                pe.wait_ge(ones_ready, 1)
                for e in range(E3):
                    for i in range(2 * DIGITS):
                        pe.wait_ge(part_ready, 2 * DIGITS * e + i + 1)
                        pe.matmul(ps_c[:, 0, 0:CAND], ones[:], part[:], start=True, stop=True).then_inc(counted, 1)
                    pe.wait_ge(masks_ready, e + 1)
                    m = masks[:].rearrange("p a t -> p (a t)")
                    pe.matmul(ps_c[:, 1, 0:2 * NT], ones[:], m, start=True, stop=True)
                    pe.matmul(ps_c[:, 1, 2 * NT:3 * NT], not_yet[:], masks[:, 0, :], start=True, stop=True)\
                      .then_inc(masks_counted, 1)
                pe.wait_ge(members_ready, 1)
                m = member16[:].rearrange("p e t -> p (e t)")
                pe.matmul(ps_s[:, 0:E3 * NT], before[:], m, start=True, stop=True)
                pe.matmul(ps_s[:, E3 * NT:2 * E3 * NT], ones[:], m, start=True, stop=True).then_inc(ranked, 1)

            @block.vector
            def _(dve):
                link = Chain(dve, chain)

                def search(e, half, keys, lowest):
                    result = threshold[:, half:half + 1]
                    step = 2 ** (16 - DIGIT)
                    link.mark(dve.memset(result, lowest))
                    link(dve.tensor_scalar(cands[:], multiples[:], float(step), lowest, ALU.mult, ALU.add))
                    for i in range(DIGITS):
                        link(dve.tensor_tensor(reach[:], bcast(keys.unsqueeze(1), P, CAND, NT),
                                               bcast(cands[:, 0, :].unsqueeze(2), P, CAND, NT), ALU.is_ge))
                        with nc.allow_low_precision(reason="counts up to 16 are exact in bfloat16"):
                            dve.tensor_reduce(part[:], reach[:], AX_X, ALU.add).then_inc(part_ready, 1)
                        smaller = step >> DIGIT
                        if i + 1 < DIGITS:
                            link(dve.scalar_tensor_tensor(cands[:], multiples[:], float(smaller - step), cands[:],
                                                          ALU.mult, ALU.add))
                        dve.wait_ge(counted, 2 * DIGITS * e + DIGITS * half + i + 1)
                        link(dve.tensor_scalar(enough[:], ps_c[:, 0, 0:CAND], float(CAP), 0.0, ALU.is_ge, ALU.add,
                                               accum_out=digit[:]))
                        link.mark(dve.scalar_tensor_tensor(result, digit[:], float(step), result, ALU.mult, ALU.add))
                        if i + 1 < DIGITS:
                            link.mark(dve.scalar_tensor_tensor(cands[:, 0, :], bcast(digit[:], P, CAND), float(step),
                                                               cands[:, 0, :], ALU.mult, ALU.add))
                        link.wait()
                        step = smaller

                link.mark(dve.memset(ones_row[:], 1.0))
                link.mark(dve.memset(left[:], 0.0))
                dve.memset(ones[:], 1.0).then_inc(ones_ready, 1)
                dve.wait_ge(scored, 1)
                link(dve.tensor_copy(scores[:], ps_s[:, 0:E3 * NT].rearrange("p (t e) -> p e t", e=E3)))
                bits = scores[:].bitcast(I32)
                link(dve.tensor_scalar(flip[:], bits, 31, 2 ** 31 - 1, ALU.arith_shift_right, ALU.bitwise_and))
                link(dve.tensor_tensor(flip[:], flip[:], bits, ALU.bitwise_xor))
                link.mark(dve.tensor_scalar(half_int[:, 0], flip[:], 16, None, ALU.arith_shift_right))
                link(dve.tensor_scalar(half_int[:, 1], flip[:], 2 ** 16 - 1, None, ALU.bitwise_and))
                link.mark(dve.tensor_copy(high[:], half_int[:, 0]))
                link(dve.tensor_scalar(low1[:], half_int[:, 1], 1.0, None, ALU.add))
                dve.wait_ge(loaded, 16 * 5)
                for e in range(E3):
                    link(dve.tensor_tensor(h[:], high[:, e, :], left[:], ALU.add))
                    search(e, 0, h[:], -2.0 ** 15)
                    t_high, t_low = threshold[:, 0:1], threshold[:, 1:2]
                    link.mark(dve.scalar_tensor_tensor(key[:], h[:], t_high, low1[:, e, :], ALU.is_equal, ALU.mult))
                    link(dve.tensor_scalar(above[:], h[:], t_high, 2.0 ** 17, ALU.is_gt, ALU.mult))
                    link(dve.tensor_tensor(key[:], key[:], above[:], ALU.add))
                    search(e, 1, key[:], 1.0)
                    link.mark(dve.tensor_scalar(eq[:], key[:], t_low, None, ALU.is_equal))
                    link.mark(dve.tensor_scalar(masks[:, 0, :], key[:], t_low, None, ALU.is_equal))
                    dve.tensor_scalar(masks[:, 1, :], key[:], t_low, None, ALU.is_gt).then_inc(masks_ready, 1)
                    dve.wait_ge(masks_counted, e + 1)
                    equal, more, upto_here = (ps_c[:, 1, i * NT:(i + 1) * NT] for i in range(3))
                    link(dve.tensor_reduce(greater[:], more, AX_X, ALU.add))
                    link(dve.tensor_tensor_scan(upto[:], ones_row[:], equal, greater[:], ALU.mult, ALU.add))
                    link(dve.tensor_tensor(upto[:], upto[:], upto_here, ALU.add))
                    link(dve.scalar_tensor_tensor(eq[:], upto[:], float(CAP), eq[:], ALU.is_lt, ALU.mult))
                    link(dve.scalar_tensor_tensor(member[:, e, :], key[:], t_low, eq[:], ALU.is_gt, ALU.add))
                    link(dve.scalar_tensor_tensor(left[:], member[:, e, :], TAKEN, left[:], ALU.mult, ALU.add))
                dve.tensor_copy(member16[:], member[:]).then_inc(members_ready, 1)
                dve.wait_ge(ranked, 1)
                within = ps_s[:, 0:E3 * NT].rearrange("p (e t) -> p e t", e=E3)
                totals = ps_s[:, E3 * NT:2 * E3 * NT].rearrange("p (e t) -> p e t", e=E3)
                for e in range(E3):
                    link.mark(dve.tensor_tensor_scan(rank[:, e, :], ones_row[:], totals[:, e, :], 0.0, ALU.mult,
                                                     ALU.add))
                link.wait()
                link(dve.tensor_tensor(rank[:], rank[:], totals, ALU.subtract))
                link(dve.tensor_tensor(rank[:], rank[:], within, ALU.add))
                link(dve.tensor_tensor(rank[:], rank[:], base[:], ALU.add))
                link(dve.tensor_tensor(rank[:], rank[:], member[:], ALU.mult))
                link(dve.tensor_reduce(slot_f[:], rank[:].rearrange("p e t -> p t e"), AX_X, ALU.add))
                link(dve.tensor_copy(slot[:], slot_f[:]))


def stage_l3_mlp(nc, d, g, n_tm, h_tm, slot, sorted_in, sorted_out):
    with Stage(nc, "l3mlp") as st:
        w1 = st.sb("w1", [P, E3, F3])
        w2 = st.sb("w2", [P, E3, 4, P])
        b1 = st.sb("b1", [P, E3, 4])
        b2 = st.sb("b2", [1, E3, P])
        ones = st.sb("ones", [1, P])
        rows = st.sb("rows", [P, NT, P])
        rowsT = st.sb("rowsT", [P, S])
        hid = st.sb("hid", [P, 2, 4, CAP])
        y = st.sb("y", [P, NT, P])
        back = st.sb("back", [P, NT, P])
        ps_t = st.ps("ps_t", [P, 2, BANK])
        ps_h = st.ps("ps_h", [P, 4, BANK])
        ps_y = st.ps("ps_y", [P, 2, BANK])
        loaded = st.sem("loaded")
        ones_ready = st.sem("ones_ready")
        scattered = st.sem("scattered")
        rows_loaded = st.sem("rows_loaded")
        turned = st.sem("turned")
        rows_ready = st.sem("rows_ready")
        hid_done = st.sem("hid_done")
        hid_ready = st.sem("hid_ready")
        y_done = st.sem("y_done")
        y_copied = st.sem("y_copied")
        y_stored = st.sem("y_stored")
        gathered = st.sem("gathered")
        chain = st.sem("chain")
        with st.block() as block:

            @block.sync
            def _(sp):
                for dst, name in ((w1, "l3_w1"), (w2, "l3_w2"), (b1, "l3_b1"), (b2, "l3_b2")):
                    sp.dma_start(dst[:], d[name]).then_inc(loaded, 16)
                sp.wait_ge(scattered, 16 * NT)
                sp.dma_start(rows[:], sorted_in.rearrange("(t p) f -> p t f", p=P)).then_inc(rows_loaded, 16)
                sp.wait_ge(y_copied, E3)
                sp.dma_start(sorted_out.rearrange("(t p) f -> p t f", p=P), y[:]).then_inc(y_stored, 16)
                sp.wait_ge(y_stored, 16)

            @block.gpsimd
            def _(pool):
                for t in range(NT):
                    pool.indirect_dma_start(out=sorted_in, out_offset=bass.IndirectOffsetOnAxis(
                        ap=slot[:, t:t + 1], axis=0), in_=n_tm[:, t, :], in_offset=None).then_inc(scattered, 16)
                pool.wait_ge(y_stored, 16)
                for t in range(NT):
                    pool.indirect_dma_start(out=back[:, t, :], out_offset=None, in_=sorted_out,
                                            in_offset=bass.IndirectOffsetOnAxis(ap=slot[:, t:t + 1], axis=0))\
                        .then_inc(gathered, 16)
                pool.wait_ge(gathered, 16 * NT)

            @block.tensor
            def _(pe):
                pe.wait_ge(rows_loaded, 16)
                for j in range(NC4):
                    if j >= 2:
                        pe.wait_ge(rows_ready, j - 1)
                    for i in range(4):
                        mm = pe.transpose(ps_t[:, j % 2, c1(i)], rows[:, 4 * j + i, :], g.ident[:])
                    mm.then_inc(turned, 1)
                pe.wait_ge(loaded, 64)
                pe.wait_ge(ones_ready, 1)

                def down(e):
                    pe.wait_ge(hid_ready, 4 * (e + 1))
                    if e >= 2:
                        pe.wait_ge(y_copied, e - 1)
                    for i in range(2):
                        dst = ps_y[:, e % 2, c1(i)]
                        for f in range(4):
                            pe.matmul(dst, hid[:, e % 2, f, c1(i)], w2[:, e, f, :], start=(f == 0), stop=False,
                                      skip_group_check=True)
                        mm = pe.matmul(dst, ones[:], b2[:, e, :], start=False, stop=True, skip_group_check=True)
                    mm.then_inc(y_done, 1)

                for e in range(E3):
                    pe.wait_ge(rows_ready, e // 2 + 1)
                    if e >= 2:
                        pe.wait_ge(hid_ready, 4 * (e - 1))
                    for f in range(4):
                        pe.matmul(ps_h[:, 2 * (e % 2) + f // 2, CAP * (f % 2):CAP * (f % 2) + CAP], w1[:, e, c1(f)],
                                  rowsT[:, CAP * e:CAP * (e + 1)], start=True, stop=True).then_inc(hid_done, 1)
                    if e >= 1:
                        down(e - 1)
                down(E3 - 1)

            @block.scalar
            def _(act):
                for j in range(NC4):
                    act.wait_ge(turned, j + 1)
                    act.activation(rowsT[:, c4(j)], ps_t[:, j % 2, :], ACT.Identity).then_inc(rows_ready, 1)
                act.wait_ge(loaded, 64)
                for e in range(E3):
                    if e >= 2:
                        act.wait_ge(y_done, e - 1)
                    for f in range(4):
                        act.wait_ge(hid_done, 4 * e + 2 * (f // 2) + 2)
                        act.activation(hid[:, e % 2, f, :],
                                       ps_h[:, 2 * (e % 2) + f // 2, CAP * (f % 2):CAP * (f % 2) + CAP],
                                       ACT.Gelu_apprx_tanh, bias=b1[:, e, f:f + 1]).then_inc(hid_ready, 1)

            @block.vector
            def _(dve):
                link = Chain(dve, chain)
                dve.memset(ones[:], 1.0).then_inc(ones_ready, 1)
                gate = bcast(mod_row(g, 3, GATE_B).unsqueeze(1), P, NT, P)
                for e in range(E3):
                    dve.wait_ge(y_done, e + 1)
                    dve.tensor_copy(y[:, 2 * e:2 * e + 2, :].rearrange("p t f -> p (t f)"), ps_y[:, e % 2, 0:2 * P])\
                       .then_inc(y_copied, 1)
                dve.wait_ge(gathered, 16 * NT)
                link(dve.tensor_tensor(back[:], back[:], h_tm[:], ALU.add))
                link(dve.tensor_tensor(back[:], back[:], gate, ALU.mult))
                dve.tensor_tensor(g.x[:], g.x[:], back[:], ALU.add)


def stage_affine(nc, g, name, jobs):
    with Stage(nc, name) as st:
        done = st.sem("done")
        with st.block() as block:

            @block.gpsimd
            def _(pool):
                n = 0
                for out, in_, scale_row, shift_row in jobs:
                    pool.tensor_tensor(out[:], in_[:], bcast(scale_row.unsqueeze(1), P, NT, P), ALU.mult)\
                        .then_inc(done, 1)
                    n += 1
                    pool.wait_ge(done, n)
                    pool.tensor_tensor(out[:], out[:], bcast(shift_row.unsqueeze(1), P, NT, P), ALU.add)\
                        .then_inc(done, 1)
                    n += 1
                pool.wait_ge(done, n)


def layer3_experts(nc, d, g):
    adaln(nc, g, 3, SCALE_B, SHIFT_B)
    sorted_in = nc.dram_tensor("sorted_in", [S, P], F32, kind="Internal").ap()
    sorted_out = nc.dram_tensor("sorted_out", [S, P], F32, kind="Internal").ap()
    with Stage(nc, "l3f") as st:
        h_tm = st.sb("h_tm", [P, NT, P])
        n_tm = st.sb("n_tm", [P, NT, P])
        slot = st.sb("slot", [P, NT], I32)
        ln_cols = st.sb("ln_cols", [P, 2])
        ln_rows = st.sb("ln_rows", [P, 2, P])
        ln_loaded = st.sem("ln_loaded")
        nc.sync.dma_start(ln_cols[:], d["l3_lncols"]).then_inc(ln_loaded, 16)
        nc.sync.dma_start(ln_rows[:], d["l3_lnrows"]).then_inc(ln_loaded, 16)
        nc.scalar.wait_ge(ln_loaded, 32)
        nc.gpsimd.wait_ge(ln_loaded, 32)
        stage_affine(nc, g, "l3h", [(h_tm, g.xn, mod_row(g, 3, SCALE_B), mod_row(g, 3, SHIFT_B))])
        stage_norm(nc, g, "l3norm", h_tm, n_tm, g.hT, ln_cols[:, 0:1], ln_cols[:, 1:2])
        stage_l3_select(nc, d, g, g.hT, slot)
        stage_affine(nc, g, "l3n", [(n_tm, n_tm, ln_rows[:, 0, :], ln_rows[:, 1, :])])
        stage_l3_mlp(nc, d, g, n_tm, h_tm, slot, sorted_in, sorted_out)



class Persistent:
    pass


def program(nc, d, out, stages=None):
    with ExitStack() as ctx:
        g = Persistent()

        def sb(name, shape, dt=F32):
            return ctx.enter_context(nc.sbuf_tensor(name, shape, dt))

        d = {name: ap.bitcast(BF16) if name in BF16_CONSTANTS else ap for name, ap in d.items()}
        g.x = sb("x_res", [P, NT, P])
        g.xn = sb("xn", [P, NT, P])
        g.hT = sb("hT", [P, S])
        g.mod_rows = sb("mod_rows", [P, 4, 6, P])
        g.mod_cols = sb("mod_cols", [P, 24])
        g.ident = sb("ident_sb", [P, P])
        stage_setup(nc, d, g)
        for layer_part in (stages or ALL_STAGES):
            with nc.cleanup_on_exit():
                layer_part(nc, d, g)
        stage_store(nc, g, out)


def stage_store(nc, g, out):
    with Stage(nc, "store") as st:
        stored = st.sem("stored")
        with st.block() as block:

            @block.sync
            def _(sp):
                sp.dma_start(out.rearrange("a (t p) f -> p (a t) f", p=P), g.x[:]).then_inc(stored, 16)
                sp.wait_ge(stored, 16)


ALL_STAGES = [layer0_attention, layer0_slots, layer1_delta, layer1_experts,
              layer2_spiking, layer2_product, layer3_attention, layer3_experts]


BF16_CONSTANTS = ("ident16", "lat_causal", "mask_q", "mask_k", "before", "not_yet")


def lay_out(inp):

    def bits16(constant):
        return (constant.astype(np.float32).view(np.uint32) >> 16).astype(np.uint16)

    a = {k: np.asarray(v) for k, v in inp.items()}
    heads = lambda w: w.transpose(1, 0, 2).reshape(P, P)
    d = {
        "x": a["L0_attn_q"][0],
        "c_cols": np.concatenate([a[f"L{l}_c"] for l in range(4)], 0).T,
        "wmod": np.stack([a[f"L{l}_wmod"] for l in range(4)], 1),
        "ident": np.eye(P, dtype=np.float32),
        "ident16": bits16(np.eye(P)),
        "l0_wqkv": np.stack([heads(a[f"L0_attn_W_{n}"]) for n in ("query", "key", "val")], 1),
        "l0_wout": a["L0_attn_W_out"].reshape(P, P),
    }
    w1T = a["L0_ffn_w1"].T
    d.update({
        "l0_b1": a["L0_ffn_b1"][:, None], "l0_w1T": np.stack([w1T[:P], w1T[P:]], 1),
        "l0_w2T": np.concatenate([a["L0_ffn_w2"].T, a["L0_ffn_b2"][None]], 0),
        "l0_tau": np.repeat(a["L0_ffn_tau"][None], P, 0),
        "l0_slots": a["L0_ffn_slot_init"], "l0_slot_scale": a["L0_ffn_slot_scale"],
        "l0_wihT": a["L0_ffn_gru_wih"].T.reshape(P, 3, P), "l0_whhT": a["L0_ffn_gru_whh"].T.reshape(P, 3, P),
        "l0_bih": a["L0_ffn_gru_bih"][None], "l0_bhh": a["L0_ffn_gru_bhh"][None],
        "l0_wvT": a["L0_ffn_wv"].T, "l0_bv": a["L0_ffn_bv"][:, None], "l0_woT": a["L0_ffn_wo"].T,
        "l0_bo": a["L0_ffn_bo"][None],
    })
    i, j = np.arange(P)[:, None], np.arange(P)[None, :]
    level = lambda s: (i // (2 * s) == j // (2 * s)) & (i // s % 2 == 1) & (j // s % 2 == 0)
    rows = lambda v: np.repeat(v[None], P, 0)
    d.update({
        "masks": np.stack([level(s) for s in (1,) + LEVELS] + [j >= i], 1).astype(np.float32),
        "iota": i.astype(np.float32), "iota_row": rows(np.arange(EXPERTS, dtype=np.float32)),
        "carry": np.broadcast_to((np.arange(NT) > 0).astype(np.float32), (P, EXPERTS, NT)),
        "l1_wq": a["L1_attn_Wq"],
        "l1_wkvb": np.concatenate([a["L1_attn_Wk"], a["L1_attn_Wv"], a["L1_attn_Wb"][:, None]], 1),
        "l1_lng": rows(a["L1_attn_ln_g"]), "l1_lnb": rows(a["L1_attn_ln_b"]),
        "l1_gateT": a["L1_ffn_gate_w"].T, "l1_gate_b": a["L1_ffn_gate_b"][None],
        "l1_expert_w": a["L1_ffn_expert_w"], "l1_expert_b": a["L1_ffn_expert_b"],
    })
    d.update({
        "l2_wrkvo": np.stack([a[f"L2_attn_W{n}"].T for n in "rkvo"], 1),
        "l2_w1T": a["L2_attn_W1"].T.reshape(P, 4, P), "l2_b1": a["L2_attn_b1"].reshape(4, P).T,
        "l2_w2T": a["L2_attn_W2"].T.reshape(4, P, P).transpose(1, 0, 2), "l2_b2": a["L2_attn_b2"][:, None],
        "l2_ln1g": rows(a["L2_attn_ln1_g"]), "l2_ln1b": rows(a["L2_attn_ln1_b"]),
        "l2_ln1cols": np.stack([a["L2_attn_ln1_g"], a["L2_attn_ln1_b"]], 1),
        "l2_ln2g": rows(a["L2_attn_ln2_g"]), "l2_ln2b": rows(a["L2_attn_ln2_b"]),
        "l2_CBT": a["L2_ffn_CB"].T, "l2_SCB": rows(a["L2_ffn_SCB"]), "l2_bias": rows(a["L2_ffn_bias"]),
    })
    neg = lambda seen: bits16(np.where(seen, 0.0, MASK_BIG))
    c = np.arange(SPAN)[None, :]
    seen_q = (c > i) & (c <= i + WINDOW)
    seen_k = (c >= i) & (c < i + WINDOW)
    tokens = i + P * np.arange(NT)[None, :]
    d.update({
        "l3_wqkv": np.stack([a[f"L3_attn_w{n}"] for n in "qkv"], 1),
        "l3_wg": np.stack([a[f"L3_attn_wg{n}"] for n in "qkv"], 1),
        "l3_r_out": a["L3_attn_r_out_w"], "l3_wout": a["L3_attn_w_out"],
        "l3_gates": np.stack([a["L3_attn_gate_local_w"].reshape(P), a["L3_attn_gate_remote_w"].reshape(P)], 1),
        "head_rows": (i // L3_K == np.arange(L3_H)[None, :]).astype(np.float32),
        "lat_causal": neg(np.arange(LATENTS)[None, None, :] <= tokens[:, :, None] // (S // LATENTS)),
        "mask_q": neg(np.stack([seen_q & (c >= WINDOW), seen_q], 1)[:, :, None, :]),
        "mask_k": neg(seen_k[:, None, :]),
        "l3_centT": a["L3_ffn_centroids"].T,
        "l3_lncols": np.stack([a["L3_ffn_ln_g"], a["L3_ffn_ln_b"]], 1),
        "l3_lnrows": np.stack([rows(a["L3_ffn_ln_g"]), rows(a["L3_ffn_ln_b"])], 1),
        "l3_w1": a["L3_ffn_w1"].transpose(1, 0, 2),
        "l3_w2": a["L3_ffn_w2"].reshape(E3, 4, P, P).transpose(2, 0, 1, 3),
        "l3_b1": a["L3_ffn_b1"].reshape(E3, 4, P).transpose(2, 0, 1), "l3_b2": a["L3_ffn_b2"][None],
        "before": bits16(i < j),
        "bases": np.broadcast_to((CAP * np.arange(E3, dtype=np.float32))[None, :, None], (P, E3, NT)),
        "multiples": rows(np.arange(1, CAND + 1, dtype=np.float32)[None]),
        "not_yet": bits16(-1.0 * (i >= j)),
    })
    return {k: np.ascontiguousarray(v) for k, v in d.items()}


OUT_SHAPE = (1, S, P)


def kernel(**inputs):
    import concourse.bacc as _bacc
    from concourse.bass_utils import run_bass_kernel_spmd as _run

    nc = _bacc.Bacc("TRN2", target_bir_lowering=False, num_devices=1)
    arrays, d = {}, {}
    for name, a in lay_out(inputs).items():
        arrays[f"in_{name}_dram"] = a
        d[name] = nc.dram_tensor(f"in_{name}_dram", a.shape, mybir.dt.from_np(a.dtype), kind="ExternalInput").ap()
    out = nc.dram_tensor("out_0_dram", OUT_SHAPE, F32, kind="ExternalOutput").ap()
    program(nc, d, out)
    r = _run(nc, [arrays], core_ids=[0])
    return r.results[0]["out_0_dram"]
```

```python
from contextlib import ExitStack

import numpy as np

import concourse.bass as bass
from concourse import mybir

F32 = mybir.dt.float32
BF16 = mybir.dt.bfloat16
I32 = mybir.dt.int32
U32 = mybir.dt.uint32
ALU = mybir.AluOpType
ACT = mybir.ActivationFunctionType
AX_X = mybir.AxisListType.X

P = 128
S = 2048
NT = S // P
BANK = 512
NC4 = S // BANK
LN_EPS = 1e-5
SHIFT_A, SCALE_A, GATE_A, SHIFT_B, SCALE_B, GATE_B = range(6)


class Chain:

    def __init__(self, eng, sem):
        self.eng, self.sem, self.n = eng, sem, 0

    def mark(self, ins):
        self.n += 1
        return ins.then_inc(self.sem, 1)

    def wait(self):
        self.eng.wait_ge(self.sem, self.n)

    def __call__(self, ins):
        self.mark(ins)
        self.wait()


class Stage:

    def __init__(self, nc, name):
        self.nc, self.name, self.ctx = nc, name, ExitStack()

    def __enter__(self):
        self.ctx.__enter__()
        return self

    def __exit__(self, *e):
        return self.ctx.__exit__(*e)

    def sb(self, name, shape, dt=F32):
        return self.ctx.enter_context(self.nc.sbuf_tensor(f"{self.name}_{name}", shape, dt))

    def ps(self, name, shape, dt=F32):
        return self.ctx.enter_context(self.nc.psum_tensor(f"{self.name}_{name}", shape, dt))

    def sem(self, name):
        return self.nc.alloc_semaphore(f"{self.name}_{name}")

    def block(self):
        return self.nc.Block(no_gpsimd_drain=True)


class Loads:

    def __init__(self, nc, d, st, stage, *names):
        self.done, self.all = st.sem(f"{stage}_loaded"), 16 * len(names)
        self.tiles = {}
        for name in names:
            dt = BF16 if name in BF16_CONSTANTS else F32
            self.tiles[name] = st.sb(f"{stage}_{name}", list(d[name].shape), dt)
            nc.sync.dma_start(self.tiles[name][:], d[name]).then_inc(self.done, 16)

    def __getitem__(self, name):
        return self.tiles[name]


def bcast(ap, *shape):
    return ap.broadcast_to(list(shape))


def c4(j):
    return slice(j * BANK, (j + 1) * BANK)


def c1(t):
    return slice(t * P, (t + 1) * P)



def stage_setup(nc, d, g):
    with Stage(nc, "setup") as st:
        wmod = st.sb("wmod", [P, 4, 6 * P])
        c_cols = st.sb("c_cols", [P, 4])
        sig = st.sb("sig", [P, 4])
        silu = st.sb("silu", [P, 4])
        silu_rep = st.sb("silu_rep", [P, 4, P])
        ones = st.sb("ones", [P, P])
        ps = st.ps("ps", [P, 7, BANK])
        ps_c = st.ps("ps_c", [P, BANK])
        c_loaded = st.sem("c_loaded")
        wmod_loaded = [st.sem(f"wmod_loaded{l}") for l in range(4)]
        x_loaded = st.sem("x_loaded")
        sig_done = st.sem("sig_done")
        rep_done = st.sem("rep_done")
        rows_done = st.sem("rows_done")
        rows_copied = st.sem("rows_copied")
        cols_done = st.sem("cols_done")
        chain = st.sem("chain")
        with st.block() as block:

            @block.sync
            def _(sp):
                sp.dma_start(c_cols[:], d["c_cols"]).then_inc(c_loaded, 16)
                for l in range(4):
                    sp.dma_start(wmod[:, l, :], d["wmod"][:, l, :]).then_inc(wmod_loaded[l], 16)

            @block.scalar
            def _(act):
                act.dma_start(g.x[:], d["x"].rearrange("(t p) f -> p t f", p=P)).then_inc(x_loaded, 16)
                act.dma_start(g.ident[:], d["ident"]).then_inc(x_loaded, 16)
                act.wait_ge(c_loaded, 16)
                act.activation(sig[:], c_cols[:], ACT.Sigmoid).then_inc(sig_done, 1)
                act.wait_ge(x_loaded, 32)

            @block.tensor
            def _(pe):
                pe.wait_ge(rep_done, 1)
                for l in range(4):
                    pe.wait_ge(wmod_loaded[l], 16)
                    for j in range(6):
                        mm = pe.matmul(ps_c[:, 6 * l + j:6 * l + j + 1], wmod[:, l, c1(j)],
                                       silu[:, l:l + 1], start=True, stop=True)
                    if l == 3:
                        mm.then_inc(cols_done, 1)
                    for half in range(2):
                        if 2 * l + half == 7:
                            pe.wait_ge(rows_copied, 1)
                        mm = pe.matmul(ps[:, (2 * l + half) % 7, 0:384], silu_rep[:, l, :],
                                       wmod[:, l, 384 * half:384 * half + 384], start=True, stop=True)
                        mm.then_inc(rows_done, 1)

            @block.vector
            def _(dve):
                link = Chain(dve, chain)
                link(dve.memset(ones[:], 1.0))
                dve.wait_ge(sig_done, 1)
                link(dve.tensor_tensor(silu[:], sig[:], c_cols[:], ALU.mult))
                for l in range(4):
                    ins = dve.tensor_scalar(silu_rep[:, l, :], ones[:], silu[:, l:l + 1], None, ALU.mult)
                ins.then_inc(rep_done, 1)
                for n in range(8):
                    dve.wait_ge(rows_done, n + 1)
                    rows = g.mod_rows[:, n // 2, 3 * (n % 2):3 * (n % 2) + 3, :]
                    dve.tensor_copy(rows, ps[:, n % 7, 0:384].rearrange("p (j f) -> p j f", j=3))\
                       .then_inc(rows_copied, 1)
                dve.wait_ge(cols_done, 1)
                link(dve.tensor_copy(g.mod_cols[:], ps_c[:, 0:24]))
                cols = g.mod_cols[:].rearrange("p (l j) -> p l j", l=4)
                for scale in (SCALE_A, SCALE_B):
                    link.mark(dve.tensor_scalar(cols[:, :, scale], cols[:, :, scale], 1.0, None, ALU.add))


class RowsFinish:

    def __init__(self, st, layer):
        self.layer = layer
        self.floor = st.sb("gate_floor", [P, 2, P])
        self.sign = st.sb("gate_sign", [P, 2, P])
        self.step = st.sem("rows_finish")

    def __call__(self, pool, g):
        link = Chain(pool, self.step)
        rows = g.mod_rows[:, self.layer].rearrange("p (k j) f -> p k j f", k=2)
        gates, floor, sign = rows[:, :, GATE_A, :], self.floor[:], self.sign[:]
        link.mark(pool.tensor_scalar(rows[:, :, SCALE_A, :], rows[:, :, SCALE_A, :], 1.0, None, ALU.add))
        link(pool.tensor_scalar(sign, gates, 0.0, 2.0, ALU.is_ge, ALU.mult))
        link(pool.tensor_scalar(sign, sign, -1.0, None, ALU.add))
        link(pool.tensor_tensor(floor, gates, sign, ALU.mult))
        link(pool.tensor_scalar(floor, floor, 0.25, None, ALU.max))
        link(pool.tensor_tensor(gates, floor, sign, ALU.mult))



def stage_norm(nc, g, name, src, normed, turned=None, scale_col=None, shift_col=None, beside=None):
    with Stage(nc, name) as st:
        stats = st.sb("stats", [P, NT, 6])
        mv = st.sb("mv", [P, NT, 2])
        var = st.sb("var", [P, NT])
        std = st.sb("std", [P, NT])
        rstd = st.sb("rstd", [P, NT])
        corr = st.sb("corr", [P, NT])
        ps = st.ps("ps", [P, 4, BANK])
        var_ready = st.sem("var_ready")
        std_ready = st.sem("std_ready")
        tile_normed = st.sem("tile_normed")
        bank_full = st.sem("bank_full")
        chain = st.sem("chain")
        with st.block() as block:

            @block.gpsimd
            def _(pool):
                if beside is not None:
                    beside(pool, g)

            @block.vector
            def _(dve):
                link = Chain(dve, chain)
                for t in range(NT):
                    link.mark(dve.bn_stats(stats[:, t, :], src[:, t, :]))
                link.wait()
                for t in range(NT):
                    link.mark(dve.bn_aggr(mv[:, t, :], stats[:, t, :]))
                link.wait()
                dve.tensor_scalar(var[:], mv[:, :, 1], LN_EPS, None, ALU.add).then_inc(var_ready, 1)
                dve.wait_ge(std_ready, 1)
                link(dve.reciprocal(rstd[:], std[:]))
                link(dve.tensor_tensor(corr[:], rstd[:], rstd[:], ALU.mult))
                link(dve.tensor_tensor(corr[:], corr[:], var[:], ALU.mult))
                link(dve.tensor_scalar(corr[:], corr[:], -0.5, 1.5, ALU.mult, ALU.add))
                link(dve.tensor_tensor(rstd[:], rstd[:], corr[:], ALU.mult))
                for t in range(NT):
                    dve.tensor_scalar(normed[:, t, :], src[:, t, :], mv[:, t, 0:1], rstd[:, t:t + 1],
                                      ALU.subtract, ALU.mult).then_inc(tile_normed, 1)

            @block.tensor
            def _(pe):
                for t in range(NT if turned is not None else 0):
                    pe.wait_ge(tile_normed, t + 1)
                    mm = pe.transpose(ps[:, t // 4, c1(t % 4)], normed[:, t, :], g.ident[:])
                    if t % 4 == 3:
                        mm.then_inc(bank_full, 1)

            @block.scalar
            def _(act):
                act.wait_ge(var_ready, 1)
                act.activation(std[:], var[:], ACT.Sqrt).then_inc(std_ready, 1)
                for j in range(NC4 if turned is not None else 0):
                    act.wait_ge(bank_full, j + 1)
                    act.activation(turned[:, c4(j)], ps[:, j, :], ACT.Identity, bias=shift_col, scale=scale_col)


def mod_col(g, layer, which):
    return g.mod_cols[:, 6 * layer + which:6 * layer + which + 1]


def mod_row(g, layer, which):
    return g.mod_rows[:, layer, which, :]


def adaln(nc, g, layer, scale, shift, also=None):
    with Stage(nc, f"rows{layer}{scale}") as st:
        tasks = [RowsFinish(st, layer)] if layer not in g.rows_finished else []
        if also is not None:
            tasks.append(also)
        g.rows_finished.add(layer)

        def beside(pool, g):
            for task in tasks:
                task(pool, g)

        stage_norm(nc, g, f"ada{layer}{scale}", g.x, g.xn, g.hT, mod_col(g, layer, scale), mod_col(g, layer, shift),
                   beside)



L0_H, L0_K = 16, 8
GROUP = 4
SPLITS_Q = (0, 0, 1, 0, 1, 2)
SPLITS_K = (0, 1, 0, 2, 1, 0)
HEAD_BUFS = 3
MAX_ROW = 64
MASK_BIG = -1e30
LOWEST = float(np.finfo(np.float32).min)


def splits_of(link, dve, parts, rest, full, done):
    link(dve.tensor_copy(parts[0], full))
    rest_parts(link, dve, parts, rest, full, done)


def rest_parts(link, eng, parts, rest, full, done):
    link(eng.tensor_tensor(rest, full, parts[0], ALU.subtract))
    link(eng.tensor_copy(parts[1], rest))
    eng.tensor_tensor(parts[2], rest, parts[1], ALU.subtract).then_inc(done, 1)


class ClearOperand:

    def __init__(self, st, operand):
        self.operand, self.cleared = operand, st.sem("operand_cleared")

    def __call__(self, pool, g):
        pool.memset(self.operand[:].bitcast(F32), 0.0).then_inc(self.cleared, 1)
        pool.wait_ge(self.cleared, 1)


def stage_project_parts(nc, loads, w_name, g, name, V_aug, q, qp, kp, K, ones_rows, drams=(), stored=None):
    POOL_COLS = slice(1280, S)
    with Stage(nc, name) as st:
        w = loads[w_name]
        k = st.sb("k", [P, S])
        rest = st.sb("rest", [P, S])
        pool_rest = st.sb("pool_rest", [P, POOL_COLS.stop - POOL_COLS.start])
        ps = st.ps("ps", [P, 8, BANK])
        chunk_done = st.sem("chunk_done")
        chunk_read = st.sem("chunk_read")
        v_done = st.sem("v_done")
        v_filled = st.sem("v_filled")
        pool_parts_done = st.sem("pool_parts_done")
        pool_chain = st.sem("pool_chain")
        parts_done = st.sem("parts_done")
        cleared = st.sem("cleared")
        ones_placed = st.sem("ones_placed")
        chain = st.sem("chain")
        with st.block() as block:

            @block.sync
            def _(sp):
                sp.wait_ge(cleared, 1)
                sp.dma_start(K[MAX_ROW:MAX_ROW + 3], ones_rows).then_inc(ones_placed, 16)
                sp.wait_ge(ones_placed, 16)
                for n, (parts, dram) in enumerate(zip((qp, kp), drams)):
                    sp.wait_ge(parts_done, n + 1)
                    if n == 1:
                        sp.wait_ge(pool_parts_done, 1)
                    for i in range(3):
                        sp.dma_start(dram[i], parts[i][:]).then_inc(stored, 16)

            @block.tensor
            def _(pe):
                pe.wait_ge(loads.done, loads.all)
                for m in range(2):
                    for j in range(NC4):
                        pe.matmul(ps[:, 4 * m + j, :], w[:, m, :], g.hT[:, c4(j)], start=True,
                                  stop=True).then_inc(chunk_done, 1)
                for t in range(NT):
                    if t % 4 == 0:
                        pe.wait_ge(chunk_read, t // 4 + 1)
                    mm = pe.matmul(ps[:, t // 4, c1(t % 4)], g.hT[:, c1(t)], w[:, 2, :], start=True, stop=True)
                    if t % 4 == 3:
                        mm.then_inc(v_done, 1)

            @block.scalar
            def _(act):
                for n in range(2 * NC4):
                    act.wait_ge(chunk_done, n + 1)
                    for dst in (q, qp[0]) if n < NC4 else (k, kp[0]):
                        ins = act.activation(dst[:, c4(n % NC4)], ps[:, n, :], ACT.Identity,
                                             scale=L0_K ** -0.5 if n < NC4 else 1.0)
                    ins.then_inc(chunk_read, 1)
                for j in range(NC4):
                    act.wait_ge(v_done, j + 1)
                    for t in range(4):
                        act.activation(V_aug[:, 4 * j + t, :, 0:L0_K],
                                       ps[:, j, c1(t)].rearrange("p (h k) -> p h k", h=L0_H), ACT.Identity)

            @block.vector
            def _(dve):
                link = Chain(dve, chain)
                dve.memset(K[:].bitcast(F32), 0.0).then_inc(cleared, 1)
                for n, (parts, full, cols) in enumerate(((qp, q, slice(0, S)), (kp, k, slice(0, POOL_COLS.start)))):
                    dve.wait_ge(chunk_read, NC4 * (n + 1))
                    rest_parts(link, dve, [p[:, cols] for p in parts], rest[:, cols], full[:, cols], parts_done)
                    dve.wait_ge(parts_done, n + 1)

            @block.gpsimd
            def _(pool):
                pool.memset(V_aug[:, :, :, L0_K + 1:], 0.0).then_inc(v_filled, 1)
                pool.memset(V_aug[:, :, :, L0_K:L0_K + 1], 1.0).then_inc(v_filled, 1)
                pool.wait_ge(chunk_read, 2 * NC4)
                rest_parts(Chain(pool, pool_chain), pool, [p[:, POOL_COLS] for p in kp], pool_rest[:], k[:, POOL_COLS],
                           pool_parts_done)
                pool.wait_ge(pool_parts_done, 1)
                pool.wait_ge(v_filled, 2)


def stage_l0_attend(nc, loads, g, V_aug, qp, kp, Q, K, O):
    LEAD = 4
    with Stage(nc, "l0att") as st:
        probs = st.sb("probs", [P, 2, NC4, BANK])
        half_max = st.sb("half_max", [P, 2, NT, 2])
        negmax = st.sb("negmax", [P, NT])
        rest = st.sb("rest", [P, NT])
        nm = st.sb("nm", [P, 2, 3, NT], BF16)
        nm_rows = st.sb("nm_rows", [3 * NT, 2, P], BF16)
        pv_sb = st.sb("pv_sb", [P, 2, BANK])
        rden = st.sb("rden", [P, 4, NC4])
        ident16 = loads["ident16"]
        first_half = st.sb("first_half", [P, 2, 2 * BANK])
        scanned = st.sb("scanned", [P, 2, 2 * BANK])
        ps_m = st.ps("ps_m", [P, 2, 2 * BANK])
        ps_sv = st.ps("ps_sv", [P, 4, BANK])
        ps_s = ps_sv[:, 0:3, :]
        ps_v = ps_sv[:, 3, :]
        first_scores = (ps_m[:], ps_sv[:].rearrange("p (a b) n -> p a (b n)", a=2))
        cleared = st.sem("cleared")
        loaded = [st.sem(f"loaded{b}") for b in range(HEAD_BUFS)]
        scored = st.sem("scored")
        expd = st.sem("expd")
        pv_done = st.sem("pv_done")
        pv_copied = st.sem("pv_copied")
        m_filled = st.sem("m_filled")
        m_read = st.sem("m_read")
        nm_ready = st.sem("nm_ready")
        nm_placed = [st.sem("nm_placed0"), st.sem("nm_placed1")]
        first_filled = st.sem("first_filled")
        first_copied = st.sem("first_copied")
        second_filled = st.sem("second_filled")
        second_scanned = st.sem("second_scanned")
        chain = st.sem("chain")

        turns, place = [], {}
        negate_before = {}
        copy_before = {}
        plan = {}
        for s in range(-1, L0_H + 1):
            slots = range(LEAD if s < 0 else NT if s < L0_H else 1)
            if s >= 1:
                copy_before[len(turns)] = s - 1
            for kt in slots:
                tile = NT + kt if s < 0 else NT * (s + 1) + LEAD + kt
                uses = []
                if kt == 3 and 1 <= s < L0_H or s == L0_H:
                    uses.append(("pv", s - 1))
                head, t = tile // NT, tile % NT
                if t == 0 and 1 <= head <= L0_H:
                    negate_before[len(turns) + len(uses)] = head - 1
                if t == (0 if head == 1 else 1) and 1 <= head <= L0_H:
                    uses.append(("nm", head - 1))
                if head < L0_H:
                    uses += [("max", head, t, half) for half in range(2)]
                for what in uses:
                    place[what] = len(turns)
                    turns.append(what)
                plan[s, kt] = uses

        with st.block() as block:

            @block.sync
            def _(sp):
                for h in range(L0_H):
                    if h >= HEAD_BUFS:
                        sp.wait_ge(scored, (h - HEAD_BUFS + 1) * NT * NC4)
                    for r in range(6):
                        for operand, parts, part in ((Q, qp, SPLITS_Q[r]), (K, kp, SPLITS_K[r])):
                            sp.dma_start(operand[L0_K * r:L0_K * (r + 1), h % HEAD_BUFS, :],
                                         parts[part][L0_K * h:L0_K * (h + 1), :]).then_inc(loaded[h % HEAD_BUFS], 16)

            @block.gpsimd
            def _(pool):
                for h in range(L0_H):
                    pool.wait_ge(m_read, place["nm", h] + 1)
                    pool.dma_start(Q[MAX_ROW:MAX_ROW + 3, h % HEAD_BUFS, :],
                                   nm_rows[:, h % 2, :]).then_inc(nm_placed[h % 2], 16)
                    if h >= 1 and h + HEAD_BUFS - 1 < L0_H:
                        pool.wait_ge(scored, h * NT * NC4)
                        pool.memset(Q[MAX_ROW:MAX_ROW + 3, (h - 1) % HEAD_BUFS, :], 0.0).then_inc(cleared, 1)

            @block.tensor
            def _(pe):
                def run(what):
                    n = place[what]
                    if n >= 2:
                        pe.wait_ge(m_read, n - 1)
                    dst = ps_m[:, n % 2, :]
                    if what[0] == "max":
                        _, h, t, half = what
                        if t == 0 and half == 0:
                            pe.wait_ge(loaded[h % HEAD_BUFS], 16 * 12 * (h // HEAD_BUFS + 1))
                            if h >= HEAD_BUFS:
                                pe.wait_ge(cleared, h - HEAD_BUFS + 1)
                        for c in (2 * half, 2 * half + 1):
                            mm = pe.matmul(dst[:, (c % 2) * BANK:(c % 2 + 1) * BANK], Q[:, h % HEAD_BUFS, c1(t)],
                                           K[:, h % HEAD_BUFS, c4(c)], start=True, stop=True)
                    elif what[0] == "nm":
                        h = what[1]
                        pe.wait_ge(nm_ready, h + 1)
                        if h == 0:
                            pe.wait_ge(loads.done, loads.all)
                        mm = pe.transpose(dst[0:3 * NT, 0:P // 2].bitcast(BF16), nm[:, h % 2, :, :].rearrange(
                            "p s t -> p (s t)"), ident16[:])
                    else:
                        h = what[1]
                        pe.wait_ge(pv_copied, h + 1)
                        for i in range(4):
                            mm = pe.transpose(dst[:, c1(i)], pv_sb[:, h % 2, c1(i)], g.ident[:])
                    mm.then_inc(m_filled, 1)

                def values(h, kt):
                    if kt == 0 and h >= 1:
                        pe.wait_ge(pv_copied, h)
                    for c in range(NC4):
                        pe.wait_ge(expd, (h * NT + kt) * NC4 + c + 1)
                        mm = pe.matmul(ps_v[32 * c:32 * c + 32, :], V_aug[:, kt, h, :], probs[:, kt % 2, c, :],
                                       start=(kt == 0), stop=(kt == NT - 1))
                    mm.then_inc(pv_done, 1)

                pe.wait_ge(loaded[0], 16 * 12)
                for t in range(NT):
                    for half, (filled, read) in enumerate(((first_filled, first_copied),
                                                           (second_filled, second_scanned))):
                        if t >= 2:
                            pe.wait_ge(read, t - 1)
                        for i in range(2):
                            mm = pe.matmul(first_scores[t % 2][:, half, i * BANK:(i + 1) * BANK], Q[:, 0, c1(t)],
                                           K[:, 0, c4(2 * half + i)], start=True, stop=True)
                        mm.then_inc(filled, 1)
                pe.wait_ge(first_copied, NT)
                pe.wait_ge(second_scanned, NT)
                for kt in range(LEAD):
                    for what in plan[-1, kt]:
                        run(what)
                for h in range(L0_H):
                    pe.wait_ge(nm_placed[h % 2], 16 * (h // 2 + 1))
                    for kt in range(NT):
                        todo = list(plan[h, kt])
                        for c in range(NC4):
                            n = (h * NT + kt) * NC4 + c
                            if n >= 3:
                                pe.wait_ge(expd, n - 2)
                            pe.matmul(ps_s[:, n % 3, :], K[:, h % HEAD_BUFS, c1(kt)], Q[:, h % HEAD_BUFS, c4(c)],
                                      start=True, stop=True).then_inc(scored, 1)
                            if todo:
                                run(todo.pop(0))
                        if kt >= 1:
                            values(h, kt - 1)
                    values(h, NT - 1)
                run(("pv", L0_H - 1))

            @block.scalar
            def _(act):
                for t in range(NT):
                    act.wait_ge(first_filled, t + 1)
                    if t >= 2:
                        act.wait_ge(second_scanned, t - 1)
                    act.activation(first_half[:, t % 2, :], first_scores[t % 2][:, 0, :], ACT.Identity)\
                       .then_inc(first_copied, 1)
                for n in range(L0_H * NT * NC4):
                    kt, c = n // NC4 % NT, n % NC4
                    act.wait_ge(scored, n + 1)
                    if n // NC4 >= 2:
                        act.wait_ge(pv_done, n // NC4 - 1)
                    act.activation(probs[:, kt % 2, c, :], ps_s[:, n % 3, :], ACT.Exp).then_inc(expd, 1)

            @block.vector
            def _(dve):
                link = Chain(dve, chain)

                def negate(h):
                    if h > 0:
                        dve.wait_ge(m_read, place["max", h, NT - 1, 1] + 1)
                    link(dve.tensor_tensor(negmax[:], half_max[:, h % 2, :, 0], half_max[:, h % 2, :, 1], ALU.max))
                    link(dve.tensor_scalar(negmax[:], negmax[:], -1.0, None, ALU.mult))
                    if h >= 2:
                        dve.wait_ge(m_filled, place["nm", h - 2] + 1)
                    splits_of(link, dve, [nm[:, h % 2, i, :] for i in range(3)], rest[:], negmax[:], nm_ready)

                def copy_values(h):
                    dve.wait_ge(pv_done, NT * (h + 1))
                    if h >= 2:
                        dve.wait_ge(m_filled, place["pv", h - 2] + 1)
                    dve.tensor_copy(pv_sb[:, h % 2, :], ps_v).then_inc(pv_copied, 1)

                def keep_maximum(t):
                    link.mark(dve.tensor_copy(half_max[:, 0, t, :], bcast(scanned[:, t % 2, 2 * BANK - 1:], P, 2)))

                for t in range(NT):
                    dve.wait_ge(first_copied, t + 1)
                    dve.wait_ge(second_filled, t + 1)
                    if t >= 2:
                        link.wait()
                    dve.tensor_tensor_scan(scanned[:, t % 2, :], first_half[:, t % 2, :],
                                           first_scores[t % 2][:, 1, :], LOWEST,
                                           ALU.max, ALU.max).then_inc(second_scanned, 1)
                    if t >= 1:
                        dve.wait_ge(second_scanned, t)
                        keep_maximum(t - 1)
                dve.wait_ge(second_scanned, NT)
                keep_maximum(NT - 1)
                link.wait()
                for i, what in enumerate(turns):
                    if i in copy_before:
                        copy_values(copy_before[i])
                    if i in negate_before:
                        negate(negate_before[i])
                    dve.wait_ge(m_filled, i + 1)
                    src = ps_m[:, i % 2, :]
                    h = what[1]
                    if what[0] == "max":
                        t, half = what[2:]
                        dve.tensor_reduce(half_max[:, h % 2, t, half:half + 1], src, AX_X, ALU.max)\
                           .then_inc(m_read, 1)
                    elif what[0] == "nm":
                        if h >= 2:
                            dve.wait_ge(nm_placed[h % 2], 16 * (h // 2))
                        dve.tensor_copy(nm_rows[:, h % 2, :], src[0:3 * NT, 0:P // 2].bitcast(BF16))\
                           .then_inc(m_read, 1)
                    else:
                        v = src[:, 0:BANK].rearrange("p (i c k) -> p i c k", i=4, c=NC4)
                        link(dve.reciprocal(rden[:], v[:, :, :, L0_K]))
                        o = O[:, :, L0_K * h:L0_K * (h + 1)].rearrange("p (c i) k -> p i c k", c=NC4)
                        dve.tensor_tensor(o, v[:, :, :, 0:L0_K], bcast(rden[:].unsqueeze(3), P, 4, NC4, L0_K),
                                          ALU.mult).then_inc(m_read, 1)


def stage_project_out(nc, loads, w_name, g, name, O, gate_row):
    with Stage(nc, name) as st:
        w = loads[w_name]
        OT = st.sb("OT", [P, S])
        ps_t = st.ps("ps_t", [P, 4, BANK])
        ps_o = st.ps("ps_o", [P, 4, BANK])
        w_gated = st.sem("w_gated")
        turned = st.sem("turned")
        copied = st.sem("copied")
        summed = st.sem("summed")
        with st.block() as block:

            @block.tensor
            def _(pe):
                for t in range(NT):
                    mm = pe.transpose(ps_t[:, t // 4, c1(t % 4)], O[:, t, :], g.ident[:])
                    if t % 4 == 3:
                        mm.then_inc(turned, 1)
                pe.wait_ge(w_gated, 1)
                for t in range(NT):
                    if t % 4 == 0:
                        pe.wait_ge(copied, t // 4 + 1)
                    mm = pe.matmul(ps_o[:, t // 4, c1(t % 4)], OT[:, c1(t)], w[:], start=True, stop=True)
                    if t % 4 == 3:
                        mm.then_inc(summed, 1)

            @block.scalar
            def _(act):
                for j in range(NC4):
                    act.wait_ge(turned, j + 1)
                    act.activation(OT[:, c4(j)], ps_t[:, j, :], ACT.Identity).then_inc(copied, 1)

            @block.vector
            def _(dve):
                dve.wait_ge(loads.done, loads.all)
                dve.tensor_tensor(w[:], w[:], gate_row, ALU.mult).then_inc(w_gated, 1)
                for j in range(NC4):
                    dve.wait_ge(summed, j + 1)
                    xs = g.x[:, 4 * j:4 * j + 4, :]
                    dve.tensor_tensor(xs, ps_o[:, j, :].rearrange("p (t f) -> p t f", t=4), xs, ALU.add)


def layer0_attention(nc, d, g):
    with Stage(nc, "l0") as st:
        for_parts = Loads(nc, d, st, "parts", "l0_wqkv")
        for_attend = Loads(nc, d, st, "attend", "ident16")
        for_out = Loads(nc, d, st, "out", "l0_wout")
        Q = st.sb("Q", [P, HEAD_BUFS, S], BF16)
        adaln(nc, g, 0, SCALE_A, SHIFT_A, ClearOperand(st, Q))
        O = st.sb("O", [P, NT, P])
        V_aug = st.sb("V_aug", [P, NT, L0_H, 32])
        K = st.sb("K", [P, HEAD_BUFS, S], BF16)
        qp = [st.sb(f"qp{i}", [P, S], BF16) for i in range(3)]
        kp = [st.sb(f"kp{i}", [P, S], BF16) for i in range(3)]
        with Stage(nc, "l0q") as st_q:
            q = st_q.sb("q", [P, S])
            stage_project_parts(nc, for_parts, "l0_wqkv", g, "l0proj", V_aug, q, qp, kp, K,
                                d["ones_l0"])
        stage_l0_attend(nc, for_attend, g, V_aug, qp, kp, Q, K, O)
        stage_project_out(nc, for_out, "l0_wout", g, "l0out", O, mod_row(g, 0, GATE_A))



SLOTS, TOPK, HID = 64, 8, 64


def stage_l0_route(nc, loads, g, alpha, alphaT, w):
    with Stage(nc, "l0route") as st:
        hidT = st.sb("hidT", [HID + 1, S])
        b1 = loads["l0_b1"]
        bias1 = st.sb("bias1", [HID, 1])
        w1T = loads["l0_w1T"]
        w2T = loads["l0_w2T"]
        tau = loads["l0_tau"]
        itau = st.sb("itau", [P, 1])
        mean_w = st.sb("mean_w", [SLOTS, 1])
        mean_slot = st.sb("mean_slot", [P, 1])
        logits = st.sb("logits", [P, NT, SLOTS])
        left = st.sb("left", [P, NT, SLOTS])
        top = st.sb("top", [P, NT, TOPK])
        negtop = st.sb("negtop", [P, NT])
        total = st.sb("total", [P, NT])
        ps_h = st.ps("ps_h", [HID, 4, BANK])
        ps_l = st.ps("ps_l", [P, 2, BANK])
        ps_m = st.ps("ps_m", [P, BANK])
        slots_ready = st.sem("slots_ready")
        mean_done = st.sem("mean_done")
        mean_copied = st.sem("mean_copied")
        bias_done = st.sem("bias_done")
        bias_ready = st.sem("bias_ready")
        hid_done = st.sem("hid_done")
        hid_ready = st.sem("hid_ready")
        logits_done = st.sem("logits_done")
        left_ready = st.sem("left_ready")
        exp_done = st.sem("exp_done")
        alpha_ready = st.sem("alpha_ready")
        ones_row = st.sem("ones_row")
        turned = st.sem("turned")
        chain = st.sem("chain")
        with st.block() as block:

            @block.tensor
            def _(pe):
                pe.wait_ge(slots_ready, 1)
                pe.matmul(ps_m[:, 0:1], w.slots[:], mean_w[:], start=True, stop=True).then_inc(mean_done, 1)
                for j in range(NC4):
                    pe.matmul(ps_h[:, j, :], w1T[:, 0, :], g.hT[:, c4(j)], start=True, stop=True).then_inc(hid_done, 1)
                pe.wait_ge(mean_copied, 1)
                pe.matmul(ps_m[0:HID, 1:2], w1T[:, 1, :], mean_slot[:], start=True, stop=True).then_inc(bias_done, 1)
                for t in range(NT):
                    if t % 4 == 0:
                        pe.wait_ge(hid_ready, t // 4 + 1)
                    mm = pe.matmul(ps_l[:, t // 8, (t % 8) * SLOTS:(t % 8 + 1) * SLOTS], hidT[:, c1(t)], w2T[:],
                                   start=True, stop=True)
                    if t % 8 == 7:
                        mm.then_inc(logits_done, 1)
                pe.wait_ge(alpha_ready, 1)
                for t in range(NT):
                    mm = pe.transpose(ps_h[:, t // 4, c1(t % 4)], alpha[:, t, :], g.ident[:])
                    if t % 4 == 3:
                        mm.then_inc(turned, 1)

            @block.scalar
            def _(act):
                act.wait_ge(bias_ready, 1)
                for j in range(NC4):
                    act.wait_ge(hid_done, j + 1)
                    act.activation(hidT[0:HID, c4(j)], ps_h[:, j, :], ACT.Gelu, bias=bias1[:]).then_inc(hid_ready, 1)
                for t in range(NT):
                    if t == 0:
                        act.wait_ge(left_ready, 1)
                    act.activation(alpha[:, t, :], logits[:, t, :], ACT.Exp, bias=negtop[:, t:t + 1])\
                       .then_inc(exp_done, 1)
                for j in range(NC4):
                    act.wait_ge(turned, j + 1)
                    act.activation(alphaT[0:SLOTS, c4(j)], ps_h[:, j, :], ACT.Identity)

            @block.gpsimd
            def _(pool):
                pool.memset(alphaT[SLOTS:SLOTS + 1, :], 1.0).then_inc(ones_row, 1)
                pool.wait_ge(ones_row, 1)

            @block.vector
            def _(dve):
                link = Chain(dve, chain)
                link.mark(dve.memset(mean_w[:], 1.0 / SLOTS))
                link(dve.memset(hidT[HID:HID + 1, :], 1.0))
                dve.wait_ge(loads.done, loads.all)
                dve.tensor_scalar(w.slots[:], w.slots[:], w.slot_scale[:], None, ALU.mult).then_inc(slots_ready, 1)
                link(dve.tensor_scalar(itau[:], tau[:], -1.0, None, ALU.mult))
                link(dve.tensor_tensor(itau[:], itau[:], tau[:], ALU.max))
                link(dve.tensor_scalar(itau[:], itau[:], 0.1, None, ALU.add))
                link(dve.reciprocal(itau[:], itau[:]))
                dve.wait_ge(mean_done, 1)
                dve.tensor_copy(mean_slot[:], ps_m[:, 0:1]).then_inc(mean_copied, 1)
                dve.wait_ge(bias_done, 1)
                dve.tensor_tensor(bias1[:], ps_m[0:HID, 1:2], b1[:], ALU.add).then_inc(bias_ready, 1)
                for b in range(2):
                    dve.wait_ge(logits_done, b + 1)
                    link.mark(dve.tensor_scalar(logits[:, 8 * b:8 * b + 8, :].rearrange("p t s -> p (t s)"),
                                                ps_l[:, b, :], itau[:], None, ALU.mult))
                link.wait()
                for t in range(NT):
                    link.mark(dve.max(top[:, t, :], logits[:, t, :]))
                link.wait()
                for t in range(NT):
                    link.mark(dve.match_replace(left[:, t, :], top[:, t, :], logits[:, t, :], -3e38))
                dve.tensor_scalar(negtop[:], top[:, :, 0], -1.0, None, ALU.mult).then_inc(left_ready, 1)
                link.wait()
                link(dve.tensor_tensor(left[:], left[:], logits[:], ALU.is_lt))
                dve.wait_ge(exp_done, NT)
                link(dve.tensor_tensor(alpha[:], alpha[:], left[:], ALU.mult))
                link(dve.tensor_reduce(total[:], alpha[:], AX_X, ALU.add))
                link(dve.reciprocal(total[:], total[:]))
                dve.tensor_tensor(alpha[:], alpha[:], bcast(total[:].unsqueeze(2), P, NT, SLOTS), ALU.mult)\
                   .then_inc(alpha_ready, 1)


def stage_l0_slots(nc, loads, g, alpha, alphaT, w):
    with Stage(nc, "l0slots") as st:
        wih = loads["l0_wihT"]
        whh = loads["l0_whhT"]
        b_ih = loads["l0_bih"]
        b_hh = loads["l0_bhh"]
        wv = loads["l0_wvT"]
        bv = loads["l0_bv"]
        wo = loads["l0_woT"]
        out_w = st.sb("out_w", [SLOTS + 1, P])
        ones = st.sb("ones", [P, SLOTS])
        raw = st.sb("raw", [SLOTS, P + 1])
        gi = st.sb("gi", [SLOTS, P])
        shift = st.sb("shift", [SLOTS, P])
        wsum = st.sb("wsum", [SLOTS, 1])
        giT = st.sb("giT", [P, SLOTS])
        slotsT = st.sb("slotsT", [P, SLOTS])
        rz = st.sb("rz", [SLOTS, 2 * P])
        hn = st.sb("hn", [SLOTS, P])
        n = st.sb("n", [SLOTS, P])
        newT = st.sb("newT", [P, SLOTS])
        svT = st.sb("svT", [P, SLOTS])
        ps_i = st.ps("ps_i", [SLOTS, BANK])
        ps_g = st.ps("ps_g", [SLOTS, BANK])
        ps_t = st.ps("ps_t", [P, BANK])
        ps_o = st.ps("ps_o", [P, 4, BANK])
        bo_placed = st.sem("bo_placed")
        ones_ready = st.sem("ones_ready")
        raw_done = st.sem("raw_done")
        gi_ready = st.sem("gi_ready")
        turned = st.sem("turned")
        turns_copied = st.sem("turns_copied")
        gates_done = st.sem("gates_done")
        rz_ready = st.sem("rz_ready")
        n_in = st.sem("n_in")
        n_ready = st.sem("n_ready")
        new_ready = st.sem("new_ready")
        sv_done = st.sem("sv_done")
        sv_ready = st.sem("sv_ready")
        ow_done = st.sem("ow_done")
        ow_ready = st.sem("ow_ready")
        out_done = st.sem("out_done")
        chain = st.sem("chain")
        with st.block() as block:

            @block.sync
            def _(sp):
                sp.wait_ge(loads.done, loads.all)
                sp.dma_start(out_w[SLOTS:SLOTS + 1, :], loads["l0_bo"][:]).then_inc(bo_placed, 16)

            @block.tensor
            def _(pe):
                pe.wait_ge(ones_ready, 1)
                for t in range(NT):
                    pe.matmul(ps_i[:, 0:P], alpha[:, t, :], g.xn[:, t, :], start=(t == 0), stop=(t == NT - 1))
                for t in range(NT):
                    mm = pe.matmul(ps_i[:, P:P + 1], alpha[:, t, :], ones[:, 0:1], start=(t == 0), stop=(t == NT - 1),
                                   skip_group_check=True)
                mm.then_inc(raw_done, 1)
                pe.transpose(ps_t[:, 0:SLOTS], w.slots[:], g.ident[0:SLOTS, 0:SLOTS])
                pe.wait_ge(gi_ready, 1)
                pe.transpose(ps_t[:, SLOTS:2 * SLOTS], gi[:], g.ident[0:SLOTS, 0:SLOTS]).then_inc(turned, 1)
                pe.wait_ge(turns_copied, 1)
                pe.wait_ge(loads.done, loads.all)
                one = ones[0:1, :]
                pe.matmul(ps_g[:, 0:256], giT[:], wih[:, 0:2, :].rearrange("p a b -> p (a b)"), start=True, stop=False)
                pe.matmul(ps_g[:, 0:256], one, b_ih[:, 0:256], start=False, stop=False)
                pe.matmul(ps_g[:, 0:256], slotsT[:], whh[:, 0:2, :].rearrange("p a b -> p (a b)"), start=False,
                          stop=False)
                pe.matmul(ps_g[:, 0:256], one, b_hh[:, 0:256], start=False, stop=True)
                pe.matmul(ps_g[:, 256:384], giT[:], wih[:, 2, :], start=True, stop=False, skip_group_check=True)
                pe.matmul(ps_g[:, 256:384], one, b_ih[:, 256:384], start=False, stop=True, skip_group_check=True)
                pe.matmul(ps_g[:, 384:512], slotsT[:], whh[:, 2, :], start=True, stop=False, skip_group_check=True)
                pe.matmul(ps_g[:, 384:512], one, b_hh[:, 256:384], start=False, stop=True,
                          skip_group_check=True).then_inc(gates_done, 1)
                pe.wait_ge(new_ready, 1)
                pe.transpose(ps_t[:, 0:SLOTS], n[:], g.ident[0:SLOTS, 0:SLOTS]).then_inc(turned, 1)
                pe.wait_ge(turns_copied, 2)
                pe.matmul(ps_t[:, SLOTS:2 * SLOTS], wv[:], newT[:], start=True, stop=True).then_inc(sv_done, 1)
                pe.wait_ge(sv_ready, 1)
                pe.matmul(ps_i[:, 0:P], svT[:], wo[:], start=True, stop=True).then_inc(ow_done, 1)
                pe.wait_ge(ow_ready, 2)
                for t in range(NT):
                    mm = pe.matmul(ps_o[:, t // 4, c1(t % 4)], alphaT[:, c1(t)], out_w[:], start=True, stop=True)
                    if t % 4 == 3:
                        mm.then_inc(out_done, 1)

            @block.scalar
            def _(act):
                act.wait_ge(gates_done, 1)
                act.activation(rz[:], ps_g[:, 0:256], ACT.Sigmoid).then_inc(rz_ready, 1)
                act.wait_ge(n_in, 1)
                act.activation(n[:], hn[:], ACT.Tanh).then_inc(n_ready, 1)

            @block.vector
            def _(dve):
                link = Chain(dve, chain)
                dve.memset(ones[:], 1.0).then_inc(ones_ready, 1)
                dve.wait_ge(raw_done, 1)
                link(dve.tensor_copy(raw[:], ps_i[:, 0:P + 1]))
                link.mark(dve.tensor_scalar(wsum[:], raw[:, P:P + 1], 1e-8, None, ALU.add))
                link.mark(dve.tensor_tensor(gi[:], raw[:, 0:P], mod_row(g, 0, SCALE_B)[0:SLOTS], ALU.mult))
                link(dve.tensor_scalar(shift[:], mod_row(g, 0, SHIFT_B)[0:SLOTS], raw[:, P:P + 1], None, ALU.mult))
                link.mark(dve.reciprocal(wsum[:], wsum[:]))
                link(dve.tensor_tensor(gi[:], gi[:], shift[:], ALU.add))
                dve.tensor_scalar(gi[:], gi[:], wsum[:], None, ALU.mult).then_inc(gi_ready, 1)
                dve.wait_ge(turned, 1)
                link(dve.tensor_copy(slotsT[:], ps_t[:, 0:SLOTS]))
                dve.tensor_copy(giT[:], ps_t[:, SLOTS:2 * SLOTS]).then_inc(turns_copied, 1)
                dve.wait_ge(rz_ready, 1)
                link(dve.tensor_tensor(hn[:], rz[:, 0:P], ps_g[:, 384:512], ALU.mult))
                dve.tensor_tensor(hn[:], hn[:], ps_g[:, 256:384], ALU.add).then_inc(n_in, 1)
                dve.wait_ge(n_ready, 1)
                link(dve.tensor_tensor(hn[:], w.slots[:], n[:], ALU.subtract))
                link(dve.tensor_tensor(hn[:], hn[:], rz[:, P:2 * P], ALU.mult))
                dve.tensor_tensor(n[:], n[:], hn[:], ALU.add).then_inc(new_ready, 1)
                dve.wait_ge(turned, 2)
                dve.tensor_copy(newT[:], ps_t[:, 0:SLOTS]).then_inc(turns_copied, 1)
                dve.wait_ge(sv_done, 1)
                dve.tensor_scalar(svT[:], ps_t[:, SLOTS:2 * SLOTS], bv[:], None, ALU.add).then_inc(sv_ready, 1)
                dve.wait_ge(ow_done, 1)
                dve.tensor_tensor(out_w[0:SLOTS, :], ps_i[:, 0:P], mod_row(g, 0, GATE_B)[0:SLOTS], ALU.mult)\
                   .then_inc(ow_ready, 1)
                dve.wait_ge(bo_placed, 16)
                dve.tensor_tensor(out_w[SLOTS:SLOTS + 1, :], out_w[SLOTS:SLOTS + 1, :],
                                  mod_row(g, 0, GATE_B)[SLOTS:SLOTS + 1], ALU.mult).then_inc(ow_ready, 1)
                for j in range(NC4):
                    dve.wait_ge(out_done, j + 1)
                    xs = g.x[:, 4 * j:4 * j + 4, :]
                    dve.tensor_tensor(xs, ps_o[:, j, :].rearrange("p (t f) -> p t f", t=4), xs, ALU.add)


def layer0_slots(nc, d, g):
    with Stage(nc, "l0ffn") as st:
        for_route = Loads(nc, d, st, "route", "l0_slots", "l0_slot_scale", "l0_tau", "l0_w1T", "l0_b1", "l0_w2T")
        for_slots = Loads(nc, d, st, "slots", "l0_wihT", "l0_whhT", "l0_bih", "l0_bhh", "l0_wvT", "l0_bv", "l0_woT",
                          "l0_bo")
        adaln(nc, g, 0, SCALE_B, SHIFT_B)
        w = Persistent()
        w.slots = for_route["l0_slots"]
        w.slot_scale = for_route["l0_slot_scale"]
        alpha = st.sb("alpha", [P, NT, SLOTS])
        alphaT = st.sb("alphaT", [SLOTS + 1, S])
        stage_l0_route(nc, for_route, g, alpha, alphaT, w)
        stage_l0_slots(nc, for_slots, g, alpha, alphaT, w)



LEVELS = (2, 4, 8, 16, 32, 64)


def stage_l1_project(nc, loads, g, w):
    with Stage(nc, "l1proj") as st:
        wq = loads["l1_wq"]
        wkvb = loads["l1_wkvb"]
        raw = st.sb("raw", [P, NT, 2 * P + 1])
        sq = st.sb("sq", [P, NT, P])
        ss = st.sb("ss", [P, NT])
        norm = st.sb("norm", [P, NT])
        quot = st.sb("quot", [P, NT])
        ps_q = st.ps("ps_q", [P, 4, BANK])
        ps_k = st.ps("ps_k", [P, 4, BANK])
        q_done = st.sem("q_done")
        kvb_done = st.sem("kvb_done")
        kvb_copied = st.sem("kvb_copied")
        sums_ready = st.sem("sums_ready")
        roots_done = st.sem("roots_done")
        sig_done = st.sem("sig_done")
        q_copied = st.sem("q_copied")
        k_ready = st.sem("k_ready")
        turned = st.sem("turned")
        chain = st.sem("chain")
        with st.block() as block:

            @block.tensor
            def _(pe):
                pe.wait_ge(loads.done, loads.all)
                for t in range(NT):
                    if t >= 4:
                        pe.wait_ge(kvb_copied, t - 3)
                    pe.matmul(ps_k[:, t % 4, 0:2 * P + 1], g.hT[:, c1(t)], wkvb[:], start=True, stop=True)\
                      .then_inc(kvb_done, 1)
                for j in range(NC4):
                    pe.matmul(ps_q[:, j, :], wq[:], g.hT[:, c4(j)], start=True, stop=True).then_inc(q_done, 1)
                pe.wait_ge(k_ready, 1)
                for t in range(NT):
                    if t % 4 == 0:
                        pe.wait_ge(q_copied, t // 4 + 1)
                    mm = pe.transpose(ps_q[:, t // 4, c1(t % 4)], w.k[:, t, :], g.ident[:])
                    if t % 4 == 3:
                        mm.then_inc(turned, 1)

            @block.scalar
            def _(act):
                for j in range(NC4):
                    act.wait_ge(q_done, j + 1)
                    act.activation(w.qT[:, c4(j)], ps_q[:, j, :], ACT.Identity, scale=P ** -0.5).then_inc(q_copied, 1)
                act.wait_ge(kvb_copied, NT)
                act.activation(w.bv[:], raw[:, :, P:2 * P], ACT.Sigmoid)
                act.activation(w.beta[:], raw[:, :, 2 * P], ACT.Sigmoid).then_inc(sig_done, 1)
                act.wait_ge(sums_ready, 1)
                act.activation(norm[:], ss[:], ACT.Sqrt).then_inc(roots_done, 1)
                for j in range(NC4):
                    act.wait_ge(turned, j + 1)
                    act.activation(w.kT[:, c4(j)], ps_q[:, j, :], ACT.Identity)

            @block.vector
            def _(dve):
                link = Chain(dve, chain)
                for t in range(NT):
                    dve.wait_ge(kvb_done, t + 1)
                    dve.tensor_copy(raw[:, t, :], ps_k[:, t % 4, 0:2 * P + 1]).then_inc(kvb_copied, 1)
                dve.wait_ge(kvb_copied, NT)
                k_raw, v_raw = raw[:, :, 0:P], raw[:, :, P:2 * P]
                link(dve.tensor_tensor(sq[:], k_raw, k_raw, ALU.mult))
                link(dve.tensor_reduce(ss[:], sq[:], AX_X, ALU.add))
                dve.tensor_scalar(ss[:], ss[:], 1e-30, None, ALU.max).then_inc(sums_ready, 1)
                dve.wait_ge(sig_done, 1)
                link(dve.tensor_tensor(w.bv[:], w.bv[:], v_raw, ALU.mult))
                link(dve.tensor_tensor(w.bv[:], w.bv[:], bcast(w.beta[:].unsqueeze(2), P, NT, P), ALU.mult))
                dve.wait_ge(roots_done, 1)
                link(dve.reciprocal(quot[:], norm[:]))
                link(dve.tensor_tensor(quot[:], quot[:], ss[:], ALU.mult))
                link(dve.tensor_tensor(norm[:], norm[:], quot[:], ALU.add))
                link(dve.tensor_scalar(norm[:], norm[:], 0.5, 1e-12, ALU.mult, ALU.max))
                link(dve.reciprocal(norm[:], norm[:]))
                dve.tensor_tensor(w.k[:], k_raw, bcast(norm[:].unsqueeze(2), P, NT, P), ALU.mult).then_inc(k_ready, 1)
                dve.wait_ge(k_ready, 1)
                dve.tensor_tensor(w.bk[:], w.k[:], bcast(w.beta[:].unsqueeze(2), P, NT, P), ALU.mult)


def stage_l1_chunks(nc, loads, g, w):
    with Stage(nc, "l1chunk") as st:
        masks = loads["masks"]
        A = st.sb("A", [P, NT, P])
        C = st.sb("C", [P, 2, NT, P])
        T = st.sb("T", [P, NT, P])
        X = st.sb("X", [P, NT, P])
        Y = st.sb("Y", [P, 2, BANK])
        ps_y = st.ps("ps_y", [P, 2, BANK])
        ps_t = st.ps("ps_t", [P, 2, BANK])
        ps_x = st.ps("ps_x", [P, 2, BANK])
        g_done = st.sem("g_done")
        a_ready = st.sem("a_ready")
        c_ready = st.sem("c_ready")
        t_init = st.sem("t_init")
        x_turned = st.sem("x_turned")
        x_copied = st.sem("x_copied")
        y_done = st.sem("y_done")
        y_copied = st.sem("y_copied")
        tx_done = st.sem("tx_done")
        tx_ready = st.sem("tx_ready")
        m_done = st.sem("m_done")
        m_copied = st.sem("m_copied")
        u_copied = st.sem("u_copied")
        wt_copied = st.sem("wt_copied")
        wt_done = st.sem("wt_done")
        chain = st.sem("chain")
        tiles = lambda buf, j: buf[:, 4 * j:4 * j + 4, :].rearrange("p t f -> p (t f)")

        def mask(i, n):
            return bcast(masks[:, i:i + 1, :], P, n, P)

        with st.block() as block:

            @block.tensor
            def _(pe):
                for j in range(NC4):
                    for t in range(4):
                        c = c1(4 * j + t)
                        mm = pe.matmul((ps_y if j < 2 else ps_t)[:, j % 2, c1(t)], w.kT[:, c], w.kT[:, c], start=True,
                                       stop=True)
                    mm.then_inc(g_done, 1)
                for j in range(NC4):
                    if j >= 2:
                        pe.wait_ge(m_copied, j - 1)
                    for t in range(4):
                        c = c1(4 * j + t)
                        mm = pe.matmul(ps_x[:, j % 2, c1(t)], w.kT[:, c], w.qT[:, c], start=True, stop=True)
                    mm.then_inc(m_done, 1)
                for j in range(NC4):
                    pe.wait_ge(t_init, j + 1)
                    pe.wait_ge(a_ready, min(j + 3, NC4))
                    if j >= 2:
                        pe.wait_ge(x_copied, j - 1)
                    for t in range(4):
                        mm = pe.transpose(ps_y[:, j % 2, c1(t)], T[:, 4 * j + t, :], g.ident[:])
                    mm.then_inc(x_turned, 1)
                for l in range(len(LEVELS)):
                    last = l == len(LEVELS) - 1

                    def join(j):
                        n = NC4 * l + j
                        pe.wait_ge(y_copied, n + 1)
                        if n >= 2:
                            pe.wait_ge(tx_ready, n - 1)
                        for t in range(4):
                            y = Y[:, n % 2, c1(t)]
                            if not last:
                                pe.matmul(ps_t[:, n % 2, c1(t)], y, T[:, 4 * j + t, :], start=True, stop=True)
                            mm = pe.matmul(ps_x[:, n % 2, c1(t)], T[:, 4 * j + t, :], y, start=True, stop=True)
                        mm.then_inc(tx_done, 1)

                    for j in range(NC4):
                        n = NC4 * l + j
                        if j == 0:
                            pe.wait_ge(c_ready, l + 2)
                        if l == 0:
                            pe.wait_ge(x_copied, NC4 if j == 0 else j + 1)
                            pe.wait_ge(m_copied, NC4)
                        else:
                            pe.wait_ge(tx_ready, n - NC4 + 1)
                        if n >= 2:
                            pe.wait_ge(y_copied, n - 1)
                        for t in range(4):
                            mm = pe.matmul(ps_y[:, n % 2, c1(t)], C[:, (l + 1) % 2, 4 * j + t, :], X[:, 4 * j + t, :],
                                           start=True, stop=True)
                        mm.then_inc(y_done, 1)
                        if j >= 1:
                            join(j - 1)
                    join(NC4 - 1)
                total = NC4 * len(LEVELS)
                for j in range(NC4):
                    pe.wait_ge(tx_ready, total - NC4 + j + 1)
                    if j == 0:
                        pe.wait_ge(y_copied, total)
                        pe.wait_ge(tx_ready, total)
                    if j >= 2:
                        pe.wait_ge(u_copied, j - 1)
                        pe.wait_ge(wt_copied, j - 1)
                    for t in range(4):
                        i = 4 * j + t
                        pe.matmul(ps_t[:, j % 2, c1(t)], X[:, i, :], w.bv[:, i, :], start=True, stop=True)
                        mm = pe.matmul(ps_x[:, j % 2, c1(t)], w.bk[:, i, :], X[:, i, :], start=True, stop=True)
                    mm.then_inc(wt_done, 1)

            @block.gpsimd
            def _(pool):
                pool.wait_ge(loads.done, loads.all)
                for l in range(len(LEVELS) + 1):
                    if l == 0:
                        pool.wait_ge(a_ready, NC4)
                    if l == 2:
                        pool.wait_ge(t_init, NC4)
                    if l >= 3:
                        pool.wait_ge(y_done, NC4 * (l - 2))
                    pool.tensor_tensor(C[:, l % 2, :, :], A[:], mask(l, NT), ALU.mult).then_inc(c_ready, 1)

            @block.scalar
            def _(act):
                for j in range(NC4):
                    act.wait_ge(x_turned, j + 1)
                    act.activation(tiles(X, j), ps_y[:, j % 2, :], ACT.Identity).then_inc(x_copied, 1)
                for n in range(NC4 * len(LEVELS)):
                    act.wait_ge(y_done, n + 1)
                    if n >= 2:
                        act.wait_ge(tx_done, n - 1)
                    act.activation(Y[:, n % 2, :], ps_y[:, n % 2, :], ACT.Identity).then_inc(y_copied, 1)
                for j in range(NC4):
                    act.wait_ge(wt_done, j + 1)
                    act.activation(w.WT[:, c4(j)], ps_x[:, j % 2, :], ACT.Identity).then_inc(wt_copied, 1)

            @block.vector
            def _(dve):
                link = Chain(dve, chain)
                for j in range(NC4):
                    dve.wait_ge(g_done, j + 1)
                    src = (ps_y if j < 2 else ps_t)[:, j % 2, :].rearrange("p (t f) -> p t f", t=4)
                    dve.tensor_tensor(A[:, 4 * j:4 * j + 4, :], src, bcast(
                        w.beta[:, 4 * j:4 * j + 4].unsqueeze(2), P, 4, P), ALU.mult).then_inc(a_ready, 1)
                dve.wait_ge(loads.done, loads.all)
                for j in range(NC4):
                    dve.wait_ge(m_done, j + 1)
                    dve.tensor_tensor(w.MT[:, 4 * j:4 * j + 4, :], ps_x[:, j % 2, :].rearrange(
                        "p (t f) -> p t f", t=4), mask(len(LEVELS) + 1, 4), ALU.mult).then_inc(m_copied, 1)
                dve.wait_ge(c_ready, 1)
                for j in range(NC4):
                    dve.tensor_tensor(T[:, 4 * j:4 * j + 4, :], bcast(g.ident[:].unsqueeze(1), P, 4, P),
                                      C[:, 0, 4 * j:4 * j + 4, :], ALU.subtract).then_inc(t_init, 1)
                for n in range(NC4 * len(LEVELS)):
                    j, last = n % NC4, n >= NC4 * (len(LEVELS) - 1)
                    dve.wait_ge(tx_done, n + 1)
                    if not last:
                        dve.tensor_tensor(tiles(T, j), tiles(T, j), ps_t[:, n % 2, :], ALU.subtract)
                    dve.tensor_tensor(tiles(X, j), tiles(X, j), ps_x[:, n % 2, :], ALU.subtract)\
                       .then_inc(tx_ready, 1)
                for j in range(NC4):
                    dve.wait_ge(wt_done, j + 1)
                    dve.tensor_copy(tiles(w.U, j), ps_t[:, j % 2, :]).then_inc(u_copied, 1)


def stage_l1_states(nc, w, O):
    with Stage(nc, "l1state") as st:
        state = st.sb("state", [P, 2, P])
        V = st.sb("V", [P, 2, P])
        ps_v = st.ps("ps_v", [P, 2, BANK])
        ps_s = st.ps("ps_s", [P, BANK])
        ps_o = st.ps("ps_o", [P, 2, BANK])
        ws_done = st.sem("ws_done")
        v_ready = st.sem("v_ready")
        s_done = st.sem("s_done")
        s_ready = st.sem("s_ready")
        o_done = st.sem("o_done")
        o_copied = st.sem("o_copied")
        with st.block() as block:

            @block.tensor
            def _(pe):
                for c in range(NT):
                    if c >= 1:
                        pe.wait_ge(s_ready, c)
                        pe.matmul(ps_v[:, c % 2, 0:P], w.WT[:, c1(c)], state[:, c % 2, :], start=True,
                                  stop=True).then_inc(ws_done, 1)
                    if c >= 2:
                        pe.wait_ge(o_copied, c - 1)
                    if c >= 1:
                        pe.matmul(ps_o[:, c % 2, 0:P], w.qT[:, c1(c)], state[:, c % 2, :], start=True, stop=False)
                    pe.wait_ge(v_ready, c + 1)
                    if c < NT - 1:
                        pe.matmul(ps_s[:, 0:P], w.k[:, c, :], V[:, c % 2, :], start=(c == 0), stop=True,
                                  skip_group_check=True).then_inc(s_done, 1)
                    pe.matmul(ps_o[:, c % 2, 0:P], w.MT[:, c, :], V[:, c % 2, :], start=(c == 0),
                              stop=True).then_inc(o_done, 1)

            @block.scalar
            def _(act):
                for c in range(NT):
                    act.wait_ge(o_done, c + 1)
                    act.activation(O[:, c, :], ps_o[:, c % 2, 0:P], ACT.Identity).then_inc(o_copied, 1)

            @block.vector
            def _(dve):
                for c in range(NT):
                    if c >= 2:
                        dve.wait_ge(o_done, c - 1)
                    if c == 0:
                        dve.tensor_copy(V[:, 0, :], w.U[:, 0, :]).then_inc(v_ready, 1)
                    else:
                        dve.wait_ge(ws_done, c)
                        dve.tensor_tensor(V[:, c % 2, :], w.U[:, c, :], ps_v[:, c % 2, 0:P],
                                          ALU.subtract).then_inc(v_ready, 1)
                    if c < NT - 1:
                        dve.wait_ge(s_done, c + 1)
                        dve.tensor_copy(state[:, (c + 1) % 2, :], ps_s[:, 0:P]).then_inc(s_ready, 1)


def stage_add_affine(nc, loads, g_name, b_name, g, name, normed, gate_row):
    with Stage(nc, name) as st:
        gain = loads[g_name]
        shift = loads[b_name]
        tmp = st.sb("tmp", [P, NT, P])
        rows_ready = st.sem("rows_ready")
        shifted = st.sem("shifted")
        chain = st.sem("chain")
        with st.block() as block:

            @block.gpsimd
            def _(pool):
                pool.wait_ge(rows_ready, 1)
                pool.tensor_tensor(g.x[:], g.x[:], bcast(shift[:].unsqueeze(1), P, NT, P), ALU.add)\
                    .then_inc(shifted, 1)
                pool.wait_ge(shifted, 1)

            @block.vector
            def _(dve):
                link = Chain(dve, chain)
                dve.wait_ge(loads.done, loads.all)
                link.mark(dve.tensor_tensor(gain[:], gain[:], gate_row, ALU.mult))
                dve.tensor_tensor(shift[:], shift[:], gate_row, ALU.mult).then_inc(rows_ready, 1)
                link.wait()
                link(dve.tensor_tensor(tmp[:], normed[:], bcast(gain[:].unsqueeze(1), P, NT, P), ALU.mult))
                dve.wait_ge(shifted, 1)
                dve.tensor_tensor(g.x[:], g.x[:], tmp[:], ALU.add)


def layer1_delta(nc, d, g):
    with Stage(nc, "l1") as st:
        for_project = Loads(nc, d, st, "project", "l1_wq", "l1_wkvb")
        for_chunks = Loads(nc, d, st, "chunks", "masks")
        for_add = Loads(nc, d, st, "add", "l1_lng", "l1_lnb")
        adaln(nc, g, 1, SCALE_A, SHIFT_A)
        w = Persistent()
        O = st.sb("O", [P, NT, P])
        w.qT = st.sb("qT", [P, S])
        w.kT = st.sb("kT", [P, S])
        w.k, w.bk, w.bv, w.MT, w.U = (st.sb(n, [P, NT, P]) for n in ("k", "bk", "bv", "MT", "U"))
        w.WT = st.sb("WT", [P, S])
        w.beta = st.sb("beta", [P, NT])
        stage_l1_project(nc, for_project, g, w)
        stage_l1_chunks(nc, for_chunks, g, w)
        stage_l1_states(nc, w, O)
        stage_norm(nc, g, "l1norm", O, g.xn)
        stage_add_affine(nc, for_add, "l1_lng", "l1_lnb", g, "l1add", g.xn, mod_row(g, 1, GATE_A))



EXPERTS = 64
GANG = 64
GANGS = S // GANG + EXPERTS
GANG_LOAD = 8


def stage_l1_route(nc, loads, g, slot, expert_int, gang_expert):
    with Stage(nc, "l1route") as st:
        gw = loads["l1_gateT"]
        gb = loads["l1_gate_b"]
        ones1 = st.sb("ones1", [1, P])
        ones = st.sb("ones", [P, P], BF16)
        ones_row = st.sb("ones_row", [P, EXPERTS])
        not_yet = loads["not_yet"]
        iota_row = loads["iota_row"]
        iota = loads["iota"]
        carry = loads["carry"]
        logits = st.sb("logits", [P, NT, EXPERTS])
        top = st.sb("top", [P, NT, 8])
        idx = st.sb("idx", [P, NT, 8], U32)
        expert = st.sb("expert", [P, NT])
        member = st.sb("member", [P, EXPERTS, NT], BF16)
        place = st.sb("place", [P, EXPERTS, NT])
        gangs = st.sb("gangs", [P, EXPERTS])
        gangs_int = st.sb("gangs_int", [P, EXPERTS], I32)
        gangs_upto = st.sb("gangs_upto", [P, EXPERTS])
        first = st.sb("first", [P, EXPERTS])
        ended = st.sb("ended", [P, EXPERTS])
        gang_col = st.sb("gang_col", [P, 1])
        slot_f = st.sb("slot_f", [P, NT])
        ps_l = st.ps("ps_l", [P, 2, BANK])
        ps_n = st.ps("ps_n", [P, 4, BANK])
        ps_g = st.ps("ps_g", [P, BANK])
        ones_ready = st.sem("ones_ready")
        logits_done = st.sem("logits_done")
        member_ready = st.sem("member_ready")
        counted = st.sem("counted")
        gang_ready = st.sem("gang_ready")
        gang_turned = st.sem("gang_turned")
        chain = st.sem("chain")
        with st.block() as block:

            @block.tensor
            def _(pe):
                pe.wait_ge(ones_ready, 1)
                pe.wait_ge(loads.done, loads.all)
                for t in range(NT):
                    dst = ps_l[:, t // 8, (t % 8) * EXPERTS:(t % 8 + 1) * EXPERTS]
                    pe.matmul(dst, g.hT[:, c1(t)], gw[:], start=True, stop=False, skip_group_check=True)
                    mm = pe.matmul(dst, ones1[:], gb[:], start=False, stop=True, skip_group_check=True)
                    if t % 8 == 7:
                        mm.then_inc(logits_done, 1)
                pe.wait_ge(member_ready, 1)
                m = member[:].rearrange("p e t -> p (e t)")
                for i in range(2):
                    pe.matmul(ps_n[:, i, :], ones[:], m[:, c4(i)], start=True, stop=True)
                    mm = pe.matmul(ps_n[:, 2 + i, :], not_yet[:], m[:, c4(i)], start=True, stop=True)
                mm.then_inc(counted, 1)
                pe.wait_ge(gang_ready, 1)
                pe.transpose(ps_g[0:1, 0:P], gang_col[:], g.ident[:]).then_inc(gang_turned, 1)

            @block.vector
            def _(dve):
                link = Chain(dve, chain)
                link.mark(dve.memset(ones1[:], 1.0))
                link.mark(dve.memset(ones_row[:], 1.0))
                link(dve.memset(ones[:], 1.0))
                dve.memset(gang_col[:], 0.0).then_inc(ones_ready, 1)
                for b in range(2):
                    dve.wait_ge(logits_done, b + 1)
                    link.mark(dve.tensor_copy(logits[:, 8 * b:8 * b + 8, :].rearrange("p t s -> p (t s)"),
                                              ps_l[:, b, :]))
                link.wait()
                for t in range(NT):
                    link.mark(dve.max(top[:, t, :], logits[:, t, :]))
                link.wait()
                for t in range(NT):
                    link.mark(dve.max_index(idx[:, t, :], top[:, t, :], logits[:, t, :]))
                link.wait()
                link(dve.tensor_copy(expert[:], idx[:, :, 0]))
                link.mark(dve.tensor_copy(expert_int[:], expert[:]))
                dve.wait_ge(loads.done, loads.all)
                dve.tensor_tensor(member[:], bcast(iota_row[:].unsqueeze(2), P, EXPERTS, NT),
                                  bcast(expert[:].unsqueeze(1), P, EXPERTS, NT), ALU.is_equal)\
                   .then_inc(member_ready, 1)
                dve.wait_ge(counted, 1)
                flat = place[:].rearrange("p e t -> p (e t)")
                link(dve.tensor_tensor_scan(flat, carry[:].rearrange("p e t -> p (e t)"),
                                            ps_n[:, 0:2, :].rearrange("p b n -> p (b n)"), 0.0, ALU.mult, ALU.add))
                link(dve.tensor_scalar(gangs_int[:], place[:, :, NT - 1], float(GANG - 1), None, ALU.add))
                link(dve.tensor_scalar(gangs_int[:], gangs_int[:], GANG.bit_length() - 1, None,
                                       ALU.logical_shift_right))
                link(dve.tensor_copy(gangs[:], gangs_int[:]))
                link(dve.tensor_tensor_scan(gangs_upto[:], ones_row[:], gangs[:], 0.0, ALU.mult, ALU.add))
                link.mark(dve.tensor_tensor(first[:], gangs_upto[:], gangs[:], ALU.subtract))
                link(dve.tensor_scalar(ended[:], gangs_upto[:], iota[:], None, ALU.is_le))
                link(dve.tensor_reduce(gang_col[:], ended[:], AX_X, ALU.add))
                dve.tensor_scalar(gang_col[:], gang_col[:], float(EXPERTS - 1), None, ALU.min)\
                   .then_inc(gang_ready, 1)
                link(dve.tensor_tensor(flat, flat, ps_n[:, 2:4, :].rearrange("p b n -> p (b n)"), ALU.add))
                link(dve.scalar_tensor_tensor(place[:], bcast(first[:].unsqueeze(2), P, EXPERTS, NT), float(GANG),
                                              place[:], ALU.mult, ALU.add))
                link(dve.tensor_tensor(place[:], place[:], member[:], ALU.mult))
                link(dve.tensor_reduce(slot_f[:], place[:].rearrange("p e t -> p t e"), AX_X, ALU.add))
                link.mark(dve.tensor_copy(slot[:], slot_f[:]))
                dve.wait_ge(gang_turned, 1)
                dve.tensor_copy(gang_expert[:], ps_g[0:1, 0:GANGS])


def stage_l1_experts(nc, d, g, W, sorted_in, sorted_out, zeroed, weights_loaded, slot, expert_int, gang_expert):
    LOADS = 4
    pairs = GANGS // 2
    with Stage(nc, "l1exp") as st:
        rows = st.sb("rows", [P, pairs, P])
        rowsT = st.sb("rowsT", [P, 2, BANK])
        y = st.sb("y", [GANG, GANGS, P])
        back = st.sb("back", [P, NT, P])
        bias = st.sb("bias", [P, NT, P])
        ps_t = st.ps("ps_t", [P, 2, BANK])
        ps_y = st.ps("ps_y", [P, 4, BANK])
        scattered = st.sem("scattered")
        rows_loaded = [st.sem(f"rows_loaded{i}") for i in range(LOADS)]
        turned = st.sem("turned")
        rows_ready = st.sem("rows_ready")
        y_done = st.sem("y_done")
        y_copied = [st.sem("y_copied0"), st.sem("y_copied1")]
        y_stored = st.sem("y_stored")
        bias_gathered = st.sem("bias_gathered")
        gathered = [st.sem(f"gathered{j}") for j in range(NC4)]
        chain = st.sem("chain")
        QUADS = GANGS // 4
        with st.block() as block:

            @block.sync
            def _(sp):
                sp.wait_ge(scattered, 16 * NT)
                n = pairs // LOADS
                for i in range(LOADS):
                    src = sorted_in[i * n * P:(i + 1) * n * P, :]
                    sp.dma_start(rows[:, i * n:(i + 1) * n, :], src.rearrange("(k p) f -> p k f", p=P))\
                      .then_inc(rows_loaded[i], 16)
                for i in range(LOADS):
                    for copied in y_copied:
                        sp.wait_ge(copied, QUADS // LOADS * (i + 1) // 2)
                    m = GANGS // LOADS
                    dst = sorted_out[i * m * GANG:(i + 1) * m * GANG, :]
                    sp.dma_start(dst.rearrange("(k p) f -> p k f", p=GANG), y[:, i * m:(i + 1) * m, :])\
                      .then_inc(y_stored, 16)

            @block.gpsimd
            def _(pool):
                pool.wait_ge(zeroed, 17)
                for t in range(NT):
                    pool.indirect_dma_start(out=sorted_in, out_offset=bass.IndirectOffsetOnAxis(
                        ap=slot[:, t:t + 1], axis=0), in_=g.xn[:, t, :], in_offset=None).then_inc(scattered, 16)
                for t in range(NT):
                    pool.indirect_dma_start(out=bias[:, t, :], out_offset=None, in_=d["l1_expert_b"],
                                            in_offset=bass.IndirectOffsetOnAxis(ap=expert_int[:, t:t + 1], axis=0))\
                        .then_inc(bias_gathered, 16)
                pool.wait_ge(y_stored, 16 * LOADS)
                for t in range(NT):
                    pool.indirect_dma_start(out=back[:, t, :], out_offset=None, in_=sorted_out,
                                            in_offset=bass.IndirectOffsetOnAxis(ap=slot[:, t:t + 1], axis=0))\
                        .then_inc(gathered[t // 4], 16)
                for j in range(NC4):
                    pool.wait_ge(gathered[j], 16 * 4)

            @block.tensor
            def _(pe):
                expert_regs = [pe.alloc_register(f"gang_expert{i}") for i in range(GANG_LOAD)]

                def turn(n):
                    if n % (QUADS // LOADS) == 0:
                        pe.wait_ge(rows_loaded[n // (QUADS // LOADS)], 16)
                    if n >= 2:
                        pe.wait_ge(rows_ready, n - 1)
                    for i in range(2):
                        mm = pe.transpose(ps_t[:, n % 2, c1(i)], rows[:, 2 * n + i, :], g.ident[:])
                    mm.then_inc(turned, 1)

                turn(0)
                pe.wait_ge(weights_loaded, 16)
                for n in range(QUADS):
                    if n + 1 < QUADS:
                        turn(n + 1)
                    if 4 * n % GANG_LOAD == 0:
                        pe.reg_load(expert_regs, gang_expert[0:1, 4 * n:4 * n + GANG_LOAD])
                    pe.wait_ge(rows_ready, n + 1)
                    if n >= 4:
                        pe.wait_ge(y_copied[n % 2], (n - 4) // 2 + 1)
                    for i in range(4):
                        e = pe.snap(expert_regs[(4 * n + i) % GANG_LOAD], min_val=0, max_val=EXPERTS - 1)
                        mm = pe.matmul(ps_y[0:GANG, n % 4, c1(i)], rowsT[:, n % 2, GANG * i:GANG * (i + 1)],
                                       W[:, bass.ds(e, 1), :].rearrange("p a f -> p (a f)"), start=True, stop=True)
                    mm.then_inc(y_done, 1)
                for reg in expert_regs:
                    pe.free_register(reg)

            @block.scalar
            def _(act):
                for n in range(QUADS):
                    act.wait_ge(turned, n + 1)
                    if n >= 2:
                        act.wait_ge(y_done, n - 1)
                    act.activation(rowsT[:, n % 2, 0:2 * P], ps_t[:, n % 2, 0:2 * P], ACT.Identity,
                                   bias=mod_col(g, 1, SHIFT_B), scale=mod_col(g, 1, SCALE_B)).then_inc(rows_ready, 1)
                    if n % 2 == 1:
                        act.wait_ge(y_done, n)
                        act.activation(y[:, 4 * n - 4:4 * n, :].rearrange("p k f -> p (k f)"),
                                       ps_y[0:GANG, (n - 1) % 4, :], ACT.Identity).then_inc(y_copied[0], 1)

            @block.vector
            def _(dve):
                link = Chain(dve, chain)
                for n in range(1, QUADS, 2):
                    dve.wait_ge(y_done, n + 1)
                    dve.tensor_copy(y[:, 4 * n:4 * n + 4, :].rearrange("p k f -> p (k f)"), ps_y[0:GANG, n % 4, :])\
                       .then_inc(y_copied[1], 1)
                gate = bcast(mod_row(g, 1, GATE_B).unsqueeze(1), P, NT, P)
                dve.wait_ge(bias_gathered, 16 * NT)
                link(dve.tensor_tensor(bias[:], bias[:], gate, ALU.mult))
                link(dve.tensor_tensor(g.x[:], g.x[:], bias[:], ALU.add))
                for j in range(NC4):
                    dve.wait_ge(gathered[j], 16 * 4)
                    ts = slice(4 * j, 4 * j + 4)
                    link(dve.tensor_tensor(back[:, ts, :], back[:, ts, :], gate[:, ts, :], ALU.mult))
                    dve.tensor_tensor(g.x[:, ts, :], g.x[:, ts, :], back[:, ts, :], ALU.add)


def layer1_experts(nc, d, g):
    sorted_in = nc.dram_tensor("l1_sorted_in", [GANGS * GANG, P], F32, kind="Internal").ap()
    sorted_out = nc.dram_tensor("l1_sorted_out", [GANGS * GANG, P], F32, kind="Internal").ap()
    with Stage(nc, "l1ffn") as st:
        W = st.sb("W", [P, EXPERTS, P])
        zeros = st.sb("zeros", [P, P])
        slot = st.sb("slot", [P, NT], I32)
        expert_int = st.sb("expert_int", [P, NT], I32)
        gang_expert = st.sb("gang_expert", [1, GANGS], I32)
        zeroed = st.sem("zeroed")
        weights_loaded = st.sem("weights_loaded")
        for_route = Loads(nc, d, st, "route", "l1_gateT", "l1_gate_b", "iota", "iota_row", "not_yet", "carry")
        nc.gpsimd.memset(zeros[:], 0.0).then_inc(zeroed, 1)
        nc.sync.wait_ge(zeroed, 1)
        nc.sync.dma_start(sorted_in.rearrange("(p i) f -> p i f", p=P),
                          bcast(zeros[:].unsqueeze(1), P, GANGS * GANG // P, P)).then_inc(zeroed, 16)
        nc.sync.dma_start(W[:], d["l1_expert_w"].rearrange("e d o -> d e o")).then_inc(weights_loaded, 16)
        adaln(nc, g, 1, SCALE_B, SHIFT_B)
        stage_l1_route(nc, for_route, g, slot, expert_int, gang_expert)
        stage_l1_experts(nc, d, g, W, sorted_in, sorted_out, zeroed, weights_loaded, slot, expert_int, gang_expert)



LIF_CELLS = 256


class LifMemory:

    def __init__(self, st):
        self.v = st.sb("lif_v", [P, LIF_CELLS])
        self.mid = st.sb("lif_mid", [P, LIF_CELLS])
        self.differ = st.sb("lif_differ", [P, LIF_CELLS])
        self.shifted = st.sb("lif_shifted", [P, LIF_CELLS])
        self.count = st.sb("lif_count", [P, 32])
        self.count_turned = st.sb("lif_count_turned", [P, 32])
        self.count_int = st.sb("lif_count_int", [P, 1], I32)
        self.step = st.sem("lif_step")


def lif(dve, name, X, U, groups, length, check, m):
    chunks = S // length
    cells = groups * chunks
    assert cells <= LIF_CELLS and 0 < check <= length
    u_of = U.rearrange("p g (c l) -> p (g c) l", l=length)
    x_of = X.rearrange("p g (c l) -> p (g c) l", l=length)
    v, mid, differ, shifted = (buf[:, 0:cells] for buf in (m.v, m.mid, m.differ, m.shifted))
    by_group = lambda ap: ap.rearrange("p (g c) -> p g c", g=groups)
    unsettled = dve.alloc_register(f"{name}_unsettled")
    parts = [dve.alloc_register(f"{name}_unsettled_in_quadrant{i}") for i in range(4)]

    halves = (slice(0, cells // 2), slice(cells // 2, cells))

    def steps(link, first, last):
        for t in range(first, last):
            before = v if t > 0 else shifted
            for half in halves:
                link.mark(dve.scalar_tensor_tensor(u_of[:, half, t], before[:, half], 0.5, x_of[:, half, t],
                                                   ALU.mult, ALU.add))
                dve.wait_ge(m.step, link.n - 1)
            for half in halves:
                link.mark(dve.scalar_tensor_tensor(v[:, half], u_of[:, half, t], 1.0, u_of[:, half, t],
                                                   ALU.is_lt, ALU.mult))
                dve.wait_ge(m.step, link.n - 1)
        link.wait()

    dve.sem_clear(m.step)
    link = Chain(dve, m.step)
    link.mark(dve.memset(m.shifted[:], 0.0))
    link(dve.memset(m.count[:], 0.0))
    steps(link, 0, check)
    link(dve.tensor_copy(mid, v))
    dve.reg_mov(unsettled, 1)
    with dve.While(lambda: dve.snap(unsettled)):
        dve.sem_clear(m.step)
        link = Chain(dve, m.step)
        steps(link, check, length)
        link(dve.tensor_copy(by_group(shifted)[:, :, 1:chunks], by_group(v)[:, :, 0:chunks - 1]))
        steps(link, 0, check)
        link(dve.tensor_tensor(differ, v, mid, ALU.not_equal))
        link.mark(dve.tensor_copy(mid, v))
        link(dve.tensor_reduce(m.count[:, 0:1], differ, AX_X, ALU.add))
        link(dve.transpose(m.count_turned[:], m.count[:]))
        link(dve.tensor_reduce(m.differ[:, 0:1], m.count_turned[:], AX_X, ALU.add))
        link(dve.tensor_copy(m.count_int[:], m.differ[:, 0:1]))
        for i, part in enumerate(parts):
            dve.reg_load(part, m.count_int[32 * i:32 * i + 1, 0:1])
        dve.reg_add(unsettled, parts[0], parts[1])
        dve.reg_add(unsettled, unsettled, parts[2])
        dve.reg_add(unsettled, unsettled, parts[3])
    for r in parts + [unsettled]:
        dve.free_register(r)


def stage_l2_mix(nc, loads, g, h_tm, r):
    with Stage(nc, "l2mix") as st:
        w = loads["l2_wrkvo"]
        X = st.sb("X", [P, 3, S])
        U = st.sb("U", [P, 3, S])
        decay = st.sb("decay", [P, S])
        m = LifMemory(st)
        ps = st.ps("ps", [P, 8, BANK])
        in_done = st.sem("in_done")
        in_copied = st.sem("in_copied")
        h_scaled = st.sem("h_scaled")
        y_ready = st.sem("y_ready")
        out_done = st.sem("out_done")
        chain = st.sem("chain")
        with st.block() as block:

            @block.tensor
            def _(pe):
                pe.wait_ge(loads.done, loads.all)
                for n in range(3 * NC4):
                    if n >= 8:
                        pe.wait_ge(in_copied, n - 7)
                    pe.matmul(ps[:, n % 8, :], w[:, n // NC4, :], g.hT[:, c4(n % NC4)], start=True,
                              stop=True).then_inc(in_done, 1)
                pe.wait_ge(y_ready, 1)
                for t in range(NT):
                    mm = pe.matmul(ps[:, t // 4, c1(t % 4)], X[:, 0, c1(t)], w[:, 3, :], start=True, stop=True)
                    if t % 4 == 3:
                        mm.then_inc(out_done, 1)

            @block.scalar
            def _(act):
                for n in range(3 * NC4):
                    act.wait_ge(in_done, n + 1)
                    act.activation(X[:, n // NC4, c4(n % NC4)], ps[:, n % 8, :], ACT.Identity,
                                   scale=0.5).then_inc(in_copied, 1)

            @block.gpsimd
            def _(pool):
                pool.tensor_tensor(h_tm[:], g.xn[:], bcast(mod_row(g, 2, SCALE_A).unsqueeze(1), P, NT, P),
                                   ALU.mult).then_inc(h_scaled, 1)
                pool.wait_ge(h_scaled, 1)
                pool.tensor_tensor(h_tm[:], h_tm[:], bcast(mod_row(g, 2, SHIFT_A).unsqueeze(1), P, NT, P),
                                   ALU.add).then_inc(h_scaled, 1)
                pool.wait_ge(h_scaled, 2)

            @block.vector
            def _(dve):
                link = Chain(dve, chain)
                link.mark(dve.memset(decay[:], 0.9))
                dve.wait_ge(in_copied, 3 * NC4)
                lif(dve, "rkv", X[:], U[:], 3, 32, 32, m)
                r_u, k_u, v_u = (U[:, i, :] for i in range(3))
                y, kv, acc = (X[:, i, :] for i in range(3))
                link(dve.tensor_scalar(v_u, v_u, 1.0, None, ALU.is_ge))
                link(dve.scalar_tensor_tensor(kv, k_u, 1.0, v_u, ALU.is_ge, ALU.mult))
                link(dve.tensor_tensor_scan(acc, decay[:], kv, 0.0, ALU.mult, ALU.add))
                dve.scalar_tensor_tensor(y, r_u, 1.0, acc, ALU.is_ge, ALU.mult).then_inc(y_ready, 1)
                dve.wait_ge(h_scaled, 2)
                for j in range(NC4):
                    dve.wait_ge(out_done, j + 1)
                    ts = slice(4 * j, 4 * j + 4)
                    dve.tensor_tensor(r[:, ts, :], ps[:, j, :].rearrange("p (t f) -> p t f", t=4), h_tm[:, ts, :],
                                      ALU.add)


def stage_l2_hidden(nc, loads, x1n, x1T, x1_tm, X):
    with Stage(nc, "l2hid") as st:
        w1 = loads["l2_w1T"]
        b1 = loads["l2_b1"]
        half_b = st.sb("half_b", [P, 4])
        gain = loads["l2_ln1g"]
        shift = loads["l2_ln1b"]
        ps = st.ps("ps", [P, 8, BANK])
        bias_ready = st.sem("bias_ready")
        in_done = st.sem("in_done")
        in_copied = st.sem("in_copied")
        x1_scaled = st.sem("x1_scaled")
        with st.block() as block:

            @block.tensor
            def _(pe):
                pe.wait_ge(loads.done, loads.all)
                for n in range(4 * NC4):
                    if n >= 8:
                        pe.wait_ge(in_copied, n - 7)
                    pe.matmul(ps[:, n % 8, :], w1[:, n // NC4, :], x1T[:, c4(n % NC4)], start=True,
                              stop=True).then_inc(in_done, 1)

            @block.scalar
            def _(act):
                act.wait_ge(bias_ready, 1)
                for n in range(4 * NC4):
                    act.wait_ge(in_done, n + 1)
                    f = n // NC4
                    act.activation(X[:, f, c4(n % NC4)], ps[:, n % 8, :], ACT.Identity, scale=0.5,
                                   bias=half_b[:, f:f + 1]).then_inc(in_copied, 1)

            @block.vector
            def _(dve):
                dve.wait_ge(loads.done, loads.all)
                dve.tensor_scalar(half_b[:], b1[:], 0.5, None, ALU.mult).then_inc(bias_ready, 1)

            @block.gpsimd
            def _(pool):
                pool.wait_ge(loads.done, loads.all)
                pool.tensor_tensor(x1_tm[:], x1n[:], bcast(gain[:].unsqueeze(1), P, NT, P), ALU.mult)\
                    .then_inc(x1_scaled, 1)
                pool.wait_ge(x1_scaled, 1)
                pool.tensor_tensor(x1_tm[:], x1_tm[:], bcast(shift[:].unsqueeze(1), P, NT, P), ALU.add)\
                    .then_inc(x1_scaled, 1)
                pool.wait_ge(x1_scaled, 2)


def stage_l2_spikes(nc, loads, g, X, x1_tm):
    with Stage(nc, "l2spk") as st:
        w2 = loads["l2_w2T"]
        b2 = loads["l2_b2"]
        half_b = st.sb("half_b", [P, 1])
        U = st.sb("U", [P, 4, S])
        m = LifMemory(st)
        ps = st.ps("ps", [P, 4, BANK])
        ps_t = st.ps("ps_t", [P, 4, BANK])
        bias_ready = st.sem("bias_ready")
        s_ready = st.sem("s_ready")
        h2_done = st.sem("h2_done")
        h2_copied = st.sem("h2_copied")
        out_ready = st.sem("out_ready")
        turned = st.sem("turned")
        with st.block() as block:

            @block.tensor
            def _(pe):
                pe.wait_ge(loads.done, loads.all)
                for f in range(4):
                    pe.wait_ge(s_ready, f + 1)
                    for j in range(NC4):
                        mm = pe.matmul(ps[:, j, :], w2[:, f, :], U[:, f, c4(j)], start=(f == 0), stop=(f == 3))
                mm.then_inc(h2_done, 1)
                pe.wait_ge(out_ready, 1)
                for t in range(NT):
                    mm = pe.transpose(ps_t[:, t // 4, c1(t % 4)], U[:, 0, c1(t)], g.ident[:])
                    if t % 4 == 3:
                        mm.then_inc(turned, 1)

            @block.scalar
            def _(act):
                act.wait_ge(bias_ready, 1)
                act.wait_ge(h2_done, 1)
                for j in range(NC4):
                    act.activation(X[:, 0, c4(j)], ps[:, j, :], ACT.Identity, scale=0.5, bias=half_b[:])\
                       .then_inc(h2_copied, 1)

            @block.vector
            def _(dve):
                dve.wait_ge(loads.done, loads.all)
                dve.tensor_scalar(half_b[:], b2[:], 0.5, None, ALU.mult).then_inc(bias_ready, 1)
                lif(dve, "hidden", X[:], U[:], 4, 64, 44, m)
                for f in range(4):
                    dve.tensor_scalar(U[:, f, :], U[:, f, :], 1.0, None, ALU.is_ge).then_inc(s_ready, 1)
                dve.wait_ge(h2_copied, NC4)
                lif(dve, "out", X[:, 0:1, :], U[:, 0:1, :], 1, 16, 16, m)
                dve.tensor_scalar(U[:, 0, :], U[:, 0, :], 1.0, None, ALU.is_ge).then_inc(out_ready, 1)
                for j in range(NC4):
                    dve.wait_ge(turned, j + 1)
                    ts = slice(4 * j, 4 * j + 4)
                    dve.tensor_tensor(x1_tm[:, ts, :], ps_t[:, j, :].rearrange("p (t f) -> p t f", t=4),
                                      x1_tm[:, ts, :], ALU.add)


def layer2_spiking(nc, d, g):
    with Stage(nc, "l2") as st:
        for_mix = Loads(nc, d, st, "mix", "l2_wrkvo")
        for_norm = Loads(nc, d, st, "norm", "l2_ln1cols")
        for_hidden = Loads(nc, d, st, "hidden", "l2_w1T", "l2_b1", "l2_ln1g", "l2_ln1b")
        for_spikes = Loads(nc, d, st, "spikes", "l2_w2T", "l2_b2")
        for_add = Loads(nc, d, st, "add", "l2_ln2g", "l2_ln2b")
        adaln(nc, g, 2, SCALE_A, SHIFT_A)
        h_tm = st.sb("h_tm", [P, NT, P])
        x1_tm = st.sb("x1_tm", [P, NT, P])
        ln_cols = for_norm["l2_ln1cols"]
        nc.scalar.wait_ge(for_norm.done, for_norm.all)
        stage_l2_mix(nc, for_mix, g, h_tm, x1_tm)
        stage_norm(nc, g, "l2norm1", x1_tm, h_tm, g.hT, ln_cols[:, 0:1], ln_cols[:, 1:2])
        X = st.sb("X", [P, 4, S])
        stage_l2_hidden(nc, for_hidden, h_tm, g.hT, x1_tm, X)
        stage_l2_spikes(nc, for_spikes, g, X, x1_tm)
        stage_norm(nc, g, "l2norm2", x1_tm, g.xn)
        stage_add_affine(nc, for_add, "l2_ln2g", "l2_ln2b", g, "l2add", g.xn, mod_row(g, 2, GATE_A))



def layer2_product(nc, d, g):
    with Stage(nc, "l2ffn") as st:
        loads = Loads(nc, d, st, "product", "l2_CBT", "l2_SCB", "l2_bias")
        adaln(nc, g, 2, SCALE_B, SHIFT_B)
        w = loads["l2_CBT"]
        scale = loads["l2_SCB"]
        bias = loads["l2_bias"]
        tmp = st.sb("tmp", [P, 2, 4, P])
        ps = st.ps("ps", [P, 4, BANK])
        rows_ready = st.sem("rows_ready")
        done = st.sem("done")
        shifted = st.sem("shifted")
        chain = st.sem("chain")
        with st.block() as block:

            @block.tensor
            def _(pe):
                pe.wait_ge(loads.done, loads.all)
                for t in range(NT):
                    mm = pe.matmul(ps[:, t // 4, c1(t % 4)], g.hT[:, c1(t)], w[:], start=True, stop=True)
                    if t % 4 == 3:
                        mm.then_inc(done, 1)

            @block.gpsimd
            def _(pool):
                pool.wait_ge(rows_ready, 1)
                pool.tensor_tensor(g.x[:], g.x[:], bcast(bias[:].unsqueeze(1), P, NT, P), ALU.add).then_inc(shifted, 1)
                pool.wait_ge(shifted, 1)

            @block.vector
            def _(dve):
                link = Chain(dve, chain)
                gate = mod_row(g, 2, GATE_B)
                dve.wait_ge(loads.done, loads.all)
                link(dve.tensor_scalar(scale[:], scale[:], 1.0 / 127.0, None, ALU.mult))
                link.mark(dve.tensor_tensor(scale[:], scale[:], gate, ALU.mult))
                dve.tensor_tensor(bias[:], bias[:], gate, ALU.mult).then_inc(rows_ready, 1)
                link.wait()
                for j in range(NC4):
                    dve.wait_ge(done, j + 1)
                    link(dve.tensor_tensor(tmp[:, j % 2], ps[:, j, :].rearrange("p (t f) -> p t f", t=4),
                                           bcast(scale[:].unsqueeze(1), P, 4, P), ALU.mult))
                    if j == 0:
                        dve.wait_ge(shifted, 1)
                    xs = g.x[:, 4 * j:4 * j + 4, :]
                    dve.tensor_tensor(xs, xs, tmp[:, j % 2], ALU.add)



WINDOW = 32
SPAN = P + WINDOW
L3_H, L3_K = 16, 8
LAT_H, LAT_K, LATENTS = 8, 8, 64


def load_group(sp, Q, K, q_parts, k_parts, grp, loaded):
    for r in range(6):
        for operand, dram, part, at in ((Q, q_parts, SPLITS_Q[r], 0), (K, k_parts, SPLITS_K[r], WINDOW)):
            src = dram[part, GROUP * L3_K * grp:GROUP * L3_K * (grp + 1), :].rearrange("(h k) t -> k h t", k=L3_K)
            sp.dma_start(operand[L3_K * r:L3_K * (r + 1), grp % 2, :, at:at + S], src).then_inc(loaded[grp % 2], 16)


def stage_l3_latent(nc, loads, g, q, rem, gates, Q, K, q_parts, k_parts, stored, group_loaded):
    PROBS = 3
    with Stage(nc, "l3lat") as st:
        wg = loads["l3_wg"]
        r_out = loads["l3_r_out"]
        head_rows = loads["head_rows"]
        gate_w = loads["l3_gates"]
        gate_m = st.sb("gate_m", [P, 2, L3_H])
        causal = loads["lat_causal"]
        ident16 = loads["ident16"]
        gqT = st.sb("gqT", [LATENTS, S])
        pooled = st.sb("pooled", [P, LATENTS])
        gk = st.sb("gk", [LATENTS, LAT_H, LATENTS])
        gv = st.sb("gv", [LATENTS, LAT_H, LATENTS])
        R = st.sb("R", [P, 4, P])
        sc = st.sb("sc", [P, 2, LAT_H, LATENTS])
        probs = st.sb("probs", [P, PROBS, LAT_H, LATENTS])
        top = st.sb("top", [P, 2, LAT_H])
        den = st.sb("den", [P, 2, LAT_H])
        rden = st.sb("rden", [P, 2, LAT_H])
        PT = st.sb("PT", [P, 2, BANK])
        ps_a = st.ps("ps_a", [P, 4, BANK])
        ps_t = st.ps("ps_t", [P, 2, BANK])
        ps_r = st.ps("ps_r", [P, 2, BANK])
        gq_done = st.sem("gq_done")
        gq_copied = st.sem("gq_copied")
        pool_ready = st.sem("pool_ready")
        gkv_done = st.sem("gkv_done")
        gkv_ready = st.sem("gkv_ready")
        r_done = st.sem("r_done")
        r_copied = st.sem("r_copied")
        gm_ready = st.sem("gm_ready")
        gates_done = st.sem("gates_done")
        gates_read = st.sem("gates_read")
        scored = st.sem("scored")
        sub_ready = st.sem("sub_ready")
        expd = st.sem("expd")
        rden_ready = st.sem("rden_ready")
        p_ready = st.sem("p_ready")
        turned = st.sem("turned")
        pt_copied = st.sem("pt_copied")
        rem_done = st.sem("rem_done")
        rem_copied = st.sem("rem_copied")
        chain = st.sem("chain")
        with st.block() as block:

            @block.sync
            def _(sp):
                sp.wait_ge(stored, 16 * 6)
                for grp in range(2):
                    load_group(sp, Q, K, q_parts, k_parts, grp, group_loaded)

            @block.tensor
            def _(pe):
                pe.wait_ge(loads.done, loads.all)
                for j in range(NC4):
                    pe.matmul(ps_a[0:LATENTS, j, :], wg[:, 0, :], g.hT[:, c4(j)], start=True, stop=True)\
                      .then_inc(gq_done, 1)
                pe.wait_ge(pool_ready, 1)
                for i in range(2):
                    mm = pe.matmul(ps_t[0:LATENTS, i, 0:LATENTS], wg[:, 1 + i, :], pooled[:], start=True, stop=True)
                mm.then_inc(gkv_done, 1)
                pe.wait_ge(gm_ready, 1)
                for t in range(NT):
                    mm = pe.matmul(ps_r[:, 0, 2 * L3_H * t:2 * L3_H * (t + 1)], q[:, c1(t)],
                                   gate_m[:].rearrange("p a h -> p (a h)"), start=True, stop=True)
                mm.then_inc(gates_done, 1)
                pe.wait_ge(gkv_ready, 2)
                for c in range(4):
                    mm = pe.matmul(ps_r[:, 1, c1(c)], gv[:, 2 * c:2 * c + 2, :].rearrange("p h n -> p (h n)"),
                                   r_out[:], start=True, stop=True)
                mm.then_inc(r_done, 1)

                def score(t):
                    if t < 4:
                        pe.wait_ge(gq_copied, NC4)
                    else:
                        pe.wait_ge(sub_ready, t - 3)
                    pe.matmul(ps_a[:, t % 4, :], ident16[:], bcast(causal[:, t:t + 1, :], P, LAT_H, LATENTS),
                              start=True, stop=False)
                    pe.matmul(ps_a[:, t % 4, :], gqT[:, c1(t)], gk[:].rearrange("p h n -> p (h n)"), start=False,
                              stop=True).then_inc(scored, 1)

                def turn(t):
                    pe.wait_ge(p_ready, t + 1)
                    if t == 0:
                        pe.wait_ge(gkv_ready, 2)
                    if t >= 2:
                        pe.wait_ge(pt_copied, t - 1)
                    p = probs[:, t % PROBS, :, :].rearrange("p h n -> p (h n)")
                    for c in range(4):
                        mm = pe.transpose(ps_t[:, t % 2, c1(c)], p[:, c1(c)], g.ident[:])
                    mm.then_inc(turned, 1)

                def values(t):
                    pe.wait_ge(pt_copied, t + 1)
                    if t < 2:
                        pe.wait_ge(r_copied, 1)
                        pe.wait_ge(gates_read, 1)
                    else:
                        pe.wait_ge(rem_copied, t - 1)
                    for c in range(4):
                        mm = pe.matmul(ps_r[:, t % 2, 0:P], PT[:, t % 2, c1(c)], R[:, c, :], start=(c == 0),
                                       stop=(c == 3))
                    mm.then_inc(rem_done, 1)

                score(0)
                score(1)
                for t in range(NT + 1):
                    if t + 2 < NT:
                        score(t + 2)
                    if t < NT:
                        turn(t)
                    if t >= 1:
                        values(t - 1)

            @block.scalar
            def _(act):
                for j in range(NC4):
                    act.wait_ge(gq_done, j + 1)
                    act.activation(gqT[:, c4(j)], ps_a[0:LATENTS, j, :], ACT.Identity, scale=LAT_K ** -0.5)\
                       .then_inc(gq_copied, 1)
                act.wait_ge(gates_done, 1)
                act.activation(gates[:].rearrange("p a t h -> p t a h"),
                               ps_r[:, 0, :].rearrange("p (t a h) -> p t a h", t=NT, a=2), ACT.Sigmoid,
                               scale=L3_K ** 0.5).then_inc(gates_read, 1)
                act.wait_ge(r_done, 1)
                act.activation(R[:].rearrange("p c f -> p (c f)"), ps_r[:, 1, :], ACT.Identity).then_inc(r_copied, 1)
                for t in range(NT + 1):
                    if t < NT:
                        act.wait_ge(sub_ready, t + 1)
                        if t >= PROBS:
                            act.wait_ge(turned, t - PROBS + 1)
                        act.activation(probs[:, t % PROBS], sc[:, t % 2], ACT.Exp).then_inc(expd, 1)
                    if t >= 1:
                        act.wait_ge(turned, t)
                        if t >= 3:
                            act.wait_ge(rem_done, t - 2)
                        act.activation(PT[:, (t - 1) % 2, :], ps_t[:, (t - 1) % 2, :], ACT.Identity)\
                           .then_inc(pt_copied, 1)

            @block.gpsimd
            def _(pool):
                for t in range(NT):
                    pool.wait_ge(rden_ready, t + 1)
                    p = probs[:, t % PROBS]
                    pool.tensor_tensor(p, p, bcast(rden[:, t % 2, :].unsqueeze(2), P, LAT_H, LATENTS), ALU.mult)\
                        .then_inc(p_ready, 1)
                pool.wait_ge(p_ready, NT)

            @block.vector
            def _(dve):
                link = Chain(dve, chain)
                dve.wait_ge(loads.done, loads.all)
                link.mark(dve.tensor_scalar(gate_m[:, 0, :], head_rows[:], gate_w[:, 0:1], None, ALU.mult))
                dve.tensor_scalar(gate_m[:, 1, :], head_rows[:], gate_w[:, 1:2], None, ALU.mult).then_inc(gm_ready, 1)
                link(dve.tensor_reduce(pooled[:], g.hT[:].rearrange("p (n c) -> p n c", c=S // LATENTS), AX_X,
                                       ALU.add))
                dve.tensor_scalar(pooled[:], pooled[:], LATENTS / S, None, ALU.mult).then_inc(pool_ready, 1)
                dve.wait_ge(gkv_done, 1)
                for i, blocks in enumerate((gk, gv)):
                    dve.tensor_tensor(blocks[:], bcast(ps_t[0:LATENTS, i:i + 1, 0:LATENTS], LATENTS, LAT_H, LATENTS),
                                      bcast(head_rows[0:LATENTS, 0:LAT_H].unsqueeze(2), LATENTS, LAT_H, LATENTS),
                                      ALU.mult).then_inc(gkv_ready, 1)
                for t in range(NT + 3):
                    if t < NT:
                        b = t % 2
                        dve.wait_ge(scored, t + 1)
                        s3 = ps_a[:, t % 4, :].rearrange("p (h n) -> p h n", h=LAT_H)
                        link(dve.tensor_reduce(top[:, b, :], s3, AX_X, ALU.max))
                        if t >= 2:
                            dve.wait_ge(expd, t - 1)
                        dve.tensor_tensor(sc[:, b], s3, bcast(top[:, b, :].unsqueeze(2), P, LAT_H, LATENTS),
                                          ALU.subtract).then_inc(sub_ready, 1)
                    if 1 <= t <= NT:
                        b, pb = (t - 1) % 2, (t - 1) % PROBS
                        dve.wait_ge(expd, t)
                        link(dve.tensor_reduce(den[:, b, :], probs[:, pb], AX_X, ALU.add))
                        if t >= 3:
                            dve.wait_ge(p_ready, t - 2)
                        dve.reciprocal(rden[:, b, :], den[:, b, :]).then_inc(rden_ready, 1)
                    if t >= 3:
                        dve.wait_ge(rem_done, t - 2)
                        dve.tensor_copy(rem[:, t - 3, :], ps_r[:, (t - 3) % 2, 0:P]).then_inc(rem_copied, 1)


def stage_l3_local(nc, loads, g, V_aug, Q, K, q_parts, k_parts, loaded, O):
    NG = L3_H // GROUP
    FIRST, PACE = 6, 2
    ahead = lambda t: range(PACE * (t - FIRST), PACE * (t - FIRST + 1)) if FIRST <= t < FIRST + NT // PACE else ()
    NEGATE = FIRST + NT // PACE
    with Stage(nc, "l3loc") as st:
        mask_q = loads["mask_q"]
        mask_k = loads["mask_k"]
        ident16 = loads["ident16"]
        maxima = st.sb("maxima", [P, NT, GROUP])
        negmax = st.sb("negmax", [P, GROUP, NT])
        rest = st.sb("rest", [P, GROUP, NT])
        nm = st.sb("nm", [P, GROUP, 3, NT], BF16)
        nm_rows = st.sb("nm_rows", [3 * NT, GROUP, P], BF16)
        probs = st.sb("probs", [P, 3, GROUP, SPAN])
        pv_sb = st.sb("pv_sb", [P, 2, BANK])
        rden = st.sb("rden", [P, 4, GROUP])
        ps_m = st.ps("ps_m", [P, 2, BANK])
        ps_s = st.ps("ps_s", [P, 4, BANK])
        ps_v = st.ps("ps_v", [P, BANK])
        ps_t = st.ps("ps_t", [P, BANK])
        cleared = st.sem("cleared")
        m_done = st.sem("m_done")
        m_read = st.sem("m_read")
        nm_ready = st.sem("nm_ready")
        nm_turned = st.sem("nm_turned")
        nm_rows_ready = st.sem("nm_rows_ready")
        nm_placed = st.sem("nm_placed")
        scored = st.sem("scored")
        expd = st.sem("expd")
        pv_done = st.sem("pv_done")
        pv_copied = st.sem("pv_copied")
        pv_turned = st.sem("pv_turned")
        o_ready = st.sem("o_ready")
        chain = st.sem("chain")
        heads2 = lambda ap: ap.rearrange("p (h c) -> p h c", h=2)

        with st.block() as block:

            @block.sync
            def _(sp):
                for grp in range(NG):
                    if grp >= 2:
                        sp.wait_ge(scored, (grp - 1) * NT)
                        load_group(sp, Q, K, q_parts, k_parts, grp, loaded)
                        sp.wait_ge(cleared, grp - 1)
                    sp.wait_ge(nm_rows_ready, grp + 1)
                    for h in range(GROUP):
                        sp.dma_start(Q[MAX_ROW:MAX_ROW + 3, grp % 2, h, 0:S], nm_rows[:, h, :]).then_inc(nm_placed, 16)

            @block.gpsimd
            def _(pool):
                for grp in range(2, NG):
                    pool.wait_ge(scored, (grp - 1) * NT)
                    pool.memset(Q[MAX_ROW:MAX_ROW + 3, grp % 2, :, :], 0.0).then_inc(cleared, 1)

            @block.tensor
            def _(pe):
                pe.wait_ge(loads.done, loads.all)

                def maxima_of(grp, t):
                    par = grp % 2
                    if t == 0:
                        pe.wait_ge(loaded[par], 16 * 12 * (grp // 2 + 1))
                        if grp >= 2:
                            pe.wait_ge(cleared, grp - 1)
                    for half in range(2):
                        n = 2 * (NT * grp + t) + half
                        if n >= 2:
                            pe.wait_ge(m_read, n - 1)
                        dst = ps_m[:, n % 2, 0:2 * SPAN]
                        pe.matmul(dst, ident16[:], bcast(mask_q[:, min(t, 1), :, :], P, 2, SPAN), start=True,
                                  stop=False)
                        for i in range(2):
                            h = 2 * half + i
                            mm = pe.matmul(dst[:, i * SPAN:(i + 1) * SPAN], Q[:, par, h, c1(t)],
                                           K[:, par, h, t * P:t * P + SPAN], start=False, stop=(i == 1))
                        mm.then_inc(m_done, 1)

                def turn_maxima(grp):
                    pe.wait_ge(nm_ready, grp + 1)
                    if grp >= 1:
                        pe.wait_ge(o_ready, NC4 * (grp - 1) + 3)
                    for h in range(GROUP):
                        mm = pe.transpose(ps_t[0:3 * NT, h * 64:h * 64 + 64].bitcast(BF16),
                                          nm[:, h, :, :].rearrange("p s t -> p (s t)"), ident16[:])
                    mm.then_inc(nm_turned, 1)

                def values(grp, t):
                    n = NT * grp + t
                    pe.wait_ge(expd, n + 1)
                    if t % 4 == 0 and n >= 4:
                        pe.wait_ge(pv_copied, n // 4)
                    for h in range(GROUP):
                        out = ps_v[32 * h:32 * h + 32, c1(t % 4)]
                        mm = pe.matmul(out, V_aug[:, t, GROUP * grp + h, :], probs[:, n % 3, h, 0:P], start=True,
                                       stop=(t == 0), skip_group_check=True)
                    if t >= 1:
                        for h in range(GROUP):
                            out = ps_v[32 * h:32 * h + 32, c1(t % 4)]
                            mm = pe.matmul(out[:, 0:WINDOW], V_aug[:, t - 1, GROUP * grp + h, :],
                                           probs[:, (n - 1) % 3, h, P:SPAN], start=False, stop=True,
                                           skip_group_check=True)
                    mm.then_inc(pv_done, 1)

                def turn_values(n):
                    pe.wait_ge(pv_copied, n + 1)
                    if n >= 1:
                        pe.wait_ge(o_ready, n)
                    if n % NC4 == NC4 - 1 and n // NC4 + 1 < NG:
                        pe.wait_ge(nm_rows_ready, n // NC4 + 2)
                    elif n == 0:
                        pe.wait_ge(nm_rows_ready, 1)
                    for i in range(4):
                        mm = pe.transpose(ps_t[:, c1(i)], pv_sb[:, n % 2, c1(i)], g.ident[:])
                    mm.then_inc(pv_turned, 1)

                for t in range(NT):
                    maxima_of(0, t)
                turn_maxima(0)
                for grp in range(NG):
                    pe.wait_ge(nm_placed, 16 * GROUP * (grp + 1))
                    par = grp % 2
                    for t in range(NT + 1):
                        if grp + 1 < NG:
                            for m in ahead(t)[:1]:
                                maxima_of(grp + 1, m)
                            if t == NT - 1:
                                turn_maxima(grp + 1)
                        if t < NT:
                            n = NT * grp + t
                            if n >= 2:
                                pe.wait_ge(expd, n - 1)
                            for half in range(2):
                                dst = ps_s[:, 2 * (n % 2) + half, 0:2 * SPAN]
                                pe.matmul(dst, ident16[:], bcast(mask_k[:], P, 2, SPAN), start=True, stop=False)
                                for i in range(2):
                                    h = 2 * half + i
                                    mm = pe.matmul(dst[:, i * SPAN:(i + 1) * SPAN],
                                                   K[:, par, h, WINDOW + t * P:WINDOW + (t + 1) * P],
                                                   Q[:, par, h, t * P:t * P + SPAN], start=False, stop=(i == 1))
                            mm.then_inc(scored, 1)
                        if grp + 1 < NG:
                            for m in ahead(t)[1:]:
                                maxima_of(grp + 1, m)
                        if t >= 1:
                            values(grp, t - 1)
                        if t >= 6 and (t - 6) % 4 == 0:
                            turn_values(NC4 * grp + (t - 6) // 4)
                    turn_values(NC4 * grp + NC4 - 1)

            @block.scalar
            def _(act):
                for n in range(NG * NT):
                    act.wait_ge(scored, n + 1)
                    if n >= 3:
                        act.wait_ge(pv_done, n - 1)
                    b = 2 * (n % 2)
                    act.activation(probs[:, n % 3, :, :].rearrange("p (b h) c -> p b (h c)", b=2),
                                   ps_s[:, b:b + 2, 0:2 * SPAN], ACT.Exp).then_inc(expd, 1)

            @block.vector
            def _(dve):
                link = Chain(dve, chain)

                def maxima_of(grp, t):
                    for half in range(2):
                        n = 2 * (NT * grp + t) + half
                        dve.wait_ge(m_done, n + 1)
                        dve.tensor_reduce(maxima[:, t, 2 * half:2 * half + 2], heads2(ps_m[:, n % 2, 0:2 * SPAN]),
                                          AX_X, ALU.max).then_inc(m_read, 1)

                def negate(grp):
                    dve.wait_ge(m_read, 2 * NT * (grp + 1))
                    link(dve.tensor_scalar(negmax[:], maxima[:].rearrange("p t h -> p h t"), -1.0, None, ALU.mult))
                    if grp >= 1:
                        dve.wait_ge(nm_turned, grp)
                    splits_of(link, dve, [nm[:, :, i, :] for i in range(3)], rest[:], negmax[:], nm_ready)

                def copy_maxima(grp):
                    dve.wait_ge(nm_turned, grp + 1)
                    if grp >= 1:
                        dve.wait_ge(nm_placed, 16 * GROUP * grp)
                    dve.tensor_copy(nm_rows[:], ps_t[0:3 * NT, 0:4 * 64].bitcast(BF16).rearrange(
                        "p (h q) -> p h q", h=GROUP)).then_inc(nm_rows_ready, 1)

                def copy_values(n):
                    dve.wait_ge(pv_done, 4 * (n + 1))
                    if n >= 2:
                        dve.wait_ge(pv_turned, n - 1)
                    dve.tensor_copy(pv_sb[:, n % 2, :], ps_v[:]).then_inc(pv_copied, 1)

                def values_of(n):
                    grp, c = n // NC4, n % NC4
                    dve.wait_ge(pv_turned, n + 1)
                    v = ps_t[:, 0:BANK].rearrange("p (t h k) -> p t h k", t=4, h=GROUP)
                    link(dve.reciprocal(rden[:], v[:, :, :, L3_K]))
                    o = O[:, 4 * c:4 * c + 4, L3_K * GROUP * grp:L3_K * GROUP * (grp + 1)].rearrange(
                        "p t (h k) -> p t h k", k=L3_K)
                    dve.tensor_tensor(o, v[:, :, :, 0:L3_K], bcast(rden[:].unsqueeze(3), P, 4, GROUP, L3_K),
                                      ALU.mult).then_inc(o_ready, 1)

                for t in range(NT):
                    maxima_of(0, t)
                negate(0)
                copy_maxima(0)
                for grp in range(NG):
                    for t in range(NT):
                        if grp + 1 < NG:
                            for m in ahead(t):
                                maxima_of(grp + 1, m)
                            if t == NEGATE:
                                negate(grp + 1)
                        if t >= 4 and t % 4 == 0:
                            copy_values(NC4 * grp + t // 4 - 1)
                        if t >= 6 and t % 4 == 2:
                            values_of(NC4 * grp + t // 4 - 1)
                    if grp + 1 < NG:
                        copy_maxima(grp + 1)
                    copy_values(NC4 * grp + NC4 - 1)
                    values_of(NC4 * grp + NC4 - 1)


def stage_l3_mix(nc, O, rem, gates):
    with Stage(nc, "l3mix") as st:
        gated = st.sb("gated", [P, NT, P])
        remote_scaled = st.sem("remote_scaled")
        local_scaled = st.sem("local_scaled")
        heads = lambda ap: ap.rearrange("p t (h k) -> p (t h) k", k=L3_K)
        gate = lambda i: bcast(gates[:, i, :, :].rearrange("p t h -> p (t h)").unsqueeze(2), P, NT * L3_H, L3_K)
        with st.block() as block:

            @block.gpsimd
            def _(pool):
                pool.tensor_tensor(heads(gated[:]), heads(rem[:]), gate(1), ALU.mult)\
                    .then_inc(remote_scaled, 1)
                pool.wait_ge(remote_scaled, 1)

            @block.vector
            def _(dve):
                dve.tensor_tensor(heads(O[:]), heads(O[:]), gate(0), ALU.mult).then_inc(local_scaled, 1)
                dve.wait_ge(local_scaled, 1)
                dve.wait_ge(remote_scaled, 1)
                dve.tensor_tensor(O[:], O[:], gated[:], ALU.add)


def layer3_attention(nc, d, g):
    q_parts = nc.dram_tensor("l3_q_parts", [3, P, S], BF16, kind="Internal").ap()
    k_parts = nc.dram_tensor("l3_k_parts", [3, P, S], BF16, kind="Internal").ap()
    with Stage(nc, "l3") as st:
        for_parts = Loads(nc, d, st, "parts", "l3_wqkv")
        for_latent = Loads(nc, d, st, "latent", "l3_wg", "l3_r_out", "head_rows", "l3_gates", "lat_causal", "ident16")
        for_local = Loads(nc, d, st, "local", "mask_q", "mask_k", "ident16")
        for_out = Loads(nc, d, st, "out", "l3_wout")
        Q = st.sb("Q", [P, 2, GROUP, S + WINDOW], BF16)
        adaln(nc, g, 3, SCALE_A, SHIFT_A, ClearOperand(st, Q))
        V_aug = st.sb("V_aug", [P, NT, L3_H, 32])
        rem = g.xn
        gates = st.sb("gates", [P, 2, NT, L3_H])
        K = st.sb("K", [P, 2, GROUP, WINDOW + S], BF16)
        loaded = [st.sem("loaded0"), st.sem("loaded1")]
        stored = st.sem("stored")
        with Stage(nc, "l3q") as st_q:
            q = st_q.sb("q", [P, S])
            qp = [st_q.sb(f"qp{i}", [P, S], BF16) for i in range(3)]
            kp = [st_q.sb(f"kp{i}", [P, S], BF16) for i in range(3)]
            stage_project_parts(nc, for_parts, "l3_wqkv", g, "l3proj", V_aug, q, qp, kp, K,
                                d["ones_l3"], (q_parts, k_parts), stored)
            stage_l3_latent(nc, for_latent, g, q, rem, gates, Q, K, q_parts, k_parts, stored, loaded)
        O = st.sb("O", [P, NT, P])
        stage_l3_local(nc, for_local, g, V_aug, Q, K, q_parts, k_parts, loaded, O)
        stage_l3_mix(nc, O, rem, gates)
        stage_project_out(nc, for_out, "l3_wout", g, "l3out", O, mod_row(g, 3, GATE_A))



E3, F3 = 8, 512
CAP = S // E3
DIGIT, DIGITS = 4, 4
CAND = 2 ** DIGIT - 1
TAKEN = -4.0 * 2 ** 16


def stage_l3_select(nc, loads, nT, slot):
    with Stage(nc, "l3sel") as st:
        cent = loads["l3_centT"]
        multiples = loads["multiples"]
        before = loads["before"]
        not_yet = loads["not_yet"]
        ones = st.sb("ones", [P, P], BF16)
        scores = st.sb("scores", [P, E3, NT])
        flip = st.sb("flip", [P, E3, NT], I32)
        half_int = st.sb("half_int", [P, 2, E3, NT], I32)
        high = st.sb("high", [P, E3, NT])
        low1 = st.sb("low1", [P, E3, NT])
        left = st.sb("left", [P, NT])
        h = st.sb("h", [P, NT])
        key = st.sb("key", [P, NT])
        above = st.sb("above", [P, NT])
        cands = st.sb("cands", [P, 1, CAND])
        threshold = st.sb("threshold", [P, 2])
        reach = st.sb("reach", [P, CAND, NT])
        part = st.sb("part", [P, CAND], BF16)
        enough = st.sb("enough", [P, CAND])
        digit = st.sb("digit", [P, 1])
        masks = st.sb("masks", [P, 2, NT], BF16)
        eq = st.sb("eq", [P, NT])
        upto = st.sb("upto", [P, NT])
        ones_row = st.sb("ones_row", [P, NT])
        greater = st.sb("greater", [P, 1])
        member = st.sb("member", [P, E3, NT])
        member16 = st.sb("member16", [P, E3, NT], BF16)
        rank = st.sb("rank", [P, E3, NT])
        base = loads["bases"]
        slot_f = st.sb("slot_f", [P, NT])
        ps_s = st.ps("ps_s", [P, BANK])
        ps_c = st.ps("ps_c", [P, 2, BANK])
        ones_ready = st.sem("ones_ready")
        scored = st.sem("scored")
        part_ready = st.sem("part_ready")
        counted = st.sem("counted")
        masks_ready = st.sem("masks_ready")
        masks_counted = st.sem("masks_counted")
        members_ready = st.sem("members_ready")
        ranked = st.sem("ranked")
        chain = st.sem("chain")
        with st.block() as block:

            @block.tensor
            def _(pe):
                pe.wait_ge(loads.done, loads.all)
                for t in range(NT):
                    mm = pe.matmul(ps_s[:, E3 * t:E3 * t + E3], nT[:, c1(t)], cent[:], start=True, stop=True)
                mm.then_inc(scored, 1)
                pe.wait_ge(ones_ready, 1)
                for e in range(E3 - 1):
                    for i in range(2 * DIGITS):
                        pe.wait_ge(part_ready, 2 * DIGITS * e + i + 1)
                        pe.matmul(ps_c[:, 0, 0:CAND], ones[:], part[:], start=True, stop=True).then_inc(counted, 1)
                    pe.wait_ge(masks_ready, e + 1)
                    m = masks[:].rearrange("p a t -> p (a t)")
                    pe.matmul(ps_c[:, 1, 0:2 * NT], ones[:], m, start=True, stop=True)
                    pe.matmul(ps_c[:, 1, 2 * NT:3 * NT], not_yet[:], masks[:, 0, :], start=True, stop=True)\
                      .then_inc(masks_counted, 1)
                pe.wait_ge(members_ready, 1)
                m = member16[:].rearrange("p e t -> p (e t)")
                pe.matmul(ps_s[:, 0:E3 * NT], before[:], m, start=True, stop=True)
                pe.matmul(ps_s[:, E3 * NT:2 * E3 * NT], ones[:], m, start=True, stop=True).then_inc(ranked, 1)

            @block.vector
            def _(dve):
                link = Chain(dve, chain)

                def search(e, half, keys, lowest):
                    result = threshold[:, half:half + 1]
                    step = 2 ** (16 - DIGIT)
                    link.mark(dve.memset(result, lowest))
                    link(dve.tensor_scalar(cands[:], multiples[:], float(step), lowest, ALU.mult, ALU.add))
                    for i in range(DIGITS):
                        link(dve.tensor_tensor(reach[:], bcast(keys.unsqueeze(1), P, CAND, NT),
                                               bcast(cands[:, 0, :].unsqueeze(2), P, CAND, NT), ALU.is_ge))
                        with nc.allow_low_precision(reason="counts up to 16 are exact in bfloat16"):
                            dve.tensor_reduce(part[:], reach[:], AX_X, ALU.add).then_inc(part_ready, 1)
                        smaller = step >> DIGIT
                        if i + 1 < DIGITS:
                            link(dve.scalar_tensor_tensor(cands[:], multiples[:], float(smaller - step), cands[:],
                                                          ALU.mult, ALU.add))
                        dve.wait_ge(counted, 2 * DIGITS * e + DIGITS * half + i + 1)
                        link(dve.tensor_scalar(enough[:], ps_c[:, 0, 0:CAND], float(CAP), 0.0, ALU.is_ge, ALU.add,
                                               accum_out=digit[:]))
                        link.mark(dve.scalar_tensor_tensor(result, digit[:], float(step), result, ALU.mult, ALU.add))
                        if i + 1 < DIGITS:
                            link.mark(dve.scalar_tensor_tensor(cands[:, 0, :], bcast(digit[:], P, CAND), float(step),
                                                               cands[:, 0, :], ALU.mult, ALU.add))
                        link.wait()
                        step = smaller

                link.mark(dve.memset(ones_row[:], 1.0))
                link.mark(dve.memset(left[:], 0.0))
                dve.memset(ones[:], 1.0).then_inc(ones_ready, 1)
                dve.wait_ge(scored, 1)
                link(dve.tensor_copy(scores[:], ps_s[:, 0:E3 * NT].rearrange("p (t e) -> p e t", e=E3)))
                bits = scores[:].bitcast(I32)
                link(dve.tensor_scalar(flip[:], bits, 31, 2 ** 31 - 1, ALU.arith_shift_right, ALU.bitwise_and))
                link(dve.tensor_tensor(flip[:], flip[:], bits, ALU.bitwise_xor))
                link.mark(dve.tensor_scalar(half_int[:, 0], flip[:], 16, None, ALU.arith_shift_right))
                link(dve.tensor_scalar(half_int[:, 1], flip[:], 2 ** 16 - 1, None, ALU.bitwise_and))
                link.mark(dve.tensor_copy(high[:], half_int[:, 0]))
                link(dve.tensor_scalar(low1[:], half_int[:, 1], 1.0, None, ALU.add))
                dve.wait_ge(loads.done, loads.all)
                for e in range(E3 - 1):
                    link(dve.tensor_tensor(h[:], high[:, e, :], left[:], ALU.add))
                    search(e, 0, h[:], -2.0 ** 15)
                    t_high, t_low = threshold[:, 0:1], threshold[:, 1:2]
                    link.mark(dve.scalar_tensor_tensor(key[:], h[:], t_high, low1[:, e, :], ALU.is_equal, ALU.mult))
                    link(dve.tensor_scalar(above[:], h[:], t_high, 2.0 ** 17, ALU.is_gt, ALU.mult))
                    link(dve.tensor_tensor(key[:], key[:], above[:], ALU.add))
                    search(e, 1, key[:], 1.0)
                    link.mark(dve.tensor_scalar(eq[:], key[:], t_low, None, ALU.is_equal))
                    link.mark(dve.tensor_scalar(masks[:, 0, :], key[:], t_low, None, ALU.is_equal))
                    dve.tensor_scalar(masks[:, 1, :], key[:], t_low, None, ALU.is_gt).then_inc(masks_ready, 1)
                    dve.wait_ge(masks_counted, e + 1)
                    equal, more, upto_here = (ps_c[:, 1, i * NT:(i + 1) * NT] for i in range(3))
                    link(dve.tensor_reduce(greater[:], more, AX_X, ALU.add))
                    link(dve.tensor_tensor_scan(upto[:], ones_row[:], equal, greater[:], ALU.mult, ALU.add))
                    link(dve.tensor_tensor(upto[:], upto[:], upto_here, ALU.add))
                    link(dve.scalar_tensor_tensor(eq[:], upto[:], float(CAP), eq[:], ALU.is_lt, ALU.mult))
                    link(dve.scalar_tensor_tensor(member[:, e, :], key[:], t_low, eq[:], ALU.is_gt, ALU.add))
                    link(dve.scalar_tensor_tensor(left[:], member[:, e, :], TAKEN, left[:], ALU.mult, ALU.add))
                link(dve.tensor_scalar(member[:, E3 - 1, :], left[:], 0.0, None, ALU.is_equal))
                dve.tensor_copy(member16[:], member[:]).then_inc(members_ready, 1)
                dve.wait_ge(ranked, 1)
                within = ps_s[:, 0:E3 * NT].rearrange("p (e t) -> p e t", e=E3)
                totals = ps_s[:, E3 * NT:2 * E3 * NT].rearrange("p (e t) -> p e t", e=E3)
                for e in range(E3):
                    link.mark(dve.tensor_tensor_scan(rank[:, e, :], ones_row[:], totals[:, e, :], 0.0, ALU.mult,
                                                     ALU.add))
                link.wait()
                link(dve.tensor_tensor(rank[:], rank[:], totals, ALU.subtract))
                link(dve.tensor_tensor(rank[:], rank[:], within, ALU.add))
                link(dve.tensor_tensor(rank[:], rank[:], base[:], ALU.add))
                link(dve.tensor_tensor(rank[:], rank[:], member[:], ALU.mult))
                link(dve.tensor_reduce(slot_f[:], rank[:].rearrange("p e t -> p t e"), AX_X, ALU.add))
                link(dve.tensor_copy(slot[:], slot_f[:]))


def stage_l3_mlp(nc, loads, g, ln_cols, n_tm, h_tm, slot, sorted_in, sorted_out):
    with Stage(nc, "l3mlp") as st:
        w1, w2, b1, b2 = (loads[name] for name in ("l3_w1", "l3_w2", "l3_b1", "l3_b2"))
        ones = st.sb("ones", [1, P])
        rows = st.sb("rows", [P, NT, P])
        rowsT = st.sb("rowsT", [P, S])
        hid = st.sb("hid", [P, 2, 4, CAP])
        y = st.sb("y", [P, NT, P])
        back = st.sb("back", [P, NT, P])
        ps_t = st.ps("ps_t", [P, 2, BANK])
        ps_h = st.ps("ps_h", [P, 4, BANK])
        ps_y = st.ps("ps_y", [P, 2, BANK])
        ones_ready = st.sem("ones_ready")
        scattered = st.sem("scattered")
        rows_loaded = [st.sem(f"rows_loaded{j}") for j in range(NC4)]
        turned = st.sem("turned")
        rows_ready = st.sem("rows_ready")
        hid_done = st.sem("hid_done")
        hid_ready = st.sem("hid_ready")
        y_done = st.sem("y_done")
        y_copied = st.sem("y_copied")
        y_stored = st.sem("y_stored")
        gathered = [st.sem(f"gathered{j}") for j in range(NC4)]
        x_complete = st.sem("x_complete")
        x_stored = st.sem("x_stored")
        chain = st.sem("chain")
        with st.block() as block:

            @block.sync
            def _(sp):
                sp.wait_ge(scattered, 16 * NT)
                tiled = lambda dram, j: dram[c4(j), :].rearrange("(t p) f -> p t f", p=P)
                for j in range(NC4):
                    sp.dma_start(rows[:, 4 * j:4 * j + 4, :], tiled(sorted_in, j)).then_inc(rows_loaded[j], 16)
                for j in range(NC4):
                    sp.wait_ge(y_copied, E3 // NC4 * (j + 1))
                    sp.dma_start(tiled(sorted_out, j), y[:, 4 * j:4 * j + 4, :]).then_inc(y_stored, 16)
                for j in range(NC4):
                    sp.wait_ge(x_complete, j + 1)
                    sp.dma_start(tiled(g.out[0], j), g.x[:, 4 * j:4 * j + 4, :]).then_inc(x_stored, 16)
                sp.wait_ge(x_stored, 16 * NC4)

            @block.gpsimd
            def _(pool):
                for t in range(NT):
                    pool.indirect_dma_start(out=sorted_in, out_offset=bass.IndirectOffsetOnAxis(
                        ap=slot[:, t:t + 1], axis=0), in_=n_tm[:, t, :], in_offset=None).then_inc(scattered, 16)
                pool.wait_ge(y_stored, 16 * NC4)
                for t in range(NT):
                    pool.indirect_dma_start(out=back[:, t, :], out_offset=None, in_=sorted_out,
                                            in_offset=bass.IndirectOffsetOnAxis(ap=slot[:, t:t + 1], axis=0))\
                        .then_inc(gathered[t // 4], 16)
                for j in range(NC4):
                    pool.wait_ge(gathered[j], 16 * 4)

            @block.tensor
            def _(pe):
                for j in range(NC4):
                    pe.wait_ge(rows_loaded[j], 16)
                    if j >= 2:
                        pe.wait_ge(rows_ready, j - 1)
                    for i in range(4):
                        mm = pe.transpose(ps_t[:, j % 2, c1(i)], rows[:, 4 * j + i, :], g.ident[:])
                    mm.then_inc(turned, 1)
                pe.wait_ge(loads.done, loads.all)
                pe.wait_ge(ones_ready, 1)

                def down(e):
                    pe.wait_ge(hid_ready, 4 * (e + 1))
                    if e >= 2:
                        pe.wait_ge(y_copied, e - 1)
                    for i in range(2):
                        dst = ps_y[:, e % 2, c1(i)]
                        for f in range(4):
                            pe.matmul(dst, hid[:, e % 2, f, c1(i)], w2[:, e, f, :], start=(f == 0), stop=False,
                                      skip_group_check=True)
                        mm = pe.matmul(dst, ones[:], b2[:, e, :], start=False, stop=True, skip_group_check=True)
                    mm.then_inc(y_done, 1)

                for e in range(E3):
                    pe.wait_ge(rows_ready, e // 2 + 1)
                    if e >= 2:
                        pe.wait_ge(hid_ready, 4 * (e - 1))
                    for f in range(4):
                        pe.matmul(ps_h[:, 2 * (e % 2) + f // 2, CAP * (f % 2):CAP * (f % 2) + CAP], w1[:, e, c1(f)],
                                  rowsT[:, CAP * e:CAP * (e + 1)], start=True, stop=True).then_inc(hid_done, 1)
                    if e >= 1:
                        down(e - 1)
                down(E3 - 1)

            @block.scalar
            def _(act):
                for j in range(NC4):
                    act.wait_ge(turned, j + 1)
                    act.activation(rowsT[:, c4(j)], ps_t[:, j % 2, :], ACT.Identity, bias=ln_cols[:, 1:2],
                                   scale=ln_cols[:, 0:1]).then_inc(rows_ready, 1)
                act.wait_ge(loads.done, loads.all)
                for e in range(E3):
                    if e >= 2:
                        act.wait_ge(y_done, e - 1)
                    for f in range(4):
                        act.wait_ge(hid_done, 4 * e + 2 * (f // 2) + 2)
                        act.activation(hid[:, e % 2, f, :],
                                       ps_h[:, 2 * (e % 2) + f // 2, CAP * (f % 2):CAP * (f % 2) + CAP],
                                       ACT.Gelu_apprx_tanh, bias=b1[:, e, f:f + 1]).then_inc(hid_ready, 1)

            @block.vector
            def _(dve):
                link = Chain(dve, chain)
                dve.memset(ones[:], 1.0).then_inc(ones_ready, 1)
                gate = bcast(mod_row(g, 3, GATE_B).unsqueeze(1), P, NT, P)
                link(dve.tensor_tensor(h_tm[:], h_tm[:], gate, ALU.mult))
                link(dve.tensor_tensor(g.x[:], g.x[:], h_tm[:], ALU.add))
                for e in range(E3):
                    dve.wait_ge(y_done, e + 1)
                    dve.tensor_copy(y[:, 2 * e:2 * e + 2, :].rearrange("p t f -> p (t f)"), ps_y[:, e % 2, 0:2 * P])\
                       .then_inc(y_copied, 1)
                for j in range(NC4):
                    dve.wait_ge(gathered[j], 16 * 4)
                    ts = slice(4 * j, 4 * j + 4)
                    link(dve.tensor_tensor(back[:, ts, :], back[:, ts, :], gate[:, ts, :], ALU.mult))
                    dve.tensor_tensor(g.x[:, ts, :], g.x[:, ts, :], back[:, ts, :], ALU.add).then_inc(x_complete, 1)


def stage_affine(nc, name, out, in_, scale_row, shift_row):
    SPLIT = 10
    with Stage(nc, name) as st:
        dve_step = st.sem("dve_step")
        pool_step = st.sem("pool_step")

        def affine(eng, step, tiles):
            n = tiles.stop - tiles.start
            spread = lambda row: bcast(row.unsqueeze(1), P, n, P)
            eng.tensor_tensor(out[:, tiles, :], in_[:, tiles, :], spread(scale_row), ALU.mult).then_inc(step, 1)
            eng.wait_ge(step, 1)
            eng.tensor_tensor(out[:, tiles, :], out[:, tiles, :], spread(shift_row), ALU.add).then_inc(step, 1)
            eng.wait_ge(step, 2)

        with st.block() as block:

            @block.vector
            def _(dve):
                affine(dve, dve_step, slice(0, SPLIT))

            @block.gpsimd
            def _(pool):
                affine(pool, pool_step, slice(SPLIT, NT))


def layer3_experts(nc, d, g):
    sorted_in = nc.dram_tensor("sorted_in", [S, P], F32, kind="Internal").ap()
    sorted_out = nc.dram_tensor("sorted_out", [S, P], F32, kind="Internal").ap()
    with Stage(nc, "l3f") as st:
        for_norm = Loads(nc, d, st, "norm", "l3_lncols")
        for_select = Loads(nc, d, st, "select", "l3_centT", "multiples", "before", "not_yet", "bases")
        for_mlp = Loads(nc, d, st, "mlp", "l3_w1", "l3_w2", "l3_b1", "l3_b2")
        adaln(nc, g, 3, SCALE_B, SHIFT_B)
        h_tm = st.sb("h_tm", [P, NT, P])
        n_tm = st.sb("n_tm", [P, NT, P])
        slot = st.sb("slot", [P, NT], I32)
        ln_cols = for_norm["l3_lncols"]
        nc.scalar.wait_ge(for_norm.done, for_norm.all)
        stage_affine(nc, "l3h", h_tm, g.xn, mod_row(g, 3, SCALE_B), mod_row(g, 3, SHIFT_B))
        stage_norm(nc, g, "l3norm", h_tm, n_tm, g.hT, ln_cols[:, 0:1], ln_cols[:, 1:2])
        stage_l3_select(nc, for_select, g.hT, slot)
        stage_l3_mlp(nc, for_mlp, g, ln_cols, n_tm, h_tm, slot, sorted_in, sorted_out)



class Persistent:
    pass


def program(nc, d, out, stages=None):
    with ExitStack() as ctx:
        g = Persistent()

        def sb(name, shape, dt=F32):
            return ctx.enter_context(nc.sbuf_tensor(name, shape, dt))

        d = {name: ap.bitcast(BF16) if name in BF16_CONSTANTS else ap for name, ap in d.items()}
        g.rows_finished = set()
        g.x = sb("x_res", [P, NT, P])
        g.xn = sb("xn", [P, NT, P])
        g.hT = sb("hT", [P, S])
        g.mod_rows = sb("mod_rows", [P, 4, 6, P])
        g.mod_cols = sb("mod_cols", [P, 24])
        g.ident = sb("ident_sb", [P, P])
        g.out = out
        stage_setup(nc, d, g)
        for layer_part in (stages or ALL_STAGES):
            with nc.cleanup_on_exit():
                layer_part(nc, d, g)


ALL_STAGES = [layer0_attention, layer0_slots, layer1_delta, layer1_experts,
              layer2_spiking, layer2_product, layer3_attention, layer3_experts]


BF16_CONSTANTS = ("ident16", "lat_causal", "mask_q", "mask_k", "before", "not_yet",
                  "ones_l0", "ones_l3")


def lay_out(inp):

    def bits16(constant):
        return (constant.astype(np.float32).view(np.uint32) >> 16).astype(np.uint16)

    a = {k: np.asarray(v) for k, v in inp.items()}
    heads = lambda w: w.transpose(1, 0, 2).reshape(P, P)
    d = {
        "x": a["L0_attn_q"][0],
        "c_cols": np.concatenate([a[f"L{l}_c"] for l in range(4)], 0).T,
        "wmod": np.stack([a[f"L{l}_wmod"] for l in range(4)], 1),
        "ident": np.eye(P, dtype=np.float32),
        "ident16": bits16(np.eye(P)),
        "ones_l0": bits16(np.ones((3, HEAD_BUFS, S))), "ones_l3": bits16(np.ones((3, 2, GROUP, WINDOW + S))),
        "l0_wqkv": np.stack([heads(a[f"L0_attn_W_{n}"]) for n in ("query", "key", "val")], 1),
        "l0_wout": a["L0_attn_W_out"].reshape(P, P),
    }
    w1T = a["L0_ffn_w1"].T
    d.update({
        "l0_b1": a["L0_ffn_b1"][:, None], "l0_w1T": np.stack([w1T[:P], w1T[P:]], 1),
        "l0_w2T": np.concatenate([a["L0_ffn_w2"].T, a["L0_ffn_b2"][None]], 0),
        "l0_tau": np.repeat(a["L0_ffn_tau"][None], P, 0),
        "l0_slots": a["L0_ffn_slot_init"], "l0_slot_scale": a["L0_ffn_slot_scale"],
        "l0_wihT": a["L0_ffn_gru_wih"].T.reshape(P, 3, P), "l0_whhT": a["L0_ffn_gru_whh"].T.reshape(P, 3, P),
        "l0_bih": a["L0_ffn_gru_bih"][None], "l0_bhh": a["L0_ffn_gru_bhh"][None],
        "l0_wvT": a["L0_ffn_wv"].T, "l0_bv": a["L0_ffn_bv"][:, None], "l0_woT": a["L0_ffn_wo"].T,
        "l0_bo": a["L0_ffn_bo"][None],
    })
    i, j = np.arange(P)[:, None], np.arange(P)[None, :]
    level = lambda s: (i // (2 * s) == j // (2 * s)) & (i // s % 2 == 1) & (j // s % 2 == 0)
    rows = lambda v: np.repeat(v[None], P, 0)
    d.update({
        "masks": np.stack([level(s) for s in (1,) + LEVELS] + [j >= i], 1).astype(np.float32),
        "iota": i.astype(np.float32), "iota_row": rows(np.arange(EXPERTS, dtype=np.float32)),
        "carry": np.broadcast_to((np.arange(NT) > 0).astype(np.float32), (P, EXPERTS, NT)),
        "l1_wq": a["L1_attn_Wq"],
        "l1_wkvb": np.concatenate([a["L1_attn_Wk"], a["L1_attn_Wv"], a["L1_attn_Wb"][:, None]], 1),
        "l1_lng": rows(a["L1_attn_ln_g"]), "l1_lnb": rows(a["L1_attn_ln_b"]),
        "l1_gateT": a["L1_ffn_gate_w"].T, "l1_gate_b": a["L1_ffn_gate_b"][None],
        "l1_expert_w": a["L1_ffn_expert_w"], "l1_expert_b": a["L1_ffn_expert_b"],
    })
    d.update({
        "l2_wrkvo": np.stack([a[f"L2_attn_W{n}"].T for n in "rkvo"], 1),
        "l2_w1T": a["L2_attn_W1"].T.reshape(P, 4, P), "l2_b1": a["L2_attn_b1"].reshape(4, P).T,
        "l2_w2T": a["L2_attn_W2"].T.reshape(4, P, P).transpose(1, 0, 2), "l2_b2": a["L2_attn_b2"][:, None],
        "l2_ln1g": rows(a["L2_attn_ln1_g"]), "l2_ln1b": rows(a["L2_attn_ln1_b"]),
        "l2_ln1cols": np.stack([a["L2_attn_ln1_g"], a["L2_attn_ln1_b"]], 1),
        "l2_ln2g": rows(a["L2_attn_ln2_g"]), "l2_ln2b": rows(a["L2_attn_ln2_b"]),
        "l2_CBT": a["L2_ffn_CB"].T, "l2_SCB": rows(a["L2_ffn_SCB"]), "l2_bias": rows(a["L2_ffn_bias"]),
    })
    neg = lambda seen: bits16(np.where(seen, 0.0, MASK_BIG))
    c = np.arange(SPAN)[None, :]
    seen_q = (c > i) & (c <= i + WINDOW)
    seen_k = (c >= i) & (c < i + WINDOW)
    tokens = i + P * np.arange(NT)[None, :]
    d.update({
        "l3_wqkv": np.stack([a[f"L3_attn_w{n}"] for n in "qkv"], 1),
        "l3_wg": np.stack([a[f"L3_attn_wg{n}"] for n in "qkv"], 1),
        "l3_r_out": a["L3_attn_r_out_w"], "l3_wout": a["L3_attn_w_out"],
        "l3_gates": np.stack([a["L3_attn_gate_local_w"].reshape(P), a["L3_attn_gate_remote_w"].reshape(P)], 1),
        "head_rows": (i // L3_K == np.arange(L3_H)[None, :]).astype(np.float32),
        "lat_causal": neg(np.arange(LATENTS)[None, None, :] <= tokens[:, :, None] // (S // LATENTS)),
        "mask_q": neg(np.stack([seen_q & (c >= WINDOW), seen_q], 1)[:, :, None, :]),
        "mask_k": neg(seen_k[:, None, :]),
        "l3_centT": a["L3_ffn_centroids"].T,
        "l3_lncols": np.stack([a["L3_ffn_ln_g"], a["L3_ffn_ln_b"]], 1),
        "l3_w1": a["L3_ffn_w1"].transpose(1, 0, 2),
        "l3_w2": a["L3_ffn_w2"].reshape(E3, 4, P, P).transpose(2, 0, 1, 3),
        "l3_b1": a["L3_ffn_b1"].reshape(E3, 4, P).transpose(2, 0, 1), "l3_b2": a["L3_ffn_b2"][None],
        "before": bits16(i < j),
        "bases": np.broadcast_to((CAP * np.arange(E3, dtype=np.float32))[None, :, None], (P, E3, NT)),
        "multiples": rows(np.arange(1, CAND + 1, dtype=np.float32)[None]),
        "not_yet": bits16(-1.0 * (i >= j)),
    })
    return {k: np.ascontiguousarray(v) for k, v in d.items()}


OUT_SHAPE = (1, S, P)


def kernel(**inputs):
    import concourse.bacc as _bacc
    from concourse.bass_utils import run_bass_kernel_spmd as _run

    nc = _bacc.Bacc("TRN2", target_bir_lowering=False, num_devices=1)
    arrays, d = {}, {}
    for name, a in lay_out(inputs).items():
        arrays[f"in_{name}_dram"] = a
        d[name] = nc.dram_tensor(f"in_{name}_dram", a.shape, mybir.dt.from_np(a.dtype), kind="ExternalInput").ap()
    out = nc.dram_tensor("out_0_dram", OUT_SHAPE, F32, kind="ExternalOutput").ap()
    program(nc, d, out)
    r = _run(nc, [arrays], core_ids=[0])
    return r.results[0]["out_0_dram"]
```
